# Optimizing a Trainium2 kernel written in Bass

```python
import numpy as np
import jax
import jax.numpy as jnp

def _softmax(x, axis=-1):
    return jax.nn.softmax(x, axis=axis)

def _gelu(x):
    return jax.nn.gelu(x, approximate=True)

def _silu(x):
    return jax.nn.silu(x)

def _sigmoid(x):
    return jax.nn.sigmoid(x)

def _layernorm(x, axis=-1, eps=1e-05):
    m = jnp.mean(x, axis=axis, keepdims=True)
    v = jnp.var(x, axis=axis, keepdims=True)
    return (x - m) / jnp.sqrt(v + eps)

def _scatter_add(tgt, idx, src, axis=0):
    return tgt.at[idx].add(src)

def _segment_sum(src, seg, n):
    return jax.ops.segment_sum(src, seg, n)
kernel_name = 'mk_perceiver_d4_seqx_r2_40ef1f'

def setup_inputs(seed: int=0):
    np.random.seed(seed)
    _w = jnp.asarray

    def _rec_inputs():
        import jax
        import jax.numpy as jnp
        _rk = jax.random.key(seed)
        x = -0.0003929 + 0.9999 * jax.random.normal(jax.random.fold_in(_rk, 1), (8, 64, 512), jnp.float32)
        _lenS = 64 - jax.random.randint(jax.random.fold_in(_rk, 7), (8,), 0, max(1, 64 // 4) + 1, jnp.int32)
        _lenS2 = 512 - jax.random.randint(jax.random.fold_in(_rk, 8), (8,), 0, max(1, 512 // 4) + 1, jnp.int32)
        _ctx_1024P = jax.random.normal(jax.random.fold_in(_rk, 11), (8, 16, 512), jnp.float32)
        _ctx_1024c = jax.random.dirichlet(jax.random.fold_in(_rk, 511), 0.3 * jnp.ones((16,), jnp.float32), (8, 512))
        _ctx_1024t = jnp.einsum('bsk,bkd->bsd', _ctx_1024c, _ctx_1024P)
        _ctx_1024t = _ctx_1024t * jax.lax.rsqrt(jnp.mean(jnp.square(_ctx_1024t)) + 1e-12) * 0.953939
        ctx_1024 = 0.00208318 + 0.999174 * (_ctx_1024t + 0.3 * jax.random.normal(jax.random.fold_in(_rk, 611), (8, 512, 512), jnp.float32))
        _validS = jnp.arange(64)[None, :] < _lenS[:, None]
        _validS2 = jnp.arange(512)[None, :] < _lenS2[:, None]
        _causal = jnp.tril(jnp.ones((64, 64), dtype=bool))
        mask_BxSxS2_ff0 = jnp.where(jnp.ones((8, 64, 512), dtype=bool), 0.0, -1000000000.0).astype(jnp.float32)
        return (x, ctx_1024, mask_BxSxS2_ff0)
    x, ctx_1024, mask_BxSxS2_ff0 = _rec_inputs()

    def _L0_xattn_setup():
        import jax, jax.numpy as jnp
        import numpy as np
        NUM_HEADS = 16
        DIM = 512
        key = jax.random.key(seed)
        ks = jax.random.split(key, 12)
        B, N, T, C = (4, 2048, 77, DIM)
        s = 1.0 / np.sqrt(C)
        return {'hidden_states': jax.random.normal(ks[0], (B, N, C), jnp.float32), 'encoder_hidden_states': jax.random.normal(ks[1], (B, T, C), jnp.float32), 'attention_mask': jnp.zeros((B, N, T), jnp.float32), 'Wq': jax.random.normal(ks[2], (C, C), jnp.float32) * s, 'bq': jnp.zeros((C,), jnp.float32), 'Wk': jax.random.normal(ks[3], (C, C), jnp.float32) * s, 'bk': jnp.zeros((C,), jnp.float32), 'Wv': jax.random.normal(ks[4], (C, C), jnp.float32) * s, 'bv': jnp.zeros((C,), jnp.float32), 'Wo': jax.random.normal(ks[5], (C, C), jnp.float32) * s, 'bo': jnp.zeros((C,), jnp.float32)}
    _L0_xattn_all = _L0_xattn_setup()
    _L0_xattn_in = {k: v for k, v in _L0_xattn_all.items() if k in ('Wq', 'bq', 'Wk', 'bk', 'Wv', 'bv', 'Wo', 'bo')}
    del _L0_xattn_all

    def _L0_attn_setup():
        import jax, jax.numpy as jnp
        import numpy as np
        B, T, DIM, H = (2, 1024, 512, 16)
        HD = DIM // H

        def _custom_softmax(a):
            a = jnp.clip(a, -100.0, 100.0)
            m = jnp.max(a, axis=-1, keepdims=True)
            e = jnp.exp(a - m)
            p = e / (jnp.sum(e, axis=-1, keepdims=True) + 1e-06)
            p = p + 1e-08
            return p / jnp.sum(p, axis=-1, keepdims=True)
        key = jax.random.key(seed)
        k1, k2, k3 = jax.random.split(key, 3)
        x = jax.random.normal(k1, (B, T, DIM), dtype=jnp.float32)
        w_qkv = jax.random.normal(k2, (3 * DIM, DIM), dtype=jnp.float32) / np.sqrt(DIM)
        w_proj = jax.random.normal(k3, (DIM, DIM), dtype=jnp.float32) / np.sqrt(DIM)
        return {'x': x, 'w_qkv': w_qkv, 'w_proj': w_proj}
    _L0_attn_all = _L0_attn_setup()
    _L0_attn_in = {k: v for k, v in _L0_attn_all.items() if k in ('w_qkv', 'w_proj')}
    del _L0_attn_all

    def _L0_ffn_setup():
        import jax, jax.numpy as jnp
        import numpy as np
        EPS = 1e-05
        LN_EPS = 1e-05
        NUM_EXPERTS = 8
        TOP_K = 2
        HIDDEN = 512
        INTER = 1024

        def _swiglu(x, wg, wu, wd):
            return jax.nn.silu(x @ wg) * (x @ wu) @ wd
        key = jax.random.key(seed)
        ks = jax.random.split(key, 10)
        B, S, H, I, E = (8, 2048, HIDDEN, INTER, NUM_EXPERTS)
        std_h = 1.0 / np.sqrt(H)
        std_i = 1.0 / np.sqrt(I)
        return {'x': jax.random.normal(ks[0], (B, S, H), dtype=jnp.float32), 'ln_scale': jnp.ones((H,), dtype=jnp.float32), 'ln_bias': jnp.zeros((H,), dtype=jnp.float32), 'gate_w': jax.random.normal(ks[1], (E, H), dtype=jnp.float32) * 0.01, 'Wg': jax.random.normal(ks[2], (E, H, I), dtype=jnp.float32) * std_h, 'Wu': jax.random.normal(ks[3], (E, H, I), dtype=jnp.float32) * std_h, 'Wd': jax.random.normal(ks[4], (E, I, H), dtype=jnp.float32) * std_i, 'sWg': jax.random.normal(ks[5], (H, I), dtype=jnp.float32) * std_h, 'sWu': jax.random.normal(ks[6], (H, I), dtype=jnp.float32) * std_h, 'sWd': jax.random.normal(ks[7], (I, H), dtype=jnp.float32) * std_i}
    _L0_ffn_all = _L0_ffn_setup()
    _L0_ffn_in = {k: v for k, v in _L0_ffn_all.items() if k in ('ln_scale', 'ln_bias', 'gate_w', 'Wg', 'Wu', 'Wd', 'sWg', 'sWu', 'sWd')}
    del _L0_ffn_all

    def _L1_xattn_setup():
        import jax, jax.numpy as jnp
        import numpy as np
        import math
        D = 512
        H = 8
        HD = D // H
        TEMP = math.sqrt(D)
        EPS = 1e-05

        def _layernorm(x, g, b):
            mu = jnp.mean(x, axis=-1, keepdims=True)
            var = jnp.var(x, axis=-1, keepdims=True)
            return (x - mu) * jax.lax.rsqrt(var + EPS) * g + b
        key = jax.random.key(seed)
        ks = jax.random.split(key, 8)
        B, Lq, Lk = (4, 1024, 1024)
        Q = jax.random.normal(ks[0], (B, Lq, D), dtype=jnp.float32)
        K = jax.random.normal(ks[1], (B, Lk, D), dtype=jnp.float32)
        V = jax.random.normal(ks[2], (B, Lk, D), dtype=jnp.float32)
        Wq = jax.random.normal(ks[3], (D, D), dtype=jnp.float32) * 0.02
        Wk = jax.random.normal(ks[4], (D, D), dtype=jnp.float32) * 0.02
        Wv = jax.random.normal(ks[5], (D, D), dtype=jnp.float32) * 0.02
        Wo = jax.random.normal(ks[6], (D, D), dtype=jnp.float32) * 0.02
        pre_g = jnp.ones((D,), jnp.float32)
        pre_b = jnp.zeros((D,), jnp.float32)
        ln_g = jnp.ones((D,), jnp.float32)
        ln_b = jnp.zeros((D,), jnp.float32)
        return {'Q': Q, 'K': K, 'V': V, 'Wq': Wq, 'Wk': Wk, 'Wv': Wv, 'Wo': Wo, 'pre_g': pre_g, 'pre_b': pre_b, 'ln_g': ln_g, 'ln_b': ln_b}
    _L1_xattn_all = _L1_xattn_setup()
    _L1_xattn_in = {k: v for k, v in _L1_xattn_all.items() if k in ('Wq', 'Wk', 'Wv', 'Wo', 'pre_g', 'pre_b', 'ln_g', 'ln_b')}
    del _L1_xattn_all

    def _L1_attn_setup():
        import jax, jax.numpy as jnp
        import numpy as np
        B, S, DM, DI, H = (2, 1024, 512, 1024, 32)
        HD = DI // H
        G = 32

        def _forward(x, in_proj_W, in_proj_b, conv_w, conv_b, dyn_W, dyn_b, dt_c, selB_W, selC_W, seldt_W, beta_W, beta_b, rg_W, rg_b, ug_W, ug_b, Q_W, out_W, D, rms_w, gn_w, gn_b):
            b, s, _ = x.shape
            residual = x
            xn = x * jax.lax.rsqrt(jnp.mean(x * x, -1, keepdims=True) + 1e-06) * rms_w
            proj = xn @ in_proj_W.T + in_proj_b
            z = proj[..., :DI]
            K = proj[..., DI:3 * DI].reshape(b, s, DI, 2)
            V = proj[..., 3 * DI:]
            vc = jax.lax.conv_general_dilated(V.transpose(0, 2, 1), conv_w[:, None, :], (1,), [(3, 0)], feature_group_count=DI, dimension_numbers=('NCH', 'OIH', 'NCH'))
            u = jax.nn.silu(vc + conv_b[None, :, None]).transpose(0, 2, 1)
            dyn = u @ dyn_W.T + dyn_b
            alpha = jax.nn.softplus(dyn[..., :H])
            omega = dyn[..., H:2 * H] + dyn[..., 2 * H:3 * H]
            rope = 1.0 / 10000.0 ** (jnp.arange(H, dtype=jnp.float32) / H)
            omega = omega + jnp.arange(s, dtype=jnp.float32)[None, :, None] * rope
            dt = jax.nn.softplus(dt_c) / (alpha + jnp.abs(omega) + 0.0001)
            dt = dt + jax.nn.softplus(u @ seldt_W.T)
            sel_B = (u @ selB_W.T).reshape(b, s, H, 1, 2)
            sel_C = (u @ selC_W.T).reshape(b, s, H, 1, 2)
            Kh = K.reshape(b, s, H, HD, 2) * sel_B
            a = 0.5 * dt * alpha
            w = 0.5 * dt * omega
            det = (1.0 + a) ** 2 + w * w
            lam2 = ((1.0 - a) ** 2 + w * w) / det
            r_gate = jax.nn.sigmoid(u @ rg_W.T + rg_b)
            vp = jnp.sqrt(jnp.clip(1.0 - lam2 ** r_gate, 1e-06))
            u_gate = jax.nn.sigmoid(u @ ug_W.T + ug_b)
            Vg = u.reshape(b, s, H, HD) * (vp * u_gate)[..., None]
            Q = (u @ Q_W.T).reshape(b, s, H, HD, 2) * sel_C
            beta = jax.nn.sigmoid(u @ beta_W.T + beta_b)
            A11 = (1.0 - a * a - w * w) / det
            A12 = 2.0 * w / det

            def step(Sc, inp):
                a11, a12, bt, k, v = inp
                S0, S1 = (Sc[..., 0], Sc[..., 1])
                r0 = a11[..., None] * S0 + a12[..., None] * S1
                r1 = -a12[..., None] * S0 + a11[..., None] * S1
                Sr = jnp.stack([r0, r1], -1)
                err = v - jnp.sum(k * Sr, -1)
                Sn = Sr + bt[..., None, None] * err[..., None] * k
                return (Sn, Sn)
            xs = (jnp.swapaxes(A11, 0, 1), jnp.swapaxes(A12, 0, 1), jnp.swapaxes(beta, 0, 1), jnp.swapaxes(Kh, 0, 1), jnp.swapaxes(Vg, 0, 1))
            S0 = jnp.zeros((b, H, HD, 2), x.dtype)
            _, Y = jax.lax.scan(step, S0, xs)
            Y = jnp.moveaxis(Y, 0, 1)
            y = jnp.sum(Q * Y, -1).reshape(b, s, DI)
            yg = y.transpose(0, 2, 1).reshape(b, G, DI // G, s)
            mu = jnp.mean(yg, (2, 3), keepdims=True)
            var = jnp.var(yg, (2, 3), keepdims=True)
            yg = (yg - mu) * jax.lax.rsqrt(var + 1e-05)
            y = (yg.reshape(b, DI, s) * gn_w[None, :, None] + gn_b[None, :, None]).transpose(0, 2, 1)
            y = y * jax.nn.silu(z)
            y = y + D * u
            return residual + y @ out_W.T
        key = jax.random.key(seed)
        ks = list(jax.random.split(key, 12))
        r = lambda k, shp, std: jax.random.normal(k, shp, jnp.float32) * std
        sel_std = 1.0 / float(np.sqrt(DI))
        return dict(x=jax.random.normal(ks[0], (B, S, DM), jnp.float32), in_proj_W=r(ks[1], (4 * DI, DM), 0.02), in_proj_b=jnp.zeros((4 * DI,), jnp.float32), conv_w=r(ks[2], (DI, 4), 0.3), conv_b=jnp.zeros((DI,), jnp.float32), dyn_W=r(ks[3], (3 * H, DI), 0.02), dyn_b=jnp.zeros((3 * H,), jnp.float32), dt_c=jnp.full((H,), 0.5, jnp.float32), selB_W=r(ks[4], (2 * H, DI), sel_std), selC_W=r(ks[5], (2 * H, DI), sel_std), seldt_W=r(ks[6], (H, DI), sel_std), beta_W=r(ks[7], (H, DI), sel_std), beta_b=jnp.zeros((H,), jnp.float32), rg_W=r(ks[8], (H, DI), sel_std), rg_b=jnp.ones((H,), jnp.float32), ug_W=r(ks[9], (H, DI), sel_std), ug_b=jnp.full((H,), -1.0, jnp.float32), Q_W=jnp.repeat(jnp.eye(DI, dtype=jnp.float32), 2, axis=0), out_W=r(ks[10], (DM, DI), 0.02), D=jnp.zeros((DI,), jnp.float32), rms_w=jnp.ones((DM,), jnp.float32), gn_w=jnp.ones((DI,), jnp.float32), gn_b=jnp.zeros((DI,), jnp.float32))
    _L1_attn_all = _L1_attn_setup()
    _L1_attn_in = {k: v for k, v in _L1_attn_all.items() if k in ('in_proj_W', 'in_proj_b', 'conv_w', 'conv_b', 'dyn_W', 'dyn_b', 'dt_c', 'selB_W', 'selC_W', 'seldt_W', 'beta_W', 'beta_b', 'rg_W', 'rg_b', 'ug_W', 'ug_b', 'Q_W', 'out_W', 'D', 'rms_w', 'gn_w', 'gn_b')}
    del _L1_attn_all

    def _L1_ffn_setup():
        import jax, jax.numpy as jnp
        import numpy as np
        LN_EPS = 1e-05

        def _layernorm(x, g, b):
            m = jnp.mean(x, axis=-1, keepdims=True)
            v = jnp.mean(jnp.square(x - m), axis=-1, keepdims=True)
            return (x - m) * jax.lax.rsqrt(v + LN_EPS) * g + b
        K_TOP = 2
        key = jax.random.key(seed)
        ks = jax.random.split(key, 4)
        B, N, D, E = (8, 1024, 512, 4)
        s = 0.02
        return {'x': jax.random.normal(ks[0], (B, N, D), dtype=jnp.float32), 'gate_W': jax.random.normal(ks[1], (D, E), dtype=jnp.float32) * s, 'gate_b': jnp.zeros((E,), jnp.float32), 'W1': jax.random.normal(ks[2], (E, D, D), dtype=jnp.float32) * s, 'b1': jnp.zeros((E, D), jnp.float32), 'g1': jnp.ones((E, D), jnp.float32), 'be1': jnp.zeros((E, D), jnp.float32), 'W2': jax.random.normal(ks[3], (E, D, D), dtype=jnp.float32) * s, 'b2': jnp.zeros((E, D), jnp.float32), 'g2': jnp.ones((E, D), jnp.float32), 'be2': jnp.zeros((E, D), jnp.float32)}
    _L1_ffn_all = _L1_ffn_setup()
    _L1_ffn_in = {k: v for k, v in _L1_ffn_all.items() if k in ('gate_W', 'gate_b', 'W1', 'b1', 'g1', 'be1', 'W2', 'b2', 'g2', 'be2')}
    del _L1_ffn_all

    def _L2_xattn_setup():
        import jax, jax.numpy as jnp
        import numpy as np
        B, SQ, SK, D, H = (4, 1024, 1024, 512, 16)
        SCALE = (D / H) ** 0.5
        key = jax.random.key(seed)
        ks = jax.random.split(key, 8)
        s = 1.0 / np.sqrt(D)
        return {'x1': jax.random.normal(ks[0], (B, SQ, D), dtype=jnp.float32), 'x2': jax.random.normal(ks[1], (B, SK, D), dtype=jnp.float32), 'Wq': jax.random.uniform(ks[2], (D, D), jnp.float32, -s, s), 'bq': jax.random.uniform(ks[3], (D,), jnp.float32, -s, s), 'Wk': jax.random.uniform(ks[4], (D, D), jnp.float32, -s, s), 'bk': jax.random.uniform(ks[5], (D,), jnp.float32, -s, s), 'Wv': jax.random.uniform(ks[6], (D, D), jnp.float32, -s, s), 'bv': jax.random.uniform(ks[7], (D,), jnp.float32, -s, s)}
    _L2_xattn_all = _L2_xattn_setup()
    _L2_xattn_in = {k: v for k, v in _L2_xattn_all.items() if k in ('Wq', 'bq', 'Wk', 'bk', 'Wv', 'bv')}
    del _L2_xattn_all

    def _L2_attn_setup():
        import jax, jax.numpy as jnp
        import numpy as np
        L, H = (2, 16)
        B, T, C = (2, 1024, 512)
        EPS = 1e-05

        def layernorm(x, g, b):
            mu = jnp.mean(x, axis=-1, keepdims=True)
            var = jnp.mean((x - mu) ** 2, axis=-1, keepdims=True)
            return (x - mu) / jnp.sqrt(var + EPS) * g + b
        key = jax.random.key(seed)
        ks = jax.random.split(key, 8)
        s = 0.02
        return {'x': jax.random.normal(ks[0], (B, T, C), jnp.float32), 'ln1_g': jnp.ones((L, C), jnp.float32), 'ln1_b': jnp.zeros((L, C), jnp.float32), 'wq': jax.random.normal(ks[1], (L, C, C), jnp.float32) * s, 'bq': jnp.zeros((L, C), jnp.float32), 'wk': jax.random.normal(ks[2], (L, C, C), jnp.float32) * s, 'bk': jnp.zeros((L, C), jnp.float32), 'wv': jax.random.normal(ks[3], (L, C, C), jnp.float32) * s, 'bv': jnp.zeros((L, C), jnp.float32), 'wo': jax.random.normal(ks[4], (L, C, C), jnp.float32) * s, 'bo': jnp.zeros((L, C), jnp.float32), 'ln2_g': jnp.ones((L, C), jnp.float32), 'ln2_b': jnp.zeros((L, C), jnp.float32), 'w1': jax.random.normal(ks[5], (L, C, 4 * C), jnp.float32) * s, 'b1': jnp.zeros((L, 4 * C), jnp.float32), 'w2': jax.random.normal(ks[6], (L, 4 * C, C), jnp.float32) * s, 'b2': jnp.zeros((L, C), jnp.float32), 'lnf_g': jnp.ones((C,), jnp.float32), 'lnf_b': jnp.zeros((C,), jnp.float32)}
    _L2_attn_all = _L2_attn_setup()
    _L2_attn_in = {k: v for k, v in _L2_attn_all.items() if k in ('ln1_g', 'ln1_b', 'wq', 'bq', 'wk', 'bk', 'wv', 'bv', 'wo', 'bo', 'ln2_g', 'ln2_b', 'w1', 'b1', 'w2', 'b2', 'lnf_g', 'lnf_b')}
    del _L2_attn_all

    def _L2_ffn_setup():
        import jax, jax.numpy as jnp
        import numpy as np
        CAPACITY_FACTOR = 1.0

        def _route(token_inputs, Wg, capacity):
            dt = token_inputs.dtype
            logits = jnp.einsum('bnd,de->bne', token_inputs, Wg)
            gates = jax.nn.softmax(logits, axis=-1)
            expert_idx = jnp.argmax(gates, axis=-1)
            mask = jax.nn.one_hot(expert_idx, Wg.shape[1], dtype=dt)
            gate = jnp.sum(gates * mask, axis=-1)
            pos = jnp.cumsum(mask, axis=1) * mask - mask
            keep = mask * (pos < capacity).astype(dt)
            pos_oh = jax.nn.one_hot(pos.astype(jnp.int32), capacity, dtype=dt)
            dispatch = keep[..., None] * pos_oh
            combine = dispatch * gate[:, :, None, None]
            return (dispatch, combine)
        key = jax.random.key(seed)
        k1, k2, k3, k4 = jax.random.split(key, 4)
        B, N, D, E, H = (8, 1024, 512, 8, 2048)
        return {'token_inputs': jax.random.normal(k1, (B, N, D), dtype=jnp.float32), 'Wg': jax.random.normal(k2, (D, E), dtype=jnp.float32) * 0.02, 'W1': jax.random.normal(k3, (E, D, H), dtype=jnp.float32) * 0.02, 'W2': jax.random.normal(k4, (E, H, D), dtype=jnp.float32) * 0.02}
    _L2_ffn_all = _L2_ffn_setup()
    _L2_ffn_in = {k: v for k, v in _L2_ffn_all.items() if k in ('Wg', 'W1', 'W2')}
    del _L2_ffn_all

    def _L3_xattn_setup():
        import jax, jax.numpy as jnp
        import numpy as np
        HIDDEN = 512
        HEADS = 16
        HEAD_DIM = HIDDEN // HEADS
        key = jax.random.key(seed)
        ks = jax.random.split(key, 11)
        B, S = (4, 1024)
        scale = 1.0 / np.sqrt(HIDDEN)
        inp = {'queries': jax.random.normal(ks[0], (B, S, HIDDEN), jnp.float32), 'keys': jax.random.normal(ks[1], (B, S, HIDDEN), jnp.float32), 'values': jax.random.normal(ks[2], (B, S, HIDDEN), jnp.float32), 'Wq': jax.random.normal(ks[3], (HIDDEN, HIDDEN), jnp.float32) * scale, 'bq': jnp.zeros((HIDDEN,), jnp.float32), 'Wk': jax.random.normal(ks[4], (HIDDEN, HIDDEN), jnp.float32) * scale, 'bk': jnp.zeros((HIDDEN,), jnp.float32), 'Wv': jax.random.normal(ks[5], (HIDDEN, HIDDEN), jnp.float32) * scale, 'bv': jnp.zeros((HIDDEN,), jnp.float32), 'Wo': jax.random.normal(ks[6], (HIDDEN, HIDDEN), jnp.float32) * scale, 'bo': jnp.zeros((HIDDEN,), jnp.float32)}
        return inp
    _L3_xattn_all = _L3_xattn_setup()
    _L3_xattn_in = {k: v for k, v in _L3_xattn_all.items() if k in ('Wq', 'bq', 'Wk', 'bk', 'Wv', 'bv', 'Wo', 'bo')}
    del _L3_xattn_all

    def _L3_attn_setup():
        import jax, jax.numpy as jnp
        import numpy as np
        D_MODEL = 512
        NUM_HEADS = 16
        HEAD_DIM = D_MODEL // NUM_HEADS
        D_FF = 2048
        EPS = 1e-05

        def layer_norm(x, gamma, beta):
            mu = jnp.mean(x, axis=-1, keepdims=True)
            var = jnp.mean((x - mu) ** 2, axis=-1, keepdims=True)
            return (x - mu) * jax.lax.rsqrt(var + EPS) * gamma + beta

        def apply_rope(t):
            S, d = (t.shape[-2], t.shape[-1])
            inv_freq = 1.0 / 10000.0 ** (jnp.arange(0, d, 2, dtype=jnp.float32) / d)
            angles = jnp.arange(S, dtype=jnp.float32)[:, None] * inv_freq[None, :]
            sin, cos = (jnp.sin(angles), jnp.cos(angles))
            tp = t.reshape(*t.shape[:-1], d // 2, 2)
            t0, t1 = (tp[..., 0], tp[..., 1])
            rot = jnp.stack([t0 * cos - t1 * sin, t0 * sin + t1 * cos], axis=-1)
            return rot.reshape(t.shape)
        key = jax.random.key(seed)
        ks = jax.random.split(key, 18)
        s = 0.02
        d, f = (D_MODEL, D_FF)
        return {'x': jax.random.normal(ks[0], (2, 1024, d), dtype=jnp.float32), 'Wq': jax.random.normal(ks[1], (d, d), dtype=jnp.float32) * s, 'bq': jnp.zeros((d,), jnp.float32), 'Wk': jax.random.normal(ks[2], (d, d), dtype=jnp.float32) * s, 'bk': jnp.zeros((d,), jnp.float32), 'Wv': jax.random.normal(ks[3], (d, d), dtype=jnp.float32) * s, 'bv': jnp.zeros((d,), jnp.float32), 'Wo': jax.random.normal(ks[4], (d, d), dtype=jnp.float32) * s, 'bo': jnp.zeros((d,), jnp.float32), 'W1': jax.random.normal(ks[5], (d, f), dtype=jnp.float32) * s, 'b1': jnp.zeros((f,), jnp.float32), 'W2': jax.random.normal(ks[6], (f, d), dtype=jnp.float32) * s, 'b2': jnp.zeros((d,), jnp.float32), 'g1': jnp.ones((d,), jnp.float32), 'beta1': jnp.zeros((d,), jnp.float32), 'g2': jnp.ones((d,), jnp.float32), 'beta2': jnp.zeros((d,), jnp.float32)}
    _L3_attn_all = _L3_attn_setup()
    _L3_attn_in = {k: v for k, v in _L3_attn_all.items() if k in ('Wq', 'bq', 'Wk', 'bk', 'Wv', 'bv', 'Wo', 'bo', 'W1', 'b1', 'W2', 'b2', 'g1', 'beta1', 'g2', 'beta2')}
    del _L3_attn_all

    def _L3_ffn_setup():
        import jax, jax.numpy as jnp
        import numpy as np
        B, S, D, E, H, K = (64, 1024, 512, 32, 2048, 8)
        key = jax.random.key(seed)
        k0, k1, k2, k3 = jax.random.split(key, 4)
        x = jax.random.normal(k0, (B, S, D), jnp.float32)
        gate_w = jax.random.normal(k1, (E, D), jnp.float32) * (1.0 / np.sqrt(D))
        gate_b = jnp.zeros((E,), jnp.float32)
        w1 = jax.random.normal(k2, (E, D + 1, H), jnp.float32) * (1.0 / np.sqrt(D + 1))
        w2 = jax.random.normal(k3, (E, H + 1, D), jnp.float32) * (1.0 / np.sqrt(H + 1))
        return {'x': x, 'gate_w': gate_w, 'gate_b': gate_b, 'w1': w1, 'w2': w2}
    _L3_ffn_all = _L3_ffn_setup()
    _L3_ffn_in = {k: v for k, v in _L3_ffn_all.items() if k in ('gate_w', 'gate_b', 'w1', 'w2')}
    del _L3_ffn_all
    return {'x': x, 'ctx_1024': ctx_1024, 'mask_BxSxS2_ff0': mask_BxSxS2_ff0, 'L0_xattn_Wq': _L0_xattn_in['Wq'], 'L0_xattn_bq': _L0_xattn_in['bq'], 'L0_xattn_Wk': _L0_xattn_in['Wk'], 'L0_xattn_bk': _L0_xattn_in['bk'], 'L0_xattn_Wv': _L0_xattn_in['Wv'], 'L0_xattn_bv': _L0_xattn_in['bv'], 'L0_xattn_Wo': _L0_xattn_in['Wo'], 'L0_xattn_bo': _L0_xattn_in['bo'], 'L0_attn_w_qkv': _L0_attn_in['w_qkv'], 'L0_attn_w_proj': _L0_attn_in['w_proj'], 'L0_ffn_ln_scale': _L0_ffn_in['ln_scale'], 'L0_ffn_ln_bias': _L0_ffn_in['ln_bias'], 'L0_ffn_gate_w': _L0_ffn_in['gate_w'], 'L0_ffn_Wg': _L0_ffn_in['Wg'], 'L0_ffn_Wu': _L0_ffn_in['Wu'], 'L0_ffn_Wd': _L0_ffn_in['Wd'], 'L0_ffn_sWg': _L0_ffn_in['sWg'], 'L0_ffn_sWu': _L0_ffn_in['sWu'], 'L0_ffn_sWd': _L0_ffn_in['sWd'], 'L1_xattn_Wq': _L1_xattn_in['Wq'], 'L1_xattn_Wk': _L1_xattn_in['Wk'], 'L1_xattn_Wv': _L1_xattn_in['Wv'], 'L1_xattn_Wo': _L1_xattn_in['Wo'], 'L1_xattn_pre_g': _L1_xattn_in['pre_g'], 'L1_xattn_pre_b': _L1_xattn_in['pre_b'], 'L1_xattn_ln_g': _L1_xattn_in['ln_g'], 'L1_xattn_ln_b': _L1_xattn_in['ln_b'], 'L1_attn_in_proj_W': _L1_attn_in['in_proj_W'], 'L1_attn_in_proj_b': _L1_attn_in['in_proj_b'], 'L1_attn_conv_w': _L1_attn_in['conv_w'], 'L1_attn_conv_b': _L1_attn_in['conv_b'], 'L1_attn_dyn_W': _L1_attn_in['dyn_W'], 'L1_attn_dyn_b': _L1_attn_in['dyn_b'], 'L1_attn_dt_c': _L1_attn_in['dt_c'], 'L1_attn_selB_W': _L1_attn_in['selB_W'], 'L1_attn_selC_W': _L1_attn_in['selC_W'], 'L1_attn_seldt_W': _L1_attn_in['seldt_W'], 'L1_attn_beta_W': _L1_attn_in['beta_W'], 'L1_attn_beta_b': _L1_attn_in['beta_b'], 'L1_attn_rg_W': _L1_attn_in['rg_W'], 'L1_attn_rg_b': _L1_attn_in['rg_b'], 'L1_attn_ug_W': _L1_attn_in['ug_W'], 'L1_attn_ug_b': _L1_attn_in['ug_b'], 'L1_attn_Q_W': _L1_attn_in['Q_W'], 'L1_attn_out_W': _L1_attn_in['out_W'], 'L1_attn_D': _L1_attn_in['D'], 'L1_attn_rms_w': _L1_attn_in['rms_w'], 'L1_attn_gn_w': _L1_attn_in['gn_w'], 'L1_attn_gn_b': _L1_attn_in['gn_b'], 'L1_ffn_gate_W': _L1_ffn_in['gate_W'], 'L1_ffn_gate_b': _L1_ffn_in['gate_b'], 'L1_ffn_W1': _L1_ffn_in['W1'], 'L1_ffn_b1': _L1_ffn_in['b1'], 'L1_ffn_g1': _L1_ffn_in['g1'], 'L1_ffn_be1': _L1_ffn_in['be1'], 'L1_ffn_W2': _L1_ffn_in['W2'], 'L1_ffn_b2': _L1_ffn_in['b2'], 'L1_ffn_g2': _L1_ffn_in['g2'], 'L1_ffn_be2': _L1_ffn_in['be2'], 'L2_xattn_Wq': _L2_xattn_in['Wq'], 'L2_xattn_bq': _L2_xattn_in['bq'], 'L2_xattn_Wk': _L2_xattn_in['Wk'], 'L2_xattn_bk': _L2_xattn_in['bk'], 'L2_xattn_Wv': _L2_xattn_in['Wv'], 'L2_xattn_bv': _L2_xattn_in['bv'], 'L2_attn_ln1_g': _L2_attn_in['ln1_g'], 'L2_attn_ln1_b': _L2_attn_in['ln1_b'], 'L2_attn_wq': _L2_attn_in['wq'], 'L2_attn_bq': _L2_attn_in['bq'], 'L2_attn_wk': _L2_attn_in['wk'], 'L2_attn_bk': _L2_attn_in['bk'], 'L2_attn_wv': _L2_attn_in['wv'], 'L2_attn_bv': _L2_attn_in['bv'], 'L2_attn_wo': _L2_attn_in['wo'], 'L2_attn_bo': _L2_attn_in['bo'], 'L2_attn_ln2_g': _L2_attn_in['ln2_g'], 'L2_attn_ln2_b': _L2_attn_in['ln2_b'], 'L2_attn_w1': _L2_attn_in['w1'], 'L2_attn_b1': _L2_attn_in['b1'], 'L2_attn_w2': _L2_attn_in['w2'], 'L2_attn_b2': _L2_attn_in['b2'], 'L2_attn_lnf_g': _L2_attn_in['lnf_g'], 'L2_attn_lnf_b': _L2_attn_in['lnf_b'], 'L2_ffn_Wg': _L2_ffn_in['Wg'], 'L2_ffn_W1': _L2_ffn_in['W1'], 'L2_ffn_W2': _L2_ffn_in['W2'], 'L3_xattn_Wq': _L3_xattn_in['Wq'], 'L3_xattn_bq': _L3_xattn_in['bq'], 'L3_xattn_Wk': _L3_xattn_in['Wk'], 'L3_xattn_bk': _L3_xattn_in['bk'], 'L3_xattn_Wv': _L3_xattn_in['Wv'], 'L3_xattn_bv': _L3_xattn_in['bv'], 'L3_xattn_Wo': _L3_xattn_in['Wo'], 'L3_xattn_bo': _L3_xattn_in['bo'], 'L3_attn_Wq': _L3_attn_in['Wq'], 'L3_attn_bq': _L3_attn_in['bq'], 'L3_attn_Wk': _L3_attn_in['Wk'], 'L3_attn_bk': _L3_attn_in['bk'], 'L3_attn_Wv': _L3_attn_in['Wv'], 'L3_attn_bv': _L3_attn_in['bv'], 'L3_attn_Wo': _L3_attn_in['Wo'], 'L3_attn_bo': _L3_attn_in['bo'], 'L3_attn_W1': _L3_attn_in['W1'], 'L3_attn_b1': _L3_attn_in['b1'], 'L3_attn_W2': _L3_attn_in['W2'], 'L3_attn_b2': _L3_attn_in['b2'], 'L3_attn_g1': _L3_attn_in['g1'], 'L3_attn_beta1': _L3_attn_in['beta1'], 'L3_attn_g2': _L3_attn_in['g2'], 'L3_attn_beta2': _L3_attn_in['beta2'], 'L3_ffn_gate_w': _L3_ffn_in['gate_w'], 'L3_ffn_gate_b': _L3_ffn_in['gate_b'], 'L3_ffn_w1': _L3_ffn_in['w1'], 'L3_ffn_w2': _L3_ffn_in['w2']}

def reference(x, ctx_1024, mask_BxSxS2_ff0, L0_xattn_Wq, L0_xattn_bq, L0_xattn_Wk, L0_xattn_bk, L0_xattn_Wv, L0_xattn_bv, L0_xattn_Wo, L0_xattn_bo, L0_attn_w_qkv, L0_attn_w_proj, L0_ffn_ln_scale, L0_ffn_ln_bias, L0_ffn_gate_w, L0_ffn_Wg, L0_ffn_Wu, L0_ffn_Wd, L0_ffn_sWg, L0_ffn_sWu, L0_ffn_sWd, L1_xattn_Wq, L1_xattn_Wk, L1_xattn_Wv, L1_xattn_Wo, L1_xattn_pre_g, L1_xattn_pre_b, L1_xattn_ln_g, L1_xattn_ln_b, L1_attn_in_proj_W, L1_attn_in_proj_b, L1_attn_conv_w, L1_attn_conv_b, L1_attn_dyn_W, L1_attn_dyn_b, L1_attn_dt_c, L1_attn_selB_W, L1_attn_selC_W, L1_attn_seldt_W, L1_attn_beta_W, L1_attn_beta_b, L1_attn_rg_W, L1_attn_rg_b, L1_attn_ug_W, L1_attn_ug_b, L1_attn_Q_W, L1_attn_out_W, L1_attn_D, L1_attn_rms_w, L1_attn_gn_w, L1_attn_gn_b, L1_ffn_gate_W, L1_ffn_gate_b, L1_ffn_W1, L1_ffn_b1, L1_ffn_g1, L1_ffn_be1, L1_ffn_W2, L1_ffn_b2, L1_ffn_g2, L1_ffn_be2, L2_xattn_Wq, L2_xattn_bq, L2_xattn_Wk, L2_xattn_bk, L2_xattn_Wv, L2_xattn_bv, L2_attn_ln1_g, L2_attn_ln1_b, L2_attn_wq, L2_attn_bq, L2_attn_wk, L2_attn_bk, L2_attn_wv, L2_attn_bv, L2_attn_wo, L2_attn_bo, L2_attn_ln2_g, L2_attn_ln2_b, L2_attn_w1, L2_attn_b1, L2_attn_w2, L2_attn_b2, L2_attn_lnf_g, L2_attn_lnf_b, L2_ffn_Wg, L2_ffn_W1, L2_ffn_W2, L3_xattn_Wq, L3_xattn_bq, L3_xattn_Wk, L3_xattn_bk, L3_xattn_Wv, L3_xattn_bv, L3_xattn_Wo, L3_xattn_bo, L3_attn_Wq, L3_attn_bq, L3_attn_Wk, L3_attn_bk, L3_attn_Wv, L3_attn_bv, L3_attn_Wo, L3_attn_bo, L3_attn_W1, L3_attn_b1, L3_attn_W2, L3_attn_b2, L3_attn_g1, L3_attn_beta1, L3_attn_g2, L3_attn_beta2, L3_ffn_gate_w, L3_ffn_gate_b, L3_ffn_w1, L3_ffn_w2):
    import jax
    import jax.numpy as jnp

    def _L0_xattn_ref(hidden_states, encoder_hidden_states, attention_mask, Wq, bq, Wk, bk, Wv, bv, Wo, bo):
        import jax, jax.numpy as jnp
        import numpy as np
        NUM_HEADS = 16
        DIM = 512
        B, N, C = hidden_states.shape
        T = encoder_hidden_states.shape[1]
        H = NUM_HEADS
        D = C // H
        q = (hidden_states @ Wq.T + bq).reshape(B, N, H, D).transpose(0, 2, 1, 3)
        k = (encoder_hidden_states @ Wk.T + bk).reshape(B, T, H, D).transpose(0, 2, 1, 3)
        v = (encoder_hidden_states @ Wv.T + bv).reshape(B, T, H, D).transpose(0, 2, 1, 3)
        scale = 1.0 / jnp.sqrt(jnp.asarray(D, q.dtype))
        scores = jnp.einsum('bhnd,bhtd->bhnt', q, k) * scale + attention_mask[:, None, :, :]
        attn = jax.nn.softmax(scores, axis=-1)
        out = jnp.einsum('bhnt,bhtd->bhnd', attn, v)
        out = out.transpose(0, 2, 1, 3).reshape(B, N, C)
        return out @ Wo.T + bo

    def _L0_attn_ref(x, w_qkv, w_proj):
        import jax, jax.numpy as jnp
        import numpy as np
        B, T, DIM, H = (2, 1024, 512, 16)
        HD = DIM // H

        def _custom_softmax(a):
            a = jnp.clip(a, -100.0, 100.0)
            m = jnp.max(a, axis=-1, keepdims=True)
            e = jnp.exp(a - m)
            p = e / (jnp.sum(e, axis=-1, keepdims=True) + 1e-06)
            p = p + 1e-08
            return p / jnp.sum(p, axis=-1, keepdims=True)
        b, t, c = x.shape
        scale = HD ** (-0.5)
        qkv = jnp.einsum('btc,oc->bto', x, w_qkv)
        qkv = qkv.reshape(b, t, 3, H, HD)
        q = jnp.transpose(qkv[:, :, 0], (0, 2, 1, 3))
        k = jnp.transpose(qkv[:, :, 1], (0, 2, 1, 3))
        v = jnp.transpose(qkv[:, :, 2], (0, 2, 1, 3))
        attn = jnp.einsum('bhqd,bhkd->bhqk', q, k) * scale
        causal = jnp.tril(jnp.ones((t, t), dtype=bool))
        attn = jnp.where(causal, attn, -jnp.inf)
        attn = _custom_softmax(attn)
        out = jnp.einsum('bhqk,bhkd->bhqd', attn, v)
        out = jnp.transpose(out, (0, 2, 1, 3)).reshape(b, t, c)
        return jnp.einsum('btc,oc->bto', out, w_proj)

    def _L0_ffn_ref(x, ln_scale, ln_bias, gate_w, Wg, Wu, Wd, sWg, sWu, sWd):
        import jax, jax.numpy as jnp
        import numpy as np
        EPS = 1e-05
        LN_EPS = 1e-05
        NUM_EXPERTS = 8
        TOP_K = 2
        HIDDEN = 512
        INTER = 1024

        def _swiglu(x, wg, wu, wd):
            return jax.nn.silu(x @ wg) * (x @ wu) @ wd
        B, S, H = x.shape
        xf = x.reshape(-1, H)
        mu = jnp.mean(xf, axis=-1, keepdims=True)
        var = jnp.var(xf, axis=-1, keepdims=True)
        xn = (xf - mu) * jax.lax.rsqrt(var + LN_EPS) * ln_scale + ln_bias
        logits = xn @ gate_w.T
        probs = jax.nn.softmax(logits, axis=-1)
        tk_probs, tk_idx = jax.lax.top_k(probs, TOP_K)
        tk_probs = tk_probs / (jnp.sum(tk_probs, axis=-1, keepdims=True) + EPS)
        onehot = tk_idx[..., None] == jnp.arange(NUM_EXPERTS)[None, None, :]
        w = jnp.sum(tk_probs[..., None] * onehot.astype(tk_probs.dtype), axis=1)
        out = _swiglu(xf, sWg, sWu, sWd)
        for e in range(NUM_EXPERTS):
            out = out + w[:, e:e + 1] * _swiglu(xf, Wg[e], Wu[e], Wd[e])
        return out.reshape(B, S, H)

    def _L1_xattn_ref(Q, K, V, Wq, Wk, Wv, Wo, pre_g, pre_b, ln_g, ln_b):
        import jax, jax.numpy as jnp
        import numpy as np
        import math
        D = 512
        H = 8
        HD = D // H
        TEMP = math.sqrt(D)
        EPS = 1e-05

        def _layernorm(x, g, b):
            mu = jnp.mean(x, axis=-1, keepdims=True)
            var = jnp.var(x, axis=-1, keepdims=True)
            return (x - mu) * jax.lax.rsqrt(var + EPS) * g + b
        B, Lq, _ = Q.shape
        Lk = K.shape[1]
        Qn = _layernorm(Q, pre_g, pre_b)
        Kn = _layernorm(K, pre_g, pre_b)
        q = (Qn @ Wq).reshape(B, Lq, H, HD)
        k = (Kn @ Wk).reshape(B, Lk, H, HD)
        v = (V @ Wv).reshape(B, Lk, H, HD)
        scores = jnp.einsum('bqhd,bkhd->bhqk', q, k) / TEMP
        scores = jnp.clip(scores, -10000.0, 10000.0)
        A = jax.nn.softmax(scores, axis=-1)
        O = jnp.einsum('bhqk,bkhd->bqhd', A, v).reshape(B, Lq, D)
        O = _layernorm(O, ln_g, ln_b)
        O = O + jax.nn.gelu(O @ Wo, approximate=False)
        return O

    def _L1_attn_ref(x, in_proj_W, in_proj_b, conv_w, conv_b, dyn_W, dyn_b, dt_c, selB_W, selC_W, seldt_W, beta_W, beta_b, rg_W, rg_b, ug_W, ug_b, Q_W, out_W, D, rms_w, gn_w, gn_b):
        import jax, jax.numpy as jnp
        import numpy as np
        B, S, DM, DI, H = (2, 1024, 512, 1024, 32)
        HD = DI // H
        G = 32

        def _forward(x, in_proj_W, in_proj_b, conv_w, conv_b, dyn_W, dyn_b, dt_c, selB_W, selC_W, seldt_W, beta_W, beta_b, rg_W, rg_b, ug_W, ug_b, Q_W, out_W, D, rms_w, gn_w, gn_b):
            b, s, _ = x.shape
            residual = x
            xn = x * jax.lax.rsqrt(jnp.mean(x * x, -1, keepdims=True) + 1e-06) * rms_w
            proj = xn @ in_proj_W.T + in_proj_b
            z = proj[..., :DI]
            K = proj[..., DI:3 * DI].reshape(b, s, DI, 2)
            V = proj[..., 3 * DI:]
            vc = jax.lax.conv_general_dilated(V.transpose(0, 2, 1), conv_w[:, None, :], (1,), [(3, 0)], feature_group_count=DI, dimension_numbers=('NCH', 'OIH', 'NCH'))
            u = jax.nn.silu(vc + conv_b[None, :, None]).transpose(0, 2, 1)
            dyn = u @ dyn_W.T + dyn_b
            alpha = jax.nn.softplus(dyn[..., :H])
            omega = dyn[..., H:2 * H] + dyn[..., 2 * H:3 * H]
            rope = 1.0 / 10000.0 ** (jnp.arange(H, dtype=jnp.float32) / H)
            omega = omega + jnp.arange(s, dtype=jnp.float32)[None, :, None] * rope
            dt = jax.nn.softplus(dt_c) / (alpha + jnp.abs(omega) + 0.0001)
            dt = dt + jax.nn.softplus(u @ seldt_W.T)
            sel_B = (u @ selB_W.T).reshape(b, s, H, 1, 2)
            sel_C = (u @ selC_W.T).reshape(b, s, H, 1, 2)
            Kh = K.reshape(b, s, H, HD, 2) * sel_B
            a = 0.5 * dt * alpha
            w = 0.5 * dt * omega
            det = (1.0 + a) ** 2 + w * w
            lam2 = ((1.0 - a) ** 2 + w * w) / det
            r_gate = jax.nn.sigmoid(u @ rg_W.T + rg_b)
            vp = jnp.sqrt(jnp.clip(1.0 - lam2 ** r_gate, 1e-06))
            u_gate = jax.nn.sigmoid(u @ ug_W.T + ug_b)
            Vg = u.reshape(b, s, H, HD) * (vp * u_gate)[..., None]
            Q = (u @ Q_W.T).reshape(b, s, H, HD, 2) * sel_C
            beta = jax.nn.sigmoid(u @ beta_W.T + beta_b)
            A11 = (1.0 - a * a - w * w) / det
            A12 = 2.0 * w / det

            def step(Sc, inp):
                a11, a12, bt, k, v = inp
                S0, S1 = (Sc[..., 0], Sc[..., 1])
                r0 = a11[..., None] * S0 + a12[..., None] * S1
                r1 = -a12[..., None] * S0 + a11[..., None] * S1
                Sr = jnp.stack([r0, r1], -1)
                err = v - jnp.sum(k * Sr, -1)
                Sn = Sr + bt[..., None, None] * err[..., None] * k
                return (Sn, Sn)
            xs = (jnp.swapaxes(A11, 0, 1), jnp.swapaxes(A12, 0, 1), jnp.swapaxes(beta, 0, 1), jnp.swapaxes(Kh, 0, 1), jnp.swapaxes(Vg, 0, 1))
            S0 = jnp.zeros((b, H, HD, 2), x.dtype)
            _, Y = jax.lax.scan(step, S0, xs)
            Y = jnp.moveaxis(Y, 0, 1)
            y = jnp.sum(Q * Y, -1).reshape(b, s, DI)
            yg = y.transpose(0, 2, 1).reshape(b, G, DI // G, s)
            mu = jnp.mean(yg, (2, 3), keepdims=True)
            var = jnp.var(yg, (2, 3), keepdims=True)
            yg = (yg - mu) * jax.lax.rsqrt(var + 1e-05)
            y = (yg.reshape(b, DI, s) * gn_w[None, :, None] + gn_b[None, :, None]).transpose(0, 2, 1)
            y = y * jax.nn.silu(z)
            y = y + D * u
            return residual + y @ out_W.T
        return _forward(x, in_proj_W, in_proj_b, conv_w, conv_b, dyn_W, dyn_b, dt_c, selB_W, selC_W, seldt_W, beta_W, beta_b, rg_W, rg_b, ug_W, ug_b, Q_W, out_W, D, rms_w, gn_w, gn_b)

    def _L1_ffn_ref(x, gate_W, gate_b, W1, b1, g1, be1, W2, b2, g2, be2):
        import jax, jax.numpy as jnp
        import numpy as np
        LN_EPS = 1e-05

        def _layernorm(x, g, b):
            m = jnp.mean(x, axis=-1, keepdims=True)
            v = jnp.mean(jnp.square(x - m), axis=-1, keepdims=True)
            return (x - m) * jax.lax.rsqrt(v + LN_EPS) * g + b
        K_TOP = 2
        B, N, D = x.shape
        BN = B * N
        xf = x.reshape(BN, D)
        gate_scores = xf @ gate_W + gate_b
        topk_scores, topk_idx = jax.lax.top_k(gate_scores, K_TOP)
        weights = jax.nn.softmax(topk_scores, axis=-1)

        def expert(w1, bb1, gg1, bbe1, w2, bb2, gg2, bbe2):
            h = jax.nn.relu(_layernorm(xf @ w1 + bb1, gg1, bbe1))
            return _layernorm(h @ w2 + bb2, gg2, bbe2)
        all_out = jax.vmap(expert)(W1, b1, g1, be1, W2, b2, g2, be2)
        exp_out = all_out[topk_idx, jnp.arange(BN)[:, None]]
        out = jnp.sum(weights[..., None] * exp_out, axis=1)
        return (out + xf).reshape(B, N, D)

    def _L2_xattn_ref(x1, x2, Wq, bq, Wk, bk, Wv, bv):
        import jax, jax.numpy as jnp
        import numpy as np
        B, SQ, SK, D, H = (4, 1024, 1024, 512, 16)
        SCALE = (D / H) ** 0.5
        q = x1 @ Wq.T + bq
        k = x2 @ Wk.T + bk
        v = x2 @ Wv.T + bv
        qk = jnp.einsum('bqd,bkd->bqk', q, k) * SCALE
        attn = jax.nn.softmax(qk, axis=-1)
        return jnp.einsum('bqk,bkd->bqd', attn, v)

    def _L2_attn_ref(x, ln1_g, ln1_b, wq, bq, wk, bk, wv, bv, wo, bo, ln2_g, ln2_b, w1, b1, w2, b2, lnf_g, lnf_b):
        import jax, jax.numpy as jnp
        import numpy as np
        L, H = (2, 16)
        B, T, C = (2, 1024, 512)
        EPS = 1e-05

        def layernorm(x, g, b):
            mu = jnp.mean(x, axis=-1, keepdims=True)
            var = jnp.mean((x - mu) ** 2, axis=-1, keepdims=True)
            return (x - mu) / jnp.sqrt(var + EPS) * g + b
        Bx, Tx, Cx = x.shape
        hd = Cx // H
        scale = 1.0 / np.sqrt(hd).astype(np.float32)
        rows = jnp.arange(Tx)
        allowed = (rows[:, None] % 3 != 0) | (rows[None, :] <= rows[:, None])
        neg_inf = jnp.float32(float('-inf'))
        for i in range(L):
            h = layernorm(x, ln1_g[i], ln1_b[i])
            q = (h @ wq[i] + bq[i]).reshape(Bx, Tx, H, hd).transpose(0, 2, 1, 3)
            k = (h @ wk[i] + bk[i]).reshape(Bx, Tx, H, hd).transpose(0, 2, 1, 3)
            v = (h @ wv[i] + bv[i]).reshape(Bx, Tx, H, hd).transpose(0, 2, 1, 3)
            att = jnp.einsum('bhqd,bhkd->bhqk', q, k) * scale
            att = jnp.where(allowed[None, None], att, neg_inf)
            att = jax.nn.softmax(att, axis=-1)
            y = jnp.einsum('bhqk,bhkd->bhqd', att, v)
            y = y.transpose(0, 2, 1, 3).reshape(Bx, Tx, Cx)
            x = x + y @ wo[i] + bo[i]
            h2 = layernorm(x, ln2_g[i], ln2_b[i])
            x = x + jax.nn.gelu(h2 @ w1[i] + b1[i], approximate=False) @ w2[i] + b2[i]
        return layernorm(x, lnf_g, lnf_b)

    def _L2_ffn_ref(token_inputs, Wg, W1, W2):
        import jax, jax.numpy as jnp
        import numpy as np
        CAPACITY_FACTOR = 1.0

        def _route(token_inputs, Wg, capacity):
            dt = token_inputs.dtype
            logits = jnp.einsum('bnd,de->bne', token_inputs, Wg)
            gates = jax.nn.softmax(logits, axis=-1)
            expert_idx = jnp.argmax(gates, axis=-1)
            mask = jax.nn.one_hot(expert_idx, Wg.shape[1], dtype=dt)
            gate = jnp.sum(gates * mask, axis=-1)
            pos = jnp.cumsum(mask, axis=1) * mask - mask
            keep = mask * (pos < capacity).astype(dt)
            pos_oh = jax.nn.one_hot(pos.astype(jnp.int32), capacity, dtype=dt)
            dispatch = keep[..., None] * pos_oh
            combine = dispatch * gate[:, :, None, None]
            return (dispatch, combine)
        B, N, D = token_inputs.shape
        E = Wg.shape[1]
        capacity = int(N * CAPACITY_FACTOR // E)
        dispatch, combine = _route(token_inputs, Wg, capacity)
        expert_inputs = jnp.einsum('bnd,bnec->becd', token_inputs, dispatch)
        h = jax.nn.gelu(jnp.einsum('becd,edh->bech', expert_inputs, W1))
        expert_outputs = jnp.einsum('bech,ehd->becd', h, W2)
        output = jnp.einsum('becd,bnec->bnd', expert_outputs, combine)
        return output

    def _L3_xattn_ref(queries, keys, values, Wq, bq, Wk, bk, Wv, bv, Wo, bo):
        import jax, jax.numpy as jnp
        import numpy as np
        HIDDEN = 512
        HEADS = 16
        HEAD_DIM = HIDDEN // HEADS
        B, Sq, _ = queries.shape
        Skv = keys.shape[1]
        q = (queries @ Wq + bq).reshape(B, Sq, HEADS, HEAD_DIM)
        k = (keys @ Wk + bk).reshape(B, Skv, HEADS, HEAD_DIM)
        v = (values @ Wv + bv).reshape(B, Skv, HEADS, HEAD_DIM)
        logits = jnp.einsum('bqhd,bkhd->bhqk', q, k) / jnp.sqrt(jnp.float32(HEAD_DIM))
        weights = jax.nn.softmax(logits, axis=-1)
        attn = jnp.einsum('bhqk,bkhd->bqhd', weights, v).reshape(B, Sq, HIDDEN)
        return attn @ Wo + bo

    def _L3_attn_ref(x, Wq, bq, Wk, bk, Wv, bv, Wo, bo, W1, b1, W2, b2, g1, beta1, g2, beta2):
        import jax, jax.numpy as jnp
        import numpy as np
        D_MODEL = 512
        NUM_HEADS = 16
        HEAD_DIM = D_MODEL // NUM_HEADS
        D_FF = 2048
        EPS = 1e-05

        def layer_norm(x, gamma, beta):
            mu = jnp.mean(x, axis=-1, keepdims=True)
            var = jnp.mean((x - mu) ** 2, axis=-1, keepdims=True)
            return (x - mu) * jax.lax.rsqrt(var + EPS) * gamma + beta

        def apply_rope(t):
            S, d = (t.shape[-2], t.shape[-1])
            inv_freq = 1.0 / 10000.0 ** (jnp.arange(0, d, 2, dtype=jnp.float32) / d)
            angles = jnp.arange(S, dtype=jnp.float32)[:, None] * inv_freq[None, :]
            sin, cos = (jnp.sin(angles), jnp.cos(angles))
            tp = t.reshape(*t.shape[:-1], d // 2, 2)
            t0, t1 = (tp[..., 0], tp[..., 1])
            rot = jnp.stack([t0 * cos - t1 * sin, t0 * sin + t1 * cos], axis=-1)
            return rot.reshape(t.shape)
        B, S, d = x.shape
        H, hd = (NUM_HEADS, HEAD_DIM)
        x_norm = layer_norm(x, g1, beta1)
        q = (x_norm @ Wq + bq).reshape(B, S, H, hd).transpose(0, 2, 1, 3)
        k = (x_norm @ Wk + bk).reshape(B, S, H, hd).transpose(0, 2, 1, 3)
        v = (x_norm @ Wv + bv).reshape(B, S, H, hd).transpose(0, 2, 1, 3)
        q = apply_rope(q)
        k = apply_rope(k)
        q = q * (1.0 / jnp.sqrt(jnp.float32(hd)))
        scores = jnp.einsum('bhqd,bhkd->bhqk', q, k)
        attn = jax.nn.softmax(scores, axis=-1)
        out = jnp.einsum('bhqk,bhkd->bhqd', attn, v)
        out = out.transpose(0, 2, 1, 3).reshape(B, S, d)
        attn_out = out @ Wo + bo
        x = x + attn_out
        x_norm2 = layer_norm(x, g2, beta2)
        ffn = jax.nn.relu(x_norm2 @ W1 + b1) @ W2 + b2
        return x + ffn

    def _L3_ffn_ref(x, gate_w, gate_b, w1, w2):
        import jax, jax.numpy as jnp
        import numpy as np
        B, S, D, E, H, K = (64, 1024, 512, 32, 2048, 8)
        b, s, d = x.shape
        logits = jnp.einsum('bsd,ed->bse', x, gate_w) + gate_b
        probs = jax.nn.softmax(logits, axis=-2)
        vals_t, idx_t = jax.lax.top_k(probs.transpose(0, 2, 1), K)
        vals = vals_t.transpose(0, 2, 1)
        idx = idx_t.transpose(0, 2, 1)
        flat_idx = idx.reshape(b, K * E)
        tok = jnp.take_along_axis(x, flat_idx[:, :, None], axis=1)
        tok = tok.reshape(b, K, E, d)
        merged = jnp.einsum('bked,bke->bed', tok, vals)
        ones = jnp.ones(merged.shape[:-1] + (1,), merged.dtype)
        h = jnp.einsum('bei,eih->beh', jnp.concatenate([merged, ones], -1), w1)
        h = jax.nn.gelu(h, approximate=False)
        o = jnp.einsum('bej,ejo->beo', jnp.concatenate([h, ones], -1), w2)
        out_tok = jnp.einsum('beo,bke->bkeo', o, vals).reshape(b, K * E, d)
        out = jnp.zeros_like(x).at[jnp.arange(b)[:, None], flat_idx].add(out_tok)
        return out
    x = x + _L0_xattn_ref(_layernorm(x, axis=-1), ctx_1024, mask_BxSxS2_ff0, L0_xattn_Wq, L0_xattn_bq, L0_xattn_Wk, L0_xattn_bk, L0_xattn_Wv, L0_xattn_bv, L0_xattn_Wo, L0_xattn_bo)
    x = x + _L0_attn_ref(_layernorm(x, axis=-1), L0_attn_w_qkv, L0_attn_w_proj)
    x = x + _L0_ffn_ref(_layernorm(x, axis=-1), L0_ffn_ln_scale, L0_ffn_ln_bias, L0_ffn_gate_w, L0_ffn_Wg, L0_ffn_Wu, L0_ffn_Wd, L0_ffn_sWg, L0_ffn_sWu, L0_ffn_sWd)
    x = x + _L1_xattn_ref(_layernorm(x, axis=-1), ctx_1024, ctx_1024, L1_xattn_Wq, L1_xattn_Wk, L1_xattn_Wv, L1_xattn_Wo, L1_xattn_pre_g, L1_xattn_pre_b, L1_xattn_ln_g, L1_xattn_ln_b)
    x = x + _L1_attn_ref(_layernorm(x, axis=-1), L1_attn_in_proj_W, L1_attn_in_proj_b, L1_attn_conv_w, L1_attn_conv_b, L1_attn_dyn_W, L1_attn_dyn_b, L1_attn_dt_c, L1_attn_selB_W, L1_attn_selC_W, L1_attn_seldt_W, L1_attn_beta_W, L1_attn_beta_b, L1_attn_rg_W, L1_attn_rg_b, L1_attn_ug_W, L1_attn_ug_b, L1_attn_Q_W, L1_attn_out_W, L1_attn_D, L1_attn_rms_w, L1_attn_gn_w, L1_attn_gn_b)
    x = x + _L1_ffn_ref(_layernorm(x, axis=-1), L1_ffn_gate_W, L1_ffn_gate_b, L1_ffn_W1, L1_ffn_b1, L1_ffn_g1, L1_ffn_be1, L1_ffn_W2, L1_ffn_b2, L1_ffn_g2, L1_ffn_be2)
    x = x + _L2_xattn_ref(_layernorm(x, axis=-1), ctx_1024, L2_xattn_Wq, L2_xattn_bq, L2_xattn_Wk, L2_xattn_bk, L2_xattn_Wv, L2_xattn_bv)
    x = x + _L2_attn_ref(_layernorm(x, axis=-1), L2_attn_ln1_g, L2_attn_ln1_b, L2_attn_wq, L2_attn_bq, L2_attn_wk, L2_attn_bk, L2_attn_wv, L2_attn_bv, L2_attn_wo, L2_attn_bo, L2_attn_ln2_g, L2_attn_ln2_b, L2_attn_w1, L2_attn_b1, L2_attn_w2, L2_attn_b2, L2_attn_lnf_g, L2_attn_lnf_b)
    x = x + _L2_ffn_ref(_layernorm(x, axis=-1), L2_ffn_Wg, L2_ffn_W1, L2_ffn_W2)
    x = x + _L3_xattn_ref(_layernorm(x, axis=-1), ctx_1024, ctx_1024, L3_xattn_Wq, L3_xattn_bq, L3_xattn_Wk, L3_xattn_bk, L3_xattn_Wv, L3_xattn_bv, L3_xattn_Wo, L3_xattn_bo)
    x = x + _L3_attn_ref(_layernorm(x, axis=-1), L3_attn_Wq, L3_attn_bq, L3_attn_Wk, L3_attn_bk, L3_attn_Wv, L3_attn_bv, L3_attn_Wo, L3_attn_bo, L3_attn_W1, L3_attn_b1, L3_attn_W2, L3_attn_b2, L3_attn_g1, L3_attn_beta1, L3_attn_g2, L3_attn_beta2)
    x = x + _L3_ffn_ref(_layernorm(x, axis=-1), L3_ffn_gate_w, L3_ffn_gate_b, L3_ffn_w1, L3_ffn_w2)
    return x

_drawn_inputs = setup_inputs


def setup_inputs(seed=0):
    import zlib

    import numpy as np

    out = dict(_drawn_inputs(seed))
    spreads = {'L0_xattn_bq': (0.0, 0.1),
     'L0_xattn_bk': (0.0, 0.1),
     'L0_xattn_bv': (0.0, 0.1),
     'L0_xattn_bo': (0.0, 0.1),
     'L0_ffn_ln_scale': (1.0, 0.2),
     'L0_ffn_ln_bias': (0.0, 0.1),
     'L1_xattn_pre_g': (1.0, 0.2),
     'L1_xattn_pre_b': (0.0, 0.1),
     'L1_xattn_ln_g': (1.0, 0.2),
     'L1_xattn_ln_b': (0.0, 0.1),
     'L1_attn_in_proj_b': (0.0, 0.1),
     'L1_attn_conv_b': (0.0, 0.1),
     'L1_attn_dyn_b': (0.0, 0.1),
     'L1_attn_dt_c': (0.5, 0.2),
     'L1_attn_beta_b': (0.0, 0.1),
     'L1_attn_rg_b': (1.0, 0.2),
     'L1_attn_ug_b': (-1.0, 0.2),
     'L1_attn_D': (0.0, 0.1),
     'L1_attn_rms_w': (1.0, 0.2),
     'L1_attn_gn_w': (1.0, 0.2),
     'L1_attn_gn_b': (0.0, 0.1),
     'L1_ffn_gate_b': (0.0, 0.1),
     'L1_ffn_b1': (0.0, 0.1),
     'L1_ffn_g1': (1.0, 0.2),
     'L1_ffn_be1': (0.0, 0.1),
     'L1_ffn_b2': (0.0, 0.1),
     'L1_ffn_g2': (1.0, 0.2),
     'L1_ffn_be2': (0.0, 0.1),
     'L2_attn_ln1_g': (1.0, 0.2),
     'L2_attn_ln1_b': (0.0, 0.1),
     'L2_attn_bq': (0.0, 0.1),
     'L2_attn_bk': (0.0, 0.1),
     'L2_attn_bv': (0.0, 0.1),
     'L2_attn_bo': (0.0, 0.1),
     'L2_attn_ln2_g': (1.0, 0.2),
     'L2_attn_ln2_b': (0.0, 0.1),
     'L2_attn_b1': (0.0, 0.1),
     'L2_attn_b2': (0.0, 0.1),
     'L2_attn_lnf_g': (1.0, 0.2),
     'L2_attn_lnf_b': (0.0, 0.1),
     'L3_xattn_bq': (0.0, 0.1),
     'L3_xattn_bk': (0.0, 0.1),
     'L3_xattn_bv': (0.0, 0.1),
     'L3_xattn_bo': (0.0, 0.1),
     'L3_attn_bq': (0.0, 0.1),
     'L3_attn_bk': (0.0, 0.1),
     'L3_attn_bv': (0.0, 0.1),
     'L3_attn_bo': (0.0, 0.1),
     'L3_attn_b1': (0.0, 0.1),
     'L3_attn_b2': (0.0, 0.1),
     'L3_attn_g1': (1.0, 0.2),
     'L3_attn_beta1': (0.0, 0.1),
     'L3_attn_g2': (1.0, 0.2),
     'L3_attn_beta2': (0.0, 0.1),
     'L3_ffn_gate_b': (0.0, 0.1)}
    factors = {}
    for name, (base, spread) in spreads.items():
        noise = np.random.default_rng([zlib.crc32(name.encode()), seed]).standard_normal(out[name].shape)
        drawn = base * np.exp(spread * noise) if base else spread * noise
        out[name] = jnp.asarray(drawn.astype(out[name].dtype))
    for name, factor in factors.items():
        out[name] = (out[name] * factor).astype(out[name].dtype)
    return out
```

```python
from contextlib import ExitStack, contextmanager

import numpy as np

import concourse.bass as bass
from concourse import mybir

F32 = mybir.dt.float32
ACT = mybir.ActivationFunctionType
ALU = mybir.AluOpType
X = mybir.AxisListType.X

P = 128
B, S, D = 8, 64, 512
N = B * S
T = N // P
C = D // P
SK = 512
KC = SK // P


class Signal:

    times = 1

    def __init__(self, sem):
        self.sem, self.made, self.base = sem, 0, 0

    def up(self, n=1):
        self.made += n * Signal.times
        return self.sem, n

    def at(self, n):
        return self.sem, self.base + n


@contextmanager
def repeat(eng, n):
    with eng.Fori(0, n) as i:
        Signal.times = n
        yield i
        Signal.times = 1


class Chain:

    def __init__(self, eng, steps, i=0, per=0):
        self.eng, self.steps, self.i, self.per = eng, steps, i, per
        self.start = steps.made if not per else steps.base
        self.n = 0

    def __call__(self, ins):
        ins.then_inc(*self.steps.up())
        self.n += 1
        self.eng.wait_ge(self.steps.sem, self.start + self.n + (self.i * self.per if self.per else 0))

    def end(self):
        assert not self.per or self.n == self.per, (self.n, self.per)


class Machine:

    def __init__(self, nc, ctx, d):
        self.nc, self.ctx, self.d = nc, ctx, d
        self.marks, self.idle = {}, []
        self.count = 0
        self.x = self.sb("x_tokens", [P, T, D])
        self.y = self.sb("normed_tokens", [P, T, D])
        self.yT = self.sb("normed_features", [P, C, N])
        self.ident = self.sb("identity", [P, P])
        self.ones = self.sb("ones_row", [1, P])
        self.minus_half = self.sb("minus_half", [P, T])
        self.stats = self.sb("stats", [P, T, 6])
        self.mv = self.sb("mean_var", [P, T, 2])
        self.den = self.sb("var_eps", [P, T])
        self.rstd = self.sb("rstd", [P, T])
        self.cols = self.sb("columns", [P, 64])
        self.ps = ctx.enter_context(nc.psum_tensor("banks", [P, 8, 512], F32))

    def sb(self, name, shape):
        return self.ctx.enter_context(self.nc.sbuf_tensor(name, shape, F32))

    @contextmanager
    def local(self, **shapes):
        with ExitStack() as s:
            self.count += 1
            yield [s.enter_context(self.nc.sbuf_tensor(f"{n}_{self.count}", sh, F32)) for n, sh in shapes.items()]

    def sig(self, name):
        if name not in self.marks:
            s = self.idle.pop() if self.idle else Signal(self.ctx.enter_context(self.nc.semaphore(name)))
            s.base = s.made
            self.marks[name] = s
        return self.marks[name]

    def stage_done(self):
        self.idle += self.marks.values()
        self.marks = {}

    @contextmanager
    def block(self, *credits):
        for s in self.marks.values():
            s.base = s.made
        if credits:
            with self.nc.Block() as b:
                @b.gpsimd
                def _(pool):
                    for signal, n in credits:
                        pool.sem_inc(*signal.up(n))
        with self.nc.Block() as b:
            yield b


def constants(m):
    made, x_landed = m.sig("constants_made"), m.sig("x_landed")
    with m.block() as block:
        @block.gpsimd
        def _(pool):
            step = Chain(pool, made)
            step(pool.memset(m.ident[:], 0.0))
            step(pool.affine_select(out=m.ident[:], in_=m.ident[:], compare_op=ALU.not_equal, fill=1.0,
                                    base=0, pattern=[[-1, P]], channel_multiplier=1))
            step(pool.memset(m.ones[:], 1.0))
            step(pool.memset(m.minus_half[:], -0.5))

        @block.sync
        def _(sp):
            sp.dma_start(m.x[:], m.d["x"]).then_inc(*x_landed.up(16))
            sp.wait_ge(*x_landed.at(16))


def normalise(m, dst, src, eps, rms=False):
    summed, ready, rooted = m.sig("moments_step"), m.sig("variance_ready"), m.sig("rstd_ready")
    with m.block() as block:
        @block.vector
        def _(dve):
            step = Chain(dve, summed)
            for t in range(T):
                ins = dve.bn_stats(m.stats[:, t, :], src[:, t, :])
            step(ins)
            for t in range(T):
                ins = dve.bn_aggr(m.mv[:, t, :], m.stats[:, t, :])
            step(ins)
            if rms:
                step(dve.tensor_tensor(m.den[:], m.mv[:, :, 0], m.mv[:, :, 0], ALU.mult))
                step(dve.tensor_tensor(m.den[:], m.den[:], m.mv[:, :, 1], ALU.add))
                dve.tensor_scalar(m.den[:], m.den[:], eps, None, ALU.add).then_inc(*ready.up())
            else:
                dve.tensor_scalar(m.den[:], m.mv[:, :, 1], eps, None, ALU.add).then_inc(*ready.up())
            dve.wait_ge(*rooted.at(1))
            for t in range(T):
                if rms:
                    ins = dve.tensor_scalar(dst[:, t, :], src[:, t, :], m.rstd[:, t:t + 1], None, ALU.mult)
                else:
                    ins = dve.tensor_scalar(dst[:, t, :], src[:, t, :], m.mv[:, t, 0:1], m.rstd[:, t:t + 1],
                                            ALU.subtract, ALU.mult)

        @block.gpsimd
        def _(pool):
            pool.wait_ge(*ready.at(1))
            pool.tensor_tensor(m.rstd[:], m.den[:], m.minus_half[:], ALU.pow).then_inc(*rooted.up())


def load(m, *pairs):
    landed = m.sig("load_landed")
    with m.block() as block:
        @block.sync
        def _(sp):
            for dst, src in pairs:
                sp.dma_start(dst, src).then_inc(*landed.up(16))
            sp.wait_ge(*landed.at(16 * len(pairs)))


def turn(m, dstT, src, chunks=C, scale=None, bias=None, relu=False):
    turned = m.sig("turned")
    with m.block() as block:
        @block.tensor
        def _(pe):
            for c in range(chunks):
                for t in range(T):
                    ins = pe.transpose(m.ps[:, c, t * P:(t + 1) * P], src[:, t, c * P:(c + 1) * P], m.ident[:])
                ins.then_inc(*turned.up())

        @block.scalar
        def _(act):
            for c in range(0, chunks, 1 if relu else 2):
                act.wait_ge(*turned.at(c + 1))
                act.activation(dstT[:, c, :], m.ps[:, c, :], ACT.Relu if relu else ACT.Identity,
                               bias=0.0 if bias is None else bias[:, c:c + 1],
                               scale=1.0 if scale is None else scale[:, c:c + 1])

        if not relu:
            @block.vector
            def _(dve):
                for c in range(1, chunks, 2):
                    dve.wait_ge(*turned.at(c + 1))
                    if scale is None:
                        dve.tensor_copy(dstT[:, c, :], m.ps[:, c, :])
                    elif bias is None:
                        dve.tensor_scalar(dstT[:, c, :], m.ps[:, c, :], scale[:, c:c + 1], None, ALU.mult)
                    else:
                        dve.tensor_scalar(dstT[:, c, :], m.ps[:, c, :], scale[:, c:c + 1], bias[:, c:c + 1],
                                          ALU.mult, ALU.add)


def linear_features(m, outs, kchunks=C):
    landed = [m.sig(f"weights_landed_{i}") for i in range(len(outs))]
    product, taken_a, taken_v = m.sig("features_product"), m.sig("features_taken_act"), m.sig("features_taken_dve")
    work = [(o, mm) for o in range(len(outs)) for mm in range(outs[o][2].shape[2] // P)]
    on_act = [outs[o][5] != ACT.Identity or n % 2 == 0 for n, (o, mm) in enumerate(work)]
    with m.block() as block:
        @block.sync
        def _(sp):
            for o, (_, w, buf, *_r) in enumerate(outs):
                sp.dma_start(buf[:], w).then_inc(*landed[o].up(16))

        @block.tensor
        def _(pe):
            for n, (o, mm) in enumerate(work):
                _, _, buf, srcT, _, _ = outs[o]
                if mm == 0:
                    pe.wait_ge(*landed[o].at(16))
                if n >= 4:
                    a = sum(on_act[:n - 3])
                    s = taken_a if on_act[n - 4] else taken_v
                    pe.wait_ge(*s.at(a if on_act[n - 4] else n - 3 - a))
                for k in range(kchunks):
                    ins = pe.matmul(m.ps[:, n % 4, :], buf[:, k, mm * P:(mm + 1) * P], srcT[:, k, :],
                                    start=(k == 0), stop=(k == kchunks - 1))
                ins.then_inc(*product.up())

        def take(eng, mine, signal):
            for n, (o, mm) in enumerate(work):
                if on_act[n] != mine:
                    continue
                dstT, _, _, _, bias, f = outs[o]
                eng.wait_ge(*product.at(n + 1))
                if mine:
                    eng.activation(dstT[:, mm, :], m.ps[:, n % 4, :], f,
                                   bias=0.0 if bias is None else bias[:, mm:mm + 1]).then_inc(*signal.up())
                elif bias is None:
                    eng.tensor_copy(dstT[:, mm, :], m.ps[:, n % 4, :]).then_inc(*signal.up())
                else:
                    eng.tensor_scalar(dstT[:, mm, :], m.ps[:, n % 4, :], bias[:, mm:mm + 1], None,
                                      ALU.add).then_inc(*signal.up())

        @block.scalar
        def _(act):
            take(act, True, taken_a)

        @block.vector
        def _(dve):
            take(dve, False, taken_v)


def linear_tokens(m, dst, srcT, w, buf, kchunks, brow=None, add=None):
    landed, product = m.sig("weights_landed_0"), m.sig("tokens_product")
    with m.block() as block:
        @block.sync
        def _(sp):
            sp.dma_start(buf[:], w).then_inc(*landed.up(16))

        @block.tensor
        def _(pe):
            pe.wait_ge(*landed.at(16))
            for t in range(T):
                for k in range(kchunks):
                    ins = pe.matmul(m.ps[:, t, :], srcT[:, k, t * P:(t + 1) * P], buf[:, k, :],
                                    start=(k == 0), stop=(k == kchunks - 1 and brow is None))
                if brow is not None:
                    ins = pe.matmul(m.ps[:, t, :], m.ones[0:1, :], brow, start=False, stop=True)
                ins.then_inc(*product.up())

        @block.vector
        def _(dve):
            for t in range(T):
                dve.wait_ge(*product.at(t + 1))
                if add is None:
                    dve.tensor_copy(dst[:, t, :], m.ps[:, t, :])
                else:
                    dve.tensor_tensor(dst[:, t, :], m.ps[:, t, :], add[:, t, :], ALU.add)


def add_into(m, dst, a, b):
    with m.block() as block:
        @block.vector
        def _(dve):
            for t in range(T):
                dve.tensor_tensor(dst[:, t, :], a[:, t, :], b[:, t, :], ALU.add)


def cross_attention(m, oT, qT, hd, scale, wk, wv, kbias=None, vbias=None, mask=None, clip=None, knorm=None):
    J = D // hd // 2
    JC = J // C
    G = P // hd
    R = 3
    s = m.sig
    w_landed, ctx_landed, ctxt_landed, mask_landed = s("xw_landed"), s("ctx_landed"), s("ctxtok_landed"), s("mask_landed")
    projected, k_taken, v_taken = s("kv_projected"), s("k_taken"), s("v_taken")
    q_spread, q_zero = s("q_spread"), s("q_zeroed")
    scored, max_ready, probs_ready, scaled = s("scored"), s("max_ready"), s("probs_ready"), s("probs_scaled")
    turned, turned_taken, attended, o_taken = s("probs_turned"), s("probs_turned_taken"), s("attended"), s("attended_taken")
    vstep, k_turned, kn_ready, kn_taken, rooted = s("xattn_step"), s("ctx_turned"), s("ctx_normed"), s("ctxn_taken"), s("ctx_rstd")
    var_ready = s("ctx_var")
    pre = mask is not None or clip is not None
    with m.local(wkb=[P, C, D], wvb=[P, C, D], ctxT=[P, C, SK], kT=[P, C, SK], v=[P, KC, D], q2=[P, J, P],
                 pr=[P, R, SK], prT=[P, 2, KC, P], sc=[P, 2, SK], col=[P, 16, 4],
                 extra=[P, C, SK], extraT=[P, C, SK]) as \
            (wkb, wvb, ctxT, kT, v, q2, pr, prT, sc, col, extra, extraT), \
            m.block((v_taken, 1), (scored, 1), (max_ready, 1)) as block:
        ps = m.ps
        keysT = extraT if knorm else ctxT

        @block.sync
        def _(sp):
            sp.dma_start(wkb[:], wk).then_inc(*w_landed.up(16))
            sp.dma_start(wvb[:], wv).then_inc(*w_landed.up(16))
            with repeat(sp, B) as b:
                sp.wait_ge(*v_taken.at(KC * b + 1))
                sp.dma_start(ctxT[:], m.d["ctxT"][b]).then_inc(*ctx_landed.up(16))
                if knorm:
                    sp.dma_start(extra[:], m.d["ctx"][b]).then_inc(*ctxt_landed.up(16))
                if mask is not None:
                    sp.wait_ge(*max_ready.at(J * b + 1))
                    for half in range(2):
                        sp.dma_start(extra[64 * half:64 * half + 64, 0, :], mask[b]).then_inc(*mask_landed.up(16))

        @block.gpsimd
        def _(pool):
            pool.memset(q2[:], 0.0).then_inc(*q_zero.up())
            if knorm:
                with repeat(pool, B) as b:
                    pool.wait_ge(*var_ready.at(b + 1))
                    pool.tensor_tensor(m.rstd[:], m.den[:], m.minus_half[:], ALU.pow).then_inc(*rooted.up())

        @block.tensor
        def _(pe):
            pe.wait_ge(*w_landed.at(32))
            with repeat(pe, B) as b:
                pe.wait_ge(*ctx_landed.at(16 * b + 16))
                if knorm:
                    pe.wait_ge(*kn_ready.at(b + 1))
                    for c in range(C):
                        for k in range(KC):
                            ins = pe.transpose(ps[:, 4 + c, k * P:(k + 1) * P], extra[:, k, c * P:(c + 1) * P],
                                               m.ident[:])
                        ins.then_inc(*k_turned.up())
                for mm in range(C):
                    if mm >= 2:
                        pe.wait_ge(*k_taken.at(C * b + mm - 1))
                    if knorm and mm == 0:
                        pe.wait_ge(*kn_taken.at(C * b + C))
                    for k in range(C):
                        ins = pe.matmul(ps[:, mm % 2, :], wkb[:, k, mm * P:(mm + 1) * P], keysT[:, k, :],
                                        start=(k == 0), stop=(k == C - 1))
                    ins.then_inc(*projected.up())

                def scores(j):
                    if j == 0:
                        pe.wait_ge(*q_spread.at(b + 1))
                        pe.wait_ge(*k_taken.at(C * b + C))
                    if j >= 2:
                        pe.wait_ge(*probs_ready.at(J * b + j - 1))
                    pe.matmul(ps[:, 2 + j % 2, :], q2[:, j, :], kT[:, j // JC, :],
                              start=True, stop=True).then_inc(*scored.up())

                def turn_probs(j):
                    pe.wait_ge(*scaled.at(J * b + j + 1))
                    if j >= 2:
                        pe.wait_ge(*turned_taken.at(J * b + j - 1))
                    for k in range(KC):
                        ins = pe.transpose(ps[:, 4 + j % 2, k * P:(k + 1) * P], pr[:, j % R, k * P:(k + 1) * P],
                                           m.ident[:])
                    ins.then_inc(*turned.up())

                def attend(j):
                    pe.wait_ge(*turned_taken.at(J * b + j + 1))
                    c, half = j // JC, j % JC
                    w = P // JC
                    for k in range(KC):
                        ins = pe.matmul(ps[w * half:w * half + w, 6, c * P:(c + 1) * P],
                                        v[:, k, c * P + w * half:c * P + w * half + w], prT[:, j % 2, k, :],
                                        start=(k == 0), stop=(k == KC - 1))
                    ins.then_inc(*attended.up())

                scores(0)
                scores(1)
                for k in range(KC):
                    if k < 2:
                        pe.wait_ge(*k_taken.at(C * b + C))
                    else:
                        pe.wait_ge(*v_taken.at(1 + KC * b + k - 1))
                    for c in range(C):
                        ins = pe.matmul(ps[:, k % 2, :], ctxT[:, c, k * P:(k + 1) * P], wvb[:, c, :],
                                        start=(c == 0), stop=(c == C - 1))
                    ins.then_inc(*projected.up())
                pe.wait_ge(*v_taken.at(1 + KC * b + KC))
                for j in range(J + 1):
                    if j < J:
                        turn_probs(j)
                    if j + 2 < J:
                        scores(j + 2)
                    if j >= 1:
                        attend(j - 1)
                pe.wait_ge(*o_taken.at(b + 1))

        @block.scalar
        def _(act):
            act.wait_ge(*q_zero.at(1))
            with repeat(act, B) as b:
                act.wait_ge(*scored.at(1 + J * b))
                for h in range(G):
                    rows = slice(hd * h, hd * h + hd)
                    dst = q2[rows, :, :].rearrange("p (c j) n -> p c j n", c=C)[:, :, h // 2 if hd == 32 else 0,
                                                                                (h % 2) * 64:(h % 2) * 64 + 64]
                    src = qT[rows, :, :].rearrange("p c (b n) -> p b c n", b=B)[:, b, :, :]
                    ins = act.activation(dst, src, ACT.Copy)
                ins.then_inc(*q_spread.up())
                if knorm:
                    for c in range(C):
                        act.wait_ge(*k_turned.at(C * b + c + 1))
                        act.activation(extraT[:, c, :], ps[:, 4 + c, :], ACT.Identity, bias=knorm[1][:, c:c + 1],
                                       scale=knorm[0][:, c:c + 1]).then_inc(*kn_taken.up())
                for mm in range(C):
                    act.wait_ge(*projected.at((C + KC) * b + mm + 1))
                    act.activation(kT[:, mm, :], ps[:, mm % 2, :], ACT.Identity,
                                   bias=0.0 if kbias is None else kbias[:, mm:mm + 1]).then_inc(*k_taken.up())
                for j in range(J):
                    act.wait_ge(*max_ready.at(1 + J * b + j + 1))
                    src = sc[:, j % 2, :] if pre else ps[:, 2 + j % 2, :]
                    act.activation(pr[:, j % R, :], src, ACT.Exp, bias=col[:, j, 1:2],
                                   scale=1.0 if mask is not None else scale,
                                   accum_out=col[:, j, 2:3]).then_inc(*probs_ready.up())

        per = (3 if pre else 2) * J + (2 if knorm else 0)

        @block.vector
        def _(dve):
            with repeat(dve, B) as b:
                step = Chain(dve, vstep, b, per)
                if knorm:
                    dve.wait_ge(*ctxt_landed.at(16 * b + 16))
                    for k in range(KC):
                        ins = dve.bn_stats(m.stats[:, k, :], extra[:, k, :])
                    step(ins)
                    dve.memset(m.den[:], 0.0)
                    for k in range(KC):
                        ins = dve.bn_aggr(m.mv[:, k, :], m.stats[:, k, :])
                    step(ins)
                    ins = dve.tensor_scalar(m.den[:], m.mv[:, :, 1], 1e-5, None, ALU.add)
                    ins.then_inc(*var_ready.up())
                    dve.wait_ge(*rooted.at(b + 1))
                    for k in range(KC):
                        ins = dve.tensor_scalar(extra[:, k, :], extra[:, k, :], m.mv[:, k, 0:1], m.rstd[:, k:k + 1],
                                                ALU.subtract, ALU.mult)
                    ins.then_inc(*kn_ready.up())

                def row_max(j):
                    dve.wait_ge(*scored.at(1 + J * b + j + 1))
                    src = ps[:, 2 + j % 2, :]
                    if j >= 2:
                        dve.wait_ge(*probs_ready.at(J * b + j - 1))
                    if mask is not None:
                        dve.wait_ge(*mask_landed.at(32 * b + 32))
                        step(dve.scalar_tensor_tensor(sc[:, j % 2, :], src, scale, extra[:, 0, :], ALU.mult, ALU.add))
                    if clip is not None:
                        step(dve.tensor_scalar(sc[:, j % 2, :], src, -clip, clip, ALU.max, ALU.min))
                    if pre:
                        src = sc[:, j % 2, :]
                    step(dve.tensor_reduce(col[:, j, 0:1], src, X, ALU.max, negate=True))
                    dve.tensor_scalar(col[:, j, 1:2], col[:, j, 0:1], 1.0 if mask is not None else scale, None,
                                      ALU.mult).then_inc(*max_ready.up())

                def finish(j):
                    dve.wait_ge(*probs_ready.at(J * b + j + 1))
                    step(dve.reciprocal(col[:, j, 3:4], col[:, j, 2:3]))
                    dve.tensor_scalar(pr[:, j % R, :], pr[:, j % R, :], col[:, j, 3:4], None, ALU.mult)\
                       .then_inc(*scaled.up())

                def take_turned(j):
                    dve.wait_ge(*turned.at(J * b + j + 1))
                    dve.tensor_copy(prT[:, j % 2, :, :], ps[:, 4 + j % 2, :].rearrange("p (k n) -> p k n", k=KC))\
                       .then_inc(*turned_taken.up())

                row_max(0)
                row_max(1)
                for k in range(KC):
                    dve.wait_ge(*projected.at((C + KC) * b + C + k + 1))
                    if vbias is None:
                        dve.tensor_copy(v[:, k, :], ps[:, k % 2, :]).then_inc(*v_taken.up())
                    else:
                        dve.tensor_tensor(v[:, k, :], ps[:, k % 2, :], vbias, ALU.add).then_inc(*v_taken.up())
                finish(0)
                for j in range(J):
                    if j + 1 < J:
                        finish(j + 1)
                    take_turned(j)
                    if j + 2 < J:
                        row_max(j + 2)
                dve.wait_ge(*attended.at(J * b + J))
                for h in range(G):
                    rows = slice(hd * h, hd * h + hd)
                    src = ps[rows, 6, :].rearrange("p (c n) -> p c n", c=C)[:, :, (h % 2) * 64:(h % 2) * 64 + 64]
                    dst = oT[rows, :, :].rearrange("p c (b n) -> p b c n", b=B)[:, b, :, :]
                    ins = dve.tensor_copy(dst, src)
                ins.then_inc(*o_taken.up())
                step.end()


def self_attention(m, oT, qT, kT, v, scale, clip=None, allowed=None, masked=None, custom=False):
    H, hd, R = 16, 32, 4
    s = m.sig
    scored, scores_taken, step_s = s("self_scored"), s("self_scores_taken"), s("self_step")
    centred, powered, probs_ready, zeroed = s("self_centred"), s("self_exp"), s("self_probs_ready"), s("self_zeroed")
    turned, turned_taken = s("self_turned"), s("self_turned_taken")
    attended, o_taken = s("self_attended"), s("self_attended_taken")
    with m.local(sc=[P, 2, H, S], bd=[P, 2, H, P], prT=[P, H, P], col=[P, 2, 3, H]) as (sc, bd, prT, col), \
            m.block() as block:
        ps = m.ps

        @block.gpsimd
        def _(pool):
            pool.memset(bd[:], 0.0).then_inc(*zeroed.up())

        @block.tensor
        def _(pe):
            def scores(t):
                if t >= 1:
                    pe.wait_ge(*scores_taken.at(2 * t))
                for h in range(H):
                    rows = slice(hd * (h % R), hd * (h % R) + hd)
                    ins = pe.matmul(ps[:, h % R, (h // R) * P:(h // R) * P + P],
                                    qT[rows, h // R, t * P:(t + 1) * P], kT[rows, h // R, t * P:(t + 1) * P],
                                    start=True, stop=True)
                ins.then_inc(*scored.up())

            scores(0)
            for t in range(T):
                if t + 1 < T:
                    scores(t + 1)
                pe.wait_ge(*probs_ready.at(2 * t + 2))
                for g in range(R):
                    n = R * t + g
                    if n >= 2:
                        pe.wait_ge(*turned_taken.at(n - 1))
                    for k in range(R):
                        ins = pe.transpose(ps[:, 4 + g % 2, k * P:(k + 1) * P], bd[:, t % 2, R * g + k, :], m.ident[:])
                    ins.then_inc(*turned.up())
                pe.wait_ge(*turned_taken.at(R * t + R))
                if t >= 1:
                    pe.wait_ge(*o_taken.at(t))
                for n in range(H):
                    r, c = n // R, n % R
                    h = R * c + r
                    ins = pe.matmul(ps[hd * r:hd * r + hd, 6, c * P:(c + 1) * P], v[:, t, hd * h:hd * h + hd],
                                    prT[:, n, :], start=True, stop=True)
                ins.then_inc(*attended.up())

        @block.scalar
        def _(act):
            for t in range(T):
                act.wait_ge(*scored.at(t + 1))
                if t >= 2:
                    act.wait_ge(*probs_ready.at(2 * t - 2))
                for half in range(2):
                    rows = slice(64 * half, 64 * half + 64)
                    src = ps[rows, 0:R, :].rearrange("p r (c n) -> p r c n", c=R)[:, :, :, 64 * half:64 * half + 64]
                    act.activation(sc[rows, t % 2, :, :].rearrange("p (r c) n -> p r c n", r=R), src, ACT.Copy,
                                   scale=scale).then_inc(*scores_taken.up())
                act.wait_ge(*centred.at(t + 1))
                act.activation(sc[:, t % 2, :, :], sc[:, t % 2, :, :], ACT.Exp).then_inc(*powered.up())

        @block.vector
        def _(dve):
            step = Chain(dve, step_s)

            def wide(a):
                return a.unsqueeze(2).to_broadcast([P, H, S])

            def rows_of(a):
                return a.unsqueeze(1).to_broadcast([P, H, S])

            def centre(t):
                w = sc[:, t % 2, :, :]
                dve.wait_ge(*scores_taken.at(2 * t + 2))
                if clip is not None:
                    step(dve.tensor_scalar(w, w, -clip, clip, ALU.max, ALU.min))
                if allowed is not None:
                    step(dve.tensor_tensor(w, w, rows_of(allowed), ALU.mult))
                    step(dve.tensor_tensor(w, w, rows_of(masked), ALU.add))
                step(dve.tensor_reduce(col[:, t % 2, 0, :], w, X, ALU.max))
                dve.tensor_tensor(w, w, wide(col[:, t % 2, 0, :]), ALU.subtract).then_inc(*centred.up())

            def finish(t):
                w = sc[:, t % 2, :, :]
                dve.wait_ge(*powered.at(t + 1))
                step(dve.tensor_reduce(col[:, t % 2, 1, :], w, X, ALU.add))
                if custom:
                    step(dve.tensor_scalar(col[:, t % 2, 1, :], col[:, t % 2, 1, :], 1e-6, None, ALU.add))
                step(dve.reciprocal(col[:, t % 2, 2, :], col[:, t % 2, 1, :]))
                if custom:
                    step(dve.tensor_tensor(w, w, wide(col[:, t % 2, 2, :]), ALU.mult))
                    step(dve.tensor_scalar(w, w, 1e-8, None, ALU.add))
                    step(dve.tensor_reduce(col[:, t % 2, 1, :], w, X, ALU.add))
                    step(dve.reciprocal(col[:, t % 2, 2, :], col[:, t % 2, 1, :]))
                if t >= 2:
                    dve.wait_ge(*turned.at(R * t - R))
                if t == 0:
                    dve.wait_ge(*zeroed.at(1))
                for half in range(2):
                    rows = slice(64 * half, 64 * half + 64)
                    dve.tensor_tensor(bd[rows, t % 2, :, 64 * half:64 * half + 64], sc[rows, t % 2, :, :],
                                      col[rows, t % 2, 2, :].unsqueeze(2).to_broadcast([64, H, S]), ALU.mult)\
                       .then_inc(*probs_ready.up())

            def take(t):
                for g in range(R):
                    dve.wait_ge(*turned.at(R * t + g + 1))
                    if g == 0 and t >= 1:
                        dve.wait_ge(*attended.at(t))
                    dve.tensor_copy(prT[:, R * g:R * g + R, :].rearrange("p g n -> p (g n)"), ps[:, 4 + g % 2, :])\
                       .then_inc(*turned_taken.up())
                dve.wait_ge(*attended.at(t + 1))
                dve.tensor_copy(oT[:, :, t * P:(t + 1) * P],
                                ps[:, 6, :].rearrange("p (c n) -> p c n", c=C)).then_inc(*o_taken.up())

            centre(0)
            for t in range(T):
                finish(t)
                if t + 1 < T:
                    centre(t + 1)
                take(t)


def columns(m, dst, name):
    return dst, m.d[name]


def L0_xattn(m):
    d = m.d
    normalise(m, m.y, m.x, 1e-5)
    turn(m, m.yT, m.y)
    with m.local(qT=[P, C, N], oT=[P, C, N], w=[P, C, D], bv=[P, D], bo=[1, D], b=[P, 2, C]) as (qT, oT, w, bv, bo, b):
        load(m, (b[:, 0, :], d["L0_xattn_bq"]), (b[:, 1, :], d["L0_xattn_bk"]),
             (bv[:], d["L0_xattn_bv"].partition_broadcast(P)), (bo[:], d["L0_xattn_bo"].unsqueeze(0)))
        linear_features(m, [(qT, d["L0_xattn_Wq"], w, m.yT, b[:, 0, :], ACT.Identity)])
        cross_attention(m, oT, qT, 32, 32 ** -0.5, d["L0_xattn_Wk"], d["L0_xattn_Wv"], b[:, 1, :], bv[:],
                        mask=d["mask"])
        linear_tokens(m, m.x, oT, d["L0_xattn_Wo"], w, C, bo[0:1, :], m.x)


def L0_attn(m):
    d = m.d
    normalise(m, m.y, m.x, 1e-5)
    turn(m, m.yT, m.y)
    with m.local(qT=[P, C, N], kT=[P, C, N], v=[P, T, D], w=[P, C, D], w2=[P, C, D], masks=[P, 2, S]) as \
            (qT, kT, v, w, w2, masks):
        load(m, (masks[:], d["causal"]))
        linear_features(m, [(qT, d["L0_attn_w_q"], w, m.yT, None, ACT.Identity),
                            (kT, d["L0_attn_w_k"], w2, m.yT, None, ACT.Identity)])
        linear_tokens(m, v, m.yT, d["L0_attn_w_v"], w, C)
        self_attention(m, m.yT, qT, kT, v, 32 ** -0.5, 100.0, masks[:, 0, :], masks[:, 1, :], custom=True)
        linear_tokens(m, m.x, m.yT, d["L0_attn_w_proj"], w, C, add=m.x)


def L3_xattn(m):
    d = m.d
    normalise(m, m.y, m.x, 1e-5)
    turn(m, m.yT, m.y)
    with m.local(qT=[P, C, N], oT=[P, C, N], w=[P, C, D], bv=[P, D], bo=[1, D], b=[P, 2, C]) as (qT, oT, w, bv, bo, b):
        load(m, (b[:, 0, :], d["L3_xattn_bq"]), (b[:, 1, :], d["L3_xattn_bk"]),
             (bv[:], d["L3_xattn_bv"].partition_broadcast(P)), (bo[:], d["L3_xattn_bo"].unsqueeze(0)))
        linear_features(m, [(qT, d["L3_xattn_Wq"], w, m.yT, b[:, 0, :], ACT.Identity)])
        cross_attention(m, oT, qT, 32, 32 ** -0.5, d["L3_xattn_Wk"], d["L3_xattn_Wv"], b[:, 1, :], bv[:])
        linear_tokens(m, m.x, oT, d["L3_xattn_Wo"], w, C, bo[0:1, :], m.x)


def gate_scores(m, w, buf, srcT, E, brow=None):
    landed, scored = m.sig("gate_landed"), m.sig("gate_scored")
    with m.block() as block:
        @block.sync
        def _(sp):
            sp.dma_start(buf[:], w).then_inc(*landed.up(16))

        @block.tensor
        def _(pe):
            pe.wait_ge(*landed.at(16))
            for t in range(T):
                for c in range(C):
                    ins = pe.matmul(m.ps[:, 0, t * E:(t + 1) * E], srcT[:, c, t * P:(t + 1) * P], buf[:, c, :],
                                    start=(c == 0), stop=(c == C - 1 and brow is None))
                if brow is not None:
                    ins = pe.matmul(m.ps[:, 0, t * E:(t + 1) * E], m.ones[0:1, :], brow, start=False, stop=True)
            ins.then_inc(*scored.up())


def route(m, w, E, k, before, normal, eps=0.0, renormal=True):
    step_s, centred, powered = m.sig("route_step"), m.sig("route_centred"), m.sig("route_exp")
    with m.local(sc=[P, T, E], one=[P, T], cmp=[P, T, E, E], eq=[P, T, E, E], sel=[P, T, E]) as \
            (sc, one, cmp, eq, sel), m.block() as block:
        @block.scalar
        def _(act):
            act.wait_ge(*centred.at(1))
            act.activation(sc[:], sc[:], ACT.Exp).then_inc(*powered.up())

        @block.vector
        def _(dve):
            step = Chain(dve, step_s)
            wide = lambda a: a.unsqueeze(2).to_broadcast([P, T, E])
            step(dve.tensor_copy(sc[:], m.ps[:, 0, 0:T * E].rearrange("p (t e) -> p t e", t=T)))
            step(dve.tensor_reduce(one[:], sc[:], X, ALU.max))
            dve.tensor_tensor(sc[:], sc[:], wide(one[:]), ALU.subtract).then_inc(*centred.up())
            dve.wait_ge(*powered.at(1))
            if normal:
                step(dve.tensor_reduce(one[:], sc[:], X, ALU.add))
                step(dve.reciprocal(one[:], one[:]))
                step(dve.tensor_tensor(sc[:], sc[:], wide(one[:]), ALU.mult))
            for t in range(T):
                mine = sc[:, t, :].unsqueeze(2).to_broadcast([P, E, E])
                other = sc[:, t, :].unsqueeze(1).to_broadcast([P, E, E])
                dve.tensor_tensor(cmp[:, t], other, mine, ALU.is_gt)
                step(dve.tensor_tensor(eq[:, t], other, mine, ALU.is_equal))
                step(dve.tensor_tensor(eq[:, t], eq[:, t], before, ALU.mult))
            step(dve.tensor_tensor(cmp[:], cmp[:], eq[:], ALU.add))
            step(dve.tensor_reduce(sel[:], cmp[:], X, ALU.add))
            step(dve.tensor_scalar(sel[:], sel[:], float(k), None, ALU.is_lt))
            step(dve.tensor_tensor(w[:, :, 0:E], sc[:], sel[:], ALU.mult))
            if renormal:
                step(dve.tensor_reduce(one[:], w[:, :, 0:E], X, ALU.add))
                step(dve.tensor_scalar(one[:], one[:], eps, None, ALU.add))
                step(dve.reciprocal(one[:], one[:]))
                step(dve.tensor_tensor(w[:, :, 0:E], w[:, :, 0:E], wide(one[:]), ALU.mult))


def L0_ffn(m):
    d, E, F = m.d, 8, 1024
    FC = F // P
    s = m.sig
    normalise(m, m.y, m.x, 1e-5)
    with m.local(w=[P, T, E + 1]) as (w,):
        with m.local(z=[P, T, D], zT=[P, C, N], ln=[P, 2, C], gw=[P, C, E], before=[P, E, E]) as \
                (z, zT, ln, gw, before):
            load(m, (ln[:, 0, :], d["L0_ffn_ln_scale"]), (ln[:, 1, :], d["L0_ffn_ln_bias"]),
                 (before[:], d["before8"].partition_broadcast(P)))
            turn(m, m.yT, m.y)
            normalise(m, z, m.y, 1e-5)
            turn(m, zT, z, scale=ln[:, 0, :], bias=ln[:, 1, :])
            gate_scores(m, d["L0_ffn_gate_w"], gw, zT, E)
            route(m, w, E, 2, before[:], True, 1e-5)
        up_landed, down_landed = s("gated_up_landed"), s("gated_down_landed")
        up_done, silu_done, h_ready = s("gated_up_product"), s("gated_silu"), s("gated_h_ready")
        down_done, added, one_set = s("gated_down_product"), s("gated_added"), s("shared_gate_set")
        with m.local(wg=[P, C, F], wu=[P, C, F], wd=[P, FC, D], sg=[P, 2, N], h=[P, FC, N]) as \
                (wg, wu, wd, sg, h), m.block((h_ready, 1), (added, T)) as block:
            ps = m.ps

            @block.sync
            def _(sp):
                with repeat(sp, E + 1) as e:
                    sp.wait_ge(*h_ready.at(1 + FC * e))
                    sp.dma_start(wg[:], d["L0_ffn_Wg"][e]).then_inc(*up_landed.up(16))
                    sp.dma_start(wu[:], d["L0_ffn_Wu"][e]).then_inc(*up_landed.up(16))
                    sp.wait_ge(*added.at(T + T * e))
                    sp.dma_start(wd[:], d["L0_ffn_Wd"][e]).then_inc(*down_landed.up(16))

            @block.gpsimd
            def _(pool):
                pool.memset(w[:, :, E:E + 1], 1.0).then_inc(*one_set.up())

            @block.tensor
            def _(pe):
                with repeat(pe, E + 1) as e:
                    pe.wait_ge(*up_landed.at(32 * e + 32))
                    for n in range(FC):
                        if n >= 2:
                            pe.wait_ge(*h_ready.at(FC * e + n))
                        for half, wb in ((0, wg), (1, wu)):
                            for k in range(C):
                                ins = pe.matmul(ps[:, 2 * half + n % 2, :], wb[:, k, n * P:(n + 1) * P],
                                                m.yT[:, k, :], start=(k == 0), stop=(k == C - 1))
                        ins.then_inc(*up_done.up())
                    pe.wait_ge(*down_landed.at(16 * e + 16))
                    for t in range(T):
                        pe.wait_ge(*added.at(T * e + t + 1))
                        for k in range(FC):
                            if t == 0 and k >= FC - 2:
                                pe.wait_ge(*h_ready.at(1 + FC * e + k + 1))
                            ins = pe.matmul(ps[:, 4 + t, :], h[:, k, t * P:(t + 1) * P], wd[:, k, :],
                                            start=(k == 0), stop=(k == FC - 1))
                        ins.then_inc(*down_done.up())

            @block.scalar
            def _(act):
                with repeat(act, E + 1) as e:
                    for n in range(FC):
                        act.wait_ge(*up_done.at(FC * e + n + 1))
                        if n >= 2:
                            act.wait_ge(*h_ready.at(FC * e + n))
                        else:
                            act.wait_ge(*h_ready.at(1 + FC * e))
                        act.activation(sg[:, n % 2, :], ps[:, n % 2, :], ACT.Silu).then_inc(*silu_done.up())

            @block.vector
            def _(dve):
                dve.wait_ge(*one_set.at(1))
                with repeat(dve, E + 1) as e:
                    for n in range(FC):
                        dve.wait_ge(*silu_done.at(FC * e + n + 1))
                        dve.tensor_tensor(h[:, n, :], ps[:, 2 + n % 2, :], sg[:, n % 2, :], ALU.mult)\
                           .then_inc(*h_ready.up())
                    for t in range(T):
                        dve.wait_ge(*down_done.at(T * e + t + 1))
                        dve.wait_ge(*added.at(T * e + t + 1))
                        dve.scalar_tensor_tensor(m.x[:, t, :], ps[:, 4 + t, :], w[:, t, bass.ds(e, 1)], m.x[:, t, :],
                                                 ALU.mult, ALU.add).then_inc(*added.up())


def L1_xattn(m):
    d = m.d
    temp = float(D) ** 0.5
    normalise(m, m.y, m.x, 1e-5)
    with m.local(qT=[P, C, N], oT=[P, C, N], w=[P, C, D], pre=[P, 2, C], ln=[P, 2, C], rows=[P, 2, D]) as \
            (qT, oT, w, pre, ln, rows):
        load(m, (pre[:, 0, :], d["L1_xattn_pre_g"]), (pre[:, 1, :], d["L1_xattn_pre_b"]),
             (ln[:, 0, :], d["L1_xattn_ln_g"]), (ln[:, 1, :], d["L1_xattn_ln_b"]),
             (rows[:, 0, :], d["L1_xattn_ln_g_row"].partition_broadcast(P)),
             (rows[:, 1, :], d["L1_xattn_ln_b_row"].partition_broadcast(P)))
        normalise(m, m.y, m.y, 1e-5)
        turn(m, m.yT, m.y, scale=pre[:, 0, :], bias=pre[:, 1, :])
        linear_features(m, [(qT, d["L1_xattn_Wq"], w, m.yT, None, ACT.Identity)])
        cross_attention(m, oT, qT, 64, 1.0 / temp, d["L1_xattn_Wk"], d["L1_xattn_Wv"],
                        clip=10000.0 * temp, knorm=(pre[:, 0, :], pre[:, 1, :]))
        turn_back(m, m.y, oT)
        normalise(m, m.y, m.y, 1e-5)
        turn(m, m.yT, m.y, scale=ln[:, 0, :], bias=ln[:, 1, :])
        landed, product, gelu_done, step_s = m.sig("weights_landed_0"), m.sig("tokens_product"), m.sig("gelu_done"), m.sig("gelu_step")
        with m.block() as block:
            @block.sync
            def _(sp):
                sp.dma_start(w[:], d["L1_xattn_Wo"]).then_inc(*landed.up(16))

            @block.tensor
            def _(pe):
                pe.wait_ge(*landed.at(16))
                for t in range(T):
                    for k in range(C):
                        ins = pe.matmul(m.ps[:, t, :], m.yT[:, k, t * P:(t + 1) * P], w[:, k, :],
                                        start=(k == 0), stop=(k == C - 1))
                    ins.then_inc(*product.up())

            @block.scalar
            def _(act):
                for t in range(T):
                    act.wait_ge(*product.at(t + 1))
                    act.activation(qT[:, t, :], m.ps[:, t, :], ACT.Gelu).then_inc(*gelu_done.up())

            @block.vector
            def _(dve):
                step = Chain(dve, step_s)
                for t in range(T):
                    step(dve.tensor_tensor(m.y[:, t, :], m.y[:, t, :], rows[:, 0, :], ALU.mult))
                    step(dve.tensor_tensor(m.y[:, t, :], m.y[:, t, :], rows[:, 1, :], ALU.add))
                    step(dve.tensor_tensor(m.x[:, t, :], m.x[:, t, :], m.y[:, t, :], ALU.add))
                    dve.wait_ge(*gelu_done.at(t + 1))
                    dve.tensor_tensor(m.x[:, t, :], m.x[:, t, :], qT[:, t, :], ALU.add)


def turn_back(m, dst, srcT):
    turned = m.sig("turned")
    with m.block() as block:
        @block.tensor
        def _(pe):
            for t in range(T):
                for c in range(C):
                    ins = pe.transpose(m.ps[:, t, c * P:(c + 1) * P], srcT[:, c, t * P:(t + 1) * P], m.ident[:])
                ins.then_inc(*turned.up())

        @block.vector
        def _(dve):
            for t in range(T):
                dve.wait_ge(*turned.at(t + 1))
                dve.tensor_copy(dst[:, t, :], m.ps[:, t, :])


def L1_ffn(m):
    d, E = m.d, 4
    s = m.sig
    normalise(m, m.y, m.x, 1e-5)
    turn(m, m.yT, m.y)
    add_into(m, m.x, m.x, m.y)
    w1_landed, w2_landed = s("e1_landed"), s("e2_landed")
    first, second, var_ready, rooted = s("e_first"), s("e_second"), s("e_var"), s("e_rstd")
    normed, turned, relued, freed, step_s = s("e_normed"), s("e_turned"), s("e_relu"), s("e_freed"), s("e_step")
    with m.local(w=[P, T, E], gw=[P, C, E], gb=[1, E], before=[P, E, E], w1=[P, C, D], w2=[P, C, D], h=[P, T, D],
                 hT=[P, C, N], b1=[1, E, D], b2=[1, E, D], g1=[P, E, C], be1=[P, E, C], g2=[P, E, D],
                 be2=[P, E, D]) as (w, gw, gb, before, w1, w2, h, hT, b1, b2, g1, be1, g2, be2):
        load(m, (before[:], d["before4"].partition_broadcast(P)), (gb[:], d["L1_ffn_gate_b"].unsqueeze(0)),
             (b1[:], d["L1_ffn_b1"].unsqueeze(0)), (b2[:], d["L1_ffn_b2"].unsqueeze(0)),
             (g1[:], d["L1_ffn_g1"]), (be1[:], d["L1_ffn_be1"]),
             (g2[:], d["L1_ffn_g2"].partition_broadcast(P)), (be2[:], d["L1_ffn_be2"].partition_broadcast(P)))
        gate_scores(m, d["L1_ffn_gate_W"], gw, m.yT, E, gb[0:1, :])
        route(m, w, E, 2, before[:], False)
        with m.block((normed, 1)) as block:
            ps = m.ps

            @block.sync
            def _(sp):
                with repeat(sp, E) as e:
                    sp.wait_ge(*normed.at(1 + 2 * e))
                    sp.dma_start(w1[:], d["L1_ffn_W1"][e]).then_inc(*w1_landed.up(16))
                    sp.dma_start(w2[:], d["L1_ffn_W2"][e]).then_inc(*w2_landed.up(16))

            @block.tensor
            def _(pe):
                with repeat(pe, E) as e:
                    pe.wait_ge(*w1_landed.at(16 * e + 16))
                    pe.wait_ge(*normed.at(1 + 2 * e))
                    for t in range(T):
                        for k in range(C):
                            pe.matmul(ps[:, t, :], m.yT[:, k, t * P:(t + 1) * P], w1[:, k, :], start=(k == 0), stop=False)
                        ins = pe.matmul(ps[:, t, :], m.ones[0:1, :], b1[0:1, e, :], start=False, stop=True)
                        ins.then_inc(*first.up())
                    pe.wait_ge(*normed.at(1 + 2 * e + 1))
                    for c in range(C):
                        for t in range(T):
                            ins = pe.transpose(ps[:, 4 + c, t * P:(t + 1) * P], h[:, t, c * P:(c + 1) * P], m.ident[:])
                        ins.then_inc(*turned.up())
                    pe.wait_ge(*relued.at(C * e + C))
                    pe.wait_ge(*w2_landed.at(16 * e + 16))
                    for t in range(T):
                        for k in range(C):
                            pe.matmul(ps[:, t, :], hT[:, k, t * P:(t + 1) * P], w2[:, k, :], start=(k == 0), stop=False)
                        ins = pe.matmul(ps[:, t, :], m.ones[0:1, :], b2[0:1, e, :], start=False, stop=True)
                        ins.then_inc(*second.up())

            @block.scalar
            def _(act):
                with repeat(act, E) as e:
                    for c in range(C):
                        act.wait_ge(*turned.at(C * e + c + 1))
                        act.activation(hT[:, c, :], ps[:, 4 + c, :], ACT.Relu, bias=be1[:, e, c:c + 1],
                                       scale=g1[:, e, c:c + 1]).then_inc(*relued.up())

            @block.gpsimd
            def _(pool):
                with repeat(pool, 2 * E) as i:
                    pool.wait_ge(*var_ready.at(i + 1))
                    pool.tensor_tensor(m.rstd[:], m.den[:], m.minus_half[:], ALU.pow).then_inc(*rooted.up())

            @block.vector
            def _(dve):
                with repeat(dve, E) as e:
                    step = Chain(dve, step_s, e, 2 * T + 2 + 3 * T)

                    def norm(products, half):
                        for t in range(T):
                            dve.wait_ge(*products.at(T * e + t + 1))
                            step(dve.bn_stats(m.stats[:, t, :], ps[:, t, :]))
                        dve.memset(m.den[:], 0.0)
                        for t in range(T):
                            ins = dve.bn_aggr(m.mv[:, t, :], m.stats[:, t, :])
                        step(ins)
                        dve.tensor_scalar(m.den[:], m.mv[:, :, 1], 1e-5, None, ALU.add).then_inc(*var_ready.up())
                        dve.wait_ge(*rooted.at(2 * e + half + 1))
                        for t in range(T):
                            ins = dve.tensor_scalar(h[:, t, :], ps[:, t, :], m.mv[:, t, 0:1], m.rstd[:, t:t + 1],
                                                    ALU.subtract, ALU.mult)
                        ins.then_inc(*normed.up())
                        dve.wait_ge(*normed.at(1 + 2 * e + half + 1))

                    norm(first, 0)
                    norm(second, 1)
                    for t in range(T):
                        step(dve.tensor_tensor(h[:, t, :], h[:, t, :], g2[:, e, :], ALU.mult))
                        step(dve.tensor_tensor(h[:, t, :], h[:, t, :], be2[:, e, :], ALU.add))
                        step(dve.scalar_tensor_tensor(m.x[:, t, :], h[:, t, :], w[:, t, bass.ds(e, 1)], m.x[:, t, :],
                                                      ALU.mult, ALU.add))
                    step.end()


def L2_xattn(m):
    d = m.d
    scale = (D / 16) ** 0.5
    s = m.sig
    normalise(m, m.y, m.x, 1e-5)
    turn(m, m.yT, m.y)
    ctxt_landed, ctx_landed = [s("pair_ctxT_landed0"), s("pair_ctxT_landed1")], [s("pair_ctx_landed0"), s("pair_ctx_landed1")]
    scored, max_ready, powered, scaled = s("pair_scored"), s("pair_max_ready"), s("pair_exp"), s("pair_scaled")
    turned, taken, attended, o_taken, step_s = s("pair_turned"), s("pair_turned_taken"), s("pair_attended"), s("pair_attended_taken"), s("pair_step")
    biased = s("pair_bias_scored")
    with m.local(qT=[P, C, N], q2T=[P, C, N], w=[P, C, D], w2=[P, C, D], b=[P, 2, C], bv=[1, D]) as (qT, q2T, w, w2, b, bv):
        load(m, (b[:, 0, :], d["L2_xattn_bq"]), (b[:, 1, :], d["L2_xattn_bk"]), (bv[:], d["L2_xattn_bv"].unsqueeze(0)))
        linear_features(m, [(qT, d["L2_xattn_Wq"], w, m.yT, b[:, 0, :], ACT.Identity)])
        linear_features(m, [(q2T, d["L2_xattn_Wk"], w2, qT, None, ACT.Identity)])
        with m.local(ctxT=[P, 2, 2, C, SK], ctx=[P, 2, KC, D], pr=[P, SK], prT=[P, KC, P], sc=[P, SK],
                     col=[P, T, 4], qb=[P, T]) as (ctxT, ctx, pr, prT, sc, col, qb), m.block() as block:
            ps = m.ps

            @block.sync
            def _(sp):
                for t in range(T):
                    if t >= 2:
                        sp.wait_ge(*scored.at(t - 1))
                    sp.dma_start(ctxT[:, t % 2], d["ctxT"][2 * t:2 * t + 2].rearrange("b p c n -> p b c n"))\
                      .then_inc(*ctxt_landed[t % 2].up(16))
                    if t >= 1:
                        sp.wait_ge(*attended.at(t))
                    sp.dma_start(ctx[:], d["ctx"][2 * t:2 * t + 2].rearrange("b p c n -> p b c n"))\
                      .then_inc(*ctx_landed[0].up(16))

            @block.tensor
            def _(pe):
                for t in range(T):
                    for c in range(C):
                        ins = pe.matmul(ps[:, 7, t:t + 1], qT[:, c, t * P:(t + 1) * P], b[:, 1, c:c + 1],
                                        start=(c == 0), stop=(c == C - 1))
                ins.then_inc(*biased.up())

                def scores(t):
                    pe.wait_ge(*ctxt_landed[t % 2].at(16 * (t // 2 + 1)))
                    if t >= 2:
                        pe.wait_ge(*max_ready.at(t - 1))
                    for half in range(2):
                        for c in range(C):
                            ins = pe.matmul(ps[64 * half:64 * half + 64, t % 2, :],
                                            q2T[:, c, t * P + 64 * half:t * P + 64 * half + 64],
                                            ctxT[:, t % 2, half, c, :], start=(c == 0), stop=(c == C - 1))
                    ins.then_inc(*scored.up())

                scores(0)
                for t in range(T):
                    if t + 1 < T:
                        scores(t + 1)
                    pe.wait_ge(*scaled.at(t + 1))
                    for k in range(KC):
                        ins = pe.transpose(ps[:, 2, k * P:(k + 1) * P], pr[:, k * P:(k + 1) * P], m.ident[:])
                    ins.then_inc(*turned.up())
                    pe.wait_ge(*ctx_landed[0].at(16 * t + 16))
                    pe.wait_ge(*taken.at(t + 1))
                    if t >= 1:
                        pe.wait_ge(*o_taken.at(t))
                    for c in range(C):
                        for half in range(2):
                            for k in range(KC):
                                ins = pe.matmul(ps[:, 3, c * P + 64 * half:c * P + 64 * half + 64],
                                                ctx[:, half, k, c * P:(c + 1) * P],
                                                prT[:, k, 64 * half:64 * half + 64],
                                                start=(k == 0), stop=(k == KC - 1))
                    ins.then_inc(*attended.up())

            @block.scalar
            def _(act):
                for t in range(T):
                    act.wait_ge(*max_ready.at(t + 1))
                    act.activation(pr[:], sc[:], ACT.Exp, bias=col[:, t, 1:2], scale=scale,
                                   accum_out=col[:, t, 2:3]).then_inc(*powered.up())

            @block.vector
            def _(dve):
                step = Chain(dve, step_s)
                dve.wait_ge(*biased.at(1))
                step(dve.tensor_copy(qb[:], ps[:, 7, 0:T]))
                for t in range(T):
                    dve.wait_ge(*scored.at(t + 1))
                    step(dve.tensor_scalar(sc[:], ps[:, t % 2, :], qb[:, t:t + 1], None, ALU.add))
                    step(dve.tensor_reduce(col[:, t, 0:1], sc[:], X, ALU.max, negate=True))
                    dve.tensor_scalar(col[:, t, 1:2], col[:, t, 0:1], scale, None, ALU.mult).then_inc(*max_ready.up())
                    dve.wait_ge(*powered.at(t + 1))
                    step(dve.reciprocal(col[:, t, 3:4], col[:, t, 2:3]))
                    dve.tensor_scalar(pr[:], pr[:], col[:, t, 3:4], None, ALU.mult).then_inc(*scaled.up())
                    dve.wait_ge(*turned.at(t + 1))
                    dve.tensor_copy(prT[:], ps[:, 2, :].rearrange("p (k n) -> p k n", k=KC)).then_inc(*taken.up())
                    dve.wait_ge(*attended.at(t + 1))
                    dve.tensor_copy(m.yT[:, :, t * P:(t + 1) * P],
                                    ps[:, 3, :].rearrange("p (c n) -> p c n", c=C)).then_inc(*o_taken.up())
        linear_tokens(m, m.x, m.yT, d["L2_xattn_Wv"], w, C, bv[0:1, :], m.x)


def transformer_layer(m, z, n, ln1, wq, bq, wk, bk, wv, bv, wo, bo, ln2, w1, b1, w2, b2, act, allowed=None, rope=None):
    d = m.d
    FF = 2048
    with m.local(qT=[P, C, N], kT=[P, C, N], v=[P, T, D], w=[P, C, D], wb=[P, C, D], cols=[P, 6, C], bvb=[P, D],
                 bor=[1, D], masks=[P, 2, S]) as (qT, kT, v, w, wb, cols, bvb, bor, masks):
        load(m, *[(cols[:, i, :], d[a]) for i, a in enumerate((ln1[0], ln1[1], bq, bk))],
             (bvb[0:1, :], d[bv].unsqueeze(0)), (bor[:], d[bo].unsqueeze(0)),
             *([(masks[:], d[allowed])] if allowed else []))
        normalise(m, n, z, 1e-5)
        turn(m, m.yT, n, scale=cols[:, 0, :], bias=cols[:, 1, :])
        linear_features(m, [(qT, d[wq], w, m.yT, cols[:, 2, :], ACT.Identity),
                            (kT, d[wk], wb, m.yT, cols[:, 3, :], ACT.Identity)])
        linear_tokens(m, v, m.yT, d[wv], w, C, bvb[0:1, :])
        if rope:
            rotate(m, qT, kT)
        if allowed:
            self_attention(m, m.yT, qT, kT, v, 32 ** -0.5, None, masks[:, 0, :], masks[:, 1, :])
        else:
            self_attention(m, m.yT, qT, kT, v, 32 ** -0.5)
        linear_tokens(m, z, m.yT, d[wo], w, C, bor[0:1, :], z)
    with m.local(cols=[P, 2, C], b1c=[P, FF // P], b2r=[1, D], wa=[P, C, FF], wb=[P, FF // P, D], h=[P, FF // P, N]) as \
            (cols, b1c, b2r, wa, wb, h):
        load(m, (cols[:, 0, :], d[ln2[0]]), (cols[:, 1, :], d[ln2[1]]), (b1c[:], d[b1]), (b2r[:], d[b2].unsqueeze(0)))
        normalise(m, n, z, 1e-5)
        turn(m, m.yT, n, scale=cols[:, 0, :], bias=cols[:, 1, :])
        linear_features(m, [(h, d[w1], wa, m.yT, b1c, act)])
        linear_tokens(m, z, h, d[w2], wb, FF // P, b2r[0:1, :], z)


def rotate(m, qT, kT):
    turned, timed, step_s = m.sig("pairs_turned"), m.sig("cos_multiplied"), m.sig("rotate_step")
    with m.local(perm=[P, P], trig=[P, 2, S], tmp=[P, 2, N]) as (perm, trig, tmp):
        load(m, (perm[:], m.d["rope_turn"]), (trig[:], m.d["rope_trig"]))
        with m.block() as block:
            @block.tensor
            def _(pe):
                for n in range(2 * C):
                    src = (qT, kT)[n // C]
                    pe.matmul(m.ps[:, n, :], perm[:], src[:, n % C, :], start=True, stop=True).then_inc(*turned.up())

            @block.vector
            def _(dve):
                step = Chain(dve, step_s)
                over = lambda a: a.unsqueeze(1).to_broadcast([P, B, S])
                for n in range(2 * C):
                    src = (qT, kT)[n // C][:, n % C, :].rearrange("p (b s) -> p b s", b=B)
                    t = tmp[:, n % 2, :].rearrange("p (b s) -> p b s", b=B)
                    dve.wait_ge(*turned.at(n + 1))
                    dve.tensor_tensor(t, m.ps[:, n, :].rearrange("p (b s) -> p b s", b=B), over(trig[:, 1, :]), ALU.mult)
                    step(dve.tensor_tensor(src, src, over(trig[:, 0, :]), ALU.mult))
                    step(dve.tensor_tensor(src, src, t, ALU.add))


def L2_attn(m):
    normalise(m, m.y, m.x, 1e-5)
    with m.local(n=[P, T, D]) as (n,):
        for i in range(2):
            g = lambda a: f"L2_attn_{a}_{i}"
            transformer_layer(m, m.y, n, (g("ln1_g"), g("ln1_b")), g("wq"), g("bq"), g("wk"), g("bk"), g("wv"), g("bv"),
                              g("wo"), g("bo"), (g("ln2_g"), g("ln2_b")), g("w1"), g("b1"), g("w2"), g("b2"), ACT.Gelu,
                              allowed="strided")
        with m.local(rows=[P, 2, D]) as (rows,):
            load(m, (rows[:, 0, :], m.d["L2_attn_lnf_g"].partition_broadcast(P)),
                 (rows[:, 1, :], m.d["L2_attn_lnf_b"].partition_broadcast(P)))
            normalise(m, n, m.y, 1e-5)
            scaled = m.sig("final_norm_step")
            with m.block() as block:
                @block.vector
                def _(dve):
                    step = Chain(dve, scaled)
                    over = lambda a: a.unsqueeze(1).to_broadcast([P, T, D])
                    step(dve.tensor_tensor(n[:], n[:], over(rows[:, 0, :]), ALU.mult))
                    step(dve.tensor_tensor(n[:], n[:], over(rows[:, 1, :]), ALU.add))
                    step(dve.tensor_tensor(m.x[:], m.x[:], n[:], ALU.add))


def L3_attn(m):
    normalise(m, m.y, m.x, 1e-5)
    g = lambda a: f"L3_attn_{a}"
    with m.local(n=[P, T, D]) as (n,):
        transformer_layer(m, m.y, n, (g("g1"), g("beta1")), g("Wq"), g("bq"), g("Wk"), g("bk"), g("Wv"), g("bv"),
                          g("Wo"), g("bo"), (g("g2"), g("beta2")), g("W1"), g("b1"), g("W2"), g("b2"), ACT.Relu, rope=True)
    add_into(m, m.x, m.x, m.y)


def L2_ffn(m):
    d, E, F, CAP = m.d, 8, 2048, S // 8
    FC, SL = F // P, B * CAP
    s = m.sig
    normalise(m, m.y, m.x, 1e-5)
    turn(m, m.yT, m.y)
    with m.local(xT=[P, C, E, SL], cmbT=[P, E // 2, N]) as (xT, cmbT):
        with m.local(w=[P, T, E], gw=[P, C, E], before=[P, E, E], earlier=[P, P], place=[P, CAP], one=[P, T, E],
                     disp=[P, T, E, SL], hot=[P, T * E, CAP]) as (w, gw, before, earlier, place, one, disp, hot):
            load(m, (before[:], d["before8"].partition_broadcast(P)), (earlier[:], d["earlier"]),
                 (place[:], d["place"].partition_broadcast(P)))
            gate_scores(m, d["L2_ffn_Wg"], gw, m.yT, E)
            route(m, w, E, 1, before[:], True, renormal=False)
            chosen, counted, step_s, dispatched = s("chosen"), s("counted"), s("dispatch_step"), s("dispatched")
            gathered, gathered_taken, weighed, c_turned = s("gathered"), s("gathered_taken"), s("weighed"), s("combine_turned")
            zeroed = s("dispatch_zeroed")
            with m.block() as block:
                ps = m.ps

                @block.gpsimd
                def _(pool):
                    pool.memset(disp[:], 0.0).then_inc(*zeroed.up())

                @block.tensor
                def _(pe):
                    pe.wait_ge(*chosen.at(1))
                    for t in range(T):
                        ins = pe.matmul(ps[:, 0, t * E:(t + 1) * E], earlier[:], one[:, t, :], start=True, stop=True)
                    ins.then_inc(*counted.up())
                    pe.wait_ge(*dispatched.at(1))
                    for t in range(T):
                        for c in range(C):
                            ins = pe.matmul(ps[:, 1 + t % 2, c * P:(c + 1) * P], m.y[:, t, c * P:(c + 1) * P],
                                            disp[:, t, :, t * 16:(t + 1) * 16], start=True, stop=True)
                        ins.then_inc(*gathered.up())
                        if t + 1 < T and t >= 1:
                            pe.wait_ge(*gathered_taken.at(t))
                    pe.wait_ge(*weighed.at(1))
                    for j in range(E // 2):
                        for t in range(T):
                            ins = pe.transpose(ps[:, 4 + j, t * P:(t + 1) * P],
                                               disp[:, t, 2 * j:2 * j + 2, :].rearrange("p e n -> p (e n)"), m.ident[:])
                        ins.then_inc(*c_turned.up())

                @block.vector
                def _(dve):
                    step = Chain(dve, step_s)
                    dve.tensor_scalar(one[:], w[:], 0.0, None, ALU.is_gt).then_inc(*chosen.up())
                    dve.wait_ge(*counted.at(1))
                    step(dve.tensor_tensor(hot[:], ps[:, 0, 0:T * E].unsqueeze(2).to_broadcast([P, T * E, CAP]),
                                           place[:].unsqueeze(1).to_broadcast([P, T * E, CAP]), ALU.is_equal))
                    step(dve.tensor_tensor(hot[:], hot[:],
                                           one[:].rearrange("p t e -> p (t e)").unsqueeze(2).to_broadcast([P, T * E, CAP]),
                                           ALU.mult))
                    dve.wait_ge(*zeroed.at(1))
                    for t in range(T):
                        for half in range(2):
                            rows = slice(64 * half, 64 * half + 64)
                            o = 16 * t + CAP * half
                            ins = dve.tensor_copy(disp[rows, t, :, o:o + CAP], hot[rows, t * E:(t + 1) * E, :])
                    step(ins)
                    ins = dve.tensor_copy(one[:], one[:])
                    ins.then_inc(*dispatched.up())
                    for t in range(T):
                        dve.wait_ge(*gathered.at(t + 1))
                        for c in range(C):
                            ins = dve.tensor_copy(xT[:, c, :, 16 * t:16 * t + 16],
                                                  ps[:, 1 + t % 2, c * P:(c + 1) * P].rearrange("p (e n) -> p e n", e=E))
                        ins.then_inc(*gathered_taken.up())
                    ins = dve.tensor_tensor(disp[:].rearrange("p t e n -> p (t e) n"),
                                            disp[:].rearrange("p t e n -> p (t e) n"),
                                            w[:].rearrange("p t e -> p (t e)").unsqueeze(2).to_broadcast([P, T * E, SL]),
                                            ALU.mult)
                    ins.then_inc(*weighed.up())
                    for j in range(E // 2):
                        dve.wait_ge(*c_turned.at(j + 1))
                        dve.tensor_copy(cmbT[:, j, :], ps[:, 4 + j, :])

        w1_landed, w2_landed = [s(f"switch_w1_landed{i}") for i in range(4)], [s(f"switch_w2_landed{i}") for i in range(4)]
        up_done, h_ready, down_done, o_taken, combined = s("switch_up"), s("switch_h_ready"), s("switch_down"), s("switch_o_taken"), s("switch_combined")
        with m.local(wa=[P, 4, C, 512], wb=[P, 4, 4, D], h=[P, 2, FC // 2, SL], o=[P, E // 2, D]) as (wa, wb, h, o), \
                m.block((up_done, 4), (down_done, 4), (o_taken, 1)) as block:
            ps = m.ps

            @block.sync
            def _(sp):
                with repeat(sp, E) as e:
                    for g in range(4):
                        sp.wait_ge(*up_done.at(4 * e + g + 1))
                        sp.dma_start(wa[:, g], d["L2_ffn_W1"][e, g]).then_inc(*w1_landed[g].up(16))
                    for g in range(4):
                        sp.wait_ge(*down_done.at(4 * e + g + 1))
                        sp.dma_start(wb[:, g], d["L2_ffn_W2"][e, g]).then_inc(*w2_landed[g].up(16))

            @block.tensor
            def _(pe):
                with repeat(pe, E // 2) as j:
                    for half in range(2):
                        e = 2 * j + half
                        for g in range(4):
                            pe.wait_ge(*w1_landed[g].at(16 * e + 16))
                            for n in range(4):
                                f = 4 * g + n
                                for k in range(C):
                                    ins = pe.matmul(ps[:, f // 8, (f % 8) * SL:(f % 8) * SL + SL],
                                                    wa[:, g, k, n * P:(n + 1) * P], xT[:, k, e, :],
                                                    start=(k == 0), stop=(k == C - 1))
                            ins.then_inc(*up_done.up())
                        for g in range(4):
                            pe.wait_ge(*w2_landed[g].at(16 * e + 16))
                            if g == 0:
                                pe.wait_ge(*o_taken.at(e + 1))
                            if g % 2 == 0:
                                pe.wait_ge(*h_ready.at(2 * e + g // 2 + 1))
                            for n in range(4):
                                f = 4 * g + n
                                ins = pe.matmul(ps[64 * half:64 * half + 64, 2, :], h[:, f // 8, f % 8, :], wb[:, g, n, :],
                                                start=(f == 0), stop=(f == FC - 1))
                            ins.then_inc(*down_done.up())
                pe.wait_ge(*o_taken.at(E + 1))
                for t in range(T):
                    for j in range(E // 2):
                        ins = pe.matmul(ps[:, 4 + t, :], cmbT[:, j, t * P:(t + 1) * P], o[:, j, :],
                                        start=(j == 0), stop=(j == E // 2 - 1))
                    ins.then_inc(*combined.up())

            @block.scalar
            def _(act):
                with repeat(act, E) as e:
                    for half in range(2):
                        act.wait_ge(*up_done.at(4 + 4 * e + 2 * half + 2))
                        act.activation(h[:, half, :, :].rearrange("p f n -> p (f n)"), ps[:, half, :],
                                       ACT.Gelu_apprx_tanh).then_inc(*h_ready.up())

            @block.vector
            def _(dve):
                with repeat(dve, E // 2) as j:
                    for half in range(2):
                        rows = slice(64 * half, 64 * half + 64)
                        dve.wait_ge(*down_done.at(4 + 8 * j + 4 * half + 4))
                        dve.tensor_copy(o[rows, j, :], ps[rows, 2, :]).then_inc(*o_taken.up())
                for t in range(T):
                    dve.wait_ge(*combined.at(t + 1))
                    dve.tensor_tensor(m.x[:, t, :], m.x[:, t, :], ps[:, 4 + t, :], ALU.add)


def L3_ffn(m):
    d, E, F = m.d, 32, 2048
    FC = F // P
    s = m.sig
    normalise(m, m.y, m.x, 1e-5)
    turn(m, m.yT, m.y)
    with m.local(kept=[E, B, S], mT=[P, C, E + 1, B], oT=[P, C, B, E], b1c=[P, E, FC], b2c=[P, E, C]) as (kept, mT, oT, b1c, b2c):
        landed, scored, centred, powered, step_s = s("gate_landed"), s("gate_scored"), s("route_centred"), s("route_exp"), s("route_step")
        kept_ready, k_turned, kt_taken, merged, merged_taken = s("kept_ready"), s("kept_turned"), s("kept_turned_taken"), s("merged"), s("merged_taken")
        with m.local(gw=[P, C, E], gb=[E, 1], sc=[E, B, S], left=[E, B, S], top=[E, B, 8], one=[E, B], keptT=[P, T, E]) as \
                (gw, gb, sc, left, top, one, keptT), m.block() as block:
            ps = m.ps

            @block.sync
            def _(sp):
                sp.dma_start(gw[:], d["L3_ffn_gate_w"]).then_inc(*landed.up(16))
                sp.dma_start(gb[:], d["L3_ffn_gate_b"].unsqueeze(1)).then_inc(*landed.up(16))
                sp.dma_start(b1c[:], d["L3_ffn_b1"]).then_inc(*landed.up(16))
                sp.dma_start(b2c[:], d["L3_ffn_b2"]).then_inc(*landed.up(16))
                sp.wait_ge(*landed.at(64))

            @block.tensor
            def _(pe):
                pe.wait_ge(*landed.at(64))
                for c in range(C):
                    ins = pe.matmul(ps[0:E, 0, :], gw[:, c, :], m.yT[:, c, :], start=(c == 0), stop=(c == C - 1))
                ins.then_inc(*scored.up())
                pe.wait_ge(*kept_ready.at(1))
                for t in range(T):
                    ins = pe.transpose(ps[:, 1, t * E:(t + 1) * E],
                                       kept[:, 2 * t:2 * t + 2, :].rearrange("e b s -> e (b s)"), m.ident[0:E, 0:E])
                ins.then_inc(*k_turned.up())
                pe.wait_ge(*kt_taken.at(1))
                for c in range(C):
                    for half in range(2):
                        for t in range(T):
                            rows = slice(64 * half, 64 * half + 64)
                            b = 2 * t + half
                            ins = pe.matmul(ps[:, 2 + 2 * half + c % 2, t * E:(t + 1) * E], m.y[rows, t, c * P:(c + 1) * P],
                                            keptT[rows, t, :], start=True, stop=True)
                    ins.then_inc(*merged.up())
                    if c >= 1 and c + 1 < C:
                        pe.wait_ge(*merged_taken.at(c))

            @block.scalar
            def _(act):
                act.wait_ge(*centred.at(1))
                act.activation(sc[:], sc[:], ACT.Exp).then_inc(*powered.up())

            @block.vector
            def _(dve):
                step = Chain(dve, step_s)
                wide = lambda a: a.unsqueeze(2).to_broadcast([E, B, S])
                dve.wait_ge(*scored.at(1))
                step(dve.tensor_scalar(sc[:].rearrange("e b s -> e (b s)"), ps[0:E, 0, :], gb[:, 0:1], None, ALU.add))
                step(dve.tensor_reduce(one[:], sc[:], X, ALU.max))
                dve.tensor_tensor(sc[:], sc[:], wide(one[:]), ALU.subtract).then_inc(*centred.up())
                dve.wait_ge(*powered.at(1))
                step(dve.tensor_reduce(one[:], sc[:], X, ALU.add))
                step(dve.reciprocal(one[:], one[:]))
                step(dve.tensor_tensor(sc[:], sc[:], wide(one[:]), ALU.mult))
                for b in range(B):
                    ins = dve.max(top[:, b, :], sc[:, b, :])
                step(ins)
                for b in range(B):
                    ins = dve.match_replace(left[:, b, :], top[:, b, :], sc[:, b, :], 0.0)
                step(ins)
                dve.tensor_tensor(kept[:], sc[:], left[:], ALU.subtract).then_inc(*kept_ready.up())
                dve.wait_ge(*k_turned.at(1))
                dve.tensor_copy(keptT[:].rearrange("p t e -> p (t e)"), ps[:, 1, 0:T * E]).then_inc(*kt_taken.up())
                for c in range(C):
                    dve.wait_ge(*merged.at(c + 1))
                    for half in range(2):
                        ins = dve.tensor_copy(mT[:, c, 0:E, :].rearrange("p e (t h) -> p h t e", h=2)[:, half],
                                              ps[:, 2 + 2 * half + c % 2, 0:T * E].rearrange("p (t e) -> p t e", t=T))
                    ins.then_inc(*merged_taken.up())
                dve.memset(mT[:, :, E, :], 0.0)

        w1_landed, w2_landed = [s(f"last_w1_landed{i}") for i in range(4)], [s(f"last_w2_landed{i}") for i in range(4)]
        up_done, down_done, biased, h_ready, o_taken = s("last_up"), s("last_down"), s("last_biased"), s("last_h_ready"), s("last_o_taken")
        mine_ready = s("last_mine_ready")
        with m.local(wa=[P, 4, C, 512], wb=[P, 4, 4, D], pre=[P, 4, 4, B], h=[P, 4, 4, B], mine=[P, 2, C, B]) as \
                (wa, wb, pre, h, mine), m.block((up_done, 4), (down_done, 4), (biased, 2), (o_taken, 1)) as block:
            ps = m.ps

            @block.sync
            def _(sp):
                with repeat(sp, E) as e:
                    for g in range(4):
                        sp.wait_ge(*up_done.at(4 * e + g + 1))
                        sp.dma_start(wa[:, g], d["L3_ffn_w1"][e, g]).then_inc(*w1_landed[g].up(16))
                    for g in range(4):
                        sp.wait_ge(*down_done.at(4 * e + g + 1))
                        sp.dma_start(wb[:, g], d["L3_ffn_w2"][e, g]).then_inc(*w2_landed[g].up(16))

            @block.tensor
            def _(pe):
                with repeat(pe, E // 2) as pair:
                    for odd in range(2):
                        e = 2 * pair + odd
                        pe.wait_ge(*mine_ready.at(e + 1))
                        for g in range(4):
                            pe.wait_ge(*w1_landed[g].at(16 * e + 16))
                            pe.wait_ge(*biased.at(4 * e + g + 1))
                            for n in range(4):
                                for k in range(C):
                                    ins = pe.matmul(ps[:, g % 2, n * B:(n + 1) * B], wa[:, g, k, n * P:(n + 1) * P],
                                                    mine[:, odd, k, :], start=(k == 0), stop=(k == C - 1))
                            ins.then_inc(*up_done.up())
                        pe.wait_ge(*o_taken.at(e + 1))
                        for g in range(4):
                            pe.wait_ge(*w2_landed[g].at(16 * e + 16))
                            pe.wait_ge(*h_ready.at(4 * e + g + 1))
                            for c in range(C):
                                for n in range(4):
                                    ins = pe.matmul(ps[:, 2 + c, 0:B], wb[:, g, n, c * P:(c + 1) * P], h[:, g, n, :],
                                                    start=(g == 0 and n == 0), stop=(g == 3 and n == 3))
                            ins.then_inc(*down_done.up())

            @block.scalar
            def _(act):
                with repeat(act, E) as e:
                    for g in range(4):
                        act.wait_ge(*biased.at(2 + 4 * e + g + 1))
                        if g == 0:
                            act.wait_ge(*down_done.at(4 * e + 4))
                        act.activation(h[:, g], pre[:, g], ACT.Gelu).then_inc(*h_ready.up())

            @block.vector
            def _(dve):
                dve.tensor_copy(mine[:, 0], mT[:, :, 0, :]).then_inc(*mine_ready.up())
                with repeat(dve, E // 2) as pair:
                    for odd in range(2):
                        e = 2 * pair + odd
                        dve.wait_ge(*up_done.at(4 + 4 * e))
                        nxt = bass.ds(e + 1, 1)
                        dve.tensor_copy(mine[:, 1 - odd],
                                        mT[:, :, nxt, :].rearrange("p c o b -> p c (o b)")).then_inc(*mine_ready.up())
                        for g in range(4):
                            dve.wait_ge(*up_done.at(4 + 4 * e + g + 1))
                            if g == 0:
                                dve.wait_ge(*o_taken.at(e + 1))
                            dve.tensor_tensor(pre[:, g], ps[:, g % 2, 0:4 * B].rearrange("p (n b) -> p n b", n=4),
                                              b1c[:, e, 4 * g:4 * g + 4].unsqueeze(2).to_broadcast([P, 4, B]), ALU.add)\
                               .then_inc(*biased.up())
                        dve.wait_ge(*down_done.at(4 + 4 * e + 4))
                        dve.tensor_tensor(oT[:, :, :, e], ps[:, 2:2 + C, 0:B],
                                          b2c[:, e, :].unsqueeze(2).to_broadcast([P, C, B]), ALU.add)\
                           .then_inc(*o_taken.up())

        o_turned, o_copied, given = s("experts_turned"), s("experts_turned_taken"), s("given_back")
        with m.local(o=[E, B, D]) as (o,), m.block() as block:
            ps = m.ps

            @block.tensor
            def _(pe):
                def give(b):
                    rows = slice(64 * (b % 2), 64 * (b % 2) + 64)
                    pe.wait_ge(*o_copied.at(b + 1))
                    pe.matmul(ps[rows, 4 + b // 2, :], kept[:, b, :], o[:, b, :], start=True, stop=True)\
                      .then_inc(*given.up())

                for b in range(B):
                    if b >= 2:
                        pe.wait_ge(*o_copied.at(b - 1))
                    for c in range(C):
                        ins = pe.transpose(ps[0:E, b % 2, c * P:(c + 1) * P], oT[:, c, b, :], m.ident[:])
                    ins.then_inc(*o_turned.up())
                    if b >= 1:
                        give(b - 1)
                give(B - 1)

            @block.vector
            def _(dve):
                for b in range(B):
                    dve.wait_ge(*o_turned.at(b + 1))
                    dve.tensor_copy(o[:, b, :], ps[0:E, b % 2, :]).then_inc(*o_copied.up())
                for t in range(T):
                    dve.wait_ge(*given.at(2 * t + 2))
                    dve.tensor_tensor(m.x[:, t, :], m.x[:, t, :], ps[:, 4 + t, :], ALU.add)


def L1_attn(m):
    d, H, DI, NC = m.d, 32, 1024, 8
    s = m.sig
    normalise(m, m.y, m.x, 1e-5)
    with m.local(va=[P, NC, N], u=[P, NC, N], key=[P, 2, NC, N], kb=[P, 2, NC, N], a11=[P, NC, N], a12=[P, NC, N],
                 W=[P, NC, 512], vecs=[P, 8, NC], convw=[P, NC, 4], inb=[P, 4 * NC], rmsw=[P, C]) as \
            (va, u, key, kb, a11, a12, W, vecs, convw, inb, rmsw):
        flat = lambda a: a.rearrange("p c n -> p (c n)")
        load(m, (vecs[:, 0, :], d["L1_attn_conv_b"]), (vecs[:, 1, :], d["L1_attn_gn_w"]),
             (vecs[:, 2, :], d["L1_attn_gn_b"]), (vecs[:, 3, :], d["L1_attn_D"]), (convw[:], d["L1_attn_conv_w"]),
             (inb[:], d["L1_attn_in_proj_b"]), (rmsw[:], d["L1_attn_rms_w"]))
        n = a11[:, 0:T, :]
        normalise(m, n, m.y, 1e-6, rms=True)
        turn(m, m.yT, n, scale=rmsw[:])
        wbuf = [W[:].rearrange("p c n -> p (c n)").rearrange("p (k n) -> p k n", k=C),
                kb[:, 0].rearrange("p c n -> p (c n)").rearrange("p (k n) -> p k n", k=C),
                kb[:, 1].rearrange("p c n -> p (c n)").rearrange("p (k n) -> p k n", k=C)]
        linear_features(m, [(va, d["L1_attn_in_V"], wbuf[0], m.yT, inb[:, 0:NC], ACT.Identity),
                            (key[:, 0], d["L1_attn_in_K0"], wbuf[1], m.yT, inb[:, NC:2 * NC], ACT.Identity),
                            (key[:, 1], d["L1_attn_in_K1"], wbuf[2], m.yT, inb[:, 2 * NC:3 * NC], ACT.Identity)])
        L1_convolution(m, u, va, a11, convw, vecs)
        L1_coefficients(m, va, u, key, kb, a11, a12, W)
        L1_scan(m, va, key, kb, a11, a12)
        L1_readout(m, va, u, key, kb, a11, a12, W, vecs, inb)
        linear_tokens(m, m.x, va, d["L1_attn_out_W"], W, NC, add=m.x)
        add_into(m, m.x, m.x, m.y)


def L1_convolution(m, u, v, tmp, w, vecs):
    NC = 8
    done, step_s = m.sig("convolved"), m.sig("conv_step")
    with m.block() as block:
        @block.vector
        def _(dve):
            step = Chain(dve, step_s)
            for c in range(NC):
                o = tmp[:, c, :].rearrange("p (b s) -> p b s", b=B)
                i = v[:, c, :].rearrange("p (b s) -> p b s", b=B)
                step(dve.tensor_scalar(tmp[:, c, :], v[:, c, :], w[:, c, 3:4], None, ALU.mult))
                for back in range(1, 4):
                    ins = dve.scalar_tensor_tensor(o[:, :, back:], i[:, :, :S - back], w[:, c, 3 - back:4 - back],
                                                   o[:, :, back:], ALU.mult, ALU.add)
                    if back < 3:
                        step(ins)
                ins.then_inc(*done.up())

        @block.scalar
        def _(act):
            for c in range(NC):
                act.wait_ge(*done.at(c + 1))
                act.activation(u[:, c, :], tmp[:, c, :], ACT.Silu, bias=vecs[:, 0, c:c + 1])


def L1_coefficients(m, va, u, key, kb, a11, a12, W):
    d, H, NC = m.d, 32, 8
    NS = 11 * H
    Wv = W[:].rearrange("p c n -> p (c n)")[:, 0:NC * NS].rearrange("p (c n) -> p c n", c=NC)
    brow = a12[0:1, 7, 0:NS]
    flat = a11[:].rearrange("p c n -> p (c n)")
    at = [0]

    def cut(n):
        o = at[0]
        at[0] += T * n
        return flat[:, o:o + T * n].rearrange("p (t n) -> p t n", t=T)

    sm, sp3, e3, n3 = cut(NS), cut(3 * H), cut(3 * H), cut(3 * H)
    om, den, dt, a, w, a2, w2, det, num, t0 = [cut(H) for _ in range(10)]
    quant = a12[:].rearrange("p c n -> p (c n)")[:, 0:T * 8 * H].rearrange("p (t n) -> p t n", t=T)
    load(m, (Wv, d["L1_attn_small_W"]), (brow, d["L1_attn_small_b"].unsqueeze(0)),
         (e3[:, 0, 0:H], d["L1_attn_dt_c"].partition_broadcast(P)), (e3[:, 1, 0:H], d["rope_rate"]))
    product = m.sig("tokens_product")
    step_s, act_s, to_act, to_dve = m.sig("coef_step"), m.sig("coef_act_step"), m.sig("coef_to_act"), m.sig("coef_to_dve")
    with m.block() as block:
        ps = m.ps

        @block.tensor
        def _(pe):
            for t in range(T):
                for k in range(NC):
                    pe.matmul(ps[:, t, 0:NS], u[:, k, t * P:(t + 1) * P], Wv[:, k, :], start=(k == 0), stop=False)
                pe.matmul(ps[:, t, 0:NS], m.ones[0:1, :], brow, start=False, stop=True).then_inc(*product.up())

        @block.scalar
        def _(act):
            step = Chain(act, act_s)
            act.wait_ge(*to_act.at(1))
            step(act.activation(n3, n3, ACT.Exp))
            act.activation(n3, n3, ACT.Ln, bias=1.0).then_inc(*to_dve.up())
            act.wait_ge(*to_act.at(2))
            step(act.activation(num, num, ACT.Ln))
            act.activation(sm[:, :, 4 * H:7 * H], sm[:, :, 4 * H:7 * H], ACT.Sigmoid).then_inc(*to_dve.up())
            act.wait_ge(*to_act.at(3))
            act.activation(num, num, ACT.Exp).then_inc(*to_dve.up())
            act.wait_ge(*to_act.at(4))
            act.activation(num, num, ACT.Sqrt).then_inc(*to_dve.up())

        @block.vector
        def _(dve):
            step = Chain(dve, step_s)
            tt = lambda o, x, y, op: step(dve.tensor_tensor(o, x, y, op))
            ts = lambda o, x, y, z, op, op2=ALU.bypass: step(dve.tensor_scalar(o, x, y, z, op, op2)
                                                            if z is not None else dve.tensor_scalar(o, x, y, None, op))
            for t in range(T):
                dve.wait_ge(*product.at(t + 1))
                ins = dve.tensor_copy(sm[:, t, :], ps[:, t, 0:NS])
                dve.tensor_copy(sp3[:, t, 2 * H:3 * H], e3[:, 0, 0:H])
            step(ins)
            dve.tensor_copy(sp3[:, :, 0:H], sm[:, :, 0:H])
            step(dve.tensor_copy(sp3[:, :, H:2 * H], sm[:, :, 3 * H:4 * H]))
            ts(n3, sp3, -1.0, None, ALU.mult)
            dve.tensor_tensor(n3, sp3, n3, ALU.min).then_inc(*to_act.up())
            tt(om, sm[:, :, H:2 * H], sm[:, :, 2 * H:3 * H], ALU.add)
            tt(om, om, e3[:, 1, 0:H].unsqueeze(1).to_broadcast([P, T, H]), ALU.add)
            ts(sp3, sp3, 0.0, None, ALU.max)
            dve.wait_ge(*to_dve.at(1))
            tt(sp3, sp3, n3, ALU.add)
            alpha, seldt, dtc = sp3[:, :, 0:H], sp3[:, :, H:2 * H], sp3[:, :, 2 * H:3 * H]
            ts(den, om, -1.0, None, ALU.mult)
            tt(den, om, den, ALU.max)
            tt(den, den, alpha, ALU.add)
            ts(den, den, 0.0001, None, ALU.add)
            step(dve.reciprocal(den, den))
            tt(dt, dtc, den, ALU.mult)
            tt(dt, dt, seldt, ALU.add)
            ts(dt, dt, 0.5, None, ALU.mult)
            tt(a, dt, alpha, ALU.mult)
            tt(w, dt, om, ALU.mult)
            tt(w2, w, w, ALU.mult)
            ts(det, a, 1.0, None, ALU.add)
            tt(det, det, det, ALU.mult)
            tt(det, det, w2, ALU.add)
            step(dve.reciprocal(det, det))
            ts(num, a, -1.0, 1.0, ALU.mult, ALU.add)
            tt(num, num, num, ALU.mult)
            tt(num, num, w2, ALU.add)
            tt(num, num, det, ALU.mult)
            dve.tensor_scalar(num, num, 1e-19, None, ALU.max).then_inc(*to_act.up())
            tt(a2, a, a, ALU.mult)
            ts(a2, a2, -1.0, 1.0, ALU.mult, ALU.add)
            tt(a2, a2, w2, ALU.subtract)
            q = lambda i: quant[:, :, i * H:(i + 1) * H]
            tt(q(0), a2, det, ALU.mult)
            tt(t0, w, det, ALU.mult)
            ts(q(1), t0, 2.0, None, ALU.mult)
            dve.wait_ge(*to_dve.at(2))
            dve.tensor_copy(q(2), sm[:, :, 4 * H:5 * H])
            dve.tensor_copy(quant[:, :, 3 * H:5 * H], sm[:, :, 7 * H:9 * H])
            dve.tensor_copy(quant[:, :, 5 * H:7 * H], sm[:, :, 9 * H:11 * H])
            dve.tensor_tensor(num, num, sm[:, :, 5 * H:6 * H], ALU.mult).then_inc(*to_act.up())
            dve.wait_ge(*to_dve.at(3))
            ts(num, num, -1.0, 1.0, ALU.mult, ALU.add)
            dve.tensor_scalar(num, num, 1e-6, None, ALU.max).then_inc(*to_act.up())
            dve.wait_ge(*to_dve.at(4))
            tt(q(7), num, sm[:, :, 6 * H:7 * H], ALU.mult)

    qT = m.yT
    turned, spread = m.sig("quantities_turned"), m.sig("quantities_spread")
    taken_a, taken_v, sel_landed = m.sig("spread_taken_act"), m.sig("spread_taken_dve"), m.sig("selector_landed")
    sel = W[:].rearrange("p c n -> p (c n)")[:, 0:NC * P].rearrange("p (c n) -> p c n", c=NC)
    quantT = W[:].rearrange("p c n -> p (c n)")[:, NC * P:NC * P + 2 * N].rearrange("p (g n) -> p g n", g=2)
    load(m, (sel, d["head_spread"]))
    with m.block() as block:
        @block.tensor
        def _(pe):
            for g in range(2):
                for t in range(T):
                    ins = pe.transpose(ps[:, g, t * P:(t + 1) * P], quant[:, t, g * P:(g + 1) * P], m.ident[:])
                ins.then_inc(*turned.up())

        @block.vector
        def _(dve):
            for g in range(2):
                dve.wait_ge(*turned.at(g + 1))
                dve.tensor_copy(quantT[:, g, :], ps[:, g, :])

    def spread_of(pe, bank, q, c):
        rows = slice(H * (q % 4), H * (q % 4) + H)
        return pe.matmul(ps[:, bank, :], sel[rows, c, :], quantT[rows, q // 4, :], start=True, stop=True)

    m.spread_of = spread_of
    with m.block() as block:
        order = [(c, q) for c in range(NC) for q in (0, 1, 3, 4, 2, 7)]
        on_act = [q in (0, 1) for c, q in order]

        @block.tensor
        def _(pe):
            for i, (c, q) in enumerate(order):
                if i >= 8:
                    n = sum(on_act[:i - 7])
                    pe.wait_ge(*(taken_a.at(n) if on_act[i - 8] else taken_v.at(i - 7 - n)))
                spread_of(pe, i % 8, q, c).then_inc(*spread.up())

        @block.scalar
        def _(act):
            for i, (c, q) in enumerate(order):
                if on_act[i]:
                    act.wait_ge(*spread.at(i + 1))
                    act.activation((a11, a12)[q][:, c, :], ps[:, i % 8, :], ACT.Copy).then_inc(*taken_a.up())

        @block.vector
        def _(dve):
            step = Chain(dve, step_s)
            for i, (c, q) in enumerate(order):
                if on_act[i]:
                    continue
                dve.wait_ge(*spread.at(i + 1))
                if q == 2:
                    dve.wait_ge(*taken_v.at(4 * c + 2))
                    for half in range(2):
                        ins = dve.tensor_tensor(kb[:, half, c, :], ps[:, i % 8, :], key[:, half, c, :], ALU.mult)
                elif q == 7:
                    ins = dve.tensor_tensor(va[:, c, :], ps[:, i % 8, :], u[:, c, :], ALU.mult)
                else:
                    ins = dve.tensor_tensor(key[:, q - 3, c, :], ps[:, i % 8, :], key[:, q - 3, c, :], ALU.mult)
                ins.then_inc(*taken_v.up())


def L1_scan(m, va, key, kb, a11, a12):
    NC = 8
    CB = NC * B
    step_s = m.sig("scan_step")
    over = lambda a: a.rearrange("p c (b s) -> p (c b) s", b=B)
    v, A, A2 = over(va[:]), over(a11[:]), over(a12[:])
    K = key[:].rearrange("p w c (b s) -> p w (c b) s", b=B)
    KB = kb[:].rearrange("p w c (b s) -> p w (c b) s", b=B)
    with m.local(t1=[P, 2, CB], t2=[P, 2, CB], r=[P, 2, CB], e=[P, CB], st=[P, 2, CB]) as (t1, t2, r, e, st), m.block() as block:
        @block.vector
        def _(dve):
            first = Chain(dve, step_s)
            for half in range(2):
                ins = dve.tensor_tensor(st[:, half, :], KB[:, half, :, 0], v[:, :, 0], ALU.mult)
            first(ins)
            step_s.base = step_s.made
            dve.tensor_copy(K[:, :, :, 0], st[:])
            with dve.Fori(1, S) as t:
                Signal.times = S - 1
                step = Chain(dve, step_s, t - 1, 7)
                two = lambda a: a.unsqueeze(1).to_broadcast([P, 2, CB])
                now = bass.ds(t, 1)
                sq = lambda x: x.rearrange("p c o -> p (c o)")
                sq2 = lambda x: x.rearrange("p w c o -> p w (c o)")
                dve.tensor_tensor(t1[:], two(sq(A[:, :, now])), st[:], ALU.mult)
                step(dve.tensor_tensor(t2[:], two(sq(A2[:, :, now])), st[:], ALU.mult))
                dve.tensor_tensor(r[:, 0, :], t1[:, 0, :], t2[:, 1, :], ALU.add)
                step(dve.tensor_tensor(r[:, 1, :], t1[:, 1, :], t2[:, 0, :], ALU.subtract))
                step(dve.tensor_tensor(t1[:], r[:], sq2(K[:, :, :, now]), ALU.mult))
                step(dve.tensor_tensor(e[:], sq(v[:, :, now]), t1[:, 0, :], ALU.subtract))
                step(dve.tensor_tensor(e[:], e[:], t1[:, 1, :], ALU.subtract))
                step(dve.tensor_tensor(t2[:], two(e[:]), sq2(KB[:, :, :, now]), ALU.mult))
                dve.tensor_tensor(sq2(K[:, :, :, now]), r[:], t2[:], ALU.add)
                step(dve.tensor_tensor(st[:], r[:], t2[:], ALU.add))
                step.end()
                Signal.times = 1


def L1_readout(m, y, u, state, kb, a11, a12, W, vecs, inb):
    d, NC, DI = m.d, 8, 1024
    ps = m.ps
    s = m.sig
    QB = [kb[:, 0], kb[:, 1], a12[:]]
    q_landed = [s("q_landed0"), s("q_landed1"), s("q_landed2")]
    q_done, q_taken, step_s = s("q_product"), s("q_taken"), s("readout_step")
    tmp = a11
    with m.block() as block:
        pieces = [(w, half) for w in range(2) for half in range(2)]

        @block.sync
        def _(sp):
            for i, (w, half) in enumerate(pieces):
                if i == 3:
                    sp.wait_ge(*q_done.at(4))
                sp.dma_start(QB[i % 3], d["L1_attn_Q_W"][w, half]).then_inc(*q_landed[i % 3].up(16))

        @block.tensor
        def _(pe):
            for i, (w, half) in enumerate(pieces):
                pe.wait_ge(*q_landed[i % 3].at(16 * (i // 3 + 1)))
                for j in range(4):
                    n = 4 * i + j
                    if n >= 2:
                        pe.wait_ge(*q_taken.at(n - 1))
                    for k in range(NC):
                        pe.matmul(ps[:, n % 2, :], QB[i % 3][:, k, j * P:(j + 1) * P], u[:, k, :],
                                  start=(k == 0), stop=(k == NC - 1))
                    m.spread_of(pe, 2 + n % 2, 5 + w, 4 * half + j).then_inc(*q_done.up())

        @block.vector
        def _(dve):
            step = Chain(dve, step_s)
            for i, (w, half) in enumerate(pieces):
                for j in range(4):
                    n, c = 4 * i + j, 4 * half + j
                    dve.wait_ge(*q_done.at(n + 1))
                    step(dve.tensor_tensor(tmp[:, 0, :], ps[:, n % 2, :], state[:, w, c, :], ALU.mult))
                    dst = y[:, c, :] if w == 0 else tmp[:, 0, :]
                    ins = dve.tensor_tensor(dst, ps[:, 2 + n % 2, :], tmp[:, 0, :], ALU.mult)
                    ins.then_inc(*q_taken.up())
                    dve.wait_ge(*q_taken.at(n + 1))
                    if w == 1:
                        step(dve.tensor_tensor(y[:, c, :], y[:, c, :], tmp[:, 0, :], ALU.add))
    linear_features(m, [(a11, d["L1_attn_in_z"], kb[:, 0].rearrange("p c n -> p (c n)").rearrange("p (k n) -> p k n", k=C),
                         m.yT, inb[:, 3 * NC:4 * NC], ACT.Silu)])
    summed, meaned, squared, ready, rooted = s("group_summed"), s("group_mean"), s("group_squared"), s("group_var_ready"), s("group_rstd")
    CB = NC * B
    wide = lambda a: a.unsqueeze(2).to_broadcast([P, CB, S])
    Y = y[:].rearrange("p c (b s) -> p (c b) s", b=B)
    SQ = a12[:].rearrange("p c (b s) -> p (c b) s", b=B)
    with m.local(mean=[P, P], one=[P, CB], half_=[P, CB]) as (mean, one, half_):
        load(m, (mean[:], d["head_mean"]))
        with m.block() as block:
            @block.tensor
            def _(pe):
                for i in range(2):
                    pe.wait_ge(*summed.at(i + 1))
                    pe.matmul(ps[:, i, 0:CB], mean[:], one[:], start=True, stop=True).then_inc(*meaned.up())

            @block.gpsimd
            def _(pool):
                step = Chain(pool, m.sig("readout_pool_step"))
                step(pool.memset(half_[:], -0.5))
                pool.wait_ge(*ready.at(1))
                pool.tensor_tensor(one[:], one[:], half_[:], ALU.pow).then_inc(*rooted.up())

            @block.scalar
            def _(act):
                act.wait_ge(*squared.at(1))
                act.activation(a12[:], y[:], ACT.Square).then_inc(*squared.up())

            @block.vector
            def _(dve):
                step = Chain(dve, step_s)
                dve.tensor_reduce(one[:], Y, X, ALU.add).then_inc(*summed.up())
                dve.wait_ge(*meaned.at(1))
                dve.tensor_tensor(Y, Y, ps[:, 0, 0:CB].unsqueeze(2).to_broadcast([P, CB, S]), ALU.subtract)\
                   .then_inc(*squared.up())
                dve.wait_ge(*squared.at(2))
                dve.tensor_reduce(one[:], SQ, X, ALU.add).then_inc(*summed.up())
                dve.wait_ge(*meaned.at(2))
                dve.tensor_scalar(one[:], ps[:, 1, 0:CB], 1e-5, None, ALU.add).then_inc(*ready.up())
                dve.wait_ge(*rooted.at(1))
                step(dve.tensor_tensor(Y, Y, wide(one[:]), ALU.mult))
                for c in range(NC):
                    ins = dve.tensor_scalar(y[:, c, :], y[:, c, :], vecs[:, 1, c:c + 1], vecs[:, 2, c:c + 1],
                                            ALU.mult, ALU.add)
                step(ins)
                for c in range(NC):
                    ins = dve.tensor_tensor(y[:, c, :], y[:, c, :], a11[:, c, :], ALU.mult)
                step(ins)
                for c in range(NC):
                    ins = dve.scalar_tensor_tensor(y[:, c, :], u[:, c, :], vecs[:, 3, c:c + 1], y[:, c, :],
                                                   ALU.mult, ALU.add)


STAGES = (L0_xattn, L0_attn, L0_ffn, L1_xattn, L1_attn, L1_ffn,
          L2_xattn, L2_attn, L2_ffn, L3_xattn, L3_attn, L3_ffn)


def perceiver_program(nc, d, out, stages=STAGES):
    with ExitStack() as ctx:
        m = Machine(nc, ctx, d)
        constants(m)
        for stage in stages:
            stage(m)
            m.stage_done()
        stored = m.sig("stored")
        with m.block() as block:
            @block.sync
            def _(sp):
                sp.dma_start(out, m.x[:]).then_inc(*stored.up(16))
                sp.wait_ge(*stored.at(16))


def _lay_out(inputs):
    def rows(w):
        w = np.asarray(w)
        return np.ascontiguousarray(w.reshape(w.shape[0] // P, P, w.shape[1]).transpose(1, 0, 2))

    def cols(v):
        v = np.asarray(v)
        return np.ascontiguousarray(v.reshape(-1, P).T)

    def by_groups_up(w):
        return np.ascontiguousarray(w.reshape(-1, C, P, 4, w.shape[2] // 4).transpose(0, 3, 2, 1, 4))

    def by_groups_down(w):
        return np.ascontiguousarray(w.reshape(w.shape[0], 4, -1, P, D).transpose(0, 1, 3, 2, 4))

    g = {k: np.asarray(v) for k, v in inputs.items()}
    a = {"x": np.ascontiguousarray(g["x"].reshape(T, P, D).transpose(1, 0, 2)),
         "ctx": np.ascontiguousarray(g["ctx_1024"].reshape(B, KC, P, D).transpose(0, 2, 1, 3)),
         "ctxT": np.ascontiguousarray(g["ctx_1024"].transpose(0, 2, 1).reshape(B, C, P, SK).transpose(0, 2, 1, 3)),
         "mask": g["mask_BxSxS2_ff0"]}
    for L in ("L0_xattn", "L3_xattn"):
        t = (lambda w: w.T) if L == "L0_xattn" else (lambda w: w)
        for n in ("Wq", "Wk", "Wv", "Wo"):
            a[f"{L}_{n}"] = rows(t(g[f"{L}_{n}"]))
        a[f"{L}_bq"], a[f"{L}_bk"] = cols(g[f"{L}_bq"]), cols(g[f"{L}_bk"])
        a[f"{L}_bv"], a[f"{L}_bo"] = g[f"{L}_bv"], g[f"{L}_bo"]
    for i, n in enumerate("qkv"):
        a[f"L0_attn_w_{n}"] = rows(g["L0_attn_w_qkv"][i * D:(i + 1) * D].T)
    a["L0_attn_w_proj"] = rows(g["L0_attn_w_proj"].T)
    q, k = np.arange(P)[:, None] % S, np.arange(S)[None, :]
    seen = (k <= q).astype(np.float32)
    a["causal"] = np.stack([seen, (seen - 1) * np.float32(100)], 1)
    for n in (4, 8):
        a[f"before{n}"] = np.tril(np.ones((n, n), np.float32), -1)
    a["L0_ffn_ln_scale"], a["L0_ffn_ln_bias"] = cols(g["L0_ffn_ln_scale"]), cols(g["L0_ffn_ln_bias"])
    a["L0_ffn_gate_w"] = rows(g["L0_ffn_gate_w"].T)
    for n in ("Wg", "Wu", "Wd"):
        a[f"L0_ffn_{n}"] = np.stack([rows(w) for w in g[f"L0_ffn_{n}"]] + [rows(g[f"L0_ffn_s{n}"])])
    for n in ("Wq", "Wk", "Wv", "Wo"):
        a[f"L1_xattn_{n}"] = rows(g[f"L1_xattn_{n}"])
    for n in ("pre_g", "pre_b", "ln_g", "ln_b"):
        a[f"L1_xattn_{n}"] = cols(g[f"L1_xattn_{n}"])
    a["L1_xattn_ln_g_row"], a["L1_xattn_ln_b_row"] = g["L1_xattn_ln_g"], g["L1_xattn_ln_b"]
    a["L1_ffn_gate_W"], a["L1_ffn_gate_b"] = rows(g["L1_ffn_gate_W"]), g["L1_ffn_gate_b"]
    for n in ("W1", "W2"):
        a[f"L1_ffn_{n}"] = np.stack([rows(w) for w in g[f"L1_ffn_{n}"]])
    for n in ("b1", "b2", "g2", "be2"):
        a[f"L1_ffn_{n}"] = g[f"L1_ffn_{n}"]
    for n in ("g1", "be1"):
        a[f"L1_ffn_{n}"] = np.ascontiguousarray(g[f"L1_ffn_{n}"].reshape(4, C, P).transpose(2, 0, 1))
    a["L2_xattn_Wq"], a["L2_xattn_Wk"] = rows(g["L2_xattn_Wq"].T), rows(g["L2_xattn_Wk"])
    a["L2_xattn_Wv"], a["L2_xattn_bv"] = rows(g["L2_xattn_Wv"].T), g["L2_xattn_bv"]
    a["L2_xattn_bq"], a["L2_xattn_bk"] = cols(g["L2_xattn_bq"]), cols(g["L2_xattn_bk"])
    for i in range(2):
        for n in ("ln1_g", "ln1_b", "bq", "bk", "ln2_g", "ln2_b", "b1"):
            a[f"L2_attn_{n}_{i}"] = cols(g[f"L2_attn_{n}"][i])
        for n in ("bv", "bo", "b2"):
            a[f"L2_attn_{n}_{i}"] = np.ascontiguousarray(g[f"L2_attn_{n}"][i])
        for n in ("wq", "wk", "wv", "wo", "w1", "w2"):
            a[f"L2_attn_{n}_{i}"] = rows(g[f"L2_attn_{n}"][i])
    a["L2_attn_lnf_g"], a["L2_attn_lnf_b"] = g["L2_attn_lnf_g"], g["L2_attn_lnf_b"]
    seen = ((q % 3 != 0) | (k <= q)).astype(np.float32)
    a["strided"] = np.stack([seen, (seen - 1) * np.float32(1e30)], 1)
    for n in ("g1", "beta1", "bq", "bk", "g2", "beta2", "b1"):
        a[f"L3_attn_{n}"] = cols(g[f"L3_attn_{n}"])
    for n in ("bv", "bo", "b2"):
        a[f"L3_attn_{n}"] = g[f"L3_attn_{n}"]
    for n in ("Wq", "Wk", "Wv", "Wo", "W1", "W2"):
        a[f"L3_attn_{n}"] = rows(g[f"L3_attn_{n}"])
    hd = 32
    freq = np.float32(1) / np.float32(10000) ** (np.arange(0, hd, 2, dtype=np.float32) / np.float32(hd))
    angle = freq[(np.arange(P) % hd) // 2][:, None] * np.arange(S, dtype=np.float32)[None, :]
    a["rope_trig"] = np.stack([np.cos(angle), np.sin(angle)], 1).astype(np.float32)
    turn_pairs = np.zeros((P, P), np.float32)
    for i in range(0, P, 2):
        turn_pairs[i + 1, i], turn_pairs[i, i + 1] = -1, 1
    a["rope_turn"] = turn_pairs
    NC, H = 8, 32
    w, b = g["L1_attn_in_proj_W"], g["L1_attn_in_proj_b"]
    part = {"z": slice(0, 1024), "K0": slice(1024, 3072, 2), "K1": slice(1025, 3072, 2), "V": slice(3072, 4096)}
    for n, r in part.items():
        a[f"L1_attn_in_{n}"] = rows(w[r].T)
    a["L1_attn_in_proj_b"] = np.concatenate([cols(b[part[n]]) for n in ("V", "K0", "K1", "z")], 1)
    for n in ("conv_b", "gn_w", "gn_b", "D", "rms_w"):
        a[f"L1_attn_{n}"] = cols(g[f"L1_attn_{n}"])
    a["L1_attn_conv_w"] = np.ascontiguousarray(g["L1_attn_conv_w"].reshape(NC, P, 4).transpose(1, 0, 2))
    L = "L1_attn_"
    small = [g[L + "dyn_W"], g[L + "seldt_W"], g[L + "beta_W"], g[L + "rg_W"], g[L + "ug_W"], g[L + "selB_W"][0::2],
             g[L + "selB_W"][1::2], g[L + "selC_W"][0::2], g[L + "selC_W"][1::2]]
    a["L1_attn_small_W"] = rows(np.concatenate(small, 0).T)
    none = np.zeros(H, np.float32)
    a["L1_attn_small_b"] = np.concatenate([g[L + "dyn_b"], none, g[L + "beta_b"], g[L + "rg_b"], g[L + "ug_b"],
                                           none, none, none, none])
    a["L1_attn_dt_c"] = g["L1_attn_dt_c"]
    rate = np.float32(1) / np.float32(10000) ** (np.arange(H, dtype=np.float32) / np.float32(H))
    a["rope_rate"] = (np.arange(P) % S).astype(np.float32)[:, None] * rate[None, :]
    r, c, p = np.arange(P)[:, None, None], np.arange(NC)[None, :, None], np.arange(P)[None, None, :]
    a["head_spread"] = (r % H == 4 * c + p // 32).astype(np.float32)
    a["head_mean"] = (np.arange(P)[:, None] // 32 == np.arange(P)[None, :] // 32).astype(np.float32) / np.float32(32 * S)
    Q = np.stack([g["L1_attn_Q_W"][0::2], g["L1_attn_Q_W"][1::2]])
    a["L1_attn_Q_W"] = np.stack([np.stack([rows(Q[i, h * 512:(h + 1) * 512].T) for h in range(2)]) for i in range(2)])
    a["L1_attn_out_W"] = rows(g["L1_attn_out_W"].T)
    E2, F2 = 8, 2048
    a["L2_ffn_Wg"] = rows(g["L2_ffn_Wg"])
    tok = np.arange(P)
    a["earlier"] = ((tok[:, None] < tok[None, :]) & (tok[:, None] // S == tok[None, :] // S)).astype(np.float32)
    a["place"] = np.arange(S // E2, dtype=np.float32)
    a["L2_ffn_W1"] = by_groups_up(g["L2_ffn_W1"])
    a["L2_ffn_W2"] = by_groups_down(g["L2_ffn_W2"])
    a["L3_ffn_gate_w"], a["L3_ffn_gate_b"] = rows(g["L3_ffn_gate_w"].T), g["L3_ffn_gate_b"]
    w1, w2 = g["L3_ffn_w1"], g["L3_ffn_w2"]
    a["L3_ffn_w1"], a["L3_ffn_w2"] = by_groups_up(w1[:, :D]), by_groups_down(w2[:, :F2])
    a["L3_ffn_b1"] = np.ascontiguousarray(w1[:, D].reshape(-1, F2 // P, P).transpose(2, 0, 1))
    a["L3_ffn_b2"] = np.ascontiguousarray(w2[:, F2].reshape(-1, C, P).transpose(2, 0, 1))
    return a


def kernel(**inputs):
    import concourse.bacc as bacc
    from concourse.bass_utils import run_bass_kernel_spmd

    nc = bacc.Bacc("TRN2", target_bir_lowering=False, num_devices=1)
    arrays = {f"in_{k}": v for k, v in _lay_out(inputs).items()}
    d = {k[3:]: nc.dram_tensor(k, v.shape, mybir.dt.from_np(v.dtype), kind="ExternalInput").ap()
         for k, v in arrays.items()}
    out = nc.dram_tensor("out", (B, S, D), F32, kind="ExternalOutput").ap()
    perceiver_program(nc, d, out.rearrange("(t two) s d -> (two s) t d", two=2))
    r = run_bass_kernel_spmd(nc, [arrays], core_ids=[0])
    return r.results[0]["out"]
```

```python
from contextlib import ExitStack, contextmanager

import numpy as np

import concourse.bass as bass
from concourse import mybir

F32 = mybir.dt.float32
ACT = mybir.ActivationFunctionType
ALU = mybir.AluOpType
X = mybir.AxisListType.X

P = 128
B, S, D = 8, 64, 512
N = B * S
T = N // P
C = D // P
SK = 512
KC = SK // P


class Signal:

    times = 1

    def __init__(self, sem):
        self.sem, self.made, self.base = sem, 0, 0

    def up(self, n=1):
        self.made += n * Signal.times
        return self.sem, n

    def at(self, n):
        return self.sem, self.base + n


@contextmanager
def repeat(eng, n):
    with eng.Fori(0, n) as i:
        Signal.times = n
        yield i
        Signal.times = 1


class Chain:

    def __init__(self, eng, steps, i=0, per=0):
        self.eng, self.steps, self.i, self.per = eng, steps, i, per
        self.start = steps.made
        self.n = 0

    def __call__(self, ins):
        ins.then_inc(*self.steps.up())
        self.n += 1
        self.eng.wait_ge(self.steps.sem, self.start + self.n + (self.i * self.per if self.per else 0))

    def end(self):
        assert not self.per or self.n == self.per, (self.n, self.per)


class Machine:

    def __init__(self, nc, ctx, d):
        self.nc, self.ctx, self.d = nc, ctx, d
        self.marks, self.idle = {}, []
        self.count = 0
        self.x = self.sb("x_tokens", [P, T, D])
        self.y = self.sb("normed_tokens", [P, T, D])
        self.yT = self.sb("normed_features", [P, C, N])
        self.ident = self.sb("identity", [P, P])
        self.ones = self.sb("ones_row", [1, P])
        self.minus_half = self.sb("minus_half", [P, T])
        self.stats = self.sb("stats", [P, T, 6])
        self.mv = self.sb("mean_var", [P, T, 2])
        self.den = self.sb("var_eps", [P, T])
        self.rstd = self.sb("rstd", [P, T])
        self.cols = self.sb("columns", [P, 64])
        self.ps = ctx.enter_context(nc.psum_tensor("banks", [P, 8, 512], F32))

    def sb(self, name, shape):
        return self.ctx.enter_context(self.nc.sbuf_tensor(name, shape, F32))

    @contextmanager
    def local(self, **shapes):
        with ExitStack() as s:
            self.count += 1
            yield [s.enter_context(self.nc.sbuf_tensor(f"{n}_{self.count}", sh, F32)) for n, sh in shapes.items()]

    def sig(self, name):
        if name not in self.marks:
            s = self.idle.pop() if self.idle else Signal(self.ctx.enter_context(self.nc.semaphore(name)))
            s.base = s.made
            self.marks[name] = s
        return self.marks[name]

    def stage_done(self):
        self.idle += self.marks.values()
        self.marks = {}

    @contextmanager
    def block(self, *credits):
        for s in self.marks.values():
            s.base = s.made
        if credits:
            with self.nc.Block() as b:
                @b.gpsimd
                def _(pool):
                    for signal, n in credits:
                        pool.sem_inc(*signal.up(n))
        with self.nc.Block() as b:
            yield b


def constants(m):
    made, x_landed = m.sig("constants_made"), m.sig("x_landed")
    with m.block() as block:
        @block.gpsimd
        def _(pool):
            step = Chain(pool, made)
            step(pool.memset(m.ident[:], 0.0))
            step(pool.affine_select(out=m.ident[:], in_=m.ident[:], compare_op=ALU.not_equal, fill=1.0,
                                    base=0, pattern=[[-1, P]], channel_multiplier=1))
            step(pool.memset(m.ones[:], 1.0))
            step(pool.memset(m.minus_half[:], -0.5))

        @block.sync
        def _(sp):
            sp.dma_start(m.x[:], m.d["x"]).then_inc(*x_landed.up(16))
            sp.wait_ge(*x_landed.at(16))


def normalise(m, dst, src, eps, rms=False):
    summed, ready, rooted = m.sig("moments_step"), m.sig("variance_ready"), m.sig("rstd_ready")
    with m.block() as block:
        @block.vector
        def _(dve):
            step = Chain(dve, summed)
            for t in range(T):
                ins = dve.bn_stats(m.stats[:, t, :], src[:, t, :])
            step(ins)
            for t in range(T):
                ins = dve.bn_aggr(m.mv[:, t, :], m.stats[:, t, :])
            step(ins)
            if rms:
                step(dve.tensor_tensor(m.den[:], m.mv[:, :, 0], m.mv[:, :, 0], ALU.mult))
                step(dve.tensor_tensor(m.den[:], m.den[:], m.mv[:, :, 1], ALU.add))
                dve.tensor_scalar(m.den[:], m.den[:], eps, None, ALU.add).then_inc(*ready.up())
            else:
                dve.tensor_scalar(m.den[:], m.mv[:, :, 1], eps, None, ALU.add).then_inc(*ready.up())
            dve.wait_ge(*rooted.at(1))
            for t in range(T):
                if rms:
                    ins = dve.tensor_scalar(dst[:, t, :], src[:, t, :], m.rstd[:, t:t + 1], None, ALU.mult)
                else:
                    ins = dve.tensor_scalar(dst[:, t, :], src[:, t, :], m.mv[:, t, 0:1], m.rstd[:, t:t + 1],
                                            ALU.subtract, ALU.mult)

        @block.gpsimd
        def _(pool):
            pool.wait_ge(*ready.at(1))
            pool.tensor_tensor(m.rstd[:], m.den[:], m.minus_half[:], ALU.pow).then_inc(*rooted.up())


def load(m, *pairs):
    landed = m.sig("load_landed")
    with m.block() as block:
        @block.sync
        def _(sp):
            for dst, src in pairs:
                sp.dma_start(dst, src).then_inc(*landed.up(16))
            sp.wait_ge(*landed.at(16 * len(pairs)))


def turn(m, dstT, src, chunks=C, scale=None, bias=None, relu=False):
    turned = m.sig("turned")
    with m.block() as block:
        @block.tensor
        def _(pe):
            for c in range(chunks):
                for t in range(T):
                    ins = pe.transpose(m.ps[:, c, t * P:(t + 1) * P], src[:, t, c * P:(c + 1) * P], m.ident[:])
                ins.then_inc(*turned.up())

        @block.scalar
        def _(act):
            for c in range(0, chunks, 1 if relu else 2):
                act.wait_ge(*turned.at(c + 1))
                act.activation(dstT[:, c, :], m.ps[:, c, :], ACT.Relu if relu else ACT.Identity,
                               bias=0.0 if bias is None else bias[:, c:c + 1],
                               scale=1.0 if scale is None else scale[:, c:c + 1])

        if not relu:
            @block.vector
            def _(dve):
                for c in range(1, chunks, 2):
                    dve.wait_ge(*turned.at(c + 1))
                    if scale is None:
                        dve.tensor_copy(dstT[:, c, :], m.ps[:, c, :])
                    elif bias is None:
                        dve.tensor_scalar(dstT[:, c, :], m.ps[:, c, :], scale[:, c:c + 1], None, ALU.mult)
                    else:
                        dve.tensor_scalar(dstT[:, c, :], m.ps[:, c, :], scale[:, c:c + 1], bias[:, c:c + 1],
                                          ALU.mult, ALU.add)


def linear_features(m, outs, kchunks=C):
    landed = [m.sig(f"weights_landed_{i}") for i in range(len(outs))]
    product, taken_a, taken_v = m.sig("features_product"), m.sig("features_taken_act"), m.sig("features_taken_dve")
    work = [(o, mm) for o in range(len(outs)) for mm in range(outs[o][2].shape[2] // P)]
    on_act = [outs[o][5] != ACT.Identity or n % 2 == 0 for n, (o, mm) in enumerate(work)]
    with m.block() as block:
        @block.sync
        def _(sp):
            for o, (_, w, buf, *_r) in enumerate(outs):
                sp.dma_start(buf[:], w).then_inc(*landed[o].up(16))

        @block.tensor
        def _(pe):
            for n, (o, mm) in enumerate(work):
                _, _, buf, srcT, _, _ = outs[o]
                if mm == 0:
                    pe.wait_ge(*landed[o].at(16))
                if n >= 4:
                    a = sum(on_act[:n - 3])
                    s = taken_a if on_act[n - 4] else taken_v
                    pe.wait_ge(*s.at(a if on_act[n - 4] else n - 3 - a))
                for k in range(kchunks):
                    ins = pe.matmul(m.ps[:, n % 4, :], buf[:, k, mm * P:(mm + 1) * P], srcT[:, k, :],
                                    start=(k == 0), stop=(k == kchunks - 1))
                ins.then_inc(*product.up())

        def take(eng, mine, signal):
            for n, (o, mm) in enumerate(work):
                if on_act[n] != mine:
                    continue
                dstT, _, _, _, bias, f = outs[o]
                eng.wait_ge(*product.at(n + 1))
                if mine:
                    eng.activation(dstT[:, mm, :], m.ps[:, n % 4, :], f,
                                   bias=0.0 if bias is None else bias[:, mm:mm + 1]).then_inc(*signal.up())
                elif bias is None:
                    eng.tensor_copy(dstT[:, mm, :], m.ps[:, n % 4, :]).then_inc(*signal.up())
                else:
                    eng.tensor_scalar(dstT[:, mm, :], m.ps[:, n % 4, :], bias[:, mm:mm + 1], None,
                                      ALU.add).then_inc(*signal.up())

        @block.scalar
        def _(act):
            take(act, True, taken_a)

        @block.vector
        def _(dve):
            take(dve, False, taken_v)


def linear_tokens(m, dst, srcT, w, buf, kchunks, brow=None, add=None):
    landed, product = m.sig("weights_landed_0"), m.sig("tokens_product")
    with m.block() as block:
        @block.sync
        def _(sp):
            sp.dma_start(buf[:], w).then_inc(*landed.up(16))

        @block.tensor
        def _(pe):
            pe.wait_ge(*landed.at(16))
            for t in range(T):
                for k in range(kchunks):
                    ins = pe.matmul(m.ps[:, t, :], srcT[:, k, t * P:(t + 1) * P], buf[:, k, :],
                                    start=(k == 0), stop=(k == kchunks - 1 and brow is None))
                if brow is not None:
                    ins = pe.matmul(m.ps[:, t, :], m.ones[0:1, :], brow, start=False, stop=True)
                ins.then_inc(*product.up())

        @block.vector
        def _(dve):
            for t in range(T):
                dve.wait_ge(*product.at(t + 1))
                if add is None:
                    dve.tensor_copy(dst[:, t, :], m.ps[:, t, :])
                else:
                    dve.tensor_tensor(dst[:, t, :], m.ps[:, t, :], add[:, t, :], ALU.add)


def add_into(m, dst, a, b):
    with m.block() as block:
        @block.vector
        def _(dve):
            for t in range(T):
                dve.tensor_tensor(dst[:, t, :], a[:, t, :], b[:, t, :], ALU.add)




def cross_attention(m, oT, qT, hd, scale, wk, wv, kbias=None, vbias=None, mask=None, clip=None, knorm=None):
    J = D // hd // 2
    JC = J // C
    G = P // hd
    R = 4
    UN = C + KC
    U = UN // J
    s = m.sig
    w_landed, ctx_landed, tok_landed = s("xw_landed"), [s("ctx_landed0"), s("ctx_landed1")], s("ctxtok_landed")
    mask_landed = [s("mask_landed0"), s("mask_landed1")]
    projected, k_taken, v_taken, q_spread = s("kv_projected"), s("k_taken"), s("v_taken"), s("q_spread")
    scored, max_ready, exp_done, inverted, scaled = s("scored"), s("max_ready"), s("probs_exp"), s("sum_inverted"), s("probs_scaled")
    turned, turned_taken, attended, o_taken = s("probs_turned"), s("probs_turned_taken"), s("attended"), s("attended_taken")
    vstep, k_turned, kn_ready, kn_taken = s("xattn_step"), s("ctx_turned"), s("ctx_normed"), s("ctx_turned_taken")
    var_ready, rooted, zeroed = s("ctx_var"), s("ctx_rstd"), s("q_zeroed")
    pre = mask is not None or clip is not None
    few = 1 if not (mask is not None or knorm) else C
    with m.local(wkb=[P, C, D], wvb=[P, C, D], ctxT=[P, 2, C, SK], kT=[P, 2, C, SK], v=[P, 2, KC, D], q2=[P, 2, J, P],
                 pr=[P, R, SK], prT=[P, 2, KC, P], sc=[P, 2, SK], col=[P, 2, J, 4],
                 extra=[P, few, SK], extraT=[P, C if knorm else 1, SK]) as \
            (wkb, wvb, ctxT, kT, v, q2, pr, prT, sc, col, extra, extraT), \
            m.block((o_taken, 1), (turned_taken, 2)) as block:
        ps = m.ps

        def run(eng, body, per=0):
            with repeat(eng, B // 2 - 1) as i:
                step = Chain(eng, vstep, i, per) if per else None
                body(2 * i, 0, False, step)
                body(2 * i + 1, 1, False, step)
                if per:
                    step.end()
            step = Chain(eng, vstep) if per else None
            body(B - 2, 0, True, step)
            body(B - 1, 1, True, step)

        @block.sync
        def _(sp):
            sp.dma_start(ctxT[:, 0], m.d["ctxT"][0]).then_inc(*ctx_landed[0].up(16))
            if knorm:
                sp.dma_start(extra[:], m.d["ctx"][0]).then_inc(*tok_landed.up(16))
            sp.dma_start(wkb[:], wk).then_inc(*w_landed.up(16))
            sp.dma_start(wvb[:], wv).then_inc(*w_landed.up(16))
            sp.dma_start(ctxT[:, 1], m.d["ctxT"][1]).then_inc(*ctx_landed[1].up(16))
            if knorm:
                sp.wait_ge(*k_turned.at(C))
                sp.dma_start(extra[:], m.d["ctx"][1]).then_inc(*tok_landed.up(16))

            def load_mask(b, par):
                for half in range(2):
                    sp.dma_start(extra[64 * half:64 * half + 64, par, :], mask[b]).then_inc(*mask_landed[par].up(16))

            if mask is not None:
                load_mask(0, 0)

            def body(b, par, last, _):
                if mask is not None and not (last and par == 1):
                    sp.wait_ge(*max_ready.at(J * b + 1))
                    load_mask(b + 1, 1 - par)
                if not last:
                    sp.wait_ge(*projected.at(UN * b + UN))
                    sp.dma_start(ctxT[:, par], m.d["ctxT"][b + 2]).then_inc(*ctx_landed[par].up(16))
                    if knorm:
                        sp.wait_ge(*k_turned.at(C * b + 2 * C))
                        sp.dma_start(extra[:], m.d["ctx"][b + 2]).then_inc(*tok_landed.up(16))

            run(sp, body)

        @block.gpsimd
        def _(pool):
            pool.memset(q2[:], 0.0).then_inc(*zeroed.up())
            if knorm:
                with repeat(pool, B) as b:
                    pool.wait_ge(*var_ready.at(b + 1))
                    pool.tensor_tensor(m.rstd[:], m.den[:], m.minus_half[:], ALU.pow).then_inc(*rooted.up())

        @block.tensor
        def _(pe):
            def unit(b, par, u, first=False):
                if u == 0:
                    pe.wait_ge(*(ctx_landed[par].at(8 * b + 16 - 8 * par)))
                    if knorm:
                        pe.wait_ge(*kn_taken.at(C * b + C))
                if u < 2:
                    if not first:
                        pe.wait_ge(*v_taken.at(KC * b + u - 1))
                elif u < C + 2:
                    pe.wait_ge(*k_taken.at(C * b + u - 1))
                else:
                    pe.wait_ge(*v_taken.at(KC * b + u - C - 1))
                for k in range(C):
                    if u < C:
                        ins = pe.matmul(ps[:, u % 2, :], wkb[:, k, u * P:(u + 1) * P],
                                        (extraT if knorm else ctxT[:, par])[:, k, :], start=(k == 0), stop=(k == C - 1))
                    else:
                        r = u - C
                        ins = pe.matmul(ps[:, u % 2, :], ctxT[:, par, k, r * P:(r + 1) * P], wvb[:, k, :],
                                        start=(k == 0), stop=(k == C - 1))
                ins.then_inc(*projected.up())

            def turn_context(b, c, first=False):
                if c == 0:
                    pe.wait_ge(*kn_ready.at(b + 1))
                if not (first and c == 0):
                    pe.wait_ge(*kn_taken.at(C * b + c))
                for k in range(KC):
                    ins = pe.transpose(ps[:, 7, k * P:(k + 1) * P], extra[:, k, c * P:(c + 1) * P], m.ident[:])
                ins.then_inc(*k_turned.up())

            def scores(b, par, j, first=False):
                if j == 0:
                    pe.wait_ge(*q_spread.at(b + 1))
                    pe.wait_ge(*k_taken.at(C * b + C))
                if not first:
                    pe.wait_ge(*exp_done.at(J * b + j - 1))
                pe.matmul(ps[:, 2 + j % 2, :], q2[:, par, j, :], kT[:, par, j // JC, :],
                          start=True, stop=True).then_inc(*scored.up())

            if knorm:
                for c in range(C):
                    turn_context(0, c, True)
            pe.wait_ge(*w_landed.at(32))
            for u in range(UN):
                unit(0, 0, u, True)
                if u == C + 1:
                    scores(0, 0, 0, True)
                    scores(0, 0, 1, True)
            if knorm:
                for c in range(C):
                    turn_context(1, c)

            def body(b, par, last, _):
                end = last and par == 1
                for j in range(J):
                    n = J * b + j
                    pe.wait_ge(*scaled.at(n + 1))
                    pe.wait_ge(*turned_taken.at(n + 1))
                    for k in range(KC):
                        ins = pe.transpose(ps[:, 4 + j % 2, k * P:(k + 1) * P], pr[:, j % R, k * P:(k + 1) * P],
                                           m.ident[:])
                    ins.then_inc(*turned.up())
                    if j + 2 < J:
                        scores(b, par, j + 2)
                    elif not end:
                        scores(b + 1, 1 - par, j + 2 - J)
                    if not end:
                        for u in range(U * j, U * j + U):
                            unit(b + 1, 1 - par, u)
                            if knorm and not last and u >= C:
                                turn_context(b + 2, u - C)
                    pe.wait_ge(*turned_taken.at(2 + n + 1))
                    if j == 0:
                        pe.wait_ge(*v_taken.at(KC * b + KC))
                        pe.wait_ge(*o_taken.at(b + 1))
                    c, half, w = j // JC, j % JC, P // JC
                    for k in range(KC):
                        ins = pe.matmul(ps[w * half:w * half + w, 6, c * P:(c + 1) * P],
                                        v[:, par, k, c * P + w * half:c * P + w * half + w], prT[:, j % 2, k, :],
                                        start=(k == 0), stop=(k == KC - 1))
                    ins.then_inc(*attended.up())

            run(pe, body)

        @block.scalar
        def _(act):
            def spread(b, par, first=False):
                if not first:
                    act.wait_ge(*scored.at(J * b - J + 1))
                for h in range(G):
                    rows = slice(hd * h, hd * h + hd)
                    dst = q2[rows, par, :, :].rearrange("p (c j) n -> p c j n", c=C)[:, :, h // 2 if hd == 32 else 0,
                                                                                     (h % 2) * 64:(h % 2) * 64 + 64]
                    src = qT[rows, :, :].rearrange("p c (b n) -> p b c n", b=B)[:, b, :, :]
                    ins = act.activation(dst, src, ACT.Copy)
                ins.then_inc(*q_spread.up())

            def take_k(b, par, u):
                act.wait_ge(*projected.at(UN * b + u + 1))
                act.activation(kT[:, par, u, :], ps[:, u % 2, :], ACT.Identity,
                               bias=0.0 if kbias is None else kbias[:, u:u + 1]).then_inc(*k_taken.up())

            def take_context(b, c, first=False):
                act.wait_ge(*k_turned.at(C * b + c + 1))
                if c == 0 and not first:
                    act.wait_ge(*projected.at(UN * b - UN + C))
                act.activation(extraT[:, c, :], ps[:, 7, :], ACT.Identity, bias=knorm[1][:, c:c + 1],
                               scale=knorm[0][:, c:c + 1]).then_inc(*kn_taken.up())

            def power(b, par, j):
                act.wait_ge(*max_ready.at(J * b + j + 1))
                src = sc[:, j % 2, :] if pre else ps[:, 2 + j % 2, :]
                act.activation(pr[:, j % R, :], src, ACT.Exp, bias=col[:, par, j, 1:2],
                               scale=1.0 if mask is not None else scale,
                               accum_out=col[:, par, j, 2:3]).then_inc(*exp_done.up())

            def divide(b, par, j):
                act.wait_ge(*inverted.at(J * b + j + 1))
                act.activation(pr[:, j % R, :], pr[:, j % R, :], ACT.Copy, scale=col[:, par, j, 3:4])\
                   .then_inc(*scaled.up())

            act.wait_ge(*zeroed.at(1))
            spread(0, 0, True)
            if knorm:
                for c in range(C):
                    take_context(0, c, True)
            for u in range(C):
                take_k(0, 0, u)
            for j in range(2):
                power(0, 0, j)
                divide(0, 0, j)
            if knorm:
                for c in range(C):
                    take_context(1, c)

            def body(b, par, last, _):
                end = last and par == 1
                for j in range(J):
                    if j == 0 and not end:
                        spread(b + 1, 1 - par)
                    if j + 2 < J:
                        power(b, par, j + 2)
                    elif not end:
                        power(b + 1, 1 - par, j + 2 - J)
                    if not end:
                        for u in range(U * j, U * j + U):
                            if u < C:
                                take_k(b + 1, 1 - par, u)
                            elif knorm and not last:
                                take_context(b + 2, u - C)
                    if j + 2 < J:
                        divide(b, par, j + 2)
                    elif not end:
                        divide(b + 1, 1 - par, j + 2 - J)

            run(act, body)

        @block.vector
        def _(dve):
            def norm_context(b, step):
                dve.wait_ge(*tok_landed.at(16 * b + 16))
                for k in range(KC):
                    ins = dve.bn_stats(m.stats[:, k, :], extra[:, k, :])
                step(ins)
                dve.memset(m.den[:], 0.0)
                for k in range(KC):
                    ins = dve.bn_aggr(m.mv[:, k, :], m.stats[:, k, :])
                step(ins)
                dve.tensor_scalar(m.den[:], m.mv[:, :, 1], 1e-5, None, ALU.add).then_inc(*var_ready.up())
                dve.wait_ge(*rooted.at(b + 1))
                for k in range(KC):
                    ins = dve.tensor_scalar(extra[:, k, :], extra[:, k, :], m.mv[:, k, 0:1], m.rstd[:, k:k + 1],
                                            ALU.subtract, ALU.mult)
                ins.then_inc(*kn_ready.up())

            def row_max(b, par, j, step, first=False):
                dve.wait_ge(*scored.at(J * b + j + 1))
                src = ps[:, 2 + j % 2, :]
                if pre and not first:
                    dve.wait_ge(*exp_done.at(J * b + j - 1))
                if mask is not None:
                    dve.wait_ge(*mask_landed[par].at(16 * b + 32 - 16 * par))
                    step(dve.scalar_tensor_tensor(sc[:, j % 2, :], src, scale, extra[:, par, :], ALU.mult, ALU.add))
                if clip is not None:
                    step(dve.tensor_scalar(sc[:, j % 2, :], src, -clip, clip, ALU.max, ALU.min))
                if pre:
                    src = sc[:, j % 2, :]
                step(dve.tensor_reduce(col[:, par, j, 0:1], src, X, ALU.max, negate=True))
                dve.tensor_scalar(col[:, par, j, 1:2], col[:, par, j, 0:1], 1.0 if mask is not None else scale, None,
                                  ALU.mult).then_inc(*max_ready.up())

            def invert(b, par, j):
                dve.wait_ge(*exp_done.at(J * b + j + 1))
                dve.reciprocal(col[:, par, j, 3:4], col[:, par, j, 2:3]).then_inc(*inverted.up())

            def take_v(b, par, r):
                dve.wait_ge(*projected.at(UN * b + C + r + 1))
                if vbias is None:
                    dve.tensor_copy(v[:, par, r, :], ps[:, r % 2, :]).then_inc(*v_taken.up())
                else:
                    dve.tensor_tensor(v[:, par, r, :], ps[:, r % 2, :], vbias, ALU.add).then_inc(*v_taken.up())

            step = Chain(dve, vstep)
            if knorm:
                norm_context(0, step)
            take_v(0, 0, 0)
            take_v(0, 0, 1)
            for j in range(2):
                row_max(0, 0, j, step, True)
                invert(0, 0, j)
            take_v(0, 0, 2)
            take_v(0, 0, 3)
            if knorm:
                norm_context(1, step)

            def body(b, par, last, step):
                end = last and par == 1
                for j in range(J):
                    dve.wait_ge(*turned.at(J * b + j + 1))
                    dve.tensor_copy(prT[:, j % 2, :, :], ps[:, 4 + j % 2, :].rearrange("p (k n) -> p k n", k=KC))\
                       .then_inc(*turned_taken.up())
                    if j + 2 < J:
                        row_max(b, par, j + 2, step)
                    elif not end:
                        row_max(b + 1, 1 - par, j + 2 - J, step)
                    if j == 0 and knorm and not last:
                        norm_context(b + 2, step)
                    if not end:
                        for u in range(U * j, U * j + U):
                            if u >= C:
                                take_v(b + 1, 1 - par, u - C)
                    if j + 2 < J:
                        invert(b, par, j + 2)
                    elif not end:
                        invert(b + 1, 1 - par, j + 2 - J)
                dve.wait_ge(*attended.at(J * b + J))
                for h in range(G):
                    rows = slice(hd * h, hd * h + hd)
                    src = ps[rows, 6, :].rearrange("p (c n) -> p c n", c=C)[:, :, (h % 2) * 64:(h % 2) * 64 + 64]
                    dst = oT[rows, :, :].rearrange("p c (b n) -> p b c n", b=B)[:, b, :, :]
                    ins = dve.tensor_copy(dst, src)
                ins.then_inc(*o_taken.up())

            run(dve, body, 2 * ((2 if pre else 1) * J + (2 if knorm else 0)))


def self_attention(m, oT, qT, kT, v, scale, clip=None, allowed=None, masked=None, custom=False):
    H, hd, R = 16, 32, 4
    s = m.sig
    scored, scores_taken, step_s = s("self_scored"), s("self_scores_taken"), s("self_step")
    centred, powered, probs_ready, zeroed = s("self_centred"), s("self_exp"), s("self_probs_ready"), s("self_zeroed")
    turned, turned_taken = s("self_turned"), s("self_turned_taken")
    attended, o_taken = s("self_attended"), s("self_attended_taken")
    with m.local(sc=[P, 2, H, S], bd=[P, 2, H, P], prT=[P, H, P], col=[P, 2, 3, H]) as (sc, bd, prT, col), \
            m.block() as block:
        ps = m.ps

        @block.gpsimd
        def _(pool):
            pool.memset(bd[:], 0.0).then_inc(*zeroed.up())

        @block.tensor
        def _(pe):
            def scores(t):
                if t >= 1:
                    pe.wait_ge(*scores_taken.at(2 * t))
                for h in range(H):
                    rows = slice(hd * (h % R), hd * (h % R) + hd)
                    ins = pe.matmul(ps[:, h % R, (h // R) * P:(h // R) * P + P],
                                    qT[rows, h // R, t * P:(t + 1) * P], kT[rows, h // R, t * P:(t + 1) * P],
                                    start=True, stop=True)
                ins.then_inc(*scored.up())

            scores(0)
            for t in range(T):
                if t + 1 < T:
                    scores(t + 1)
                pe.wait_ge(*probs_ready.at(2 * t + 2))
                for g in range(R):
                    n = R * t + g
                    if n >= 2:
                        pe.wait_ge(*turned_taken.at(n - 1))
                    for k in range(R):
                        ins = pe.transpose(ps[:, 4 + g % 2, k * P:(k + 1) * P], bd[:, t % 2, R * g + k, :], m.ident[:])
                    ins.then_inc(*turned.up())
                pe.wait_ge(*turned_taken.at(R * t + R))
                if t >= 1:
                    pe.wait_ge(*o_taken.at(t))
                for n in range(H):
                    r, c = n // R, n % R
                    h = R * c + r
                    ins = pe.matmul(ps[hd * r:hd * r + hd, 6, c * P:(c + 1) * P], v[:, t, hd * h:hd * h + hd],
                                    prT[:, n, :], start=True, stop=True)
                ins.then_inc(*attended.up())

        @block.scalar
        def _(act):
            for t in range(T):
                act.wait_ge(*scored.at(t + 1))
                if t >= 2:
                    act.wait_ge(*probs_ready.at(2 * t - 2))
                for half in range(2):
                    rows = slice(64 * half, 64 * half + 64)
                    src = ps[rows, 0:R, :].rearrange("p r (c n) -> p r c n", c=R)[:, :, :, 64 * half:64 * half + 64]
                    act.activation(sc[rows, t % 2, :, :].rearrange("p (r c) n -> p r c n", r=R), src, ACT.Copy,
                                   scale=scale).then_inc(*scores_taken.up())
                act.wait_ge(*centred.at(t + 1))
                act.activation(sc[:, t % 2, :, :], sc[:, t % 2, :, :], ACT.Exp).then_inc(*powered.up())

        @block.vector
        def _(dve):
            step = Chain(dve, step_s)

            def wide(a):
                return a.unsqueeze(2).to_broadcast([P, H, S])

            def rows_of(a):
                return a.unsqueeze(1).to_broadcast([P, H, S])

            def centre(t):
                w = sc[:, t % 2, :, :]
                dve.wait_ge(*scores_taken.at(2 * t + 2))
                if clip is not None:
                    step(dve.tensor_scalar(w, w, -clip, clip, ALU.max, ALU.min))
                if allowed is not None:
                    step(dve.tensor_tensor(w, w, rows_of(allowed), ALU.mult))
                    step(dve.tensor_tensor(w, w, rows_of(masked), ALU.add))
                step(dve.tensor_reduce(col[:, t % 2, 0, :], w, X, ALU.max))
                dve.tensor_tensor(w, w, wide(col[:, t % 2, 0, :]), ALU.subtract).then_inc(*centred.up())

            def finish(t):
                w = sc[:, t % 2, :, :]
                dve.wait_ge(*powered.at(t + 1))
                step(dve.tensor_reduce(col[:, t % 2, 1, :], w, X, ALU.add))
                if custom:
                    step(dve.tensor_scalar(col[:, t % 2, 1, :], col[:, t % 2, 1, :], 1e-6, None, ALU.add))
                step(dve.reciprocal(col[:, t % 2, 2, :], col[:, t % 2, 1, :]))
                if custom:
                    step(dve.tensor_tensor(w, w, wide(col[:, t % 2, 2, :]), ALU.mult))
                    step(dve.tensor_scalar(w, w, 1e-8, None, ALU.add))
                    step(dve.tensor_reduce(col[:, t % 2, 1, :], w, X, ALU.add))
                    step(dve.reciprocal(col[:, t % 2, 2, :], col[:, t % 2, 1, :]))
                if t >= 2:
                    dve.wait_ge(*turned.at(R * t - R))
                if t == 0:
                    dve.wait_ge(*zeroed.at(1))
                for half in range(2):
                    rows = slice(64 * half, 64 * half + 64)
                    dve.tensor_tensor(bd[rows, t % 2, :, 64 * half:64 * half + 64], sc[rows, t % 2, :, :],
                                      col[rows, t % 2, 2, :].unsqueeze(2).to_broadcast([64, H, S]), ALU.mult)\
                       .then_inc(*probs_ready.up())

            def take(t):
                for g in range(R):
                    dve.wait_ge(*turned.at(R * t + g + 1))
                    if g == 0 and t >= 1:
                        dve.wait_ge(*attended.at(t))
                    dve.tensor_copy(prT[:, R * g:R * g + R, :].rearrange("p g n -> p (g n)"), ps[:, 4 + g % 2, :])\
                       .then_inc(*turned_taken.up())
                dve.wait_ge(*attended.at(t + 1))
                dve.tensor_copy(oT[:, :, t * P:(t + 1) * P],
                                ps[:, 6, :].rearrange("p (c n) -> p c n", c=C)).then_inc(*o_taken.up())

            centre(0)
            for t in range(T):
                finish(t)
                if t + 1 < T:
                    centre(t + 1)
                take(t)


def columns(m, dst, name):
    return dst, m.d[name]


def L0_xattn(m):
    d = m.d
    normalise(m, m.y, m.x, 1e-5)
    turn(m, m.yT, m.y)
    with m.local(qT=[P, C, N], oT=[P, C, N], w=[P, C, D], bv=[P, D], bo=[1, D], b=[P, 2, C]) as (qT, oT, w, bv, bo, b):
        load(m, (b[:, 0, :], d["L0_xattn_bq"]), (b[:, 1, :], d["L0_xattn_bk"]),
             (bv[:], d["L0_xattn_bv"].partition_broadcast(P)), (bo[:], d["L0_xattn_bo"].unsqueeze(0)))
        linear_features(m, [(qT, d["L0_xattn_Wq"], w, m.yT, b[:, 0, :], ACT.Identity)])
        cross_attention(m, oT, qT, 32, 32 ** -0.5, d["L0_xattn_Wk"], d["L0_xattn_Wv"], b[:, 1, :], bv[:],
                        mask=d["mask"])
        linear_tokens(m, m.x, oT, d["L0_xattn_Wo"], w, C, bo[0:1, :], m.x)


def L0_attn(m):
    d = m.d
    normalise(m, m.y, m.x, 1e-5)
    turn(m, m.yT, m.y)
    with m.local(qT=[P, C, N], kT=[P, C, N], v=[P, T, D], w=[P, C, D], w2=[P, C, D], masks=[P, 2, S]) as \
            (qT, kT, v, w, w2, masks):
        load(m, (masks[:], d["causal"]))
        linear_features(m, [(qT, d["L0_attn_w_q"], w, m.yT, None, ACT.Identity),
                            (kT, d["L0_attn_w_k"], w2, m.yT, None, ACT.Identity)])
        linear_tokens(m, v, m.yT, d["L0_attn_w_v"], w, C)
        self_attention(m, m.yT, qT, kT, v, 32 ** -0.5, 100.0, masks[:, 0, :], masks[:, 1, :], custom=True)
        linear_tokens(m, m.x, m.yT, d["L0_attn_w_proj"], w, C, add=m.x)


def L3_xattn(m):
    d = m.d
    normalise(m, m.y, m.x, 1e-5)
    turn(m, m.yT, m.y)
    with m.local(qT=[P, C, N], oT=[P, C, N], w=[P, C, D], bv=[P, D], bo=[1, D], b=[P, 2, C]) as (qT, oT, w, bv, bo, b):
        load(m, (b[:, 0, :], d["L3_xattn_bq"]), (b[:, 1, :], d["L3_xattn_bk"]),
             (bv[:], d["L3_xattn_bv"].partition_broadcast(P)), (bo[:], d["L3_xattn_bo"].unsqueeze(0)))
        linear_features(m, [(qT, d["L3_xattn_Wq"], w, m.yT, b[:, 0, :], ACT.Identity)])
        cross_attention(m, oT, qT, 32, 32 ** -0.5, d["L3_xattn_Wk"], d["L3_xattn_Wv"], b[:, 1, :], bv[:])
        linear_tokens(m, m.x, oT, d["L3_xattn_Wo"], w, C, bo[0:1, :], m.x)


def gate_scores(m, w, buf, srcT, E, brow=None):
    landed, scored = m.sig("gate_landed"), m.sig("gate_scored")
    with m.block() as block:
        @block.sync
        def _(sp):
            sp.dma_start(buf[:], w).then_inc(*landed.up(16))

        @block.tensor
        def _(pe):
            pe.wait_ge(*landed.at(16))
            for t in range(T):
                for c in range(C):
                    ins = pe.matmul(m.ps[:, 0, t * E:(t + 1) * E], srcT[:, c, t * P:(t + 1) * P], buf[:, c, :],
                                    start=(c == 0), stop=(c == C - 1 and brow is None))
                if brow is not None:
                    ins = pe.matmul(m.ps[:, 0, t * E:(t + 1) * E], m.ones[0:1, :], brow, start=False, stop=True)
            ins.then_inc(*scored.up())


def route(m, w, E, k, before, normal, eps=0.0, renormal=True):
    step_s, centred, powered = m.sig("route_step"), m.sig("route_centred"), m.sig("route_exp")
    with m.local(sc=[P, T, E], one=[P, T], cmp=[P, T, E, E], eq=[P, T, E, E], sel=[P, T, E]) as \
            (sc, one, cmp, eq, sel), m.block() as block:
        @block.scalar
        def _(act):
            act.wait_ge(*centred.at(1))
            act.activation(sc[:], sc[:], ACT.Exp).then_inc(*powered.up())

        @block.vector
        def _(dve):
            step = Chain(dve, step_s)
            wide = lambda a: a.unsqueeze(2).to_broadcast([P, T, E])
            step(dve.tensor_copy(sc[:], m.ps[:, 0, 0:T * E].rearrange("p (t e) -> p t e", t=T)))
            step(dve.tensor_reduce(one[:], sc[:], X, ALU.max))
            dve.tensor_tensor(sc[:], sc[:], wide(one[:]), ALU.subtract).then_inc(*centred.up())
            dve.wait_ge(*powered.at(1))
            if normal:
                step(dve.tensor_reduce(one[:], sc[:], X, ALU.add))
                step(dve.reciprocal(one[:], one[:]))
                step(dve.tensor_tensor(sc[:], sc[:], wide(one[:]), ALU.mult))
            for t in range(T):
                mine = sc[:, t, :].unsqueeze(2).to_broadcast([P, E, E])
                other = sc[:, t, :].unsqueeze(1).to_broadcast([P, E, E])
                dve.tensor_tensor(cmp[:, t], other, mine, ALU.is_gt)
                step(dve.tensor_tensor(eq[:, t], other, mine, ALU.is_equal))
                step(dve.tensor_tensor(eq[:, t], eq[:, t], before, ALU.mult))
            step(dve.tensor_tensor(cmp[:], cmp[:], eq[:], ALU.add))
            step(dve.tensor_reduce(sel[:], cmp[:], X, ALU.add))
            step(dve.tensor_scalar(sel[:], sel[:], float(k), None, ALU.is_lt))
            step(dve.tensor_tensor(w[:, :, 0:E], sc[:], sel[:], ALU.mult))
            if renormal:
                step(dve.tensor_reduce(one[:], w[:, :, 0:E], X, ALU.add))
                step(dve.tensor_scalar(one[:], one[:], eps, None, ALU.add))
                step(dve.reciprocal(one[:], one[:]))
                step(dve.tensor_tensor(w[:, :, 0:E], w[:, :, 0:E], wide(one[:]), ALU.mult))


def L0_ffn(m):
    d, E, F = m.d, 8, 1024
    FC = F // P
    s = m.sig
    normalise(m, m.y, m.x, 1e-5)
    with m.local(w=[P, T, E + 1]) as (w,):
        with m.local(z=[P, T, D], zT=[P, C, N], ln=[P, 2, C], gw=[P, C, E], before=[P, E, E]) as \
                (z, zT, ln, gw, before):
            load(m, (ln[:, 0, :], d["L0_ffn_ln_scale"]), (ln[:, 1, :], d["L0_ffn_ln_bias"]),
                 (before[:], d["before8"].partition_broadcast(P)))
            turn(m, m.yT, m.y)
            normalise(m, z, m.y, 1e-5)
            turn(m, zT, z, scale=ln[:, 0, :], bias=ln[:, 1, :])
            gate_scores(m, d["L0_ffn_gate_w"], gw, zT, E)
            route(m, w, E, 2, before[:], True, 1e-5)
        up_landed, down_landed = s("gated_up_landed"), s("gated_down_landed")
        up_done, silu_done, h_ready = s("gated_up_product"), s("gated_silu"), s("gated_h_ready")
        down_done, added, one_set = s("gated_down_product"), s("gated_added"), s("shared_gate_set")
        with m.local(wg=[P, C, F], wu=[P, C, F], wd=[P, FC, D], sg=[P, 2, N], h=[P, FC, N]) as \
                (wg, wu, wd, sg, h), m.block((h_ready, 1), (added, T)) as block:
            ps = m.ps

            @block.sync
            def _(sp):
                with repeat(sp, E + 1) as e:
                    sp.wait_ge(*h_ready.at(1 + FC * e))
                    sp.dma_start(wg[:], d["L0_ffn_Wg"][e]).then_inc(*up_landed.up(16))
                    sp.dma_start(wu[:], d["L0_ffn_Wu"][e]).then_inc(*up_landed.up(16))
                    sp.wait_ge(*added.at(T + T * e))
                    sp.dma_start(wd[:], d["L0_ffn_Wd"][e]).then_inc(*down_landed.up(16))

            @block.gpsimd
            def _(pool):
                pool.memset(w[:, :, E:E + 1], 1.0).then_inc(*one_set.up())

            @block.tensor
            def _(pe):
                with repeat(pe, E + 1) as e:
                    pe.wait_ge(*up_landed.at(32 * e + 32))
                    for n in range(FC):
                        if n >= 2:
                            pe.wait_ge(*h_ready.at(FC * e + n))
                        for half, wb in ((0, wg), (1, wu)):
                            for k in range(C):
                                ins = pe.matmul(ps[:, 2 * half + n % 2, :], wb[:, k, n * P:(n + 1) * P],
                                                m.yT[:, k, :], start=(k == 0), stop=(k == C - 1))
                        ins.then_inc(*up_done.up())
                    pe.wait_ge(*down_landed.at(16 * e + 16))
                    for t in range(T):
                        pe.wait_ge(*added.at(T * e + t + 1))
                        for k in range(FC):
                            if t == 0 and k >= FC - 2:
                                pe.wait_ge(*h_ready.at(1 + FC * e + k + 1))
                            ins = pe.matmul(ps[:, 4 + t, :], h[:, k, t * P:(t + 1) * P], wd[:, k, :],
                                            start=(k == 0), stop=(k == FC - 1))
                        ins.then_inc(*down_done.up())

            @block.scalar
            def _(act):
                with repeat(act, E + 1) as e:
                    for n in range(FC):
                        act.wait_ge(*up_done.at(FC * e + n + 1))
                        if n >= 2:
                            act.wait_ge(*h_ready.at(FC * e + n))
                        else:
                            act.wait_ge(*h_ready.at(1 + FC * e))
                        act.activation(sg[:, n % 2, :], ps[:, n % 2, :], ACT.Silu).then_inc(*silu_done.up())

            @block.vector
            def _(dve):
                dve.wait_ge(*one_set.at(1))
                with repeat(dve, E + 1) as e:
                    for n in range(FC):
                        dve.wait_ge(*silu_done.at(FC * e + n + 1))
                        dve.tensor_tensor(h[:, n, :], ps[:, 2 + n % 2, :], sg[:, n % 2, :], ALU.mult)\
                           .then_inc(*h_ready.up())
                    for t in range(T):
                        dve.wait_ge(*down_done.at(T * e + t + 1))
                        dve.wait_ge(*added.at(T * e + t + 1))
                        dve.scalar_tensor_tensor(m.x[:, t, :], ps[:, 4 + t, :], w[:, t, bass.ds(e, 1)], m.x[:, t, :],
                                                 ALU.mult, ALU.add).then_inc(*added.up())


def L1_xattn(m):
    d = m.d
    temp = float(D) ** 0.5
    normalise(m, m.y, m.x, 1e-5)
    with m.local(qT=[P, C, N], oT=[P, C, N], w=[P, C, D], pre=[P, 2, C], ln=[P, 2, C], rows=[P, 2, D]) as \
            (qT, oT, w, pre, ln, rows):
        load(m, (pre[:, 0, :], d["L1_xattn_pre_g"]), (pre[:, 1, :], d["L1_xattn_pre_b"]),
             (ln[:, 0, :], d["L1_xattn_ln_g"]), (ln[:, 1, :], d["L1_xattn_ln_b"]),
             (rows[:, 0, :], d["L1_xattn_ln_g_row"].partition_broadcast(P)),
             (rows[:, 1, :], d["L1_xattn_ln_b_row"].partition_broadcast(P)))
        normalise(m, m.y, m.y, 1e-5)
        turn(m, m.yT, m.y, scale=pre[:, 0, :], bias=pre[:, 1, :])
        linear_features(m, [(qT, d["L1_xattn_Wq"], w, m.yT, None, ACT.Identity)])
        cross_attention(m, oT, qT, 64, 1.0 / temp, d["L1_xattn_Wk"], d["L1_xattn_Wv"],
                        clip=10000.0 * temp, knorm=(pre[:, 0, :], pre[:, 1, :]))
        turn_back(m, m.y, oT)
        normalise(m, m.y, m.y, 1e-5)
        turn(m, m.yT, m.y, scale=ln[:, 0, :], bias=ln[:, 1, :])
        landed, product, gelu_done, step_s = m.sig("weights_landed_0"), m.sig("tokens_product"), m.sig("gelu_done"), m.sig("gelu_step")
        with m.block() as block:
            @block.sync
            def _(sp):
                sp.dma_start(w[:], d["L1_xattn_Wo"]).then_inc(*landed.up(16))

            @block.tensor
            def _(pe):
                pe.wait_ge(*landed.at(16))
                for t in range(T):
                    for k in range(C):
                        ins = pe.matmul(m.ps[:, t, :], m.yT[:, k, t * P:(t + 1) * P], w[:, k, :],
                                        start=(k == 0), stop=(k == C - 1))
                    ins.then_inc(*product.up())

            @block.scalar
            def _(act):
                for t in range(T):
                    act.wait_ge(*product.at(t + 1))
                    act.activation(qT[:, t, :], m.ps[:, t, :], ACT.Gelu).then_inc(*gelu_done.up())

            @block.vector
            def _(dve):
                step = Chain(dve, step_s)
                for t in range(T):
                    step(dve.tensor_tensor(m.y[:, t, :], m.y[:, t, :], rows[:, 0, :], ALU.mult))
                    step(dve.tensor_tensor(m.y[:, t, :], m.y[:, t, :], rows[:, 1, :], ALU.add))
                    step(dve.tensor_tensor(m.x[:, t, :], m.x[:, t, :], m.y[:, t, :], ALU.add))
                    dve.wait_ge(*gelu_done.at(t + 1))
                    dve.tensor_tensor(m.x[:, t, :], m.x[:, t, :], qT[:, t, :], ALU.add)


def turn_back(m, dst, srcT):
    turned = m.sig("turned")
    with m.block() as block:
        @block.tensor
        def _(pe):
            for t in range(T):
                for c in range(C):
                    ins = pe.transpose(m.ps[:, t, c * P:(c + 1) * P], srcT[:, c, t * P:(t + 1) * P], m.ident[:])
                ins.then_inc(*turned.up())

        @block.vector
        def _(dve):
            for t in range(T):
                dve.wait_ge(*turned.at(t + 1))
                dve.tensor_copy(dst[:, t, :], m.ps[:, t, :])


def L1_ffn(m):
    d, E = m.d, 4
    s = m.sig
    normalise(m, m.y, m.x, 1e-5)
    turn(m, m.yT, m.y)
    add_into(m, m.x, m.x, m.y)
    w1_landed, w2_landed = s("e1_landed"), s("e2_landed")
    first, second, var_ready, rooted = s("e_first"), s("e_second"), s("e_var"), s("e_rstd")
    normed, turned, relued, freed, step_s = s("e_normed"), s("e_turned"), s("e_relu"), s("e_freed"), s("e_step")
    with m.local(w=[P, T, E], gw=[P, C, E], gb=[1, E], before=[P, E, E], w1=[P, C, D], w2=[P, C, D], h=[P, T, D],
                 hT=[P, C, N], b1=[1, E, D], b2=[1, E, D], g1=[P, E, C], be1=[P, E, C], g2=[P, E, D],
                 be2=[P, E, D]) as (w, gw, gb, before, w1, w2, h, hT, b1, b2, g1, be1, g2, be2):
        load(m, (before[:], d["before4"].partition_broadcast(P)), (gb[:], d["L1_ffn_gate_b"].unsqueeze(0)),
             (b1[:], d["L1_ffn_b1"].unsqueeze(0)), (b2[:], d["L1_ffn_b2"].unsqueeze(0)),
             (g1[:], d["L1_ffn_g1"]), (be1[:], d["L1_ffn_be1"]),
             (g2[:], d["L1_ffn_g2"].partition_broadcast(P)), (be2[:], d["L1_ffn_be2"].partition_broadcast(P)))
        gate_scores(m, d["L1_ffn_gate_W"], gw, m.yT, E, gb[0:1, :])
        route(m, w, E, 2, before[:], False)
        with m.block((normed, 1)) as block:
            ps = m.ps

            @block.sync
            def _(sp):
                with repeat(sp, E) as e:
                    sp.wait_ge(*normed.at(1 + 2 * e))
                    sp.dma_start(w1[:], d["L1_ffn_W1"][e]).then_inc(*w1_landed.up(16))
                    sp.dma_start(w2[:], d["L1_ffn_W2"][e]).then_inc(*w2_landed.up(16))

            @block.tensor
            def _(pe):
                with repeat(pe, E) as e:
                    pe.wait_ge(*w1_landed.at(16 * e + 16))
                    pe.wait_ge(*normed.at(1 + 2 * e))
                    for t in range(T):
                        for k in range(C):
                            pe.matmul(ps[:, t, :], m.yT[:, k, t * P:(t + 1) * P], w1[:, k, :], start=(k == 0), stop=False)
                        ins = pe.matmul(ps[:, t, :], m.ones[0:1, :], b1[0:1, e, :], start=False, stop=True)
                        ins.then_inc(*first.up())
                    pe.wait_ge(*normed.at(1 + 2 * e + 1))
                    for c in range(C):
                        for t in range(T):
                            ins = pe.transpose(ps[:, 4 + c, t * P:(t + 1) * P], h[:, t, c * P:(c + 1) * P], m.ident[:])
                        ins.then_inc(*turned.up())
                    pe.wait_ge(*relued.at(C * e + C))
                    pe.wait_ge(*w2_landed.at(16 * e + 16))
                    for t in range(T):
                        for k in range(C):
                            pe.matmul(ps[:, t, :], hT[:, k, t * P:(t + 1) * P], w2[:, k, :], start=(k == 0), stop=False)
                        ins = pe.matmul(ps[:, t, :], m.ones[0:1, :], b2[0:1, e, :], start=False, stop=True)
                        ins.then_inc(*second.up())

            @block.scalar
            def _(act):
                with repeat(act, E) as e:
                    for c in range(C):
                        act.wait_ge(*turned.at(C * e + c + 1))
                        act.activation(hT[:, c, :], ps[:, 4 + c, :], ACT.Relu, bias=be1[:, e, c:c + 1],
                                       scale=g1[:, e, c:c + 1]).then_inc(*relued.up())

            @block.gpsimd
            def _(pool):
                with repeat(pool, 2 * E) as i:
                    pool.wait_ge(*var_ready.at(i + 1))
                    pool.tensor_tensor(m.rstd[:], m.den[:], m.minus_half[:], ALU.pow).then_inc(*rooted.up())

            @block.vector
            def _(dve):
                with repeat(dve, E) as e:
                    step = Chain(dve, step_s, e, 2 * T + 2 + 3 * T)

                    def norm(products, half):
                        for t in range(T):
                            dve.wait_ge(*products.at(T * e + t + 1))
                            step(dve.bn_stats(m.stats[:, t, :], ps[:, t, :]))
                        dve.memset(m.den[:], 0.0)
                        for t in range(T):
                            ins = dve.bn_aggr(m.mv[:, t, :], m.stats[:, t, :])
                        step(ins)
                        dve.tensor_scalar(m.den[:], m.mv[:, :, 1], 1e-5, None, ALU.add).then_inc(*var_ready.up())
                        dve.wait_ge(*rooted.at(2 * e + half + 1))
                        for t in range(T):
                            ins = dve.tensor_scalar(h[:, t, :], ps[:, t, :], m.mv[:, t, 0:1], m.rstd[:, t:t + 1],
                                                    ALU.subtract, ALU.mult)
                        ins.then_inc(*normed.up())
                        dve.wait_ge(*normed.at(1 + 2 * e + half + 1))

                    norm(first, 0)
                    norm(second, 1)
                    for t in range(T):
                        step(dve.tensor_tensor(h[:, t, :], h[:, t, :], g2[:, e, :], ALU.mult))
                        step(dve.tensor_tensor(h[:, t, :], h[:, t, :], be2[:, e, :], ALU.add))
                        step(dve.scalar_tensor_tensor(m.x[:, t, :], h[:, t, :], w[:, t, bass.ds(e, 1)], m.x[:, t, :],
                                                      ALU.mult, ALU.add))
                    step.end()


def L2_xattn(m):
    d = m.d
    scale = (D / 16) ** 0.5
    s = m.sig
    normalise(m, m.y, m.x, 1e-5)
    turn(m, m.yT, m.y)
    ctxt_landed, ctx_landed = [s("pair_ctxT_landed0"), s("pair_ctxT_landed1")], [s("pair_ctx_landed0"), s("pair_ctx_landed1")]
    scored, max_ready, powered, scaled = s("pair_scored"), s("pair_max_ready"), s("pair_exp"), s("pair_scaled")
    turned, taken, attended, o_taken, step_s = s("pair_turned"), s("pair_turned_taken"), s("pair_attended"), s("pair_attended_taken"), s("pair_step")
    biased = s("pair_bias_scored")
    with m.local(qT=[P, C, N], q2T=[P, C, N], w=[P, C, D], w2=[P, C, D], b=[P, 2, C], bv=[1, D]) as (qT, q2T, w, w2, b, bv):
        load(m, (b[:, 0, :], d["L2_xattn_bq"]), (b[:, 1, :], d["L2_xattn_bk"]), (bv[:], d["L2_xattn_bv"].unsqueeze(0)))
        linear_features(m, [(qT, d["L2_xattn_Wq"], w, m.yT, b[:, 0, :], ACT.Identity)])
        linear_features(m, [(q2T, d["L2_xattn_Wk"], w2, qT, None, ACT.Identity)])
        with m.local(ctxT=[P, 2, 2, C, SK], ctx=[P, 2, KC, D], pr=[P, SK], prT=[P, KC, P], sc=[P, SK],
                     col=[P, T, 4], qb=[P, T]) as (ctxT, ctx, pr, prT, sc, col, qb), m.block() as block:
            ps = m.ps

            @block.sync
            def _(sp):
                for t in range(T):
                    if t >= 2:
                        sp.wait_ge(*scored.at(t - 1))
                    sp.dma_start(ctxT[:, t % 2], d["ctxT"][2 * t:2 * t + 2].rearrange("b p c n -> p b c n"))\
                      .then_inc(*ctxt_landed[t % 2].up(16))
                    if t >= 1:
                        sp.wait_ge(*attended.at(t))
                    sp.dma_start(ctx[:], d["ctx"][2 * t:2 * t + 2].rearrange("b p c n -> p b c n"))\
                      .then_inc(*ctx_landed[0].up(16))

            @block.tensor
            def _(pe):
                for t in range(T):
                    for c in range(C):
                        ins = pe.matmul(ps[:, 7, t:t + 1], qT[:, c, t * P:(t + 1) * P], b[:, 1, c:c + 1],
                                        start=(c == 0), stop=(c == C - 1))
                ins.then_inc(*biased.up())

                def scores(t):
                    pe.wait_ge(*ctxt_landed[t % 2].at(16 * (t // 2 + 1)))
                    if t >= 2:
                        pe.wait_ge(*max_ready.at(t - 1))
                    for half in range(2):
                        for c in range(C):
                            ins = pe.matmul(ps[64 * half:64 * half + 64, t % 2, :],
                                            q2T[:, c, t * P + 64 * half:t * P + 64 * half + 64],
                                            ctxT[:, t % 2, half, c, :], start=(c == 0), stop=(c == C - 1))
                    ins.then_inc(*scored.up())

                scores(0)
                for t in range(T):
                    if t + 1 < T:
                        scores(t + 1)
                    pe.wait_ge(*scaled.at(t + 1))
                    for k in range(KC):
                        ins = pe.transpose(ps[:, 2, k * P:(k + 1) * P], pr[:, k * P:(k + 1) * P], m.ident[:])
                    ins.then_inc(*turned.up())
                    pe.wait_ge(*ctx_landed[0].at(16 * t + 16))
                    pe.wait_ge(*taken.at(t + 1))
                    if t >= 1:
                        pe.wait_ge(*o_taken.at(t))
                    for c in range(C):
                        for half in range(2):
                            for k in range(KC):
                                ins = pe.matmul(ps[:, 3, c * P + 64 * half:c * P + 64 * half + 64],
                                                ctx[:, half, k, c * P:(c + 1) * P],
                                                prT[:, k, 64 * half:64 * half + 64],
                                                start=(k == 0), stop=(k == KC - 1))
                    ins.then_inc(*attended.up())

            @block.scalar
            def _(act):
                for t in range(T):
                    act.wait_ge(*max_ready.at(t + 1))
                    act.activation(pr[:], sc[:], ACT.Exp, bias=col[:, t, 1:2], scale=scale,
                                   accum_out=col[:, t, 2:3]).then_inc(*powered.up())

            @block.vector
            def _(dve):
                step = Chain(dve, step_s)
                dve.wait_ge(*biased.at(1))
                step(dve.tensor_copy(qb[:], ps[:, 7, 0:T]))
                for t in range(T):
                    dve.wait_ge(*scored.at(t + 1))
                    step(dve.tensor_scalar(sc[:], ps[:, t % 2, :], qb[:, t:t + 1], None, ALU.add))
                    step(dve.tensor_reduce(col[:, t, 0:1], sc[:], X, ALU.max, negate=True))
                    dve.tensor_scalar(col[:, t, 1:2], col[:, t, 0:1], scale, None, ALU.mult).then_inc(*max_ready.up())
                    dve.wait_ge(*powered.at(t + 1))
                    step(dve.reciprocal(col[:, t, 3:4], col[:, t, 2:3]))
                    dve.tensor_scalar(pr[:], pr[:], col[:, t, 3:4], None, ALU.mult).then_inc(*scaled.up())
                    dve.wait_ge(*turned.at(t + 1))
                    dve.tensor_copy(prT[:], ps[:, 2, :].rearrange("p (k n) -> p k n", k=KC)).then_inc(*taken.up())
                    dve.wait_ge(*attended.at(t + 1))
                    dve.tensor_copy(m.yT[:, :, t * P:(t + 1) * P],
                                    ps[:, 3, :].rearrange("p (c n) -> p c n", c=C)).then_inc(*o_taken.up())
        linear_tokens(m, m.x, m.yT, d["L2_xattn_Wv"], w, C, bv[0:1, :], m.x)


def transformer_layer(m, z, n, ln1, wq, bq, wk, bk, wv, bv, wo, bo, ln2, w1, b1, w2, b2, act, allowed=None, rope=None):
    d = m.d
    FF = 2048
    with m.local(qT=[P, C, N], kT=[P, C, N], v=[P, T, D], w=[P, C, D], wb=[P, C, D], cols=[P, 6, C], bvb=[P, D],
                 bor=[1, D], masks=[P, 2, S]) as (qT, kT, v, w, wb, cols, bvb, bor, masks):
        load(m, *[(cols[:, i, :], d[a]) for i, a in enumerate((ln1[0], ln1[1], bq, bk))],
             (bvb[0:1, :], d[bv].unsqueeze(0)), (bor[:], d[bo].unsqueeze(0)),
             *([(masks[:], d[allowed])] if allowed else []))
        normalise(m, n, z, 1e-5)
        turn(m, m.yT, n, scale=cols[:, 0, :], bias=cols[:, 1, :])
        linear_features(m, [(qT, d[wq], w, m.yT, cols[:, 2, :], ACT.Identity),
                            (kT, d[wk], wb, m.yT, cols[:, 3, :], ACT.Identity)])
        linear_tokens(m, v, m.yT, d[wv], w, C, bvb[0:1, :])
        if rope:
            rotate(m, qT, kT)
        if allowed:
            self_attention(m, m.yT, qT, kT, v, 32 ** -0.5, None, masks[:, 0, :], masks[:, 1, :])
        else:
            self_attention(m, m.yT, qT, kT, v, 32 ** -0.5)
        linear_tokens(m, z, m.yT, d[wo], w, C, bor[0:1, :], z)
    with m.local(cols=[P, 2, C], b1c=[P, FF // P], b2r=[1, D], wa=[P, C, FF], wb=[P, FF // P, D], h=[P, FF // P, N]) as \
            (cols, b1c, b2r, wa, wb, h):
        load(m, (cols[:, 0, :], d[ln2[0]]), (cols[:, 1, :], d[ln2[1]]), (b1c[:], d[b1]), (b2r[:], d[b2].unsqueeze(0)))
        normalise(m, n, z, 1e-5)
        turn(m, m.yT, n, scale=cols[:, 0, :], bias=cols[:, 1, :])
        linear_features(m, [(h, d[w1], wa, m.yT, b1c, act)])
        linear_tokens(m, z, h, d[w2], wb, FF // P, b2r[0:1, :], z)


def rotate(m, qT, kT):
    turned, timed, step_s = m.sig("pairs_turned"), m.sig("cos_multiplied"), m.sig("rotate_step")
    with m.local(perm=[P, P], trig=[P, 2, S], tmp=[P, 2, N]) as (perm, trig, tmp):
        load(m, (perm[:], m.d["rope_turn"]), (trig[:], m.d["rope_trig"]))
        with m.block() as block:
            @block.tensor
            def _(pe):
                for n in range(2 * C):
                    src = (qT, kT)[n // C]
                    pe.matmul(m.ps[:, n, :], perm[:], src[:, n % C, :], start=True, stop=True).then_inc(*turned.up())

            @block.vector
            def _(dve):
                step = Chain(dve, step_s)
                over = lambda a: a.unsqueeze(1).to_broadcast([P, B, S])
                for n in range(2 * C):
                    src = (qT, kT)[n // C][:, n % C, :].rearrange("p (b s) -> p b s", b=B)
                    t = tmp[:, n % 2, :].rearrange("p (b s) -> p b s", b=B)
                    dve.wait_ge(*turned.at(n + 1))
                    dve.tensor_tensor(t, m.ps[:, n, :].rearrange("p (b s) -> p b s", b=B), over(trig[:, 1, :]), ALU.mult)
                    step(dve.tensor_tensor(src, src, over(trig[:, 0, :]), ALU.mult))
                    step(dve.tensor_tensor(src, src, t, ALU.add))


def L2_attn(m):
    normalise(m, m.y, m.x, 1e-5)
    with m.local(n=[P, T, D]) as (n,):
        for i in range(2):
            g = lambda a: f"L2_attn_{a}_{i}"
            transformer_layer(m, m.y, n, (g("ln1_g"), g("ln1_b")), g("wq"), g("bq"), g("wk"), g("bk"), g("wv"), g("bv"),
                              g("wo"), g("bo"), (g("ln2_g"), g("ln2_b")), g("w1"), g("b1"), g("w2"), g("b2"), ACT.Gelu,
                              allowed="strided")
        with m.local(rows=[P, 2, D]) as (rows,):
            load(m, (rows[:, 0, :], m.d["L2_attn_lnf_g"].partition_broadcast(P)),
                 (rows[:, 1, :], m.d["L2_attn_lnf_b"].partition_broadcast(P)))
            normalise(m, n, m.y, 1e-5)
            scaled = m.sig("final_norm_step")
            with m.block() as block:
                @block.vector
                def _(dve):
                    step = Chain(dve, scaled)
                    over = lambda a: a.unsqueeze(1).to_broadcast([P, T, D])
                    step(dve.tensor_tensor(n[:], n[:], over(rows[:, 0, :]), ALU.mult))
                    step(dve.tensor_tensor(n[:], n[:], over(rows[:, 1, :]), ALU.add))
                    step(dve.tensor_tensor(m.x[:], m.x[:], n[:], ALU.add))


def L3_attn(m):
    normalise(m, m.y, m.x, 1e-5)
    g = lambda a: f"L3_attn_{a}"
    with m.local(n=[P, T, D]) as (n,):
        transformer_layer(m, m.y, n, (g("g1"), g("beta1")), g("Wq"), g("bq"), g("Wk"), g("bk"), g("Wv"), g("bv"),
                          g("Wo"), g("bo"), (g("g2"), g("beta2")), g("W1"), g("b1"), g("W2"), g("b2"), ACT.Relu, rope=True)
    add_into(m, m.x, m.x, m.y)


def L2_ffn(m):
    d, E, F, CAP = m.d, 8, 2048, S // 8
    FC, SL = F // P, B * CAP
    s = m.sig
    normalise(m, m.y, m.x, 1e-5)
    turn(m, m.yT, m.y)
    with m.local(xT=[P, C, E, SL], cmbT=[P, E // 2, N]) as (xT, cmbT):
        with m.local(w=[P, T, E], gw=[P, C, E], before=[P, E, E], earlier=[P, P], place=[P, CAP], one=[P, T, E],
                     disp=[P, T, E, SL], hot=[P, T * E, CAP]) as (w, gw, before, earlier, place, one, disp, hot):
            load(m, (before[:], d["before8"].partition_broadcast(P)), (earlier[:], d["earlier"]),
                 (place[:], d["place"].partition_broadcast(P)))
            gate_scores(m, d["L2_ffn_Wg"], gw, m.yT, E)
            route(m, w, E, 1, before[:], True, renormal=False)
            chosen, counted, step_s, dispatched = s("chosen"), s("counted"), s("dispatch_step"), s("dispatched")
            gathered, gathered_taken, weighed, c_turned = s("gathered"), s("gathered_taken"), s("weighed"), s("combine_turned")
            zeroed = s("dispatch_zeroed")
            with m.block() as block:
                ps = m.ps

                @block.gpsimd
                def _(pool):
                    pool.memset(disp[:], 0.0).then_inc(*zeroed.up())

                @block.tensor
                def _(pe):
                    pe.wait_ge(*chosen.at(1))
                    for t in range(T):
                        ins = pe.matmul(ps[:, 0, t * E:(t + 1) * E], earlier[:], one[:, t, :], start=True, stop=True)
                    ins.then_inc(*counted.up())
                    pe.wait_ge(*dispatched.at(1))
                    for t in range(T):
                        for c in range(C):
                            ins = pe.matmul(ps[:, 1 + t % 2, c * P:(c + 1) * P], m.y[:, t, c * P:(c + 1) * P],
                                            disp[:, t, :, t * 16:(t + 1) * 16], start=True, stop=True)
                        ins.then_inc(*gathered.up())
                        if t + 1 < T and t >= 1:
                            pe.wait_ge(*gathered_taken.at(t))
                    pe.wait_ge(*weighed.at(1))
                    for j in range(E // 2):
                        for t in range(T):
                            ins = pe.transpose(ps[:, 4 + j, t * P:(t + 1) * P],
                                               disp[:, t, 2 * j:2 * j + 2, :].rearrange("p e n -> p (e n)"), m.ident[:])
                        ins.then_inc(*c_turned.up())

                @block.vector
                def _(dve):
                    step = Chain(dve, step_s)
                    dve.tensor_scalar(one[:], w[:], 0.0, None, ALU.is_gt).then_inc(*chosen.up())
                    dve.wait_ge(*counted.at(1))
                    step(dve.tensor_tensor(hot[:], ps[:, 0, 0:T * E].unsqueeze(2).to_broadcast([P, T * E, CAP]),
                                           place[:].unsqueeze(1).to_broadcast([P, T * E, CAP]), ALU.is_equal))
                    step(dve.tensor_tensor(hot[:], hot[:],
                                           one[:].rearrange("p t e -> p (t e)").unsqueeze(2).to_broadcast([P, T * E, CAP]),
                                           ALU.mult))
                    dve.wait_ge(*zeroed.at(1))
                    for t in range(T):
                        for half in range(2):
                            rows = slice(64 * half, 64 * half + 64)
                            o = 16 * t + CAP * half
                            ins = dve.tensor_copy(disp[rows, t, :, o:o + CAP], hot[rows, t * E:(t + 1) * E, :])
                    step(ins)
                    ins = dve.tensor_copy(one[:], one[:])
                    ins.then_inc(*dispatched.up())
                    for t in range(T):
                        dve.wait_ge(*gathered.at(t + 1))
                        for c in range(C):
                            ins = dve.tensor_copy(xT[:, c, :, 16 * t:16 * t + 16],
                                                  ps[:, 1 + t % 2, c * P:(c + 1) * P].rearrange("p (e n) -> p e n", e=E))
                        ins.then_inc(*gathered_taken.up())
                    ins = dve.tensor_tensor(disp[:].rearrange("p t e n -> p (t e) n"),
                                            disp[:].rearrange("p t e n -> p (t e) n"),
                                            w[:].rearrange("p t e -> p (t e)").unsqueeze(2).to_broadcast([P, T * E, SL]),
                                            ALU.mult)
                    ins.then_inc(*weighed.up())
                    for j in range(E // 2):
                        dve.wait_ge(*c_turned.at(j + 1))
                        dve.tensor_copy(cmbT[:, j, :], ps[:, 4 + j, :])

        w1_landed, w2_landed = [s(f"switch_w1_landed{i}") for i in range(4)], [s(f"switch_w2_landed{i}") for i in range(4)]
        up_done, h_ready, down_done, o_taken, combined = s("switch_up"), s("switch_h_ready"), s("switch_down"), s("switch_o_taken"), s("switch_combined")
        with m.local(wa=[P, 4, C, 512], wb=[P, 4, 4, D], h=[P, 2, FC // 2, SL], o=[P, E // 2, D]) as (wa, wb, h, o), \
                m.block((up_done, 4), (down_done, 4), (o_taken, 1)) as block:
            ps = m.ps

            @block.sync
            def _(sp):
                with repeat(sp, E) as e:
                    for g in range(4):
                        sp.wait_ge(*up_done.at(4 * e + g + 1))
                        sp.dma_start(wa[:, g], d["L2_ffn_W1"][e, g]).then_inc(*w1_landed[g].up(16))
                    for g in range(4):
                        sp.wait_ge(*down_done.at(4 * e + g + 1))
                        sp.dma_start(wb[:, g], d["L2_ffn_W2"][e, g]).then_inc(*w2_landed[g].up(16))

            @block.tensor
            def _(pe):
                with repeat(pe, E // 2) as j:
                    for half in range(2):
                        e = 2 * j + half
                        for g in range(4):
                            pe.wait_ge(*w1_landed[g].at(16 * e + 16))
                            for n in range(4):
                                f = 4 * g + n
                                for k in range(C):
                                    ins = pe.matmul(ps[:, f // 8, (f % 8) * SL:(f % 8) * SL + SL],
                                                    wa[:, g, k, n * P:(n + 1) * P], xT[:, k, e, :],
                                                    start=(k == 0), stop=(k == C - 1))
                            ins.then_inc(*up_done.up())
                        for g in range(4):
                            pe.wait_ge(*w2_landed[g].at(16 * e + 16))
                            if g == 0:
                                pe.wait_ge(*o_taken.at(e + 1))
                            if g % 2 == 0:
                                pe.wait_ge(*h_ready.at(2 * e + g // 2 + 1))
                            for n in range(4):
                                f = 4 * g + n
                                ins = pe.matmul(ps[64 * half:64 * half + 64, 2, :], h[:, f // 8, f % 8, :], wb[:, g, n, :],
                                                start=(f == 0), stop=(f == FC - 1))
                            ins.then_inc(*down_done.up())
                pe.wait_ge(*o_taken.at(E + 1))
                for t in range(T):
                    for j in range(E // 2):
                        ins = pe.matmul(ps[:, 4 + t, :], cmbT[:, j, t * P:(t + 1) * P], o[:, j, :],
                                        start=(j == 0), stop=(j == E // 2 - 1))
                    ins.then_inc(*combined.up())

            @block.scalar
            def _(act):
                with repeat(act, E) as e:
                    for half in range(2):
                        act.wait_ge(*up_done.at(4 + 4 * e + 2 * half + 2))
                        act.activation(h[:, half, :, :].rearrange("p f n -> p (f n)"), ps[:, half, :],
                                       ACT.Gelu_apprx_tanh).then_inc(*h_ready.up())

            @block.vector
            def _(dve):
                with repeat(dve, E // 2) as j:
                    for half in range(2):
                        rows = slice(64 * half, 64 * half + 64)
                        dve.wait_ge(*down_done.at(4 + 8 * j + 4 * half + 4))
                        dve.tensor_copy(o[rows, j, :], ps[rows, 2, :]).then_inc(*o_taken.up())
                for t in range(T):
                    dve.wait_ge(*combined.at(t + 1))
                    dve.tensor_tensor(m.x[:, t, :], m.x[:, t, :], ps[:, 4 + t, :], ALU.add)


def L3_ffn(m):
    d, E, F = m.d, 32, 2048
    FC = F // P
    s = m.sig
    normalise(m, m.y, m.x, 1e-5)
    turn(m, m.yT, m.y)
    with m.local(kept=[E, B, S], mT=[P, C, E + 1, B], oT=[P, C, B, E], b1c=[P, E, FC], b2c=[P, E, C]) as (kept, mT, oT, b1c, b2c):
        landed, scored, centred, powered, step_s = s("gate_landed"), s("gate_scored"), s("route_centred"), s("route_exp"), s("route_step")
        kept_ready, k_turned, kt_taken, merged, merged_taken = s("kept_ready"), s("kept_turned"), s("kept_turned_taken"), s("merged"), s("merged_taken")
        with m.local(gw=[P, C, E], gb=[E, 1], sc=[E, B, S], left=[E, B, S], top=[E, B, 8], one=[E, B], keptT=[P, T, E]) as \
                (gw, gb, sc, left, top, one, keptT), m.block() as block:
            ps = m.ps

            @block.sync
            def _(sp):
                sp.dma_start(gw[:], d["L3_ffn_gate_w"]).then_inc(*landed.up(16))
                sp.dma_start(gb[:], d["L3_ffn_gate_b"].unsqueeze(1)).then_inc(*landed.up(16))
                sp.dma_start(b1c[:], d["L3_ffn_b1"]).then_inc(*landed.up(16))
                sp.dma_start(b2c[:], d["L3_ffn_b2"]).then_inc(*landed.up(16))
                sp.wait_ge(*landed.at(64))

            @block.tensor
            def _(pe):
                pe.wait_ge(*landed.at(64))
                for c in range(C):
                    ins = pe.matmul(ps[0:E, 0, :], gw[:, c, :], m.yT[:, c, :], start=(c == 0), stop=(c == C - 1))
                ins.then_inc(*scored.up())
                pe.wait_ge(*kept_ready.at(1))
                for t in range(T):
                    ins = pe.transpose(ps[:, 1, t * E:(t + 1) * E],
                                       kept[:, 2 * t:2 * t + 2, :].rearrange("e b s -> e (b s)"), m.ident[0:E, 0:E])
                ins.then_inc(*k_turned.up())
                pe.wait_ge(*kt_taken.at(1))
                for c in range(C):
                    for half in range(2):
                        for t in range(T):
                            rows = slice(64 * half, 64 * half + 64)
                            b = 2 * t + half
                            ins = pe.matmul(ps[:, 2 + 2 * half + c % 2, t * E:(t + 1) * E], m.y[rows, t, c * P:(c + 1) * P],
                                            keptT[rows, t, :], start=True, stop=True)
                    ins.then_inc(*merged.up())
                    if c >= 1 and c + 1 < C:
                        pe.wait_ge(*merged_taken.at(c))

            @block.scalar
            def _(act):
                act.wait_ge(*centred.at(1))
                act.activation(sc[:], sc[:], ACT.Exp).then_inc(*powered.up())

            @block.vector
            def _(dve):
                step = Chain(dve, step_s)
                wide = lambda a: a.unsqueeze(2).to_broadcast([E, B, S])
                dve.wait_ge(*scored.at(1))
                step(dve.tensor_scalar(sc[:].rearrange("e b s -> e (b s)"), ps[0:E, 0, :], gb[:, 0:1], None, ALU.add))
                step(dve.tensor_reduce(one[:], sc[:], X, ALU.max))
                dve.tensor_tensor(sc[:], sc[:], wide(one[:]), ALU.subtract).then_inc(*centred.up())
                dve.wait_ge(*powered.at(1))
                step(dve.tensor_reduce(one[:], sc[:], X, ALU.add))
                step(dve.reciprocal(one[:], one[:]))
                step(dve.tensor_tensor(sc[:], sc[:], wide(one[:]), ALU.mult))
                for b in range(B):
                    ins = dve.max(top[:, b, :], sc[:, b, :])
                step(ins)
                for b in range(B):
                    ins = dve.match_replace(left[:, b, :], top[:, b, :], sc[:, b, :], 0.0)
                step(ins)
                dve.tensor_tensor(kept[:], sc[:], left[:], ALU.subtract).then_inc(*kept_ready.up())
                dve.wait_ge(*k_turned.at(1))
                dve.tensor_copy(keptT[:].rearrange("p t e -> p (t e)"), ps[:, 1, 0:T * E]).then_inc(*kt_taken.up())
                for c in range(C):
                    dve.wait_ge(*merged.at(c + 1))
                    for half in range(2):
                        ins = dve.tensor_copy(mT[:, c, 0:E, :].rearrange("p e (t h) -> p h t e", h=2)[:, half],
                                              ps[:, 2 + 2 * half + c % 2, 0:T * E].rearrange("p (t e) -> p t e", t=T))
                    ins.then_inc(*merged_taken.up())
                dve.memset(mT[:, :, E, :], 0.0)

        w1_landed, w2_landed = [s(f"last_w1_landed{i}") for i in range(4)], [s(f"last_w2_landed{i}") for i in range(4)]
        up_done, down_done, h_copied, h_turned = s("last_up"), s("last_down"), s("last_h_copied"), s("last_h_turned")
        biased, h_ready, parts_copied, summed, o_taken = s("last_biased"), s("last_h_ready"), s("last_parts_copied"), s("last_summed"), s("last_o_taken")
        mine_ready, zeroed = s("last_mine_ready"), s("last_zeroed")
        Q, B4 = 4, 32
        with m.local(wa=[P, Q, F], wb=[P, Q, Q, D], hq=[P, 512], pre=[P, FC, B], h=[P, FC, B4], part=[P, D],
                     mine=[P, 2, C, B4], fold=[P, B]) as (wa, wb, hq, pre, h, part, mine, fold):
            load(m, (fold[:], d["fold_quarters"]))
            with m.block((up_done, 1), (down_done, 4), (summed, 1), (o_taken, 1), (h_turned, 1), (mine_ready, 1)) as block:
                ps = m.ps

                @block.sync
                def _(sp):
                    with repeat(sp, E) as e:
                        sp.wait_ge(*up_done.at(e + 1))
                        for k in range(Q):
                            sp.dma_start(wa[:, k], d["L3_ffn_w1"][e, k]).then_inc(*w1_landed[k].up(16))
                        for n in range(Q):
                            sp.wait_ge(*down_done.at(Q * e + n + 1))
                            sp.dma_start(wb[:, n], d["L3_ffn_w2"][e, n]).then_inc(*w2_landed[n].up(16))

                @block.tensor
                def _(pe):
                    with repeat(pe, E // 2) as pair:
                        for odd in range(2):
                            e = 2 * pair + odd
                            pe.wait_ge(*mine_ready.at(1 + e + 1))
                            pe.wait_ge(*o_taken.at(e + 1))
                            for k in range(C):
                                pe.wait_ge(*w1_landed[k].at(16 * e + 16))
                                for q in range(Q):
                                    ins = pe.matmul(ps[B4 * q:B4 * q + B4, 0, :], mine[:, odd, k, :],
                                                    wa[:, k, q * 512:(q + 1) * 512], start=(k == 0), stop=(k == C - 1))
                            ins.then_inc(*up_done.up())
                            pe.wait_ge(*h_copied.at(e + 1))
                            for n in range(4):
                                ins = pe.transpose(ps[:, 1, n * P:(n + 1) * P], hq[:, n * P:(n + 1) * P], m.ident[:])
                            ins.then_inc(*h_turned.up())
                            pe.wait_ge(*h_ready.at(e + 1))
                            for n in range(Q):
                                pe.wait_ge(*w2_landed[n].at(16 * e + 16))
                                for q in range(Q):
                                    ins = pe.matmul(ps[B4 * q:B4 * q + B4, 2, :], h[:, Q * n + q, :], wb[:, n, q, :],
                                                    start=(n == 0), stop=(n == Q - 1))
                                ins.then_inc(*down_done.up())
                            pe.wait_ge(*parts_copied.at(e + 1))
                            for c in range(C):
                                ins = pe.matmul(ps[:, 3, c * B:(c + 1) * B], part[:, c * P:(c + 1) * P], fold[:],
                                                start=True, stop=True)
                            ins.then_inc(*summed.up())

                @block.scalar
                def _(act):
                    act.wait_ge(*zeroed.at(1))
                    with repeat(act, E) as e:
                        act.wait_ge(*up_done.at(1 + e + 1))
                        act.activation(hq[:], ps[:, 0, :], ACT.Copy).then_inc(*h_copied.up())
                        act.wait_ge(*biased.at(e + 1))
                        act.activation(h[:, :, 0:B], pre[:], ACT.Gelu).then_inc(*h_ready.up())
                        act.wait_ge(*down_done.at(4 + Q * e + Q))
                        act.activation(part[:], ps[:, 2, :], ACT.Copy).then_inc(*parts_copied.up())

                @block.gpsimd
                def _(pool):
                    pool.memset(h[:], 0.0).then_inc(*zeroed.up())
                    pool.memset(mine[:], 0.0).then_inc(*zeroed.up())

                @block.vector
                def _(dve):
                    dve.wait_ge(*zeroed.at(2))
                    dve.tensor_copy(mine[:, 0, :, 0:B], mT[:, :, 0, :]).then_inc(*mine_ready.up())
                    with repeat(dve, E // 2) as pair:
                        for odd in range(2):
                            e = 2 * pair + odd
                            dve.wait_ge(*up_done.at(1 + e + 1))
                            dve.tensor_copy(mine[:, 1 - odd, :, 0:B],
                                            mT[:, :, bass.ds(e + 1, 1), :].rearrange("p c o b -> p c (o b)"))\
                               .then_inc(*mine_ready.up())
                            dve.wait_ge(*h_turned.at(1 + e + 1))
                            for n in range(4):
                                ins = dve.tensor_tensor(
                                    pre[:, Q * n:Q * n + Q, :],
                                    ps[:, 1, n * P:(n + 1) * P].rearrange("p (q b) -> p q b", q=Q)[:, :, 0:B],
                                    b1c[:, e, Q * n:Q * n + Q].unsqueeze(2).to_broadcast([P, Q, B]), ALU.add)
                            ins.then_inc(*biased.up())
                            dve.wait_ge(*summed.at(1 + e + 1))
                            dve.tensor_tensor(oT[:, :, :, e], ps[:, 3, 0:C * B].rearrange("p (c b) -> p c b", c=C),
                                              b2c[:, e, :].unsqueeze(2).to_broadcast([P, C, B]), ALU.add)\
                               .then_inc(*o_taken.up())

        o_turned, o_copied, given = s("experts_turned"), s("experts_turned_taken"), s("given_back")
        with m.local(o=[E, B, D]) as (o,), m.block() as block:
            ps = m.ps

            @block.tensor
            def _(pe):
                def give(b):
                    rows = slice(64 * (b % 2), 64 * (b % 2) + 64)
                    pe.wait_ge(*o_copied.at(b + 1))
                    pe.matmul(ps[rows, 4 + b // 2, :], kept[:, b, :], o[:, b, :], start=True, stop=True)\
                      .then_inc(*given.up())

                for b in range(B):
                    if b >= 2:
                        pe.wait_ge(*o_copied.at(b - 1))
                    for c in range(C):
                        ins = pe.transpose(ps[0:E, b % 2, c * P:(c + 1) * P], oT[:, c, b, :], m.ident[:])
                    ins.then_inc(*o_turned.up())
                    if b >= 1:
                        give(b - 1)
                give(B - 1)

            @block.vector
            def _(dve):
                for b in range(B):
                    dve.wait_ge(*o_turned.at(b + 1))
                    dve.tensor_copy(o[:, b, :], ps[0:E, b % 2, :]).then_inc(*o_copied.up())
                for t in range(T):
                    dve.wait_ge(*given.at(2 * t + 2))
                    dve.tensor_tensor(m.x[:, t, :], m.x[:, t, :], ps[:, 4 + t, :], ALU.add)


def L1_attn(m):
    d, H, DI, NC = m.d, 32, 1024, 8
    s = m.sig
    normalise(m, m.y, m.x, 1e-5)
    with m.local(va=[P, NC, N], u=[P, NC, N], key=[P, 2, NC, N], kb=[P, 2, NC, N], a11=[P, NC, N], a12=[P, NC, N],
                 W=[P, NC, 512], vecs=[P, 8, NC], convw=[P, NC, 4], inb=[P, 4 * NC], rmsw=[P, C]) as \
            (va, u, key, kb, a11, a12, W, vecs, convw, inb, rmsw):
        flat = lambda a: a.rearrange("p c n -> p (c n)")
        load(m, (vecs[:, 0, :], d["L1_attn_conv_b"]), (vecs[:, 1, :], d["L1_attn_gn_w"]),
             (vecs[:, 2, :], d["L1_attn_gn_b"]), (vecs[:, 3, :], d["L1_attn_D"]), (convw[:], d["L1_attn_conv_w"]),
             (inb[:], d["L1_attn_in_proj_b"]), (rmsw[:], d["L1_attn_rms_w"]))
        n = a11[:, 0:T, :]
        normalise(m, n, m.y, 1e-6, rms=True)
        turn(m, m.yT, n, scale=rmsw[:])
        wbuf = [W[:].rearrange("p c n -> p (c n)").rearrange("p (k n) -> p k n", k=C),
                kb[:, 0].rearrange("p c n -> p (c n)").rearrange("p (k n) -> p k n", k=C),
                kb[:, 1].rearrange("p c n -> p (c n)").rearrange("p (k n) -> p k n", k=C)]
        linear_features(m, [(va, d["L1_attn_in_V"], wbuf[0], m.yT, inb[:, 0:NC], ACT.Identity),
                            (key[:, 0], d["L1_attn_in_K0"], wbuf[1], m.yT, inb[:, NC:2 * NC], ACT.Identity),
                            (key[:, 1], d["L1_attn_in_K1"], wbuf[2], m.yT, inb[:, 2 * NC:3 * NC], ACT.Identity)])
        L1_convolution(m, u, va, a11, convw, vecs)
        L1_coefficients(m, va, u, key, kb, a11, a12, W)
        L1_scan(m, va, key, kb, a11, a12)
        L1_readout(m, va, u, key, kb, a11, a12, W, vecs, inb)
        linear_tokens(m, m.x, va, d["L1_attn_out_W"], W, NC, add=m.x)
        add_into(m, m.x, m.x, m.y)


def L1_convolution(m, u, v, tmp, w, vecs):
    NC = 8
    done, step_s = m.sig("convolved"), m.sig("conv_step")
    with m.block() as block:
        @block.vector
        def _(dve):
            step = Chain(dve, step_s)
            for c in range(NC):
                o = tmp[:, c, :].rearrange("p (b s) -> p b s", b=B)
                i = v[:, c, :].rearrange("p (b s) -> p b s", b=B)
                step(dve.tensor_scalar(tmp[:, c, :], v[:, c, :], w[:, c, 3:4], None, ALU.mult))
                for back in range(1, 4):
                    ins = dve.scalar_tensor_tensor(o[:, :, back:], i[:, :, :S - back], w[:, c, 3 - back:4 - back],
                                                   o[:, :, back:], ALU.mult, ALU.add)
                    if back < 3:
                        step(ins)
                ins.then_inc(*done.up())

        @block.scalar
        def _(act):
            for c in range(NC):
                act.wait_ge(*done.at(c + 1))
                act.activation(u[:, c, :], tmp[:, c, :], ACT.Silu, bias=vecs[:, 0, c:c + 1])


def L1_coefficients(m, va, u, key, kb, a11, a12, W):
    d, H, NC = m.d, 32, 8
    NS = 11 * H
    Wv = W[:].rearrange("p c n -> p (c n)")[:, 0:NC * NS].rearrange("p (c n) -> p c n", c=NC)
    brow = a12[0:1, 7, 0:NS]
    flat = a11[:].rearrange("p c n -> p (c n)")
    at = [0]

    def cut(n):
        o = at[0]
        at[0] += T * n
        return flat[:, o:o + T * n].rearrange("p (t n) -> p t n", t=T)

    sm, sp3, e3, n3 = cut(NS), cut(3 * H), cut(3 * H), cut(3 * H)
    om, den, dt, a, w, a2, w2, det, num, t0 = [cut(H) for _ in range(10)]
    quant = a12[:].rearrange("p c n -> p (c n)")[:, 0:T * 8 * H].rearrange("p (t n) -> p t n", t=T)
    load(m, (Wv, d["L1_attn_small_W"]), (brow, d["L1_attn_small_b"].unsqueeze(0)),
         (e3[:, 0, 0:H], d["L1_attn_dt_c"].partition_broadcast(P)), (e3[:, 1, 0:H], d["rope_rate"]))
    product = m.sig("tokens_product")
    step_s, act_s, to_act, to_dve = m.sig("coef_step"), m.sig("coef_act_step"), m.sig("coef_to_act"), m.sig("coef_to_dve")
    with m.block() as block:
        ps = m.ps

        @block.tensor
        def _(pe):
            for t in range(T):
                for k in range(NC):
                    pe.matmul(ps[:, t, 0:NS], u[:, k, t * P:(t + 1) * P], Wv[:, k, :], start=(k == 0), stop=False)
                pe.matmul(ps[:, t, 0:NS], m.ones[0:1, :], brow, start=False, stop=True).then_inc(*product.up())

        @block.scalar
        def _(act):
            step = Chain(act, act_s)
            act.wait_ge(*to_act.at(1))
            step(act.activation(n3, n3, ACT.Exp))
            act.activation(n3, n3, ACT.Ln, bias=1.0).then_inc(*to_dve.up())
            act.wait_ge(*to_act.at(2))
            step(act.activation(num, num, ACT.Ln))
            act.activation(sm[:, :, 4 * H:7 * H], sm[:, :, 4 * H:7 * H], ACT.Sigmoid).then_inc(*to_dve.up())
            act.wait_ge(*to_act.at(3))
            act.activation(num, num, ACT.Exp).then_inc(*to_dve.up())
            act.wait_ge(*to_act.at(4))
            act.activation(num, num, ACT.Sqrt).then_inc(*to_dve.up())

        @block.vector
        def _(dve):
            step = Chain(dve, step_s)
            tt = lambda o, x, y, op: step(dve.tensor_tensor(o, x, y, op))
            ts = lambda o, x, y, z, op, op2=ALU.bypass: step(dve.tensor_scalar(o, x, y, z, op, op2)
                                                            if z is not None else dve.tensor_scalar(o, x, y, None, op))
            for t in range(T):
                dve.wait_ge(*product.at(t + 1))
                ins = dve.tensor_copy(sm[:, t, :], ps[:, t, 0:NS])
                dve.tensor_copy(sp3[:, t, 2 * H:3 * H], e3[:, 0, 0:H])
            step(ins)
            dve.tensor_copy(sp3[:, :, 0:H], sm[:, :, 0:H])
            step(dve.tensor_copy(sp3[:, :, H:2 * H], sm[:, :, 3 * H:4 * H]))
            ts(n3, sp3, -1.0, None, ALU.mult)
            dve.tensor_tensor(n3, sp3, n3, ALU.min).then_inc(*to_act.up())
            tt(om, sm[:, :, H:2 * H], sm[:, :, 2 * H:3 * H], ALU.add)
            tt(om, om, e3[:, 1, 0:H].unsqueeze(1).to_broadcast([P, T, H]), ALU.add)
            ts(sp3, sp3, 0.0, None, ALU.max)
            dve.wait_ge(*to_dve.at(1))
            tt(sp3, sp3, n3, ALU.add)
            alpha, seldt, dtc = sp3[:, :, 0:H], sp3[:, :, H:2 * H], sp3[:, :, 2 * H:3 * H]
            ts(den, om, -1.0, None, ALU.mult)
            tt(den, om, den, ALU.max)
            tt(den, den, alpha, ALU.add)
            ts(den, den, 0.0001, None, ALU.add)
            step(dve.reciprocal(den, den))
            tt(dt, dtc, den, ALU.mult)
            tt(dt, dt, seldt, ALU.add)
            ts(dt, dt, 0.5, None, ALU.mult)
            tt(a, dt, alpha, ALU.mult)
            tt(w, dt, om, ALU.mult)
            tt(w2, w, w, ALU.mult)
            ts(det, a, 1.0, None, ALU.add)
            tt(det, det, det, ALU.mult)
            tt(det, det, w2, ALU.add)
            step(dve.reciprocal(det, det))
            ts(num, a, -1.0, 1.0, ALU.mult, ALU.add)
            tt(num, num, num, ALU.mult)
            tt(num, num, w2, ALU.add)
            tt(num, num, det, ALU.mult)
            dve.tensor_scalar(num, num, 1e-19, None, ALU.max).then_inc(*to_act.up())
            tt(a2, a, a, ALU.mult)
            ts(a2, a2, -1.0, 1.0, ALU.mult, ALU.add)
            tt(a2, a2, w2, ALU.subtract)
            q = lambda i: quant[:, :, i * H:(i + 1) * H]
            tt(q(0), a2, det, ALU.mult)
            tt(t0, w, det, ALU.mult)
            ts(q(1), t0, 2.0, None, ALU.mult)
            dve.wait_ge(*to_dve.at(2))
            dve.tensor_copy(q(2), sm[:, :, 4 * H:5 * H])
            dve.tensor_copy(quant[:, :, 3 * H:5 * H], sm[:, :, 7 * H:9 * H])
            dve.tensor_copy(quant[:, :, 5 * H:7 * H], sm[:, :, 9 * H:11 * H])
            dve.tensor_tensor(num, num, sm[:, :, 5 * H:6 * H], ALU.mult).then_inc(*to_act.up())
            dve.wait_ge(*to_dve.at(3))
            ts(num, num, -1.0, 1.0, ALU.mult, ALU.add)
            dve.tensor_scalar(num, num, 1e-6, None, ALU.max).then_inc(*to_act.up())
            dve.wait_ge(*to_dve.at(4))
            tt(q(7), num, sm[:, :, 6 * H:7 * H], ALU.mult)

    qT = m.yT
    turned, spread = m.sig("quantities_turned"), m.sig("quantities_spread")
    taken_a, taken_v, sel_landed = m.sig("spread_taken_act"), m.sig("spread_taken_dve"), m.sig("selector_landed")
    sel = W[:].rearrange("p c n -> p (c n)")[:, 0:NC * P].rearrange("p (c n) -> p c n", c=NC)
    quantT = W[:].rearrange("p c n -> p (c n)")[:, NC * P:NC * P + 2 * N].rearrange("p (g n) -> p g n", g=2)
    load(m, (sel, d["head_spread"]))
    with m.block() as block:
        @block.tensor
        def _(pe):
            for g in range(2):
                for t in range(T):
                    ins = pe.transpose(ps[:, g, t * P:(t + 1) * P], quant[:, t, g * P:(g + 1) * P], m.ident[:])
                ins.then_inc(*turned.up())

        @block.vector
        def _(dve):
            for g in range(2):
                dve.wait_ge(*turned.at(g + 1))
                dve.tensor_copy(quantT[:, g, :], ps[:, g, :])

    def spread_of(pe, bank, q, c):
        rows = slice(H * (q % 4), H * (q % 4) + H)
        return pe.matmul(ps[:, bank, :], sel[rows, c, :], quantT[rows, q // 4, :], start=True, stop=True)

    m.spread_of = spread_of
    with m.block() as block:
        order = [(c, q) for c in range(NC) for q in (0, 1, 3, 4, 2, 7)]
        on_act = [q in (0, 1) for c, q in order]

        @block.tensor
        def _(pe):
            for i, (c, q) in enumerate(order):
                if i >= 8:
                    n = sum(on_act[:i - 7])
                    pe.wait_ge(*(taken_a.at(n) if on_act[i - 8] else taken_v.at(i - 7 - n)))
                spread_of(pe, i % 8, q, c).then_inc(*spread.up())

        @block.scalar
        def _(act):
            for i, (c, q) in enumerate(order):
                if on_act[i]:
                    act.wait_ge(*spread.at(i + 1))
                    act.activation((a11, a12)[q][:, c, :], ps[:, i % 8, :], ACT.Copy).then_inc(*taken_a.up())

        @block.vector
        def _(dve):
            step = Chain(dve, step_s)
            for i, (c, q) in enumerate(order):
                if on_act[i]:
                    continue
                dve.wait_ge(*spread.at(i + 1))
                if q == 2:
                    dve.wait_ge(*taken_v.at(4 * c + 2))
                    for half in range(2):
                        ins = dve.tensor_tensor(kb[:, half, c, :], ps[:, i % 8, :], key[:, half, c, :], ALU.mult)
                elif q == 7:
                    ins = dve.tensor_tensor(va[:, c, :], ps[:, i % 8, :], u[:, c, :], ALU.mult)
                else:
                    ins = dve.tensor_tensor(key[:, q - 3, c, :], ps[:, i % 8, :], key[:, q - 3, c, :], ALU.mult)
                ins.then_inc(*taken_v.up())


def L1_scan(m, va, key, kb, a11, a12):
    NC = 8
    CB = NC * B
    step_s = m.sig("scan_step")
    over = lambda a: a.rearrange("p c (b s) -> p (c b) s", b=B)
    v, A, A2 = over(va[:]), over(a11[:]), over(a12[:])
    K = key[:].rearrange("p w c (b s) -> p w (c b) s", b=B)
    KB = kb[:].rearrange("p w c (b s) -> p w (c b) s", b=B)
    with m.local(t1=[P, 2, CB], t2=[P, 2, CB], r=[P, 2, CB], e=[P, CB], st=[P, 2, CB]) as (t1, t2, r, e, st), m.block() as block:
        @block.vector
        def _(dve):
            first = Chain(dve, step_s)
            for half in range(2):
                ins = dve.tensor_tensor(st[:, half, :], KB[:, half, :, 0], v[:, :, 0], ALU.mult)
            first(ins)
            step_s.base = step_s.made
            dve.tensor_copy(K[:, :, :, 0], st[:])
            with dve.Fori(1, S) as t:
                Signal.times = S - 1
                step = Chain(dve, step_s, t - 1, 7)
                two = lambda a: a.unsqueeze(1).to_broadcast([P, 2, CB])
                now = bass.ds(t, 1)
                sq = lambda x: x.rearrange("p c o -> p (c o)")
                sq2 = lambda x: x.rearrange("p w c o -> p w (c o)")
                dve.tensor_tensor(t1[:], two(sq(A[:, :, now])), st[:], ALU.mult)
                step(dve.tensor_tensor(t2[:], two(sq(A2[:, :, now])), st[:], ALU.mult))
                dve.tensor_tensor(r[:, 0, :], t1[:, 0, :], t2[:, 1, :], ALU.add)
                step(dve.tensor_tensor(r[:, 1, :], t1[:, 1, :], t2[:, 0, :], ALU.subtract))
                step(dve.tensor_tensor(t1[:], r[:], sq2(K[:, :, :, now]), ALU.mult))
                step(dve.tensor_tensor(e[:], sq(v[:, :, now]), t1[:, 0, :], ALU.subtract))
                step(dve.tensor_tensor(e[:], e[:], t1[:, 1, :], ALU.subtract))
                step(dve.tensor_tensor(t2[:], two(e[:]), sq2(KB[:, :, :, now]), ALU.mult))
                dve.tensor_tensor(sq2(K[:, :, :, now]), r[:], t2[:], ALU.add)
                step(dve.tensor_tensor(st[:], r[:], t2[:], ALU.add))
                step.end()
                Signal.times = 1


def L1_readout(m, y, u, state, kb, a11, a12, W, vecs, inb):
    d, NC, DI = m.d, 8, 1024
    ps = m.ps
    s = m.sig
    QB = [kb[:, 0], kb[:, 1], a12[:]]
    q_landed = [s("q_landed0"), s("q_landed1"), s("q_landed2")]
    q_done, q_taken, step_s = s("q_product"), s("q_taken"), s("readout_step")
    tmp = a11
    with m.block() as block:
        pieces = [(w, half) for w in range(2) for half in range(2)]

        @block.sync
        def _(sp):
            for i, (w, half) in enumerate(pieces):
                if i == 3:
                    sp.wait_ge(*q_done.at(4))
                sp.dma_start(QB[i % 3], d["L1_attn_Q_W"][w, half]).then_inc(*q_landed[i % 3].up(16))

        @block.tensor
        def _(pe):
            for i, (w, half) in enumerate(pieces):
                pe.wait_ge(*q_landed[i % 3].at(16 * (i // 3 + 1)))
                for j in range(4):
                    n = 4 * i + j
                    if n >= 2:
                        pe.wait_ge(*q_taken.at(n - 1))
                    for k in range(NC):
                        pe.matmul(ps[:, n % 2, :], QB[i % 3][:, k, j * P:(j + 1) * P], u[:, k, :],
                                  start=(k == 0), stop=(k == NC - 1))
                    m.spread_of(pe, 2 + n % 2, 5 + w, 4 * half + j).then_inc(*q_done.up())

        @block.vector
        def _(dve):
            step = Chain(dve, step_s)
            for i, (w, half) in enumerate(pieces):
                for j in range(4):
                    n, c = 4 * i + j, 4 * half + j
                    dve.wait_ge(*q_done.at(n + 1))
                    step(dve.tensor_tensor(tmp[:, 0, :], ps[:, n % 2, :], state[:, w, c, :], ALU.mult))
                    dst = y[:, c, :] if w == 0 else tmp[:, 0, :]
                    ins = dve.tensor_tensor(dst, ps[:, 2 + n % 2, :], tmp[:, 0, :], ALU.mult)
                    ins.then_inc(*q_taken.up())
                    dve.wait_ge(*q_taken.at(n + 1))
                    if w == 1:
                        step(dve.tensor_tensor(y[:, c, :], y[:, c, :], tmp[:, 0, :], ALU.add))
    linear_features(m, [(a11, d["L1_attn_in_z"], kb[:, 0].rearrange("p c n -> p (c n)").rearrange("p (k n) -> p k n", k=C),
                         m.yT, inb[:, 3 * NC:4 * NC], ACT.Silu)])
    summed, meaned, squared, ready, rooted = s("group_summed"), s("group_mean"), s("group_squared"), s("group_var_ready"), s("group_rstd")
    CB = NC * B
    wide = lambda a: a.unsqueeze(2).to_broadcast([P, CB, S])
    Y = y[:].rearrange("p c (b s) -> p (c b) s", b=B)
    SQ = a12[:].rearrange("p c (b s) -> p (c b) s", b=B)
    with m.local(mean=[P, P], one=[P, CB], half_=[P, CB]) as (mean, one, half_):
        load(m, (mean[:], d["head_mean"]))
        with m.block() as block:
            @block.tensor
            def _(pe):
                for i in range(2):
                    pe.wait_ge(*summed.at(i + 1))
                    pe.matmul(ps[:, i, 0:CB], mean[:], one[:], start=True, stop=True).then_inc(*meaned.up())

            @block.gpsimd
            def _(pool):
                step = Chain(pool, m.sig("readout_pool_step"))
                step(pool.memset(half_[:], -0.5))
                pool.wait_ge(*ready.at(1))
                pool.tensor_tensor(one[:], one[:], half_[:], ALU.pow).then_inc(*rooted.up())

            @block.scalar
            def _(act):
                act.wait_ge(*squared.at(1))
                act.activation(a12[:], y[:], ACT.Square).then_inc(*squared.up())

            @block.vector
            def _(dve):
                step = Chain(dve, step_s)
                dve.tensor_reduce(one[:], Y, X, ALU.add).then_inc(*summed.up())
                dve.wait_ge(*meaned.at(1))
                dve.tensor_tensor(Y, Y, ps[:, 0, 0:CB].unsqueeze(2).to_broadcast([P, CB, S]), ALU.subtract)\
                   .then_inc(*squared.up())
                dve.wait_ge(*squared.at(2))
                dve.tensor_reduce(one[:], SQ, X, ALU.add).then_inc(*summed.up())
                dve.wait_ge(*meaned.at(2))
                dve.tensor_scalar(one[:], ps[:, 1, 0:CB], 1e-5, None, ALU.add).then_inc(*ready.up())
                dve.wait_ge(*rooted.at(1))
                step(dve.tensor_tensor(Y, Y, wide(one[:]), ALU.mult))
                for c in range(NC):
                    ins = dve.tensor_scalar(y[:, c, :], y[:, c, :], vecs[:, 1, c:c + 1], vecs[:, 2, c:c + 1],
                                            ALU.mult, ALU.add)
                step(ins)
                for c in range(NC):
                    ins = dve.tensor_tensor(y[:, c, :], y[:, c, :], a11[:, c, :], ALU.mult)
                step(ins)
                for c in range(NC):
                    ins = dve.scalar_tensor_tensor(y[:, c, :], u[:, c, :], vecs[:, 3, c:c + 1], y[:, c, :],
                                                   ALU.mult, ALU.add)


STAGES = (L0_xattn, L0_attn, L0_ffn, L1_xattn, L1_attn, L1_ffn,
          L2_xattn, L2_attn, L2_ffn, L3_xattn, L3_attn, L3_ffn)


def perceiver_program(nc, d, out, stages=STAGES):
    with ExitStack() as ctx:
        m = Machine(nc, ctx, d)
        constants(m)
        for stage in stages:
            stage(m)
            m.stage_done()
        stored = m.sig("stored")
        with m.block() as block:
            @block.sync
            def _(sp):
                sp.dma_start(out, m.x[:]).then_inc(*stored.up(16))
                sp.wait_ge(*stored.at(16))


def _lay_out(inputs):
    def rows(w):
        w = np.asarray(w)
        return np.ascontiguousarray(w.reshape(w.shape[0] // P, P, w.shape[1]).transpose(1, 0, 2))

    def cols(v):
        v = np.asarray(v)
        return np.ascontiguousarray(v.reshape(-1, P).T)

    def by_groups_up(w):
        return np.ascontiguousarray(w.reshape(-1, C, P, 4, w.shape[2] // 4).transpose(0, 3, 2, 1, 4))

    def by_groups_down(w):
        return np.ascontiguousarray(w.reshape(w.shape[0], 4, -1, P, D).transpose(0, 1, 3, 2, 4))

    g = {k: np.asarray(v) for k, v in inputs.items()}
    a = {"x": np.ascontiguousarray(g["x"].reshape(T, P, D).transpose(1, 0, 2)),
         "ctx": np.ascontiguousarray(g["ctx_1024"].reshape(B, KC, P, D).transpose(0, 2, 1, 3)),
         "ctxT": np.ascontiguousarray(g["ctx_1024"].transpose(0, 2, 1).reshape(B, C, P, SK).transpose(0, 2, 1, 3)),
         "mask": g["mask_BxSxS2_ff0"]}
    for L in ("L0_xattn", "L3_xattn"):
        t = (lambda w: w.T) if L == "L0_xattn" else (lambda w: w)
        for n in ("Wq", "Wk", "Wv", "Wo"):
            a[f"{L}_{n}"] = rows(t(g[f"{L}_{n}"]))
        a[f"{L}_bq"], a[f"{L}_bk"] = cols(g[f"{L}_bq"]), cols(g[f"{L}_bk"])
        a[f"{L}_bv"], a[f"{L}_bo"] = g[f"{L}_bv"], g[f"{L}_bo"]
    for i, n in enumerate("qkv"):
        a[f"L0_attn_w_{n}"] = rows(g["L0_attn_w_qkv"][i * D:(i + 1) * D].T)
    a["L0_attn_w_proj"] = rows(g["L0_attn_w_proj"].T)
    q, k = np.arange(P)[:, None] % S, np.arange(S)[None, :]
    seen = (k <= q).astype(np.float32)
    a["causal"] = np.stack([seen, (seen - 1) * np.float32(100)], 1)
    for n in (4, 8):
        a[f"before{n}"] = np.tril(np.ones((n, n), np.float32), -1)
    a["L0_ffn_ln_scale"], a["L0_ffn_ln_bias"] = cols(g["L0_ffn_ln_scale"]), cols(g["L0_ffn_ln_bias"])
    a["L0_ffn_gate_w"] = rows(g["L0_ffn_gate_w"].T)
    for n in ("Wg", "Wu", "Wd"):
        a[f"L0_ffn_{n}"] = np.stack([rows(w) for w in g[f"L0_ffn_{n}"]] + [rows(g[f"L0_ffn_s{n}"])])
    for n in ("Wq", "Wk", "Wv", "Wo"):
        a[f"L1_xattn_{n}"] = rows(g[f"L1_xattn_{n}"])
    for n in ("pre_g", "pre_b", "ln_g", "ln_b"):
        a[f"L1_xattn_{n}"] = cols(g[f"L1_xattn_{n}"])
    a["L1_xattn_ln_g_row"], a["L1_xattn_ln_b_row"] = g["L1_xattn_ln_g"], g["L1_xattn_ln_b"]
    a["L1_ffn_gate_W"], a["L1_ffn_gate_b"] = rows(g["L1_ffn_gate_W"]), g["L1_ffn_gate_b"]
    for n in ("W1", "W2"):
        a[f"L1_ffn_{n}"] = np.stack([rows(w) for w in g[f"L1_ffn_{n}"]])
    for n in ("b1", "b2", "g2", "be2"):
        a[f"L1_ffn_{n}"] = g[f"L1_ffn_{n}"]
    for n in ("g1", "be1"):
        a[f"L1_ffn_{n}"] = np.ascontiguousarray(g[f"L1_ffn_{n}"].reshape(4, C, P).transpose(2, 0, 1))
    a["L2_xattn_Wq"], a["L2_xattn_Wk"] = rows(g["L2_xattn_Wq"].T), rows(g["L2_xattn_Wk"])
    a["L2_xattn_Wv"], a["L2_xattn_bv"] = rows(g["L2_xattn_Wv"].T), g["L2_xattn_bv"]
    a["L2_xattn_bq"], a["L2_xattn_bk"] = cols(g["L2_xattn_bq"]), cols(g["L2_xattn_bk"])
    for i in range(2):
        for n in ("ln1_g", "ln1_b", "bq", "bk", "ln2_g", "ln2_b", "b1"):
            a[f"L2_attn_{n}_{i}"] = cols(g[f"L2_attn_{n}"][i])
        for n in ("bv", "bo", "b2"):
            a[f"L2_attn_{n}_{i}"] = np.ascontiguousarray(g[f"L2_attn_{n}"][i])
        for n in ("wq", "wk", "wv", "wo", "w1", "w2"):
            a[f"L2_attn_{n}_{i}"] = rows(g[f"L2_attn_{n}"][i])
    a["L2_attn_lnf_g"], a["L2_attn_lnf_b"] = g["L2_attn_lnf_g"], g["L2_attn_lnf_b"]
    seen = ((q % 3 != 0) | (k <= q)).astype(np.float32)
    a["strided"] = np.stack([seen, (seen - 1) * np.float32(1e30)], 1)
    for n in ("g1", "beta1", "bq", "bk", "g2", "beta2", "b1"):
        a[f"L3_attn_{n}"] = cols(g[f"L3_attn_{n}"])
    for n in ("bv", "bo", "b2"):
        a[f"L3_attn_{n}"] = g[f"L3_attn_{n}"]
    for n in ("Wq", "Wk", "Wv", "Wo", "W1", "W2"):
        a[f"L3_attn_{n}"] = rows(g[f"L3_attn_{n}"])
    hd = 32
    freq = np.float32(1) / np.float32(10000) ** (np.arange(0, hd, 2, dtype=np.float32) / np.float32(hd))
    angle = freq[(np.arange(P) % hd) // 2][:, None] * np.arange(S, dtype=np.float32)[None, :]
    a["rope_trig"] = np.stack([np.cos(angle), np.sin(angle)], 1).astype(np.float32)
    turn_pairs = np.zeros((P, P), np.float32)
    for i in range(0, P, 2):
        turn_pairs[i + 1, i], turn_pairs[i, i + 1] = -1, 1
    a["rope_turn"] = turn_pairs
    NC, H = 8, 32
    w, b = g["L1_attn_in_proj_W"], g["L1_attn_in_proj_b"]
    part = {"z": slice(0, 1024), "K0": slice(1024, 3072, 2), "K1": slice(1025, 3072, 2), "V": slice(3072, 4096)}
    for n, r in part.items():
        a[f"L1_attn_in_{n}"] = rows(w[r].T)
    a["L1_attn_in_proj_b"] = np.concatenate([cols(b[part[n]]) for n in ("V", "K0", "K1", "z")], 1)
    for n in ("conv_b", "gn_w", "gn_b", "D", "rms_w"):
        a[f"L1_attn_{n}"] = cols(g[f"L1_attn_{n}"])
    a["L1_attn_conv_w"] = np.ascontiguousarray(g["L1_attn_conv_w"].reshape(NC, P, 4).transpose(1, 0, 2))
    L = "L1_attn_"
    small = [g[L + "dyn_W"], g[L + "seldt_W"], g[L + "beta_W"], g[L + "rg_W"], g[L + "ug_W"], g[L + "selB_W"][0::2],
             g[L + "selB_W"][1::2], g[L + "selC_W"][0::2], g[L + "selC_W"][1::2]]
    a["L1_attn_small_W"] = rows(np.concatenate(small, 0).T)
    none = np.zeros(H, np.float32)
    a["L1_attn_small_b"] = np.concatenate([g[L + "dyn_b"], none, g[L + "beta_b"], g[L + "rg_b"], g[L + "ug_b"],
                                           none, none, none, none])
    a["L1_attn_dt_c"] = g["L1_attn_dt_c"]
    rate = np.float32(1) / np.float32(10000) ** (np.arange(H, dtype=np.float32) / np.float32(H))
    a["rope_rate"] = (np.arange(P) % S).astype(np.float32)[:, None] * rate[None, :]
    r, c, p = np.arange(P)[:, None, None], np.arange(NC)[None, :, None], np.arange(P)[None, None, :]
    a["head_spread"] = (r % H == 4 * c + p // 32).astype(np.float32)
    a["head_mean"] = (np.arange(P)[:, None] // 32 == np.arange(P)[None, :] // 32).astype(np.float32) / np.float32(32 * S)
    Q = np.stack([g["L1_attn_Q_W"][0::2], g["L1_attn_Q_W"][1::2]])
    a["L1_attn_Q_W"] = np.stack([np.stack([rows(Q[i, h * 512:(h + 1) * 512].T) for h in range(2)]) for i in range(2)])
    a["L1_attn_out_W"] = rows(g["L1_attn_out_W"].T)
    E2, F2 = 8, 2048
    a["L2_ffn_Wg"] = rows(g["L2_ffn_Wg"])
    tok = np.arange(P)
    a["earlier"] = ((tok[:, None] < tok[None, :]) & (tok[:, None] // S == tok[None, :] // S)).astype(np.float32)
    a["place"] = np.arange(S // E2, dtype=np.float32)
    a["L2_ffn_W1"] = by_groups_up(g["L2_ffn_W1"])
    a["L2_ffn_W2"] = by_groups_down(g["L2_ffn_W2"])
    a["L3_ffn_gate_w"], a["L3_ffn_gate_b"] = rows(g["L3_ffn_gate_w"].T), g["L3_ffn_gate_b"]
    w1, w2 = g["L3_ffn_w1"], g["L3_ffn_w2"]
    a["L3_ffn_w1"] = np.ascontiguousarray(w1[:, :D].reshape(-1, C, P, F2))
    a["L3_ffn_w2"] = np.ascontiguousarray(w2[:, :F2].reshape(-1, 4, 4, P, D).transpose(0, 2, 3, 1, 4))
    a["L3_ffn_b1"] = np.ascontiguousarray(w1[:, D].reshape(-1, 4, 4, P).transpose(3, 0, 2, 1).reshape(P, -1, F2 // P))
    a["fold_quarters"] = (np.arange(P)[:, None] % 32 == np.arange(B)[None, :]).astype(np.float32)
    a["L3_ffn_b2"] = np.ascontiguousarray(w2[:, F2].reshape(-1, C, P).transpose(2, 0, 1))
    return a


def kernel(**inputs):
    import concourse.bacc as bacc
    from concourse.bass_utils import run_bass_kernel_spmd

    nc = bacc.Bacc("TRN2", target_bir_lowering=False, num_devices=1)
    arrays = {f"in_{k}": v for k, v in _lay_out(inputs).items()}
    d = {k[3:]: nc.dram_tensor(k, v.shape, mybir.dt.from_np(v.dtype), kind="ExternalInput").ap()
         for k, v in arrays.items()}
    out = nc.dram_tensor("out", (B, S, D), F32, kind="ExternalOutput").ap()
    perceiver_program(nc, d, out.rearrange("(t two) s d -> (two s) t d", two=2))
    r = run_bass_kernel_spmd(nc, [arrays], core_ids=[0])
    return r.results[0]["out"]
```

```python
from contextlib import ExitStack, contextmanager

import numpy as np

import concourse.bass as bass
from concourse import mybir

F32 = mybir.dt.float32
ACT = mybir.ActivationFunctionType
ALU = mybir.AluOpType
X = mybir.AxisListType.X

P = 128
B, S, D = 8, 64, 512
N = B * S
T = N // P
C = D // P
SK = 512
KC = SK // P


class Signal:

    times = 1

    def __init__(self, sem):
        self.sem, self.made, self.base = sem, 0, 0

    def up(self, n=1):
        self.made += n * Signal.times
        return self.sem, n

    def at(self, n):
        return self.sem, self.base + n


@contextmanager
def repeat(eng, n):
    with eng.Fori(0, n) as i:
        Signal.times = n
        yield i
        Signal.times = 1


class Chain:

    def __init__(self, eng, steps, i=0, per=0):
        self.eng, self.steps, self.i, self.per = eng, steps, i, per
        self.start = steps.made
        self.n = 0

    def __call__(self, ins):
        ins.then_inc(*self.steps.up())
        self.n += 1
        self.eng.wait_ge(self.steps.sem, self.start + self.n + (self.i * self.per if self.per else 0))

    def end(self):
        assert not self.per or self.n == self.per, (self.n, self.per)


class Machine:

    def __init__(self, nc, ctx, d):
        self.nc, self.ctx, self.d = nc, ctx, d
        self.marks, self.idle = {}, []
        self.count = 0
        self.x = self.sb("x_tokens", [P, T, D])
        self.y = self.sb("normed_tokens", [P, T, D])
        self.yT = self.sb("normed_features", [P, C, N])
        self.ident = self.sb("identity", [P, P])
        self.ones = self.sb("ones_row", [1, P])
        self.minus_half = self.sb("minus_half", [P, T])
        self.stats = self.sb("stats", [P, T, 6])
        self.mv = self.sb("mean_var", [P, T, 2])
        self.den = self.sb("var_eps", [P, T])
        self.rstd = self.sb("rstd", [P, T])
        self.ps = ctx.enter_context(nc.psum_tensor("banks", [P, 8, 512], F32))

    def sb(self, name, shape):
        return self.ctx.enter_context(self.nc.sbuf_tensor(name, shape, F32))

    @contextmanager
    def local(self, **shapes):
        with ExitStack() as s:
            self.count += 1
            yield [s.enter_context(self.nc.sbuf_tensor(f"{n}_{self.count}", sh, F32)) for n, sh in shapes.items()]

    def sig(self, name):
        if name not in self.marks:
            if not self.idle:
                self.count += 1
                self.idle.append(Signal(self.ctx.enter_context(self.nc.semaphore(f"{name}_{self.count}"))))
            s = self.idle.pop()
            s.base = s.made
            self.marks[name] = s
        return self.marks[name]

    def stage_done(self):
        self.idle += self.marks.values()
        self.marks = {}

    @contextmanager
    def block(self, *credits):
        for s in self.marks.values():
            s.base = s.made
        if credits:
            with self.nc.Block() as b:
                @b.gpsimd
                def _(pool):
                    for signal, n in credits:
                        pool.sem_inc(*signal.up(n))
        with self.nc.Block() as b:
            yield b


def constants(m):
    made, x_landed = m.sig("constants_made"), m.sig("x_landed")
    with m.block() as block:
        @block.gpsimd
        def _(pool):
            step = Chain(pool, made)
            step(pool.memset(m.ident[:], 0.0))
            step(pool.affine_select(out=m.ident[:], in_=m.ident[:], compare_op=ALU.not_equal, fill=1.0,
                                    base=0, pattern=[[-1, P]], channel_multiplier=1))
            step(pool.memset(m.ones[:], 1.0))
            step(pool.memset(m.minus_half[:], -0.5))

        @block.sync
        def _(sp):
            sp.dma_start(m.x[:], m.d["x"]).then_inc(*x_landed.up(16))
            sp.wait_ge(*x_landed.at(16))


def start_loads(sp, ahead):
    for signal, *pairs in (ahead if isinstance(ahead, list) else [ahead] if ahead else []):
        for dst, src in pairs:
            sp.dma_start(dst, src).then_inc(*signal.up(16))


def send(block, ahead):
    if ahead:
        @block.sync
        def _(sp):
            start_loads(sp, ahead)


def normalise(m, dst, src, eps, rms=False, dstT=None, scale=None, bias=None, ahead=None, vectors=None):
    summed, ready, rooted = m.sig("moments_step"), m.sig("variance_ready"), m.sig("rstd_ready")
    normed, turned = m.sig("tile_normed"), m.sig("turned")
    with m.block() as block:
        send(block, ahead)
        landed = (vectors.sem, vectors.made) if vectors else None

        def take(eng, c):
            eng.wait_ge(*turned.at(c + 1))
            if eng is m.nc.scalar:
                m.nc.scalar.activation(dstT[:, c, :], m.ps[:, c, :], ACT.Identity,
                                       bias=0.0 if bias is None else bias[:, c:c + 1],
                                       scale=1.0 if scale is None else scale[:, c:c + 1])
            elif scale is None:
                eng.tensor_copy(dstT[:, c, :], m.ps[:, c, :])
            elif bias is None:
                eng.tensor_scalar(dstT[:, c, :], m.ps[:, c, :], scale[:, c:c + 1], None, ALU.mult)
            else:
                eng.tensor_scalar(dstT[:, c, :], m.ps[:, c, :], scale[:, c:c + 1], bias[:, c:c + 1],
                                  ALU.mult, ALU.add)

        @block.vector
        def _(dve):
            step = Chain(dve, summed)
            for t in range(T):
                ins = dve.bn_stats(m.stats[:, t, :], src[:, t, :])
            step(ins)
            for t in range(T):
                ins = dve.bn_aggr(m.mv[:, t, :], m.stats[:, t, :])
            step(ins)
            if rms:
                step(dve.tensor_tensor(m.den[:], m.mv[:, :, 0], m.mv[:, :, 0], ALU.mult))
                step(dve.tensor_tensor(m.den[:], m.den[:], m.mv[:, :, 1], ALU.add))
                dve.tensor_scalar(m.den[:], m.den[:], eps, None, ALU.add).then_inc(*ready.up())
            else:
                dve.tensor_scalar(m.den[:], m.mv[:, :, 1], eps, None, ALU.add).then_inc(*ready.up())
            dve.wait_ge(*rooted.at(1))
            for t in range(T):
                if rms:
                    ins = dve.tensor_scalar(dst[:, t, :], src[:, t, :], m.rstd[:, t:t + 1], None, ALU.mult)
                else:
                    ins = dve.tensor_scalar(dst[:, t, :], src[:, t, :], m.mv[:, t, 0:1], m.rstd[:, t:t + 1],
                                            ALU.subtract, ALU.mult)
                if dstT is not None:
                    ins.then_inc(*normed.up())
            if dstT is not None:
                if landed:
                    dve.wait_ge(*landed)
                for c in range(1, C, 2):
                    take(dve, c)

        @block.gpsimd
        def _(pool):
            pool.wait_ge(*ready.at(1))
            pool.tensor_tensor(m.rstd[:], m.den[:], m.minus_half[:], ALU.pow).then_inc(*rooted.up())

        if dstT is not None:
            @block.tensor
            def _(pe):
                for c in range(C):
                    for t in range(T):
                        if c == 0:
                            pe.wait_ge(*normed.at(t + 1))
                        ins = pe.transpose(m.ps[:, c, t * P:(t + 1) * P], dst[:, t, c * P:(c + 1) * P], m.ident[:])
                    ins.then_inc(*turned.up())

            @block.scalar
            def _(act):
                if landed:
                    act.wait_ge(*landed)
                for c in range(0, C, 2):
                    take(act, c)


def linear_features(m, outs, kchunks=C, sent=None, ahead=None, beside=None):
    landed = [m.sig(f"weights_landed_{i}") for i in range(len(outs))]
    product, taken_a, taken_v = m.sig("features_product"), m.sig("features_taken_act"), m.sig("features_taken_dve")
    work = [(o, mm) for o in range(len(outs)) for mm in range(outs[o][2].shape[2] // P)]
    on_act = [beside is not None or outs[o][5] != ACT.Identity or n % 2 == 0 for n, (o, mm) in enumerate(work)]
    with m.block() as block:
        first = (sent.sem, sent.made) if sent else landed[0].at(16)

        @block.sync
        def _(sp):
            for o, (_, w, buf, _, _, _) in enumerate(outs):
                if o or not sent:
                    sp.dma_start(buf[:], w).then_inc(*landed[o].up(16))
            start_loads(sp, ahead)

        @block.tensor
        def _(pe):
            for n, (o, mm) in enumerate(work):
                _, _, buf, srcT, _, _ = outs[o]
                if mm == 0:
                    pe.wait_ge(*(landed[o].at(16) if o else first))
                if n >= 4:
                    a = sum(on_act[:n - 3])
                    s = taken_a if on_act[n - 4] else taken_v
                    pe.wait_ge(*s.at(a if on_act[n - 4] else n - 3 - a))
                for k in range(kchunks):
                    ins = pe.matmul(m.ps[:, n % 4, :], buf[:, k, mm * P:(mm + 1) * P], srcT[:, k, :],
                                    start=(k == 0), stop=(k == kchunks - 1))
                ins.then_inc(*product.up())

        def take(eng, mine, signal):
            for n, (o, mm) in enumerate(work):
                if on_act[n] != mine:
                    continue
                dstT, _, _, _, bias, f = outs[o]
                eng.wait_ge(*product.at(n + 1))
                if mine:
                    eng.activation(dstT[:, mm, :], m.ps[:, n % 4, :], f,
                                   bias=0.0 if bias is None else bias[:, mm:mm + 1]).then_inc(*signal.up())
                    if beside:
                        beside[1](eng, n)
                elif bias is None:
                    eng.tensor_copy(dstT[:, mm, :], m.ps[:, n % 4, :]).then_inc(*signal.up())
                else:
                    eng.tensor_scalar(dstT[:, mm, :], m.ps[:, n % 4, :], bias[:, mm:mm + 1], None,
                                      ALU.add).then_inc(*signal.up())

        @block.scalar
        def _(act):
            take(act, True, taken_a)

        @block.vector
        def _(dve):
            if beside:
                beside[0](dve)
            take(dve, False, taken_v)


def linear_tokens(m, dst, srcT, w, buf, kchunks, brow=None, add=None, sent=None, ahead=None):
    landed, product = m.sig("weights_landed_0"), m.sig("tokens_product")
    with m.block() as block:
        there = (sent.sem, sent.made) if sent else landed.at(16)

        @block.sync
        def _(sp):
            if not sent:
                sp.dma_start(buf[:], w).then_inc(*landed.up(16))
            start_loads(sp, ahead)

        @block.tensor
        def _(pe):
            pe.wait_ge(*there)
            for t in range(T):
                for k in range(kchunks):
                    ins = pe.matmul(m.ps[:, t, :], srcT[:, k, t * P:(t + 1) * P], buf[:, k, :],
                                    start=(k == 0), stop=(k == kchunks - 1))
                ins.then_inc(*product.up())

        @block.vector
        def _(dve):
            step = Chain(dve, m.sig("tokens_step"))
            if brow is not None and add is not None:
                dve.wait_ge(*there)
                for t in range(T):
                    ins = dve.tensor_tensor(dst[:, t, :], add[:, t, :], brow[:, t, :] if brow is m.y else brow, ALU.add)
                step(ins)
            for t in range(T):
                dve.wait_ge(*product.at(t + 1))
                if add is not None:
                    dve.tensor_tensor(dst[:, t, :], m.ps[:, t, :], (add if brow is None else dst)[:, t, :], ALU.add)
                elif brow is not None:
                    dve.tensor_tensor(dst[:, t, :], m.ps[:, t, :], brow, ALU.add)
                else:
                    dve.tensor_copy(dst[:, t, :], m.ps[:, t, :])


def add_into(m, dst, a, b):
    with m.block() as block:
        @block.vector
        def _(dve):
            for t in range(T):
                dve.tensor_tensor(dst[:, t, :], a[:, t, :], b[:, t, :], ALU.add)




def first_loads(m, wkb, wvb, ctxT, wk, wv):
    return [(m.sig("ctx_landed0"), (ctxT[:, 0], m.d["ctxT"][0])), (m.sig("xw_landed"), (wkb[:], wk), (wvb[:], wv))]


def cross_attention(m, oT, qT, hd, scale, wkb, wvb, ctxT, kbias=None, vbias=None, mask=None, clip=None, knorm=None,
                    ahead=None):
    J = D // hd // 2
    JC = J // C
    G = P // hd
    R = 4
    UN = C + KC
    U = UN // J
    s = m.sig
    w_landed, ctx_landed, tok_landed = s("xw_landed"), [s("ctx_landed0"), s("ctx_landed1")], s("ctxtok_landed")
    mask_landed = [s("mask_landed0"), s("mask_landed1")]
    projected, k_taken, v_taken, q_spread = s("kv_projected"), s("k_taken"), s("v_taken"), s("q_spread")
    scored, max_ready, exp_done, inverted, scaled = s("scored"), s("max_ready"), s("probs_exp"), s("sum_inverted"), s("probs_scaled")
    turned, turned_taken, attended, o_taken = s("probs_turned"), s("probs_turned_taken"), s("attended"), s("attended_taken")
    vstep, k_turned, kn_ready, kn_taken = s("xattn_step"), s("ctx_turned"), s("ctx_normed"), s("ctx_turned_taken")
    var_ready, rooted, zeroed = s("ctx_var"), s("ctx_rstd"), s("q_zeroed")
    pre = mask is not None or clip is not None
    few = 1 if not (mask is not None or knorm) else C
    with m.local(kT=[P, 2, C, SK], v=[P, 2, KC, D], q2=[P, 2, J, P],
                 pr=[P, R, SK], prT=[P, 2, KC, P], sc=[P, 2, SK], col=[P, 2, J, 4],
                 extra=[P, few, SK], extraT=[P, C if knorm else 1, SK]) as \
            (kT, v, q2, pr, prT, sc, col, extra, extraT), \
            m.block((o_taken, 1), (turned_taken, 2)) as block:
        ps = m.ps

        def run(eng, body, per=0):
            with repeat(eng, B // 2 - 1) as i:
                step = Chain(eng, vstep, i, per) if per else None
                body(2 * i, 0, False, step)
                body(2 * i + 1, 1, False, step)
                if per:
                    step.end()
            step = Chain(eng, vstep) if per else None
            body(B - 2, 0, True, step)
            body(B - 1, 1, True, step)

        @block.sync
        def _(sp):
            if knorm:
                sp.dma_start(extra[:], m.d["ctx"][0]).then_inc(*tok_landed.up(16))
            sp.dma_start(ctxT[:, 1], m.d["ctxT"][1]).then_inc(*ctx_landed[1].up(16))
            start_loads(sp, ahead)
            if knorm:
                sp.wait_ge(*k_turned.at(C))
                sp.dma_start(extra[:], m.d["ctx"][1]).then_inc(*tok_landed.up(16))

            def load_mask(b, par):
                for half in range(2):
                    sp.dma_start(extra[64 * half:64 * half + 64, par, :], mask[b]).then_inc(*mask_landed[par].up(16))

            if mask is not None:
                load_mask(0, 0)

            def body(b, par, last, _):
                if mask is not None and not (last and par == 1):
                    sp.wait_ge(*max_ready.at(J * b + 1))
                    load_mask(b + 1, 1 - par)
                if not last:
                    sp.wait_ge(*projected.at(UN * b + UN))
                    sp.dma_start(ctxT[:, par], m.d["ctxT"][b + 2]).then_inc(*ctx_landed[par].up(16))
                    if knorm:
                        sp.wait_ge(*k_turned.at(C * b + 2 * C))
                        sp.dma_start(extra[:], m.d["ctx"][b + 2]).then_inc(*tok_landed.up(16))

            run(sp, body)

        @block.gpsimd
        def _(pool):
            pool.memset(q2[:], 0.0).then_inc(*zeroed.up())
            if knorm:
                with repeat(pool, B) as b:
                    pool.wait_ge(*var_ready.at(b + 1))
                    pool.tensor_tensor(m.rstd[:], m.den[:], m.minus_half[:], ALU.pow).then_inc(*rooted.up())

        @block.tensor
        def _(pe):
            def unit(b, par, u, first=False):
                if u == 0:
                    pe.wait_ge(*(ctx_landed[par].at(8 * b + 8 * par)))
                    if knorm:
                        pe.wait_ge(*kn_taken.at(C * b + C))
                if u < 2:
                    if not first:
                        pe.wait_ge(*v_taken.at(KC * b + u - 1))
                elif u < C + 2:
                    pe.wait_ge(*k_taken.at(C * b + u - 1))
                else:
                    pe.wait_ge(*v_taken.at(KC * b + u - C - 1))
                for k in range(C):
                    if u < C:
                        ins = pe.matmul(ps[:, u % 2, :], wkb[:, k, u * P:(u + 1) * P],
                                        (extraT if knorm else ctxT[:, par])[:, k, :], start=(k == 0), stop=(k == C - 1))
                    else:
                        r = u - C
                        ins = pe.matmul(ps[:, u % 2, :], ctxT[:, par, k, r * P:(r + 1) * P], wvb[:, k, :],
                                        start=(k == 0), stop=(k == C - 1))
                ins.then_inc(*projected.up())

            def turn_context(b, c, first=False):
                if c == 0:
                    pe.wait_ge(*kn_ready.at(b + 1))
                if not (first and c == 0):
                    pe.wait_ge(*kn_taken.at(C * b + c))
                for k in range(KC):
                    ins = pe.transpose(ps[:, 7, k * P:(k + 1) * P], extra[:, k, c * P:(c + 1) * P], m.ident[:])
                ins.then_inc(*k_turned.up())

            def scores(b, par, j, first=False):
                if j == 0:
                    pe.wait_ge(*q_spread.at(b + 1))
                    pe.wait_ge(*k_taken.at(C * b + C))
                if not first:
                    pe.wait_ge(*exp_done.at(J * b + j - 1))
                pe.matmul(ps[:, 2 + j % 2, :], q2[:, par, j, :], kT[:, par, j // JC, :],
                          start=True, stop=True).then_inc(*scored.up())

            if knorm:
                for c in range(C):
                    turn_context(0, c, True)
            pe.wait_ge(*w_landed.at(0))
            for u in range(UN):
                unit(0, 0, u, True)
                if u == C + 1:
                    scores(0, 0, 0, True)
                    scores(0, 0, 1, True)
            if knorm:
                for c in range(C):
                    turn_context(1, c)

            def body(b, par, last, _):
                end = last and par == 1
                for j in range(J):
                    n = J * b + j
                    pe.wait_ge(*scaled.at(n + 1))
                    pe.wait_ge(*turned_taken.at(n + 1))
                    for k in range(KC):
                        ins = pe.transpose(ps[:, 4 + j % 2, k * P:(k + 1) * P], pr[:, j % R, k * P:(k + 1) * P],
                                           m.ident[:])
                    ins.then_inc(*turned.up())
                    if j + 2 < J:
                        scores(b, par, j + 2)
                    elif not end:
                        scores(b + 1, 1 - par, j + 2 - J)
                    if not end:
                        for u in range(U * j, U * j + U):
                            unit(b + 1, 1 - par, u)
                            if knorm and not last and u >= C:
                                turn_context(b + 2, u - C)
                    pe.wait_ge(*turned_taken.at(2 + n + 1))
                    if j == 0:
                        pe.wait_ge(*v_taken.at(KC * b + KC))
                        pe.wait_ge(*o_taken.at(b + 1))
                    c, half, w = j // JC, j % JC, P // JC
                    for k in range(KC):
                        ins = pe.matmul(ps[w * half:w * half + w, 6, c * P:(c + 1) * P],
                                        v[:, par, k, c * P + w * half:c * P + w * half + w], prT[:, j % 2, k, :],
                                        start=(k == 0), stop=(k == KC - 1))
                    ins.then_inc(*attended.up())

            run(pe, body)

        @block.scalar
        def _(act):
            def spread(b, par, first=False):
                if not first:
                    act.wait_ge(*scored.at(J * b - J + 1))
                for h in range(G):
                    rows = slice(hd * h, hd * h + hd)
                    dst = q2[rows, par, :, :].rearrange("p (c j) n -> p c j n", c=C)[:, :, h // 2 if hd == 32 else 0,
                                                                                     (h % 2) * 64:(h % 2) * 64 + 64]
                    src = qT[rows, :, :].rearrange("p c (b n) -> p b c n", b=B)[:, b, :, :]
                    ins = act.activation(dst, src, ACT.Copy)
                ins.then_inc(*q_spread.up())

            def take_k(b, par, u):
                act.wait_ge(*projected.at(UN * b + u + 1))
                act.activation(kT[:, par, u, :], ps[:, u % 2, :], ACT.Identity,
                               bias=0.0 if kbias is None else kbias[:, u:u + 1]).then_inc(*k_taken.up())

            def take_context(b, c, first=False):
                act.wait_ge(*k_turned.at(C * b + c + 1))
                if c == 0 and not first:
                    act.wait_ge(*projected.at(UN * b - UN + C))
                act.activation(extraT[:, c, :], ps[:, 7, :], ACT.Identity, bias=knorm[1][:, c:c + 1],
                               scale=knorm[0][:, c:c + 1]).then_inc(*kn_taken.up())

            def power(b, par, j):
                act.wait_ge(*max_ready.at(J * b + j + 1))
                src = sc[:, j % 2, :] if pre else ps[:, 2 + j % 2, :]
                act.activation(pr[:, j % R, :], src, ACT.Exp, bias=col[:, par, j, 1:2],
                               scale=1.0 if mask is not None else scale,
                               accum_out=col[:, par, j, 2:3]).then_inc(*exp_done.up())

            def divide(b, par, j):
                act.wait_ge(*inverted.at(J * b + j + 1))
                act.activation(pr[:, j % R, :], pr[:, j % R, :], ACT.Copy, scale=col[:, par, j, 3:4])\
                   .then_inc(*scaled.up())

            act.wait_ge(*zeroed.at(1))
            spread(0, 0, True)
            if knorm:
                for c in range(C):
                    take_context(0, c, True)
            for u in range(C):
                take_k(0, 0, u)
            for j in range(2):
                power(0, 0, j)
                divide(0, 0, j)
            if knorm:
                for c in range(C):
                    take_context(1, c)

            def body(b, par, last, _):
                end = last and par == 1
                for j in range(J):
                    if j == 0 and not end:
                        spread(b + 1, 1 - par)
                    if j + 2 < J:
                        power(b, par, j + 2)
                    elif not end:
                        power(b + 1, 1 - par, j + 2 - J)
                    if not end:
                        for u in range(U * j, U * j + U):
                            if u < C:
                                take_k(b + 1, 1 - par, u)
                            elif knorm and not last:
                                take_context(b + 2, u - C)
                    if j + 2 < J:
                        divide(b, par, j + 2)
                    elif not end:
                        divide(b + 1, 1 - par, j + 2 - J)

            run(act, body)

        @block.vector
        def _(dve):
            def norm_context(b, step):
                dve.wait_ge(*tok_landed.at(16 * b + 16))
                for k in range(KC):
                    ins = dve.bn_stats(m.stats[:, k, :], extra[:, k, :])
                step(ins)
                dve.memset(m.den[:], 0.0)
                for k in range(KC):
                    ins = dve.bn_aggr(m.mv[:, k, :], m.stats[:, k, :])
                step(ins)
                dve.tensor_scalar(m.den[:], m.mv[:, :, 1], 1e-5, None, ALU.add).then_inc(*var_ready.up())
                dve.wait_ge(*rooted.at(b + 1))
                for k in range(KC):
                    ins = dve.tensor_scalar(extra[:, k, :], extra[:, k, :], m.mv[:, k, 0:1], m.rstd[:, k:k + 1],
                                            ALU.subtract, ALU.mult)
                ins.then_inc(*kn_ready.up())

            def row_max(b, par, j, step, first=False):
                dve.wait_ge(*scored.at(J * b + j + 1))
                src = ps[:, 2 + j % 2, :]
                if pre and not first:
                    dve.wait_ge(*exp_done.at(J * b + j - 1))
                if mask is not None:
                    dve.wait_ge(*mask_landed[par].at(16 * b + 32 - 16 * par))
                    step(dve.scalar_tensor_tensor(sc[:, j % 2, :], src, scale, extra[:, par, :], ALU.mult, ALU.add))
                if clip is not None:
                    step(dve.tensor_scalar(sc[:, j % 2, :], src, -clip, clip, ALU.max, ALU.min))
                if pre:
                    src = sc[:, j % 2, :]
                step(dve.tensor_reduce(col[:, par, j, 0:1], src, X, ALU.max, negate=True))
                dve.tensor_scalar(col[:, par, j, 1:2], col[:, par, j, 0:1], 1.0 if mask is not None else scale, None,
                                  ALU.mult).then_inc(*max_ready.up())

            def invert(b, par, j):
                dve.wait_ge(*exp_done.at(J * b + j + 1))
                dve.reciprocal(col[:, par, j, 3:4], col[:, par, j, 2:3]).then_inc(*inverted.up())

            def take_v(b, par, r):
                dve.wait_ge(*projected.at(UN * b + C + r + 1))
                if vbias is None:
                    dve.tensor_copy(v[:, par, r, :], ps[:, r % 2, :]).then_inc(*v_taken.up())
                else:
                    dve.tensor_tensor(v[:, par, r, :], ps[:, r % 2, :], vbias, ALU.add).then_inc(*v_taken.up())

            step = Chain(dve, vstep)
            if knorm:
                norm_context(0, step)
            take_v(0, 0, 0)
            take_v(0, 0, 1)
            for j in range(2):
                row_max(0, 0, j, step, True)
                invert(0, 0, j)
            take_v(0, 0, 2)
            take_v(0, 0, 3)
            if knorm:
                norm_context(1, step)

            def body(b, par, last, step):
                end = last and par == 1
                for j in range(J):
                    dve.wait_ge(*turned.at(J * b + j + 1))
                    dve.tensor_copy(prT[:, j % 2, :, :], ps[:, 4 + j % 2, :].rearrange("p (k n) -> p k n", k=KC))\
                       .then_inc(*turned_taken.up())
                    if j + 2 < J:
                        row_max(b, par, j + 2, step)
                    elif not end:
                        row_max(b + 1, 1 - par, j + 2 - J, step)
                    if j == 0 and knorm and not last:
                        norm_context(b + 2, step)
                    if not end:
                        for u in range(U * j, U * j + U):
                            if u >= C:
                                take_v(b + 1, 1 - par, u - C)
                    if j + 2 < J:
                        invert(b, par, j + 2)
                    elif not end:
                        invert(b + 1, 1 - par, j + 2 - J)
                dve.wait_ge(*attended.at(J * b + J))
                for h in range(G):
                    rows = slice(hd * h, hd * h + hd)
                    src = ps[rows, 6, :].rearrange("p (c n) -> p c n", c=C)[:, :, (h % 2) * 64:(h % 2) * 64 + 64]
                    dst = oT[rows, :, :].rearrange("p c (b n) -> p b c n", b=B)[:, b, :, :]
                    ins = dve.tensor_copy(dst, src)
                ins.then_inc(*o_taken.up())

            run(dve, body, 2 * ((2 if pre else 1) * J + (2 if knorm else 0)))


def self_attention(m, oT, qT, kT, v, scale, clip=None, bound=None, custom=False, ahead=None):
    H, hd, R = 16, 32, 4
    s = m.sig
    scored, scores_taken, step_s = s("self_scored"), s("self_scores_taken"), s("self_step")
    centred, powered, inverted, zeroed = s("self_centred"), s("self_exp"), s("self_sum_inverted"), s("self_zeroed")
    probs_ready = s("self_probs_ready")
    turned, turned_taken = s("self_turned"), s("self_turned_taken")
    attended, o_taken = s("self_attended"), s("self_attended_taken")
    with m.local(sc=[P, 3, H, S], bd=[P, 2, H, P], prT=[P, 2, H, P], col=[P, 3, 3, H]) as (sc, bd, prT, col), \
            m.block() as block:
        ps = m.ps
        send(block, ahead)

        @block.gpsimd
        def _(pool):
            pool.memset(bd[:], 0.0).then_inc(*zeroed.up())

        @block.tensor
        def _(pe):
            def scores(t):
                if t >= 1:
                    pe.wait_ge(*scores_taken.at(2 * t))
                for h in range(H):
                    rows = slice(hd * (h % R), hd * (h % R) + hd)
                    ins = pe.matmul(ps[:, h % R, (h // R) * P:(h // R) * P + P],
                                    qT[rows, h // R, t * P:(t + 1) * P], kT[rows, h // R, t * P:(t + 1) * P],
                                    start=True, stop=True)
                ins.then_inc(*scored.up())

            def turn_probs(t):
                pe.wait_ge(*probs_ready.at(t + 1))
                for g in range(R):
                    n = R * t + g
                    if n >= 2:
                        pe.wait_ge(*turned_taken.at(n - 1))
                    for k in range(R):
                        ins = pe.transpose(ps[:, 4 + g % 2, k * P:(k + 1) * P], bd[:, t % 2, R * g + k, :], m.ident[:])
                    ins.then_inc(*turned.up())

            def attend(t):
                pe.wait_ge(*turned_taken.at(R * t + R))
                if t >= 1:
                    pe.wait_ge(*o_taken.at(t))
                for n in range(H):
                    r, c = n // R, n % R
                    h = R * c + r
                    ins = pe.matmul(ps[hd * r:hd * r + hd, 6, c * P:(c + 1) * P], v[:, t, hd * h:hd * h + hd],
                                    prT[:, t % 2, n, :], start=True, stop=True)
                ins.then_inc(*attended.up())

            scores(0)
            scores(1)
            for t in range(T):
                turn_probs(t)
                if t + 2 < T:
                    scores(t + 2)
                    attend(t)
            attend(T - 2)
            attend(T - 1)

        @block.scalar
        def _(act):
            def take_scores(t):
                act.wait_ge(*scored.at(t + 1))
                if t >= 3:
                    act.wait_ge(*probs_ready.at(t - 2))
                for half in range(2):
                    rows = slice(64 * half, 64 * half + 64)
                    src = ps[rows, 0:R, :].rearrange("p r (c n) -> p r c n", c=R)[:, :, :, 64 * half:64 * half + 64]
                    act.activation(sc[rows, t % 3, :, :].rearrange("p (r c) n -> p r c n", r=R), src, ACT.Copy,
                                   scale=scale).then_inc(*scores_taken.up())

            def power(t):
                act.wait_ge(*centred.at(t + 1))
                act.activation(sc[:, t % 3, :, :], sc[:, t % 3, :, :], ACT.Exp).then_inc(*powered.up())

            def take_turned(t):
                for g in range(R):
                    act.wait_ge(*turned.at(R * t + g + 1))
                    if g == 0 and t >= 2:
                        act.wait_ge(*attended.at(t - 1))
                    act.activation(prT[:, t % 2, R * g:R * g + R, :].rearrange("p g n -> p (g n)"), ps[:, 4 + g % 2, :],
                                   ACT.Copy).then_inc(*turned_taken.up())

            take_scores(0)
            power(0)
            for t in range(T):
                if t + 1 < T:
                    take_scores(t + 1)
                take_turned(t)
                if t + 1 < T:
                    power(t + 1)

        @block.vector
        def _(dve):
            step = Chain(dve, step_s)

            def wide(a):
                return a.unsqueeze(2).to_broadcast([P, H, S])

            def rows_of(a):
                return a.unsqueeze(1).to_broadcast([P, H, S])

            def centre(t):
                w = sc[:, t % 3, :, :]
                dve.wait_ge(*scores_taken.at(2 * t + 2))
                if clip is not None:
                    step(dve.scalar_tensor_tensor(w, w, -clip, rows_of(bound), ALU.max, ALU.min))
                elif bound is not None:
                    step(dve.tensor_tensor(w, w, rows_of(bound), ALU.min))
                step(dve.tensor_reduce(col[:, t % 3, 0, :], w, X, ALU.max))
                dve.tensor_tensor(w, w, wide(col[:, t % 3, 0, :]), ALU.subtract).then_inc(*centred.up())

            def finish(t):
                w = sc[:, t % 3, :, :]
                dve.wait_ge(*powered.at(t + 1))
                step(dve.tensor_reduce(col[:, t % 3, 1, :], w, X, ALU.add))
                if custom:
                    step(dve.tensor_scalar(col[:, t % 3, 1, :], col[:, t % 3, 1, :], 1e-6, None, ALU.add))
                if custom:
                    step(dve.reciprocal(col[:, t % 3, 2, :], col[:, t % 3, 1, :]))
                    step(dve.tensor_tensor(w, w, wide(col[:, t % 3, 2, :]), ALU.mult))
                    step(dve.tensor_reduce(col[:, t % 3, 1, :], w, X, ALU.add))
                    step(dve.tensor_scalar(col[:, t % 3, 1, :], col[:, t % 3, 1, :], S * 1e-8, None, ALU.add))
                    dve.reciprocal(col[:, t % 3, 2, :], col[:, t % 3, 1, :]).then_inc(*inverted.up())
                else:
                    dve.reciprocal(col[:, t % 3, 2, :], col[:, t % 3, 1, :]).then_inc(*inverted.up())
                dve.wait_ge(*inverted.at(t + 1))
                if t >= 2:
                    dve.wait_ge(*turned.at(R * t - R))
                if t == 0:
                    dve.wait_ge(*zeroed.at(1))
                for half in range(2):
                    rows = slice(64 * half, 64 * half + 64)
                    dst, src = bd[rows, t % 2, :, 64 * half:64 * half + 64], sc[rows, t % 3, :, :]
                    inverse = col[rows, t % 3, 2, :].unsqueeze(2).to_broadcast([64, H, S])
                    if custom:
                        ins = dve.scalar_tensor_tensor(dst, src, 1e-8, inverse, ALU.add, ALU.mult)
                    else:
                        ins = dve.tensor_tensor(dst, src, inverse, ALU.mult)
                ins.then_inc(*probs_ready.up())

            def take_output(t):
                dve.wait_ge(*attended.at(t + 1))
                dve.tensor_copy(oT[:, :, t * P:(t + 1) * P],
                                ps[:, 6, :].rearrange("p (c n) -> p c n", c=C)).then_inc(*o_taken.up())

            centre(0)
            finish(0)
            for t in range(T):
                if t + 1 < T:
                    centre(t + 1)
                    finish(t + 1)
                if t >= 1:
                    take_output(t - 1)
            take_output(T - 1)




def L0_xattn(m):
    d = m.d
    vectors, out_sent = m.sig("vectors_and_Wq"), m.sig("Wo_sent")
    with m.local(qT=[P, C, N], oT=[P, C, N], w=[P, C, D], bv=[P, D], bo=[P, D], b=[P, 2, C],
                 wkb=[P, C, D], wvb=[P, C, D], ctxT=[P, 2, C, SK]) as (qT, oT, w, bv, bo, b, wkb, wvb, ctxT):
        normalise(m, m.y, m.x, 1e-5, dstT=m.yT, ahead=(
            vectors, (w[:], d["L0_xattn_Wq"]), (b[:, 0, :], d["L0_xattn_bq"]), (b[:, 1, :], d["L0_xattn_bk"]),
            (bv[:], d["L0_xattn_bv"].partition_broadcast(P)), (bo[:], d["L0_xattn_bo"].partition_broadcast(P))))
        linear_features(m, [(qT, None, w, m.yT, b[:, 0, :], ACT.Identity)], sent=vectors,
                        ahead=first_loads(m, wkb, wvb, ctxT, d["L0_xattn_Wk"], d["L0_xattn_Wv"]))
        cross_attention(m, oT, qT, 32, 32 ** -0.5, wkb, wvb, ctxT, b[:, 1, :], bv[:],
                        mask=d["mask"], ahead=(out_sent, (w[:], d["L0_xattn_Wo"])))
        linear_tokens(m, m.x, oT, None, w, C, bo[:], m.x, sent=out_sent)


def L0_attn(m):
    d = m.d
    q_sent, v_sent, out_sent = m.sig("Wq_and_masks_sent"), m.sig("Wv_sent"), m.sig("Wo_sent")
    with m.local(qT=[P, C, N], kT=[P, C, N], v=[P, T, D], w=[P, C, D], w2=[P, C, D], w3=[P, C, D],
                 bound=[P, S]) as (qT, kT, v, w, w2, w3, bound):
        normalise(m, m.y, m.x, 1e-5, dstT=m.yT, ahead=(q_sent, (w[:], d["L0_attn_w_q"]), (bound[:], d["causal"])))
        linear_features(m, [(qT, None, w, m.yT, None, ACT.Identity),
                            (kT, d["L0_attn_w_k"], w2, m.yT, None, ACT.Identity)], sent=q_sent,
                        ahead=(v_sent, (w3[:], d["L0_attn_w_v"])))
        linear_tokens(m, v, m.yT, None, w3, C, sent=v_sent, ahead=(out_sent, (w[:], d["L0_attn_w_proj"])))
        self_attention(m, m.yT, qT, kT, v, 32 ** -0.5, 100.0, bound[:], custom=True)
        linear_tokens(m, m.x, m.yT, None, w, C, add=m.x, sent=out_sent)


def L3_xattn(m):
    d = m.d
    vectors, out_sent = m.sig("vectors_and_Wq"), m.sig("Wo_sent")
    with m.local(qT=[P, C, N], oT=[P, C, N], w=[P, C, D], bv=[P, D], bo=[P, D], b=[P, 2, C],
                 wkb=[P, C, D], wvb=[P, C, D], ctxT=[P, 2, C, SK]) as (qT, oT, w, bv, bo, b, wkb, wvb, ctxT):
        normalise(m, m.y, m.x, 1e-5, dstT=m.yT, ahead=(
            vectors, (w[:], d["L3_xattn_Wq"]), (b[:, 0, :], d["L3_xattn_bq"]), (b[:, 1, :], d["L3_xattn_bk"]),
            (bv[:], d["L3_xattn_bv"].partition_broadcast(P)), (bo[:], d["L3_xattn_bo"].partition_broadcast(P))))
        linear_features(m, [(qT, None, w, m.yT, b[:, 0, :], ACT.Identity)], sent=vectors,
                        ahead=first_loads(m, wkb, wvb, ctxT, d["L3_xattn_Wk"], d["L3_xattn_Wv"]))
        cross_attention(m, oT, qT, 32, 32 ** -0.5, wkb, wvb, ctxT, b[:, 1, :], bv[:],
                        ahead=(out_sent, (w[:], d["L3_xattn_Wo"])))
        linear_tokens(m, m.x, oT, None, w, C, bo[:], m.x, sent=out_sent)


def gate_scores(m, weights, srcT, E, brow=None, sent=None, ahead=None):
    scored = m.sig("gate_scored")
    with m.block() as block:
        send(block, ahead)

        @block.tensor
        def _(pe):
            pe.wait_ge(sent.sem, sent.made)
            for t in range(T):
                for c in range(C):
                    ins = pe.matmul(m.ps[:, 0, t * E:(t + 1) * E], srcT[:, c, t * P:(t + 1) * P], weights[:, c, :],
                                    start=(c == 0), stop=(c == C - 1 and brow is None))
                if brow is not None:
                    ins = pe.matmul(m.ps[:, 0, t * E:(t + 1) * E], m.ones[0:1, :], brow, start=False, stop=True)
            ins.then_inc(*scored.up())


def route(m, w, E, k, before, normal, eps=0.0, renormal=True):
    step_s, centred, powered = m.sig("route_step"), m.sig("route_centred"), m.sig("route_exp")
    with m.local(sc=[P, T, E], one=[P, T], cmp=[P, T, E, E], eq=[P, T, E, E], sel=[P, T, E]) as \
            (sc, one, cmp, eq, sel), m.block() as block:
        @block.scalar
        def _(act):
            act.wait_ge(*centred.at(1))
            act.activation(sc[:], sc[:], ACT.Exp).then_inc(*powered.up())

        @block.vector
        def _(dve):
            step = Chain(dve, step_s)
            wide = lambda a: a.unsqueeze(2).to_broadcast([P, T, E])
            step(dve.tensor_copy(sc[:], m.ps[:, 0, 0:T * E].rearrange("p (t e) -> p t e", t=T)))
            step(dve.tensor_reduce(one[:], sc[:], X, ALU.max))
            dve.tensor_tensor(sc[:], sc[:], wide(one[:]), ALU.subtract).then_inc(*centred.up())
            dve.wait_ge(*powered.at(1))
            if normal:
                step(dve.tensor_reduce(one[:], sc[:], X, ALU.add))
                step(dve.reciprocal(one[:], one[:]))
                step(dve.tensor_tensor(sc[:], sc[:], wide(one[:]), ALU.mult))
            for t in range(T):
                mine = sc[:, t, :].unsqueeze(2).to_broadcast([P, E, E])
                other = sc[:, t, :].unsqueeze(1).to_broadcast([P, E, E])
                dve.tensor_tensor(cmp[:, t], other, mine, ALU.is_gt)
                step(dve.tensor_tensor(eq[:, t], other, mine, ALU.is_equal))
                step(dve.tensor_tensor(eq[:, t], eq[:, t], before, ALU.mult))
            step(dve.tensor_tensor(cmp[:], cmp[:], eq[:], ALU.add))
            step(dve.tensor_reduce(sel[:], cmp[:], X, ALU.add))
            step(dve.tensor_scalar(sel[:], sel[:], float(k), None, ALU.is_lt))
            step(dve.tensor_tensor(w[:, :, 0:E], sc[:], sel[:], ALU.mult))
            if renormal:
                step(dve.tensor_reduce(one[:], w[:, :, 0:E], X, ALU.add))
                step(dve.tensor_scalar(one[:], one[:], eps, None, ALU.add))
                step(dve.reciprocal(one[:], one[:]))
                step(dve.tensor_tensor(w[:, :, 0:E], w[:, :, 0:E], wide(one[:]), ALU.mult))


def L0_ffn(m):
    d, E, F = m.d, 8, 1024
    FC = F // P
    s = m.sig
    vectors, up_landed, down_landed = s("gate_vectors"), s("gated_up_landed"), s("gated_down_landed")
    with m.local(w=[P, T, E + 1], wg=[P, C, F], wu=[P, C, F], wd=[P, FC, D]) as (w, wg, wu, wd):
        with m.local(z=[P, T, D], zT=[P, C, N], ln=[P, 2, C], gw=[P, C, E], before=[P, E, E]) as \
                (z, zT, ln, gw, before):
            normalise(m, m.y, m.x, 1e-5, dstT=m.yT, ahead=(
                vectors, (ln[:, 0, :], d["L0_ffn_ln_scale"]), (ln[:, 1, :], d["L0_ffn_ln_bias"]),
                (gw[:], d["L0_ffn_gate_w"]), (before[:], d["before8"].partition_broadcast(P))))
            normalise(m, z, m.y, 1e-5, dstT=zT, scale=ln[:, 0, :], bias=ln[:, 1, :], vectors=vectors,
                      ahead=(up_landed, (wg[:], d["L0_ffn_Wg"][0]), (wu[:], d["L0_ffn_Wu"][0])))
            gate_scores(m, gw, zT, E, sent=vectors, ahead=(down_landed, (wd[:], d["L0_ffn_Wd"][0])))
            route(m, w, E, 2, before[:], True, 1e-5)
        up_done, silu_done, h_ready = s("gated_up_product"), s("gated_silu"), s("gated_h_ready")
        down_done, added, one_set = s("gated_down_product"), s("gated_added"), s("shared_gate_set")
        with m.local(sg=[P, 2, N], h=[P, FC, N]) as (sg, h), m.block((h_ready, 1), (added, T)) as block:
            ps = m.ps

            @block.sync
            def _(sp):
                with repeat(sp, E) as e:
                    sp.wait_ge(*h_ready.at(1 + FC * e + FC))
                    sp.dma_start(wg[:], d["L0_ffn_Wg"][e + 1]).then_inc(*up_landed.up(16))
                    sp.dma_start(wu[:], d["L0_ffn_Wu"][e + 1]).then_inc(*up_landed.up(16))
                    sp.wait_ge(*added.at(T + T * e + T))
                    sp.dma_start(wd[:], d["L0_ffn_Wd"][e + 1]).then_inc(*down_landed.up(16))

            @block.gpsimd
            def _(pool):
                pool.memset(w[:, :, E:E + 1], 1.0).then_inc(*one_set.up())

            @block.tensor
            def _(pe):
                with repeat(pe, E + 1) as e:
                    pe.wait_ge(*up_landed.at(32 * e))
                    for n in range(FC):
                        if n >= 2:
                            pe.wait_ge(*h_ready.at(FC * e + n))
                        for half, wb in ((0, wg), (1, wu)):
                            for k in range(C):
                                ins = pe.matmul(ps[:, 2 * half + n % 2, :], wb[:, k, n * P:(n + 1) * P],
                                                m.yT[:, k, :], start=(k == 0), stop=(k == C - 1))
                        ins.then_inc(*up_done.up())
                    pe.wait_ge(*down_landed.at(16 * e))
                    for t in range(T):
                        pe.wait_ge(*added.at(T * e + t + 1))
                        for k in range(FC):
                            if t == 0 and k >= FC - 2:
                                pe.wait_ge(*h_ready.at(1 + FC * e + k + 1))
                            ins = pe.matmul(ps[:, 4 + t, :], h[:, k, t * P:(t + 1) * P], wd[:, k, :],
                                            start=(k == 0), stop=(k == FC - 1))
                        ins.then_inc(*down_done.up())

            @block.scalar
            def _(act):
                with repeat(act, E + 1) as e:
                    for n in range(FC):
                        act.wait_ge(*up_done.at(FC * e + n + 1))
                        if n >= 2:
                            act.wait_ge(*h_ready.at(FC * e + n))
                        else:
                            act.wait_ge(*h_ready.at(1 + FC * e))
                        act.activation(sg[:, n % 2, :], ps[:, n % 2, :], ACT.Silu).then_inc(*silu_done.up())

            @block.vector
            def _(dve):
                dve.wait_ge(*one_set.at(1))
                with repeat(dve, E + 1) as e:
                    for n in range(FC):
                        dve.wait_ge(*silu_done.at(FC * e + n + 1))
                        dve.tensor_tensor(h[:, n, :], ps[:, 2 + n % 2, :], sg[:, n % 2, :], ALU.mult)\
                           .then_inc(*h_ready.up())
                    for t in range(T):
                        dve.wait_ge(*down_done.at(T * e + t + 1))
                        dve.wait_ge(*added.at(T * e + t + 1))
                        dve.scalar_tensor_tensor(m.x[:, t, :], ps[:, 4 + t, :], w[:, t, bass.ds(e, 1)], m.x[:, t, :],
                                                 ALU.mult, ALU.add).then_inc(*added.up())


def L1_xattn(m):
    d = m.d
    temp = float(D) ** 0.5
    vectors, out_sent = m.sig("vectors_and_Wq"), m.sig("Wo_sent")
    with m.local(qT=[P, C, N], oT=[P, C, N], w=[P, C, D], pre=[P, 2, C], ln=[P, 2, C], rows=[P, 2, D],
                 wkb=[P, C, D], wvb=[P, C, D], ctxT=[P, 2, C, SK]) as (qT, oT, w, pre, ln, rows, wkb, wvb, ctxT):
        normalise(m, m.y, m.x, 1e-5, ahead=(
             vectors, (pre[:, 0, :], d["L1_xattn_pre_g"]), (pre[:, 1, :], d["L1_xattn_pre_b"]),
             (ln[:, 0, :], d["L1_xattn_ln_g"]), (ln[:, 1, :], d["L1_xattn_ln_b"]),
             (rows[:, 0, :], d["L1_xattn_ln_g_row"].partition_broadcast(P)),
             (rows[:, 1, :], d["L1_xattn_ln_b_row"].partition_broadcast(P)), (w[:], d["L1_xattn_Wq"])))
        normalise(m, m.y, m.y, 1e-5, dstT=m.yT, scale=pre[:, 0, :], bias=pre[:, 1, :], vectors=vectors)
        linear_features(m, [(qT, None, w, m.yT, None, ACT.Identity)], sent=vectors,
                        ahead=first_loads(m, wkb, wvb, ctxT, d["L1_xattn_Wk"], d["L1_xattn_Wv"]))
        cross_attention(m, oT, qT, 64, 1.0 / temp, wkb, wvb, ctxT,
                        clip=10000.0 * temp, knorm=(pre[:, 0, :], pre[:, 1, :]), ahead=(out_sent, (w[:], d["L1_xattn_Wo"])))
        turn_back(m, m.y, oT)
        normalise(m, m.y, m.y, 1e-5, dstT=m.yT, scale=ln[:, 0, :], bias=ln[:, 1, :])
        product, gelu_done, step_s = m.sig("tokens_product"), m.sig("gelu_done"), m.sig("gelu_step")
        with m.block() as block:
            @block.tensor
            def _(pe):
                pe.wait_ge(out_sent.sem, out_sent.made)
                for t in range(T):
                    for k in range(C):
                        ins = pe.matmul(m.ps[:, t, :], m.yT[:, k, t * P:(t + 1) * P], w[:, k, :],
                                        start=(k == 0), stop=(k == C - 1))
                    ins.then_inc(*product.up())

            @block.scalar
            def _(act):
                for t in range(T):
                    act.wait_ge(*product.at(t + 1))
                    act.activation(qT[:, t, :], m.ps[:, t, :], ACT.Gelu).then_inc(*gelu_done.up())

            @block.vector
            def _(dve):
                step = Chain(dve, step_s)
                for t in range(T):
                    step(dve.tensor_tensor(m.y[:, t, :], m.y[:, t, :], rows[:, 0, :], ALU.mult))
                    step(dve.tensor_tensor(m.y[:, t, :], m.y[:, t, :], rows[:, 1, :], ALU.add))
                    step(dve.tensor_tensor(m.x[:, t, :], m.x[:, t, :], m.y[:, t, :], ALU.add))
                    dve.wait_ge(*gelu_done.at(t + 1))
                    dve.tensor_tensor(m.x[:, t, :], m.x[:, t, :], qT[:, t, :], ALU.add)


def turn_back(m, dst, srcT):
    turned = m.sig("turned")
    with m.block() as block:
        @block.tensor
        def _(pe):
            for t in range(T):
                for c in range(C):
                    ins = pe.transpose(m.ps[:, t, c * P:(c + 1) * P], srcT[:, c, t * P:(t + 1) * P], m.ident[:])
                ins.then_inc(*turned.up())

        @block.vector
        def _(dve):
            for t in range(T):
                dve.wait_ge(*turned.at(t + 1))
                dve.tensor_copy(dst[:, t, :], m.ps[:, t, :])


def L1_ffn(m):
    d, E = m.d, 4
    s = m.sig
    vectors, first_sent = s("gate_vectors"), s("first_expert_sent")
    w1_landed, w2_landed = s("e1_landed"), s("e2_landed")
    first, second, var_ready, rooted = s("e_first"), s("e_second"), s("e_var"), s("e_rstd")
    hidden, normed, turned, relued, step_s = s("e_hidden_normed"), s("e_normed"), s("e_turned"), s("e_relu"), s("e_step")
    with m.local(w=[P, T, E], gw=[P, C, E], gb=[1, E], before=[P, E, E], w1=[P, C, D], w2=[P, C, D], h=[P, T, D],
                 o=[P, T, D], hT=[P, C, N], b1=[1, E, D], b2=[1, E, D], g1=[P, E, C], be1=[P, E, C], g2=[P, E, D],
                 be2=[P, E, D]) as (w, gw, gb, before, w1, w2, h, o, hT, b1, b2, g1, be1, g2, be2):
        normalise(m, m.y, m.x, 1e-5, dstT=m.yT, ahead=[
            (vectors, (gw[:], d["L1_ffn_gate_W"]), (before[:], d["before4"].partition_broadcast(P)),
             (gb[:], d["L1_ffn_gate_b"].unsqueeze(0))),
            (first_sent, (w1[:], d["L1_ffn_W1"][0]),
             (b1[:], d["L1_ffn_b1"].unsqueeze(0)), (b2[:], d["L1_ffn_b2"].unsqueeze(0)),
             (g1[:], d["L1_ffn_g1"]), (be1[:], d["L1_ffn_be1"]),
             (g2[:], d["L1_ffn_g2"].partition_broadcast(P)), (be2[:], d["L1_ffn_be2"].partition_broadcast(P)))])
        gate_scores(m, gw, m.yT, E, gb[0:1, :], sent=vectors)
        route(m, w, E, 2, before[:], False)
        with m.block((normed, 1)) as block:
            ps = m.ps

            @block.sync
            def _(sp):
                sp.dma_start(w2[:], d["L1_ffn_W2"][0]).then_inc(*w2_landed.up(16))
                sp.wait_ge(*first.at(T))
                sp.dma_start(w1[:], d["L1_ffn_W1"][1]).then_inc(*w1_landed.up(16))
                with repeat(sp, E - 2) as e:
                    sp.wait_ge(*first.at(T * e + 2 * T))
                    sp.dma_start(w1[:], d["L1_ffn_W1"][e + 2]).then_inc(*w1_landed.up(16))
                    sp.wait_ge(*second.at(T * e + T))
                    sp.dma_start(w2[:], d["L1_ffn_W2"][e + 1]).then_inc(*w2_landed.up(16))
                sp.wait_ge(*second.at(T * (E - 1)))
                sp.dma_start(w2[:], d["L1_ffn_W2"][E - 1]).then_inc(*w2_landed.up(16))

            @block.tensor
            def _(pe):
                def products(bank, srcT, weights, bias, signal):
                    for t in range(T):
                        for k in range(C):
                            pe.matmul(ps[:, bank + t, :], srcT[:, k, t * P:(t + 1) * P], weights[:, k, :],
                                      start=(k == 0), stop=False)
                        pe.matmul(ps[:, bank + t, :], m.ones[0:1, :], bias, start=False, stop=True)\
                          .then_inc(*signal.up())

                def turn_hidden(e):
                    pe.wait_ge(*hidden.at(e + 1))
                    for c in range(C):
                        for t in range(T):
                            ins = pe.transpose(ps[:, c, t * P:(t + 1) * P], h[:, t, c * P:(c + 1) * P], m.ident[:])
                        ins.then_inc(*turned.up())

                pe.wait_ge(first_sent.sem, first_sent.made)
                products(0, m.yT, w1, b1[0:1, 0, :], first)
                turn_hidden(0)
                with repeat(pe, E - 1) as e:
                    pe.wait_ge(*w1_landed.at(16 * e + 16))
                    pe.wait_ge(*relued.at(C * e + C))
                    products(0, m.yT, w1, b1[0:1, e + 1, :], first)
                    pe.wait_ge(*w2_landed.at(16 * e + 16))
                    pe.wait_ge(*normed.at(1 + e))
                    products(4, hT, w2, b2[0:1, e, :], second)
                    turn_hidden(e + 1)
                pe.wait_ge(*normed.at(E))
                pe.wait_ge(*relued.at(C * E))
                pe.wait_ge(*w2_landed.at(16 * E))
                products(4, hT, w2, b2[0:1, E - 1, :], second)

            @block.scalar
            def _(act):
                with repeat(act, E) as e:
                    for c in range(C):
                        act.wait_ge(*turned.at(C * e + c + 1))
                        act.activation(hT[:, c, :], ps[:, c, :], ACT.Relu, bias=be1[:, e, c:c + 1],
                                       scale=g1[:, e, c:c + 1]).then_inc(*relued.up())

            @block.gpsimd
            def _(pool):
                with repeat(pool, 2 * E) as i:
                    pool.wait_ge(*var_ready.at(i + 1))
                    pool.tensor_tensor(m.rstd[:], m.den[:], m.minus_half[:], ALU.pow).then_inc(*rooted.up())

            @block.vector
            def _(dve):
                def norm(step, products, e, bank, dst, signal, n):
                    for t in range(T):
                        dve.wait_ge(*products.at(T * e + t + 1))
                        ins = dve.bn_stats(m.stats[:, t, :], ps[:, bank + t, :])
                    step(ins)
                    dve.memset(m.den[:], 0.0)
                    for t in range(T):
                        ins = dve.bn_aggr(m.mv[:, t, :], m.stats[:, t, :])
                    step(ins)
                    dve.tensor_scalar(m.den[:], m.mv[:, :, 1], 1e-5, None, ALU.add).then_inc(*var_ready.up())
                    dve.wait_ge(*rooted.at(n + 1))
                    for t in range(T):
                        ins = dve.tensor_scalar(dst[:, t, :], ps[:, bank + t, :], m.mv[:, t, 0:1], m.rstd[:, t:t + 1],
                                                ALU.subtract, ALU.mult)
                    ins.then_inc(*signal.up())

                def combine(step, e):
                    dve.wait_ge(*normed.at(1 + e + 1))
                    over = lambda a: a.unsqueeze(1).to_broadcast([P, T, D])
                    step(dve.tensor_tensor(o[:], o[:], over(g2[:, e, :]), ALU.mult))
                    step(dve.tensor_tensor(o[:], o[:], over(be2[:, e, :]), ALU.add))
                    for t in range(T):
                        ins = dve.scalar_tensor_tensor(m.x[:, t, :], o[:, t, :], w[:, t, bass.ds(e, 1)], m.x[:, t, :],
                                                       ALU.mult, ALU.add)
                    step(ins)

                step = Chain(dve, step_s)
                for t in range(T):
                    ins = dve.tensor_tensor(m.x[:, t, :], m.x[:, t, :], m.y[:, t, :], ALU.add)
                step(ins)
                norm(step, first, 0, 0, h, hidden, 0)
                with repeat(dve, E - 1) as e:
                    step = Chain(dve, step_s, e, 7)
                    norm(step, first, e + 1, 0, h, hidden, 2 * e + 1)
                    norm(step, second, e, 4, o, normed, 2 * e + 2)
                    combine(step, e)
                    step.end()
                step = Chain(dve, step_s)
                norm(step, second, E - 1, 4, o, normed, 2 * E - 1)
                combine(step, E - 1)


def L2_xattn(m):
    d = m.d
    scale = (D / 16) ** 0.5
    s = m.sig
    ctxt_landed, ctx_landed = [s("pair_ctxT_landed0"), s("pair_ctxT_landed1")], [s("pair_ctx_landed0"), s("pair_ctx_landed1")]
    scored, max_ready, powered, scaled = s("pair_scored"), s("pair_max_ready"), s("pair_exp"), s("pair_scaled")
    turned, taken, attended, o_taken, step_s = s("pair_turned"), s("pair_turned_taken"), s("pair_attended"), s("pair_attended_taken"), s("pair_step")
    biased = s("pair_bias_scored")
    with m.local(qT=[P, C, N], q2T=[P, C, N], w=[P, C, D], w2=[P, C, D], b=[P, 2, C], bv=[P, D],
                 ctxT=[P, 2, 2, C, SK], ctx=[P, 2, 2, KC, D]) as (qT, q2T, w, w2, b, bv, ctxT, ctx):
        def context(t):
            source = lambda a: d[a][2 * t:2 * t + 2].rearrange("b p c n -> p b c n")
            return [(ctxt_landed[t % 2], (ctxT[:, t % 2], source("ctxT"))), (ctx_landed[t % 2], (ctx[:, t % 2], source("ctx")))]

        vectors, k_sent = s("vectors_and_Wq"), s("Wk_sent")
        normalise(m, m.y, m.x, 1e-5, dstT=m.yT, ahead=(
            vectors, (w[:], d["L2_xattn_Wq"]), (b[:, 0, :], d["L2_xattn_bq"]), (b[:, 1, :], d["L2_xattn_bk"]),
            (bv[:], d["L2_xattn_bv"].partition_broadcast(P))))
        linear_features(m, [(qT, None, w, m.yT, b[:, 0, :], ACT.Identity)], sent=vectors,
                        ahead=[(k_sent, (w2[:], d["L2_xattn_Wk"]))] + context(0))
        linear_features(m, [(q2T, None, w2, qT, None, ACT.Identity)], sent=k_sent,
                        ahead=context(1) + [(vectors, (w[:], d["L2_xattn_Wv"]))])
        with m.local(pr=[P, SK], prT=[P, KC, P], sc=[P, SK],
                     col=[P, T, 4], qb=[P, T]) as (pr, prT, sc, col, qb), m.block() as block:
            ps = m.ps

            @block.sync
            def _(sp):
                for t in range(2, T):
                    features, positions = context(t)
                    sp.wait_ge(*scored.at(t - 1))
                    start_loads(sp, features)
                    sp.wait_ge(*attended.at(t - 1))
                    start_loads(sp, positions)

            @block.tensor
            def _(pe):
                for t in range(T):
                    for c in range(C):
                        ins = pe.matmul(ps[:, 7, t:t + 1], qT[:, c, t * P:(t + 1) * P], b[:, 1, c:c + 1],
                                        start=(c == 0), stop=(c == C - 1))
                ins.then_inc(*biased.up())

                def scores(t):
                    pe.wait_ge(*ctxt_landed[t % 2].at(16 * (t // 2)))
                    if t >= 2:
                        pe.wait_ge(*max_ready.at(t - 1))
                    for half in range(2):
                        for c in range(C):
                            ins = pe.matmul(ps[64 * half:64 * half + 64, t % 2, :],
                                            q2T[:, c, t * P + 64 * half:t * P + 64 * half + 64],
                                            ctxT[:, t % 2, half, c, :], start=(c == 0), stop=(c == C - 1))
                    ins.then_inc(*scored.up())

                scores(0)
                for t in range(T):
                    if t + 1 < T:
                        scores(t + 1)
                    pe.wait_ge(*scaled.at(t + 1))
                    for k in range(KC):
                        ins = pe.transpose(ps[:, 2, k * P:(k + 1) * P], pr[:, k * P:(k + 1) * P], m.ident[:])
                    ins.then_inc(*turned.up())
                    pe.wait_ge(*ctx_landed[t % 2].at(16 * (t // 2)))
                    pe.wait_ge(*taken.at(t + 1))
                    if t >= 1:
                        pe.wait_ge(*o_taken.at(t))
                    for c in range(C):
                        for half in range(2):
                            for k in range(KC):
                                ins = pe.matmul(ps[:, 3, c * P + 64 * half:c * P + 64 * half + 64],
                                                ctx[:, t % 2, half, k, c * P:(c + 1) * P],
                                                prT[:, k, 64 * half:64 * half + 64],
                                                start=(k == 0), stop=(k == KC - 1))
                    ins.then_inc(*attended.up())

            @block.scalar
            def _(act):
                for t in range(T):
                    act.wait_ge(*max_ready.at(t + 1))
                    act.activation(pr[:], sc[:], ACT.Exp, bias=col[:, t, 1:2], scale=scale,
                                   accum_out=col[:, t, 2:3]).then_inc(*powered.up())

            @block.vector
            def _(dve):
                step = Chain(dve, step_s)
                dve.wait_ge(*biased.at(1))
                step(dve.tensor_copy(qb[:], ps[:, 7, 0:T]))
                for t in range(T):
                    dve.wait_ge(*scored.at(t + 1))
                    step(dve.tensor_scalar(sc[:], ps[:, t % 2, :], qb[:, t:t + 1], None, ALU.add))
                    step(dve.tensor_reduce(col[:, t, 0:1], sc[:], X, ALU.max, negate=True))
                    dve.tensor_scalar(col[:, t, 1:2], col[:, t, 0:1], scale, None, ALU.mult).then_inc(*max_ready.up())
                    dve.wait_ge(*powered.at(t + 1))
                    step(dve.reciprocal(col[:, t, 3:4], col[:, t, 2:3]))
                    dve.tensor_scalar(pr[:], pr[:], col[:, t, 3:4], None, ALU.mult).then_inc(*scaled.up())
                    dve.wait_ge(*turned.at(t + 1))
                    dve.tensor_copy(prT[:], ps[:, 2, :].rearrange("p (k n) -> p k n", k=KC)).then_inc(*taken.up())
                    dve.wait_ge(*attended.at(t + 1))
                    dve.tensor_copy(m.yT[:, :, t * P:(t + 1) * P],
                                    ps[:, 3, :].rearrange("p (c n) -> p c n", c=C)).then_inc(*o_taken.up())
        linear_tokens(m, m.x, m.yT, None, w, C, bv[:], m.x, sent=vectors)


def transformer_layer(m, z, n, ln1, wq, bq, wk, bk, wv, bv, wo, bo, ln2, w1, b1, w2, b2, act, allowed=None, rope=None):
    d = m.d
    FF = 2048
    q_sent, v_sent, out_sent, ffn_sent = m.sig("Wq_sent"), m.sig("Wv_sent"), m.sig("Wo_sent"), m.sig("ffn_weights_sent")
    second_sent = m.sig("ffn_second_sent")
    with m.local(wa=[P, C, FF], wb=[P, FF // P, D], cols2=[P, 2, C], b1c=[P, FF // P], b2r=[P, D]) as \
            (wa, wb, cols2, b1c, b2r):
        with m.local(qT=[P, C, N], kT=[P, C, N], v=[P, T, D], wqo=[P, C, D], wkk=[P, C, D], cols=[P, 6, C],
                     bvr=[P, D], bor=[P, D], bound=[P, S], trig=[P, 2, S], perm=[P, P]) as \
                (qT, kT, v, wqo, wkk, cols, bvr, bor, bound, trig, perm):
            wvv = wb[:, 0:C, :]
            normalise(m, n, z, 1e-5, dstT=m.yT, scale=cols[:, 0, :], bias=cols[:, 1, :], vectors=q_sent, ahead=(
                q_sent, *[(cols[:, i, :], d[a]) for i, a in enumerate((ln1[0], ln1[1], bq, bk))],
                (wqo[:], d[wq]), (bvr[:], d[bv].partition_broadcast(P)), (bor[:], d[bo].partition_broadcast(P)),
                *([(bound[:], d[allowed])] if allowed else []),
                *([(perm[:], d["rope_turn"]), (trig[:], d["rope_trig"])] if rope else [])))
            linear_features(m, [(qT, None, wqo, m.yT, cols[:, 2, :], ACT.Identity),
                                (kT, d[wk], wkk, m.yT, cols[:, 3, :], ACT.Identity)], sent=q_sent,
                            ahead=(v_sent, (wvv, d[wv])))
            linear_tokens(m, v, m.yT, None, wvv, C, bvr[:], sent=v_sent, ahead=(out_sent, (wqo[:], d[wo])))
            if rope:
                rotate(m, qT, kT, perm, trig)
            ahead = (ffn_sent, (cols2[:, 0, :], d[ln2[0]]), (cols2[:, 1, :], d[ln2[1]]), (b1c[:], d[b1]),
                     (b2r[:], d[b2].partition_broadcast(P)), (wa[:], d[w1]))
            self_attention(m, m.yT, qT, kT, v, 32 ** -0.5, None, bound[:] if allowed else None, ahead=ahead)
            linear_tokens(m, z, m.yT, None, wqo, C, bor[:], z, sent=out_sent, ahead=(second_sent, (wb[:], d[w2])))
        with m.local(h=[P, FF // P, N]) as (h,):
            normalise(m, n, z, 1e-5, dstT=m.yT, scale=cols2[:, 0, :], bias=cols2[:, 1, :], vectors=ffn_sent)
            linear_features(m, [(h, None, wa, m.yT, b1c, act)], sent=ffn_sent)
            linear_tokens(m, z, h, None, wb, FF // P, b2r[:], z, sent=second_sent)


def rotate(m, qT, kT, perm, trig):
    turned, sin_s, cos_s = m.sig("pairs_turned"), m.sig("sin_multiplied"), m.sig("cos_multiplied")
    with m.local(tmp=[P, 2 * C, N]) as (tmp,), m.block() as block:
        over = lambda a: a.unsqueeze(1).to_broadcast([P, B, S])
        part = lambda n: (qT, kT)[n // C][:, n % C, :].rearrange("p (b s) -> p b s", b=B)
        by_batch = lambda a: a.rearrange("p (b s) -> p b s", b=B)

        @block.tensor
        def _(pe):
            for n in range(2 * C):
                pe.matmul(m.ps[:, n, :], perm[:], (qT, kT)[n // C][:, n % C, :], start=True, stop=True)\
                  .then_inc(*turned.up())

        @block.gpsimd
        def _(pool):
            for n in range(2 * C):
                pool.wait_ge(*turned.at(n + 1))
                pool.tensor_tensor(part(n), part(n), over(trig[:, 0, :]), ALU.mult).then_inc(*cos_s.up())

        @block.vector
        def _(dve):
            for n in range(2 * C):
                dve.wait_ge(*turned.at(n + 1))
                dve.tensor_tensor(by_batch(tmp[:, n, :]), by_batch(m.ps[:, n, :]), over(trig[:, 1, :]), ALU.mult)\
                   .then_inc(*sin_s.up())
            for n in range(2 * C):
                dve.wait_ge(*sin_s.at(n + 1))
                dve.wait_ge(*cos_s.at(n + 1))
                dve.tensor_tensor(part(n), part(n), by_batch(tmp[:, n, :]), ALU.add)


def L2_attn(m):
    normalise(m, m.y, m.x, 1e-5)
    with m.local(n=[P, T, D]) as (n,):
        for i in range(2):
            g = lambda a: f"L2_attn_{a}_{i}"
            transformer_layer(m, m.y, n, (g("ln1_g"), g("ln1_b")), g("wq"), g("bq"), g("wk"), g("bk"), g("wv"), g("bv"),
                              g("wo"), g("bo"), (g("ln2_g"), g("ln2_b")), g("w1"), g("b1"), g("w2"), g("b2"), ACT.Gelu,
                              allowed="strided")
        with m.local(rows=[P, 2, D]) as (rows,):
            scaled, rows_sent = m.sig("final_norm_step"), m.sig("final_rows_sent")
            normalise(m, n, m.y, 1e-5, ahead=(rows_sent, (rows[:, 0, :], m.d["L2_attn_lnf_g"].partition_broadcast(P)),
                                              (rows[:, 1, :], m.d["L2_attn_lnf_b"].partition_broadcast(P))))
            with m.block() as block:
                @block.vector
                def _(dve):
                    step = Chain(dve, scaled)
                    over = lambda a: a.unsqueeze(1).to_broadcast([P, T, D])
                    dve.wait_ge(rows_sent.sem, rows_sent.made)
                    step(dve.tensor_tensor(n[:], n[:], over(rows[:, 0, :]), ALU.mult))
                    step(dve.tensor_tensor(n[:], n[:], over(rows[:, 1, :]), ALU.add))
                    step(dve.tensor_tensor(m.x[:], m.x[:], n[:], ALU.add))


def L3_attn(m):
    normalise(m, m.y, m.x, 1e-5)
    g = lambda a: f"L3_attn_{a}"
    with m.local(n=[P, T, D]) as (n,):
        transformer_layer(m, m.y, n, (g("g1"), g("beta1")), g("Wq"), g("bq"), g("Wk"), g("bk"), g("Wv"), g("bv"),
                          g("Wo"), g("bo"), (g("g2"), g("beta2")), g("W1"), g("b1"), g("W2"), g("b2"), ACT.Relu, rope=True)
    add_into(m, m.x, m.x, m.y)


def L2_ffn(m):
    d, E, F, CAP = m.d, 8, 2048, S // 8
    SL = B * CAP
    s = m.sig
    vectors = s("switch_vectors")
    w1_landed = [[s(f"switch_w1_landed{odd}{i}") for i in range(4)] for odd in range(2)]
    w2_landed = [s(f"switch_w2_landed{i}") for i in range(4)]
    with m.local(xT=[P, C, E + 1, SL], cmbT=[P, E, N], wa=[P, 2, 4, C, 512], wb=[P, 4, 4, D]) as (xT, cmbT, wa, wb):
        with m.local(w=[P, T, E], gw=[P, C, E], before=[P, E, E], earlier=[P, P], place=[P, CAP], one=[P, T, E],
                     disp=[P, T, E, SL], hot=[P, T * E, CAP]) as (w, gw, before, earlier, place, one, disp, hot):
            normalise(m, m.y, m.x, 1e-5, dstT=m.yT, ahead=[
                (vectors, (gw[:], d["L2_ffn_Wg"]), (before[:], d["before8"].partition_broadcast(P)),
                 (earlier[:], d["earlier"]), (place[:], d["place"].partition_broadcast(P))),
                *[(w1_landed[0][g], (wa[:, 0, g], d["L2_ffn_W1"][0, g])) for g in range(4)],
                *[(w2_landed[g], (wb[:, g], d["L2_ffn_W2"][0, g])) for g in range(4)],
                *[(w1_landed[1][g], (wa[:, 1, g], d["L2_ffn_W1"][1, g])) for g in range(4)]])
            gate_scores(m, gw, m.yT, E, sent=vectors)
            route(m, w, E, 1, before[:], True, renormal=False)
            chosen, counted, step_s, dispatched = s("chosen"), s("counted"), s("dispatch_step"), s("dispatched")
            gathered, gathered_taken, weighed, c_turned = s("gathered"), s("gathered_taken"), s("weighed"), s("combine_turned")
            zeroed, c_taken = s("dispatch_zeroed"), s("combine_turned_taken")
            with m.block() as block:
                ps = m.ps

                @block.gpsimd
                def _(pool):
                    pool.memset(disp[:], 0.0).then_inc(*zeroed.up())

                @block.tensor
                def _(pe):
                    pe.wait_ge(*chosen.at(1))
                    for t in range(T):
                        ins = pe.matmul(ps[:, 0, t * E:(t + 1) * E], earlier[:], one[:, t, :], start=True, stop=True)
                    ins.then_inc(*counted.up())
                    pe.wait_ge(*dispatched.at(1))
                    for t in range(T):
                        for c in range(C):
                            ins = pe.matmul(ps[:, 1 + t % 2, c * P:(c + 1) * P], m.y[:, t, c * P:(c + 1) * P],
                                            disp[:, t, :, t * 16:(t + 1) * 16], start=True, stop=True)
                        ins.then_inc(*gathered.up())
                        if t + 1 < T and t >= 1:
                            pe.wait_ge(*gathered_taken.at(t))
                    pe.wait_ge(*weighed.at(1))
                    for e in range(E):
                        if e >= 4:
                            pe.wait_ge(*c_taken.at(e - 3))
                        for t in range(T):
                            for side in range(2):
                                ins = pe.matmul(ps[SL * side:SL * side + SL, 4 + e % 4, t * P:(t + 1) * P],
                                                disp[:, t, e, :], m.ident[:], start=True, stop=True)
                        ins.then_inc(*c_turned.up())

                @block.vector
                def _(dve):
                    step = Chain(dve, step_s)
                    dve.tensor_scalar(one[:], w[:], 0.0, None, ALU.is_gt).then_inc(*chosen.up())
                    dve.wait_ge(*counted.at(1))
                    step(dve.tensor_tensor(hot[:], ps[:, 0, 0:T * E].unsqueeze(2).to_broadcast([P, T * E, CAP]),
                                           place[:].unsqueeze(1).to_broadcast([P, T * E, CAP]), ALU.is_equal))
                    step(dve.tensor_tensor(hot[:], hot[:],
                                           one[:].rearrange("p t e -> p (t e)").unsqueeze(2).to_broadcast([P, T * E, CAP]),
                                           ALU.mult))
                    dve.wait_ge(*zeroed.at(1))
                    for t in range(T):
                        for half in range(2):
                            rows = slice(64 * half, 64 * half + 64)
                            o = 16 * t + CAP * half
                            ins = dve.tensor_copy(disp[rows, t, :, o:o + CAP], hot[rows, t * E:(t + 1) * E, :])
                    step(ins)
                    ins = dve.tensor_copy(one[:], one[:])
                    ins.then_inc(*dispatched.up())
                    for t in range(T):
                        dve.wait_ge(*gathered.at(t + 1))
                        for c in range(C):
                            ins = dve.tensor_copy(xT[:, c, 0:E, 16 * t:16 * t + 16],
                                                  ps[:, 1 + t % 2, c * P:(c + 1) * P].rearrange("p (e n) -> p e n", e=E))
                        ins.then_inc(*gathered_taken.up())
                    ins = dve.tensor_tensor(disp[:].rearrange("p t e n -> p (t e) n"),
                                            disp[:].rearrange("p t e n -> p (t e) n"),
                                            w[:].rearrange("p t e -> p (t e)").unsqueeze(2).to_broadcast([P, T * E, SL]),
                                            ALU.mult)
                    ins.then_inc(*weighed.up())
                    dve.memset(xT[:, :, E, :], 0.0)
                    for e in range(E):
                        dve.wait_ge(*c_turned.at(e + 1))
                        dve.tensor_copy(cmbT[:, e, :], ps[:, 4 + e % 4, :]).then_inc(*c_taken.up())

        up_done, gelu_done, turned, mine_ready = s("switch_up"), s("switch_gelu"), s("switch_turned"), s("switch_mine_ready")
        taken = [s("switch_turned_taken_dve"), s("switch_turned_taken_act")]
        down_done, o_taken, combined, cleared = s("switch_down"), s("switch_o_taken"), s("switch_combined"), s("switch_cleared")
        HALF = 64
        with m.local(mine=[P, 2, C, SL], cm=[P, 2, N], hq=[P, 2, 512], hT=[P, 2, 512], o=[P, 2, D]) as \
                (mine, cm, hq, hT, o), m.block((o_taken, 1)) as block:
            ps = m.ps

            @block.sync
            def _(sp):
                def load_second(e):
                    for g in range(4):
                        if g % 2 == 0:
                            sp.wait_ge(*down_done.at(2 * e + g // 2 + 1))
                        sp.dma_start(wb[:, g], d["L2_ffn_W2"][e + 1, g]).then_inc(*w2_landed[g].up(16))

                with repeat(sp, E // 2 - 1) as pair:
                    for odd in range(2):
                        e = 2 * pair + odd
                        for g in range(4):
                            if g % 2 == 0:
                                sp.wait_ge(*up_done.at(2 * e + g // 2 + 1))
                            sp.dma_start(wa[:, odd, g], d["L2_ffn_W1"][e + 2, g]).then_inc(*w1_landed[odd][g].up(16))
                        load_second(e)
                load_second(E - 2)

            @block.gpsimd
            def _(pool):
                pool.memset(cm[:, 1, :], 0.0).then_inc(*cleared.up())
                pool.memset(o[:, 1, :], 0.0).then_inc(*cleared.up())

            @block.tensor
            def _(pe):
                def combine(par, first=False, last=False):
                    for t in range(T):
                        ins = pe.matmul(ps[:, 4 + t, :], cm[:, par, t * P:(t + 1) * P], o[:, par, :],
                                        start=first, stop=last)
                    ins.then_inc(*combined.up())

                pe.wait_ge(*cleared.at(2))
                combine(1, True)
                with repeat(pe, E // 2) as pair:
                    for odd in range(2):
                        e = 2 * pair + odd
                        pe.wait_ge(*mine_ready.at(e + 1))
                        for half in range(2):
                            for g in (2 * half, 2 * half + 1):
                                pe.wait_ge(*w1_landed[odd][g].at(16 * pair))
                            for k in range(C):
                                for side in range(2):
                                    ins = pe.matmul(ps[HALF * side:HALF * side + HALF, half, :], mine[:, odd, k, :],
                                                    wa[:, odd, 2 * half + side, k, :], start=(k == 0), stop=(k == C - 1))
                            ins.then_inc(*up_done.up())
                        pe.wait_ge(*o_taken.at(1 + e))
                        combine(1 - odd)
                        for half in range(2):
                            pe.wait_ge(*gelu_done.at(2 * e + half + 1))
                            for n in range(4):
                                ins = pe.transpose(ps[:, 2 + half, n * P:(n + 1) * P], hq[:, half, n * P:(n + 1) * P],
                                                   m.ident[:])
                            ins.then_inc(*turned.up())
                        for half in range(2):
                            pe.wait_ge(*taken[0].at(e + 1))
                            pe.wait_ge(*taken[half].at(e + 1))
                            for g in (2 * half, 2 * half + 1):
                                pe.wait_ge(*w2_landed[g].at(16 * e))
                            for n in range(4):
                                for side in range(2):
                                    f = n * P + HALF * side
                                    ins = pe.matmul(ps[HALF * side:HALF * side + HALF, 2, :], hT[:, half, f:f + HALF],
                                                    wb[:, 2 * half + side, n, :], start=(half == 0 and n == 0),
                                                    stop=(half == 1 and n == 3))
                            ins.then_inc(*down_done.up())
                pe.wait_ge(*o_taken.at(1 + E))
                combine(1, last=True)

            @block.scalar
            def _(act):
                with repeat(act, E) as e:
                    for half in range(2):
                        act.wait_ge(*up_done.at(2 * e + half + 1))
                        act.activation(hq[:, half, :], ps[:, half, :], ACT.Gelu_apprx_tanh).then_inc(*gelu_done.up())
                    act.wait_ge(*turned.at(2 * e + 2))
                    act.activation(hT[:, 1, :], ps[:, 3, :], ACT.Copy).then_inc(*taken[1].up())

            @block.vector
            def _(dve):
                dve.tensor_copy(mine[:, 0], xT[:, :, 0, :]).then_inc(*mine_ready.up())
                with repeat(dve, E // 2) as pair:
                    for odd in range(2):
                        e = 2 * pair + odd
                        dve.wait_ge(*up_done.at(2 * e + 2))
                        dve.tensor_copy(mine[:, 1 - odd], xT[:, :, bass.ds(e + 1, 1), :].rearrange("p c o n -> p c (o n)"))\
                           .then_inc(*mine_ready.up())
                        dve.wait_ge(*combined.at(e + 1))
                        dve.tensor_copy(cm[:, odd, :], cmbT[:, bass.ds(e, 1), :].rearrange("p o n -> p (o n)"))
                        dve.wait_ge(*turned.at(2 * e + 1))
                        dve.tensor_copy(hT[:, 0, :], ps[:, 2, :]).then_inc(*taken[0].up())
                        dve.wait_ge(*down_done.at(2 * e + 2))
                        dve.tensor_copy(o[:, odd, :], ps[:, 2, :]).then_inc(*o_taken.up())
                dve.wait_ge(*combined.at(E + 2))
                for t in range(T):
                    dve.tensor_tensor(m.x[:, t, :], m.x[:, t, :], ps[:, 4 + t, :], ALU.add)


def L3_ffn(m):
    d, E, F = m.d, 32, 2048
    FC = F // P
    s = m.sig
    Q, B4 = 4, 32
    w1_landed, w2_landed = [[[s(f"last_w{w}_landed{odd}{i}") for i in range(4)] for odd in range(2)] for w in (1, 2)]
    vectors = s("last_vectors")
    with m.local(kept=[E, B, S], mT=[P, C, E + 1, B], oT=[P, C, B, E], b1c=[P, E, FC], b2c=[P, E, C],
                 wa=[P, 2, Q, F], wb=[P, 2, Q, Q, D], fold=[P, B], gw=[P, C, E], gb=[E, 1]) as \
            (kept, mT, oT, b1c, b2c, wa, wb, fold, gw, gb):
        normalise(m, m.y, m.x, 1e-5, dstT=m.yT, ahead=(
            vectors, (gw[:], d["L3_ffn_gate_w"]), (gb[:], d["L3_ffn_gate_b"].unsqueeze(1)), (b1c[:], d["L3_ffn_b1"]),
            (b2c[:], d["L3_ffn_b2"]), (fold[:], d["fold_quarters"])))

        def first_weights(e, k):
            return w1_landed[e % 2][k], (wa[:, e % 2, k], d["L3_ffn_w1"][e, k])

        def second_weights(e, n):
            return w2_landed[e % 2][n], (wb[:, e % 2, n], d["L3_ffn_w2"][e, n])

        scored, centred, powered, step_s = s("gate_scored"), s("route_centred"), s("route_exp"), s("route_step")
        kept_ready, k_turned, kt_taken, merged, merged_taken = s("kept_ready"), s("kept_turned"), s("kept_turned_taken"), s("merged"), s("merged_taken")
        with m.local(sc=[E, B, S], left=[E, B, S], top=[E, B, 8], one=[E, B], keptT=[P, T, E]) as \
                (sc, left, top, one, keptT), m.block() as block:
            ps = m.ps

            @block.sync
            def _(sp):
                for e in range(2):
                    for k in range(Q):
                        start_loads(sp, first_weights(e, k))
                    for n in range(Q):
                        start_loads(sp, second_weights(e, n))

            @block.tensor
            def _(pe):
                pe.wait_ge(vectors.sem, vectors.made)
                for c in range(C):
                    ins = pe.matmul(ps[0:E, 0, :], gw[:, c, :], m.yT[:, c, :], start=(c == 0), stop=(c == C - 1))
                ins.then_inc(*scored.up())
                pe.wait_ge(*kept_ready.at(1))
                for t in range(T):
                    ins = pe.transpose(ps[:, 1, t * E:(t + 1) * E],
                                       kept[:, 2 * t:2 * t + 2, :].rearrange("e b s -> e (b s)"), m.ident[0:E, 0:E])
                ins.then_inc(*k_turned.up())
                pe.wait_ge(*kt_taken.at(1))
                for c in range(C):
                    for half in range(2):
                        for t in range(T):
                            rows = slice(64 * half, 64 * half + 64)
                            b = 2 * t + half
                            ins = pe.matmul(ps[:, 2 + 2 * half + c % 2, t * E:(t + 1) * E], m.y[rows, t, c * P:(c + 1) * P],
                                            keptT[rows, t, :], start=True, stop=True)
                    ins.then_inc(*merged.up())
                    if c >= 1 and c + 1 < C:
                        pe.wait_ge(*merged_taken.at(c))

            @block.scalar
            def _(act):
                act.wait_ge(*centred.at(1))
                act.activation(sc[:], sc[:], ACT.Exp).then_inc(*powered.up())

            @block.vector
            def _(dve):
                step = Chain(dve, step_s)
                wide = lambda a: a.unsqueeze(2).to_broadcast([E, B, S])
                dve.wait_ge(*scored.at(1))
                step(dve.tensor_scalar(sc[:].rearrange("e b s -> e (b s)"), ps[0:E, 0, :], gb[:, 0:1], None, ALU.add))
                step(dve.tensor_reduce(one[:], sc[:], X, ALU.max))
                dve.tensor_tensor(sc[:], sc[:], wide(one[:]), ALU.subtract).then_inc(*centred.up())
                dve.wait_ge(*powered.at(1))
                step(dve.tensor_reduce(one[:], sc[:], X, ALU.add))
                step(dve.reciprocal(one[:], one[:]))
                step(dve.tensor_tensor(sc[:], sc[:], wide(one[:]), ALU.mult))
                for b in range(B):
                    ins = dve.max(top[:, b, :], sc[:, b, :])
                step(ins)
                for b in range(B):
                    ins = dve.match_replace(left[:, b, :], top[:, b, :], sc[:, b, :], 0.0)
                step(ins)
                dve.tensor_tensor(kept[:], sc[:], left[:], ALU.subtract).then_inc(*kept_ready.up())
                dve.wait_ge(*k_turned.at(1))
                dve.tensor_copy(keptT[:].rearrange("p t e -> p (t e)"), ps[:, 1, 0:T * E]).then_inc(*kt_taken.up())
                for c in range(C):
                    dve.wait_ge(*merged.at(c + 1))
                    for half in range(2):
                        ins = dve.tensor_copy(mT[:, c, 0:E, :].rearrange("p e (t h) -> p h t e", h=2)[:, half],
                                              ps[:, 2 + 2 * half + c % 2, 0:T * E].rearrange("p (t e) -> p t e", t=T))
                    ins.then_inc(*merged_taken.up())
                dve.memset(mT[:, :, E, :], 0.0)

        up_done, down_done, h_copied, h_turned = s("last_up"), s("last_down"), s("last_h_copied"), s("last_h_turned")
        biased, h_ready, parts_copied, summed, o_taken = s("last_biased"), s("last_h_ready"), s("last_parts_copied"), s("last_summed"), s("last_o_taken")
        mine_ready, zeroed = s("last_mine_ready"), s("last_zeroed")
        with m.local(hq=[P, 512], pre=[P, FC, B], h=[P, FC, B4], part=[P, D],
                     mine=[P, 2, C, B4]) as (hq, pre, h, part, mine):
            with m.block((up_done, 1), (summed, 1), (o_taken, 1), (h_turned, 1), (mine_ready, 1)) as block:
                ps = m.ps

                @block.sync
                def _(sp):
                    with repeat(sp, E // 2 - 1) as pair:
                        for odd in range(2):
                            e = 2 * pair + odd
                            sp.wait_ge(*up_done.at(1 + e + 1))
                            for k in range(Q):
                                sp.dma_start(wa[:, odd, k], d["L3_ffn_w1"][e + 2, k]).then_inc(*w1_landed[odd][k].up(16))
                            for n in range(Q):
                                sp.wait_ge(*down_done.at(Q * e + n + 1))
                                sp.dma_start(wb[:, odd, n], d["L3_ffn_w2"][e + 2, n]).then_inc(*w2_landed[odd][n].up(16))

                @block.tensor
                def _(pe):
                    with repeat(pe, E // 2) as pair:
                        for odd in range(2):
                            e = 2 * pair + odd
                            pe.wait_ge(*mine_ready.at(1 + e + 1))
                            pe.wait_ge(*o_taken.at(e + 1))
                            for k in range(C):
                                pe.wait_ge(*w1_landed[odd][k].at(16 * pair))
                                for q in range(Q):
                                    ins = pe.matmul(ps[B4 * q:B4 * q + B4, 0, :], mine[:, odd, k, :],
                                                    wa[:, odd, k, q * 512:(q + 1) * 512], start=(k == 0), stop=(k == C - 1))
                            ins.then_inc(*up_done.up())
                            pe.wait_ge(*h_copied.at(e + 1))
                            for n in range(4):
                                ins = pe.transpose(ps[:, 1, n * P:(n + 1) * P], hq[:, n * P:(n + 1) * P], m.ident[:])
                            ins.then_inc(*h_turned.up())
                            pe.wait_ge(*h_ready.at(e + 1))
                            for n in range(Q):
                                pe.wait_ge(*w2_landed[odd][n].at(16 * pair))
                                for q in range(Q):
                                    ins = pe.matmul(ps[B4 * q:B4 * q + B4, 2, :], h[:, Q * n + q, :], wb[:, odd, n, q, :],
                                                    start=(n == 0), stop=(n == Q - 1))
                                ins.then_inc(*down_done.up())
                            pe.wait_ge(*parts_copied.at(e + 1))
                            for c in range(C):
                                ins = pe.matmul(ps[:, 3, c * B:(c + 1) * B], part[:, c * P:(c + 1) * P], fold[:],
                                                start=True, stop=True)
                            ins.then_inc(*summed.up())

                @block.scalar
                def _(act):
                    act.wait_ge(*zeroed.at(1))
                    with repeat(act, E) as e:
                        act.wait_ge(*up_done.at(1 + e + 1))
                        act.activation(hq[:], ps[:, 0, :], ACT.Copy).then_inc(*h_copied.up())
                        act.wait_ge(*biased.at(e + 1))
                        act.activation(h[:, :, 0:B], pre[:], ACT.Gelu).then_inc(*h_ready.up())
                        act.wait_ge(*down_done.at(Q * e + Q))
                        act.activation(part[:], ps[:, 2, :], ACT.Copy).then_inc(*parts_copied.up())

                @block.gpsimd
                def _(pool):
                    pool.memset(h[:], 0.0).then_inc(*zeroed.up())
                    pool.memset(mine[:], 0.0).then_inc(*zeroed.up())

                @block.vector
                def _(dve):
                    dve.wait_ge(*zeroed.at(2))
                    dve.tensor_copy(mine[:, 0, :, 0:B], mT[:, :, 0, :]).then_inc(*mine_ready.up())
                    with repeat(dve, E // 2) as pair:
                        for odd in range(2):
                            e = 2 * pair + odd
                            dve.wait_ge(*up_done.at(1 + e + 1))
                            dve.tensor_copy(mine[:, 1 - odd, :, 0:B],
                                            mT[:, :, bass.ds(e + 1, 1), :].rearrange("p c o b -> p c (o b)"))\
                               .then_inc(*mine_ready.up())
                            dve.wait_ge(*h_turned.at(1 + e + 1))
                            for n in range(4):
                                ins = dve.tensor_tensor(
                                    pre[:, Q * n:Q * n + Q, :],
                                    ps[:, 1, n * P:(n + 1) * P].rearrange("p (q b) -> p q b", q=Q)[:, :, 0:B],
                                    b1c[:, e, Q * n:Q * n + Q].unsqueeze(2).to_broadcast([P, Q, B]), ALU.add)
                            ins.then_inc(*biased.up())
                            dve.wait_ge(*summed.at(1 + e + 1))
                            dve.tensor_tensor(oT[:, :, :, e], ps[:, 3, 0:C * B].rearrange("p (c b) -> p c b", c=C),
                                              b2c[:, e, :].unsqueeze(2).to_broadcast([P, C, B]), ALU.add)\
                               .then_inc(*o_taken.up())

        o_turned, o_copied, given = s("experts_turned"), s("experts_turned_taken"), s("given_back")
        with m.local(o=[E, B, D]) as (o,), m.block() as block:
            ps = m.ps

            @block.tensor
            def _(pe):
                def give(b):
                    rows = slice(64 * (b % 2), 64 * (b % 2) + 64)
                    pe.wait_ge(*o_copied.at(b + 1))
                    pe.matmul(ps[rows, 4 + b // 2, :], kept[:, b, :], o[:, b, :], start=True, stop=True)\
                      .then_inc(*given.up())

                for b in range(B):
                    if b >= 2:
                        pe.wait_ge(*o_copied.at(b - 1))
                    for c in range(C):
                        ins = pe.transpose(ps[0:E, b % 2, c * P:(c + 1) * P], oT[:, c, b, :], m.ident[:])
                    ins.then_inc(*o_turned.up())
                    if b >= 1:
                        give(b - 1)
                give(B - 1)

            @block.vector
            def _(dve):
                for b in range(B):
                    dve.wait_ge(*o_turned.at(b + 1))
                    dve.tensor_copy(o[:, b, :], ps[0:E, b % 2, :]).then_inc(*o_copied.up())
                for t in range(T):
                    dve.wait_ge(*given.at(2 * t + 2))
                    dve.tensor_tensor(m.x[:, t, :], m.x[:, t, :], ps[:, 4 + t, :], ALU.add)


def L1_attn(m):
    d, NC = m.d, 8
    s = m.sig
    with m.local(pairs=[P, 6, NC, N], va=[P, NC, N], u=[P, NC, N], W=[P, NC, 512], vecs=[P, 8, NC], convw=[P, NC, 4],
                 inb=[P, 4 * NC], rmsw=[P, C]) as (pairs, va, u, W, vecs, convw, inb, rmsw):
        key = pairs[:, 4:6]
        flat = lambda a: a.rearrange("p c n -> p (c n)")
        weights = [flat(a).rearrange("p (k n) -> p k n", k=C) for a in (W[:], pairs[:, 2], pairs[:, 3])]
        out_sent = s("out_weights_sent")
        vectors, k_sent, small_sent = s("vectors_and_V"), s("K0_sent"), s("small_sent")
        rms_normed = pairs[:, 0, 0:T, :]
        normalise(m, m.y, m.x, 1e-5, ahead=(
            vectors, (rmsw[:], d["L1_attn_rms_w"]), (weights[0], d["L1_attn_in_V"]), (inb[:], d["L1_attn_in_proj_b"]),
            (vecs[:, 0, :], d["L1_attn_conv_b"]), (vecs[:, 1, :], d["L1_attn_gn_w"]), (vecs[:, 2, :], d["L1_attn_gn_b"]),
            (vecs[:, 3, :], d["L1_attn_D"]), (convw[:], d["L1_attn_conv_w"])))
        normalise(m, rms_normed, m.y, 1e-6, rms=True, dstT=m.yT, scale=rmsw[:], vectors=vectors)
        linear_features(m, [(va, None, weights[0], m.yT, inb[:, 0:NC], ACT.Identity)], sent=vectors,
                        ahead=(k_sent, (weights[1], d["L1_attn_in_K0"])))
        small = SmallParts(pairs, W)
        linear_features(m, [(key[:, 0], None, weights[1], m.yT, inb[:, NC:2 * NC], ACT.Identity),
                            (key[:, 1], d["L1_attn_in_K1"], weights[2], m.yT, inb[:, 2 * NC:3 * NC], ACT.Identity)],
                        sent=k_sent, beside=convolution(m, u, va, convw, vecs), ahead=(
                            small_sent, (small.weights, d["L1_attn_small_W"]),
                            (small.bias, d["L1_attn_small_b"].unsqueeze(0)),
                            (small.e3[:, 0, 0:32], d["L1_attn_dt_c"].partition_broadcast(P)),
                            (small.e3[:, 1, 0:32], d["rope_rate"])))
        with m.local(quantT=[P, 2, N], qw=[P, 2, NC, P], mean=[P, P]) as (quantT, qw, mean):
            L1_coefficients(m, va, u, pairs, W, quantT, small, small_sent)
            L1_scan(m, pairs, va, u, qw)
            zw, z = pairs[:, 2].rearrange("p c n -> p (c n)").rearrange("p (k n) -> p k n", k=C), pairs[:, 0]
            z_landed = L1_readout(m, va, u, pairs, qw, zw, mean)
            L1_gate_and_norm(m, va, u, z, pairs[:, 1], zw, mean, z_landed, vecs, inb,
                             ahead=(out_sent, (W[:], d["L1_attn_out_W"])))
        linear_tokens(m, m.x, va, None, W, NC, m.y, m.x, sent=out_sent)


def convolution(m, u, v, w, vecs):
    NC = 8
    done, step_s = m.sig("convolved"), m.sig("conv_step")

    def convolve(dve):
        step = Chain(dve, step_s)
        for c in range(NC):
            o = u[:, c, :].rearrange("p (b s) -> p b s", b=B)
            i = v[:, c, :].rearrange("p (b s) -> p b s", b=B)
            step(dve.tensor_scalar(u[:, c, :], v[:, c, :], w[:, c, 3:4], None, ALU.mult))
            for back in range(1, 4):
                ins = dve.scalar_tensor_tensor(o[:, :, back:], i[:, :, :S - back], w[:, c, 3 - back:4 - back],
                                               o[:, :, back:], ALU.mult, ALU.add)
                if back < 3:
                    step(ins)
            ins.then_inc(*done.up())

    def activate(act, n):
        if n % 2:
            c = n // 2
            act.wait_ge(*done.at(c + 1))
            act.activation(u[:, c, :], u[:, c, :], ACT.Silu, bias=vecs[:, 0, c:c + 1])

    return convolve, activate


class SmallParts:

    def __init__(self, pairs, W):
        H, NC = 32, 8
        NS = 11 * H
        self.weights = W[:].rearrange("p c n -> p (c n)")[:, 0:NC * NS].rearrange("p (c n) -> p c n", c=NC)
        self.bias = pairs[0:1, 1, 7, 0:NS]
        flat = pairs[:, 0].rearrange("p c n -> p (c n)")
        self.used = 0

        def cut(n):
            o = self.used
            self.used += T * n
            return flat[:, o:o + T * n].rearrange("p (t n) -> p t n", t=T)

        self.sm, self.sp3, self.e3, self.n3 = cut(NS), cut(3 * H), cut(3 * H), cut(3 * H)
        self.rest = [cut(H) for _ in range(10)]
        self.quant = pairs[:, 1].rearrange("p c n -> p (c n)")[:, 0:T * 8 * H].rearrange("p (t n) -> p t n", t=T)


def L1_coefficients(m, va, u, pairs, W, quantT, small, small_sent):
    d, H, NC = m.d, 32, 8
    a11, a12, kb, key = pairs[:, 0], pairs[:, 1], pairs[:, 2:4], pairs[:, 4:6]
    NS = 11 * H
    Wv, brow, quant = small.weights, small.bias, small.quant
    sm, sp3, e3, n3 = small.sm, small.sp3, small.e3, small.n3
    om, den, dt, a, w, a2, w2, det, num, t0 = small.rest
    sel = W[:].rearrange("p c n -> p (c n)").rearrange("p (g c n) -> p g c n", g=4, c=NC)
    sel_sent = m.sig("selector_sent")
    product = m.sig("tokens_product")
    step_s, act_s, to_act, to_dve = m.sig("coef_step"), m.sig("coef_act_step"), m.sig("coef_to_act"), m.sig("coef_to_dve")
    with m.block() as block:
        ps = m.ps

        @block.sync
        def _(sp):
            sp.wait_ge(*product.at(T))
            sp.dma_start(sel, d["head_spread"]).then_inc(*sel_sent.up(16))

        @block.tensor
        def _(pe):
            pe.wait_ge(small_sent.sem, small_sent.made)
            for t in range(T):
                for k in range(NC):
                    pe.matmul(ps[:, t, 0:NS], u[:, k, t * P:(t + 1) * P], Wv[:, k, :], start=(k == 0), stop=False)
                pe.matmul(ps[:, t, 0:NS], m.ones[0:1, :], brow, start=False, stop=True).then_inc(*product.up())

        @block.scalar
        def _(act):
            step = Chain(act, act_s)
            act.wait_ge(*to_act.at(1))
            step(act.activation(n3, n3, ACT.Exp))
            act.activation(n3, n3, ACT.Ln, bias=1.0).then_inc(*to_dve.up())
            act.wait_ge(*to_act.at(2))
            step(act.activation(num, num, ACT.Ln))
            act.activation(sm[:, :, 4 * H:7 * H], sm[:, :, 4 * H:7 * H], ACT.Sigmoid).then_inc(*to_dve.up())
            act.wait_ge(*to_act.at(3))
            act.activation(num, num, ACT.Exp).then_inc(*to_dve.up())
            act.wait_ge(*to_act.at(4))
            act.activation(num, num, ACT.Sqrt).then_inc(*to_dve.up())

        @block.vector
        def _(dve):
            step = Chain(dve, step_s)
            tt = lambda o, x, y, op: step(dve.tensor_tensor(o, x, y, op))
            ts = lambda o, x, y, z, op, op2=ALU.bypass: step(dve.tensor_scalar(o, x, y, z, op, op2)
                                                            if z is not None else dve.tensor_scalar(o, x, y, None, op))
            for t in range(T):
                dve.wait_ge(*product.at(t + 1))
                ins = dve.tensor_copy(sm[:, t, :], ps[:, t, 0:NS])
                dve.tensor_copy(sp3[:, t, 2 * H:3 * H], e3[:, 0, 0:H])
            step(ins)
            dve.tensor_copy(sp3[:, :, 0:H], sm[:, :, 0:H])
            step(dve.tensor_copy(sp3[:, :, H:2 * H], sm[:, :, 3 * H:4 * H]))
            ts(n3, sp3, -1.0, None, ALU.mult)
            dve.tensor_tensor(n3, sp3, n3, ALU.min).then_inc(*to_act.up())
            tt(om, sm[:, :, H:2 * H], sm[:, :, 2 * H:3 * H], ALU.add)
            tt(om, om, e3[:, 1, 0:H].unsqueeze(1).to_broadcast([P, T, H]), ALU.add)
            ts(sp3, sp3, 0.0, None, ALU.max)
            dve.wait_ge(*to_dve.at(1))
            tt(sp3, sp3, n3, ALU.add)
            alpha, seldt, dtc = sp3[:, :, 0:H], sp3[:, :, H:2 * H], sp3[:, :, 2 * H:3 * H]
            ts(den, om, -1.0, None, ALU.mult)
            tt(den, om, den, ALU.max)
            tt(den, den, alpha, ALU.add)
            ts(den, den, 0.0001, None, ALU.add)
            step(dve.reciprocal(den, den))
            tt(dt, dtc, den, ALU.mult)
            tt(dt, dt, seldt, ALU.add)
            ts(dt, dt, 0.5, None, ALU.mult)
            tt(a, dt, alpha, ALU.mult)
            tt(w, dt, om, ALU.mult)
            tt(w2, w, w, ALU.mult)
            ts(det, a, 1.0, None, ALU.add)
            tt(det, det, det, ALU.mult)
            tt(det, det, w2, ALU.add)
            step(dve.reciprocal(det, det))
            ts(num, a, -1.0, 1.0, ALU.mult, ALU.add)
            tt(num, num, num, ALU.mult)
            tt(num, num, w2, ALU.add)
            tt(num, num, det, ALU.mult)
            dve.tensor_scalar(num, num, 1e-19, None, ALU.max).then_inc(*to_act.up())
            tt(a2, a, a, ALU.mult)
            ts(a2, a2, -1.0, 1.0, ALU.mult, ALU.add)
            tt(a2, a2, w2, ALU.subtract)
            q = lambda i: quant[:, :, i * H:(i + 1) * H]
            tt(q(0), a2, det, ALU.mult)
            tt(t0, w, det, ALU.mult)
            ts(q(1), t0, 2.0, None, ALU.mult)
            dve.wait_ge(*to_dve.at(2))
            dve.tensor_copy(q(2), sm[:, :, 4 * H:5 * H])
            dve.tensor_copy(quant[:, :, 3 * H:5 * H], sm[:, :, 7 * H:9 * H])
            dve.tensor_copy(quant[:, :, 5 * H:7 * H], sm[:, :, 9 * H:11 * H])
            dve.tensor_tensor(num, num, sm[:, :, 5 * H:6 * H], ALU.mult).then_inc(*to_act.up())
            dve.wait_ge(*to_dve.at(3))
            ts(num, num, -1.0, 1.0, ALU.mult, ALU.add)
            dve.tensor_scalar(num, num, 1e-6, None, ALU.max).then_inc(*to_act.up())
            dve.wait_ge(*to_dve.at(4))
            tt(q(7), num, sm[:, :, 6 * H:7 * H], ALU.mult)

    turned, spread = m.sig("quantities_turned"), m.sig("quantities_spread")
    taken_a, taken_v = m.sig("spread_taken_act"), m.sig("spread_taken_dve")
    with m.block() as block:
        @block.tensor
        def _(pe):
            for g in range(2):
                for t in range(T):
                    ins = pe.transpose(ps[:, g, t * P:(t + 1) * P], quant[:, t, g * P:(g + 1) * P], m.ident[:])
                ins.then_inc(*turned.up())

        @block.vector
        def _(dve):
            for g in range(2):
                dve.wait_ge(*turned.at(g + 1))
                dve.tensor_copy(quantT[:, g, :], ps[:, g, :])

    def spread_of(pe, bank, q, c):
        return pe.matmul(ps[:, bank, :], sel[:, q % 4, c, :], quantT[:, q // 4, :], start=True, stop=True)

    m.spread_of = spread_of
    const_ready, mixed = m.sig("scan_constant_ready"), m.sig("scan_mix_ready")
    tb_ready, chunk_done = m.sig("scan_tb_ready"), m.sig("scan_chunk_done")
    with m.local(ta=[P, 2, N], tb=[P, 2, N], tc=[P, 2, N]) as (ta, tb, tc), m.block() as block:
        order = [(c, q) for c in range(NC) for q in (0, 1, 3, 4, 2, 7)]
        on_act = [q in (0, 1) for c, q in order]
        both = lambda a: a.unsqueeze(1).to_broadcast([P, 2, N])

        @block.tensor
        def _(pe):
            pe.wait_ge(sel_sent.sem, sel_sent.made)
            for i, (c, q) in enumerate(order):
                if i >= 8:
                    n = sum(on_act[:i - 7])
                    pe.wait_ge(*(taken_a.at(n) if on_act[i - 8] else taken_v.at(i - 7 - n)))
                spread_of(pe, i % 8, q, c).then_inc(*spread.up())

        @block.scalar
        def _(act):
            for i, (c, q) in enumerate(order):
                if on_act[i]:
                    act.wait_ge(*spread.at(i + 1))
                    act.activation((a11, a12)[q][:, c, :], ps[:, i % 8, :], ACT.Copy).then_inc(*taken_a.up())

        @block.gpsimd
        def _(pool):
            for c in range(NC):
                pool.wait_ge(*taken_v.at(4 * c + 4))
                pool.wait_ge(*taken_a.at(2 * c + 2))
                if c >= 1:
                    pool.wait_ge(*chunk_done.at(c))
                    pool.wait_ge(*const_ready.at(c))
                pool.tensor_tensor(tb[:], key[:, :, c, :], both(a12[:, c, :]), ALU.mult).then_inc(*tb_ready.up())
                pool.wait_ge(*tb_ready.at(c + 1))
                pool.wait_ge(*mixed.at(c + 1))
                pool.tensor_tensor(key[:, :, c, :], kb[:, :, c, :], both(va[:, c, :]), ALU.mult)\
                    .then_inc(*const_ready.up())

        @block.vector
        def _(dve):
            step = Chain(dve, step_s)

            def take_spreads(c):
                for j, q in enumerate((3, 4, 2, 7)):
                    i = 6 * c + 2 + j
                    dve.wait_ge(*spread.at(i + 1))
                    if q == 2:
                        dve.wait_ge(*taken_v.at(4 * c + 2))
                        ins = dve.tensor_tensor(kb[:, :, c, :], both(ps[:, i % 8, :]), key[:, :, c, :], ALU.mult)
                    elif q == 7:
                        ins = dve.tensor_tensor(va[:, c, :], ps[:, i % 8, :], u[:, c, :], ALU.mult)
                    else:
                        ins = dve.tensor_tensor(key[:, q - 3, c, :], ps[:, i % 8, :], key[:, q - 3, c, :], ALU.mult)
                    ins.then_inc(*taken_v.up())

            take_spreads(0)
            for c in range(NC):
                dve.wait_ge(*taken_a.at(2 * c + 2))
                dve.wait_ge(*taken_v.at(4 * c + 4))
                dve.tensor_tensor(ta[:], key[:, :, c, :], both(a11[:, c, :]), ALU.mult).then_inc(*mixed.up())
                if c + 1 < NC:
                    take_spreads(c + 1)
                dve.wait_ge(*mixed.at(c + 1))
                dve.wait_ge(*tb_ready.at(c + 1))
                dve.tensor_tensor(ta[:, 0, :], ta[:, 0, :], tb[:, 1, :], ALU.subtract)
                step(dve.tensor_tensor(ta[:, 1, :], ta[:, 1, :], tb[:, 0, :], ALU.add))
                dve.tensor_tensor(tb[:], ta[:], both(kb[:, 0, c, :]), ALU.mult)
                ins = dve.tensor_tensor(tc[:], ta[:], both(kb[:, 1, c, :]), ALU.mult)
                step(ins)
                dve.wait_ge(*const_ready.at(c + 1))
                dve.scalar_tensor_tensor(kb[:, 0, c, :], tc[:, 0, :], -1.0, a12[:, c, :], ALU.mult, ALU.subtract)
                step(dve.tensor_tensor(kb[:, 1, c, :], a11[:, c, :], tc[:, 1, :], ALU.subtract))
                dve.tensor_tensor(pairs[:, 0:2, c, :], pairs[:, 0:2, c, :], tb[:], ALU.subtract).then_inc(*chunk_done.up())


def L1_scan(m, pairs, q, u, qw):
    NC = 8
    CB = NC * B
    step_s = m.sig("scan_step")
    q_landed, q_done, q_taken = [m.sig("q_landed0"), m.sig("q_landed1")], m.sig("q_product"), m.sig("q_taken")
    over = lambda a: a.rearrange("p w c (b s) -> p w (c b) s", b=B)
    M, state = over(pairs[:, 0:4]).rearrange("p (i j) c s -> p i j c s", i=2), over(pairs[:, 4:6])
    UNROLL = 7
    AHEAD = NC + 4
    with m.local(terms=[P, 2, 2, CB], r=[P, 2, CB]) as (terms, r), m.block() as block:
        ps = m.ps

        @block.sync
        def _(sp):
            for n in range(AHEAD):
                if n >= 2:
                    sp.wait_ge(*q_done.at(n - 1))
                sp.dma_start(qw[:, n % 2], m.d["L1_attn_Q_W"][n]).then_inc(*q_landed[n % 2].up(16))

        @block.tensor
        def _(pe):
            for n in range(AHEAD):
                pe.wait_ge(*q_landed[n % 2].at(16 * (n // 2 + 1)))
                if 2 <= n < NC:
                    pe.wait_ge(*q_taken.at(n - 1))
                for k in range(NC):
                    ins = pe.matmul(ps[:, n % 2 if n < NC else 2 + n - NC, :], qw[:, n % 2, k, :], u[:, k, :],
                                    start=(k == 0), stop=(k == NC - 1))
                ins.then_inc(*q_done.up())

        @block.scalar
        def _(act):
            for n in range(NC):
                act.wait_ge(*q_done.at(n + 1))
                act.activation(q[:, n, :], ps[:, n % 2, :], ACT.Copy).then_inc(*q_taken.up())

        @block.vector
        def _(dve):
            with dve.Fori(0, (S - 1) // UNROLL) as i:
                Signal.times = (S - 1) // UNROLL
                step = Chain(dve, step_s, i, 3 * UNROLL)
                for j in range(1, UNROLL + 1):
                    before, now = bass.ds(i * UNROLL + j - 1, 1), bass.ds(i * UNROLL + j, 1)
                    at = lambda where: state[:, :, :, where].rearrange("p w c o -> p w (c o)")
                    step(dve.tensor_tensor(terms[:], M[:, :, :, :, now].rearrange("p i j c o -> p i j (c o)"),
                                           at(before).unsqueeze(1).to_broadcast([P, 2, 2, CB]), ALU.mult))
                    step(dve.tensor_tensor(r[:], terms[:, :, 0, :], terms[:, :, 1, :], ALU.add))
                    step(dve.tensor_tensor(at(now), at(now), r[:], ALU.add))
                step.end()
                Signal.times = 1


def L1_readout(m, y, u, pairs, qw, zw, mean):
    d, NC = m.d, 8
    ps = m.ps
    state = pairs[:, 4:6]
    q_landed, q_done, q_taken = [m.sig("q_landed0"), m.sig("q_landed1")], m.sig("q_product"), m.sig("q_taken")
    spread, used, z_landed = m.sig("quantities_spread"), m.sig("spread_used"), m.sig("z_landed")
    step_s = m.sig("readout_step")
    bank = (2, 3, 4, 5, 6, 7, 2, 3)
    with m.block() as block:
        @block.sync
        def _(sp):
            for n in range(4):
                if n >= 2:
                    sp.wait_ge(*q_done.at(n - 1))
                sp.dma_start(qw[:, n % 2], d["L1_attn_Q_W"][NC + 4 + n]).then_inc(*q_landed[n % 2].up(16))
                if n == 1:
                    sp.dma_start(zw, d["L1_attn_in_z"]).then_inc(*z_landed.up(16))
                    sp.dma_start(mean[:], d["head_mean"]).then_inc(*z_landed.up(16))

        @block.tensor
        def _(pe):
            for c in range(NC):
                for w in range(2):
                    if c >= 1:
                        pe.wait_ge(*used.at(2 * c + w - 1))
                    m.spread_of(pe, w, 5 + w, c).then_inc(*spread.up())
                if c < 4:
                    n = 4 + c
                    pe.wait_ge(*q_landed[c % 2].at(16 * (c // 2 + 1)))
                    if n >= 6:
                        pe.wait_ge(*q_taken.at(n - 5))
                    for k in range(NC):
                        ins = pe.matmul(ps[:, bank[n], :], qw[:, c % 2, k, :], u[:, k, :],
                                        start=(k == 0), stop=(k == NC - 1))
                    ins.then_inc(*q_done.up())

        @block.vector
        def _(dve):
            step = Chain(dve, step_s)
            for c in range(NC):
                for w in range(2):
                    dve.wait_ge(*spread.at(2 * c + w + 1))
                    dve.tensor_tensor(state[:, w, c, :], ps[:, w, :], state[:, w, c, :], ALU.mult).then_inc(*used.up())
                dve.wait_ge(*used.at(2 * c + 2))
                dve.tensor_tensor(y[:, c, :], y[:, c, :], state[:, 0, c, :], ALU.mult)
                if c >= 4:
                    dve.wait_ge(*q_done.at(c - 3))
                dve.tensor_tensor(state[:, 1, c, :], ps[:, bank[c], :], state[:, 1, c, :], ALU.mult).then_inc(*q_taken.up())
                dve.wait_ge(*q_taken.at(c + 1))
                step(dve.tensor_tensor(y[:, c, :], y[:, c, :], state[:, 1, c, :], ALU.add))
    return z_landed.sem, z_landed.made


def L1_gate_and_norm(m, y, u, z, squares, zw, mean, z_landed, vecs, inb, ahead):
    NC, CB = 8, 8 * B
    ps, s = m.ps, m.sig
    z_done, z_taken, step_s = s("z_product"), s("z_taken"), s("readout_step")
    centred, gated = s("group_centred"), s("y_gated")
    summed, meaned, squared, ready, rooted = s("group_summed"), s("group_mean"), s("group_squared"), s("group_var_ready"), s("group_rstd")
    Y = y[:].rearrange("p c (b s) -> p (c b) s", b=B)
    SQ = squares.rearrange("p c (b s) -> p (c b) s", b=B)
    with m.local(one=[P, CB]) as (one,), m.block() as block:
        send(block, ahead)

        @block.tensor
        def _(pe):
            pe.wait_ge(*z_landed)
            for n in range(NC):
                if n >= 4:
                    pe.wait_ge(*z_taken.at(n - 3))
                for k in range(C):
                    ins = pe.matmul(ps[:, 4 + n % 4, :], zw[:, k, n * P:(n + 1) * P], m.yT[:, k, :],
                                    start=(k == 0), stop=(k == C - 1))
                ins.then_inc(*z_done.up())
                if n in (0, 4):
                    i = n // 4
                    pe.wait_ge(*summed.at(i + 1))
                    pe.matmul(ps[:, i, 0:CB], mean[:], one[:], start=True, stop=True).then_inc(*meaned.up())

        @block.scalar
        def _(act):
            def take_z(n):
                act.wait_ge(*z_done.at(n + 1))
                act.activation(z[:, n, :], ps[:, 4 + n % 4, :], ACT.Silu, bias=inb[:, 3 * NC + n:3 * NC + n + 1])\
                   .then_inc(*z_taken.up())

            take_z(0)
            for half in range(2):
                act.wait_ge(*centred.at(half + 1))
                act.activation(squares[:, 4 * half:4 * half + 4, :], y[:, 4 * half:4 * half + 4, :], ACT.Square)\
                   .then_inc(*squared.up())
            for n in range(1, NC):
                take_z(n)
                if n == 4:
                    act.wait_ge(*ready.at(1))
                    act.activation(one[:], one[:], ACT.Sqrt).then_inc(*rooted.up())

        @block.vector
        def _(dve):
            step = Chain(dve, step_s)
            dve.tensor_reduce(one[:], Y, X, ALU.add).then_inc(*summed.up())
            dve.wait_ge(*meaned.at(1))
            for half in range(2):
                cols = slice(CB // 2 * half, CB // 2 * half + CB // 2)
                dve.tensor_tensor(Y[:, cols], Y[:, cols],
                                  ps[:, 0, cols].unsqueeze(2).to_broadcast([P, CB // 2, S]), ALU.subtract)\
                   .then_inc(*centred.up())
            for half in range(2):
                cols = slice(CB // 2 * half, CB // 2 * half + CB // 2)
                dve.wait_ge(*squared.at(half + 1))
                ins = dve.tensor_reduce(one[:, cols], SQ[:, cols], X, ALU.add)
            ins.then_inc(*summed.up())
            dve.wait_ge(*meaned.at(2))
            dve.tensor_scalar(one[:], ps[:, 1, 0:CB], 1e-5, None, ALU.add).then_inc(*ready.up())
            dve.wait_ge(*rooted.at(1))
            step(dve.reciprocal(one[:], one[:]))
            step(dve.tensor_tensor(one[:].rearrange("p (c b) -> p c b", b=B), one[:].rearrange("p (c b) -> p c b", b=B),
                                   vecs[:, 1, :].unsqueeze(2).to_broadcast([P, NC, B]), ALU.mult))
            for c in range(NC):
                cols = slice(B * c, B * c + B)
                ins = dve.tensor_tensor(Y[:, cols], Y[:, cols], one[:, cols].unsqueeze(2).to_broadcast([P, B, S]), ALU.mult)
            step(ins)
            for c in range(NC):
                dve.wait_ge(*z_taken.at(c + 1))
                ins = dve.scalar_tensor_tensor(y[:, c, :], y[:, c, :], vecs[:, 2, c:c + 1], z[:, c, :], ALU.add, ALU.mult)
                ins.then_inc(*gated.up())
            for c in range(NC):
                dve.wait_ge(*gated.at(c + 1))
                dve.scalar_tensor_tensor(y[:, c, :], u[:, c, :], vecs[:, 3, c:c + 1], y[:, c, :], ALU.mult, ALU.add)


STAGES = (L0_xattn, L0_attn, L0_ffn, L1_xattn, L1_attn, L1_ffn,
          L2_xattn, L2_attn, L2_ffn, L3_xattn, L3_attn, L3_ffn)


def perceiver_program(nc, d, out, stages=STAGES):
    with ExitStack() as ctx:
        m = Machine(nc, ctx, d)
        constants(m)
        for stage in stages:
            stage(m)
            m.stage_done()
        stored = m.sig("stored")
        with m.block() as block:
            @block.sync
            def _(sp):
                sp.dma_start(out, m.x[:]).then_inc(*stored.up(16))
                sp.wait_ge(*stored.at(16))


def _lay_out(inputs):
    def rows(w):
        w = np.asarray(w)
        return np.ascontiguousarray(w.reshape(w.shape[0] // P, P, w.shape[1]).transpose(1, 0, 2))

    def cols(v):
        v = np.asarray(v)
        return np.ascontiguousarray(v.reshape(-1, P).T)

    def by_groups_up(w):
        return np.ascontiguousarray(w.reshape(-1, C, P, 4, w.shape[2] // 4).transpose(0, 3, 2, 1, 4))

    def by_groups_down(w):
        return np.ascontiguousarray(w.reshape(w.shape[0], 4, -1, P, D).transpose(0, 1, 3, 2, 4))

    g = {k: np.asarray(v) for k, v in inputs.items()}
    a = {"x": np.ascontiguousarray(g["x"].reshape(T, P, D).transpose(1, 0, 2)),
         "ctx": np.ascontiguousarray(g["ctx_1024"].reshape(B, KC, P, D).transpose(0, 2, 1, 3)),
         "ctxT": np.ascontiguousarray(g["ctx_1024"].transpose(0, 2, 1).reshape(B, C, P, SK).transpose(0, 2, 1, 3)),
         "mask": g["mask_BxSxS2_ff0"]}
    for L in ("L0_xattn", "L3_xattn"):
        t = (lambda w: w.T) if L == "L0_xattn" else (lambda w: w)
        for n in ("Wq", "Wk", "Wv", "Wo"):
            a[f"{L}_{n}"] = rows(t(g[f"{L}_{n}"]))
        a[f"{L}_bq"], a[f"{L}_bk"] = cols(g[f"{L}_bq"]), cols(g[f"{L}_bk"])
        a[f"{L}_bv"], a[f"{L}_bo"] = g[f"{L}_bv"], g[f"{L}_bo"]
    for i, n in enumerate("qkv"):
        a[f"L0_attn_w_{n}"] = rows(g["L0_attn_w_qkv"][i * D:(i + 1) * D].T)
    a["L0_attn_w_proj"] = rows(g["L0_attn_w_proj"].T)
    q, k = np.arange(P)[:, None] % S, np.arange(S)[None, :]
    a["causal"] = np.where(k <= q, np.float32(100), np.float32(-100))
    for n in (4, 8):
        a[f"before{n}"] = np.tril(np.ones((n, n), np.float32), -1)
    a["L0_ffn_ln_scale"], a["L0_ffn_ln_bias"] = cols(g["L0_ffn_ln_scale"]), cols(g["L0_ffn_ln_bias"])
    a["L0_ffn_gate_w"] = rows(g["L0_ffn_gate_w"].T)
    for n in ("Wg", "Wu", "Wd"):
        a[f"L0_ffn_{n}"] = np.stack([rows(w) for w in g[f"L0_ffn_{n}"]] + [rows(g[f"L0_ffn_s{n}"])])
    for n in ("Wq", "Wk", "Wv", "Wo"):
        a[f"L1_xattn_{n}"] = rows(g[f"L1_xattn_{n}"])
    for n in ("pre_g", "pre_b", "ln_g", "ln_b"):
        a[f"L1_xattn_{n}"] = cols(g[f"L1_xattn_{n}"])
    a["L1_xattn_ln_g_row"], a["L1_xattn_ln_b_row"] = g["L1_xattn_ln_g"], g["L1_xattn_ln_b"]
    a["L1_ffn_gate_W"], a["L1_ffn_gate_b"] = rows(g["L1_ffn_gate_W"]), g["L1_ffn_gate_b"]
    for n in ("W1", "W2"):
        a[f"L1_ffn_{n}"] = np.stack([rows(w) for w in g[f"L1_ffn_{n}"]])
    for n in ("b1", "b2", "g2", "be2"):
        a[f"L1_ffn_{n}"] = g[f"L1_ffn_{n}"]
    for n in ("g1", "be1"):
        a[f"L1_ffn_{n}"] = np.ascontiguousarray(g[f"L1_ffn_{n}"].reshape(4, C, P).transpose(2, 0, 1))
    a["L2_xattn_Wq"], a["L2_xattn_Wk"] = rows(g["L2_xattn_Wq"].T), rows(g["L2_xattn_Wk"])
    a["L2_xattn_Wv"], a["L2_xattn_bv"] = rows(g["L2_xattn_Wv"].T), g["L2_xattn_bv"]
    a["L2_xattn_bq"], a["L2_xattn_bk"] = cols(g["L2_xattn_bq"]), cols(g["L2_xattn_bk"])
    for i in range(2):
        for n in ("ln1_g", "ln1_b", "bq", "bk", "ln2_g", "ln2_b", "b1"):
            a[f"L2_attn_{n}_{i}"] = cols(g[f"L2_attn_{n}"][i])
        for n in ("bv", "bo", "b2"):
            a[f"L2_attn_{n}_{i}"] = np.ascontiguousarray(g[f"L2_attn_{n}"][i])
        for n in ("wq", "wk", "wv", "wo", "w1", "w2"):
            a[f"L2_attn_{n}_{i}"] = rows(g[f"L2_attn_{n}"][i])
    a["L2_attn_lnf_g"], a["L2_attn_lnf_b"] = g["L2_attn_lnf_g"], g["L2_attn_lnf_b"]
    a["strided"] = np.where((q % 3 != 0) | (k <= q), np.finfo(np.float32).max, np.float32(-1e30))
    for n in ("g1", "beta1", "bq", "bk", "g2", "beta2", "b1"):
        a[f"L3_attn_{n}"] = cols(g[f"L3_attn_{n}"])
    for n in ("bv", "bo", "b2"):
        a[f"L3_attn_{n}"] = g[f"L3_attn_{n}"]
    for n in ("Wq", "Wk", "Wv", "Wo", "W1", "W2"):
        a[f"L3_attn_{n}"] = rows(g[f"L3_attn_{n}"])
    hd = 32
    freq = np.float32(1) / np.float32(10000) ** (np.arange(0, hd, 2, dtype=np.float32) / np.float32(hd))
    angle = freq[(np.arange(P) % hd) // 2][:, None] * np.arange(S, dtype=np.float32)[None, :]
    a["rope_trig"] = np.stack([np.cos(angle), np.sin(angle)], 1).astype(np.float32)
    turn_pairs = np.zeros((P, P), np.float32)
    for i in range(0, P, 2):
        turn_pairs[i + 1, i], turn_pairs[i, i + 1] = -1, 1
    a["rope_turn"] = turn_pairs
    NC, H = 8, 32
    w, b = g["L1_attn_in_proj_W"], g["L1_attn_in_proj_b"]
    part = {"z": slice(0, 1024), "K0": slice(1024, 3072, 2), "K1": slice(1025, 3072, 2), "V": slice(3072, 4096)}
    for n, r in part.items():
        a[f"L1_attn_in_{n}"] = rows(w[r].T)
    a["L1_attn_in_proj_b"] = np.concatenate([cols(b[part[n]]) for n in ("V", "K0", "K1", "z")], 1)
    for n in ("conv_b", "gn_w", "gn_b", "D", "rms_w"):
        a[f"L1_attn_{n}"] = cols(g[f"L1_attn_{n}"])
    a["L1_attn_conv_w"] = np.ascontiguousarray(g["L1_attn_conv_w"].reshape(NC, P, 4).transpose(1, 0, 2))
    L = "L1_attn_"
    small = [g[L + "dyn_W"], g[L + "seldt_W"], g[L + "beta_W"], g[L + "rg_W"], g[L + "ug_W"], g[L + "selB_W"][0::2],
             g[L + "selB_W"][1::2], g[L + "selC_W"][0::2], g[L + "selC_W"][1::2]]
    a["L1_attn_small_W"] = rows(np.concatenate(small, 0).T)
    none = np.zeros(H, np.float32)
    a["L1_attn_small_b"] = np.concatenate([g[L + "dyn_b"], none, g[L + "beta_b"], g[L + "rg_b"], g[L + "ug_b"],
                                           none, none, none, none])
    a["L1_attn_dt_c"] = g["L1_attn_dt_c"]
    rate = np.float32(1) / np.float32(10000) ** (np.arange(H, dtype=np.float32) / np.float32(H))
    a["rope_rate"] = (np.arange(P) % S).astype(np.float32)[:, None] * rate[None, :]
    r, q, c, p = np.ogrid[0:P, 0:4, 0:NC, 0:P]
    a["head_spread"] = (r == H * q + 4 * c + p // 32).astype(np.float32)
    a["head_mean"] = (np.arange(P)[:, None] // 32 == np.arange(P)[None, :] // 32).astype(np.float32) / np.float32(32 * S)
    Q = np.stack([g["L1_attn_Q_W"][0::2], g["L1_attn_Q_W"][1::2]])
    a["L1_attn_Q_W"] = np.stack([rows(Q[i, c * P:(c + 1) * P].T) for i in range(2) for c in range(NC)])
    a["L1_attn_out_W"] = rows(g["L1_attn_out_W"].T)
    E2, F2 = 8, 2048
    a["L2_ffn_Wg"] = rows(g["L2_ffn_Wg"])
    tok = np.arange(P)
    a["earlier"] = ((tok[:, None] < tok[None, :]) & (tok[:, None] // S == tok[None, :] // S)).astype(np.float32)
    a["place"] = np.arange(S // E2, dtype=np.float32)
    a["L2_ffn_W1"] = by_groups_up(g["L2_ffn_W1"])
    a["L2_ffn_W2"] = by_groups_down(g["L2_ffn_W2"])
    a["L3_ffn_gate_w"], a["L3_ffn_gate_b"] = rows(g["L3_ffn_gate_w"].T), g["L3_ffn_gate_b"]
    w1, w2 = g["L3_ffn_w1"], g["L3_ffn_w2"]
    a["L3_ffn_w1"] = np.ascontiguousarray(w1[:, :D].reshape(-1, C, P, F2))
    a["L3_ffn_w2"] = np.ascontiguousarray(w2[:, :F2].reshape(-1, 4, 4, P, D).transpose(0, 2, 3, 1, 4))
    a["L3_ffn_b1"] = np.ascontiguousarray(w1[:, D].reshape(-1, 4, 4, P).transpose(3, 0, 2, 1).reshape(P, -1, F2 // P))
    a["fold_quarters"] = (np.arange(P)[:, None] % 32 == np.arange(B)[None, :]).astype(np.float32)
    a["L3_ffn_b2"] = np.ascontiguousarray(w2[:, F2].reshape(-1, C, P).transpose(2, 0, 1))
    return a


def kernel(**inputs):
    import concourse.bacc as bacc
    from concourse.bass_utils import run_bass_kernel_spmd

    nc = bacc.Bacc("TRN2", target_bir_lowering=False, num_devices=1)
    arrays = {f"in_{k}": v for k, v in _lay_out(inputs).items()}
    d = {k[3:]: nc.dram_tensor(k, v.shape, mybir.dt.from_np(v.dtype), kind="ExternalInput").ap()
         for k, v in arrays.items()}
    out = nc.dram_tensor("out", (B, S, D), F32, kind="ExternalOutput").ap()
    perceiver_program(nc, d, out.rearrange("(t two) s d -> (two s) t d", two=2))
    r = run_bass_kernel_spmd(nc, [arrays], core_ids=[0])
    return r.results[0]["out"]
```
